# Optimizing a Trainium2 kernel written in Bass

```python
import numpy as np
import jax
import jax.numpy as jnp

def _softmax(x, axis=-1):
    return jax.nn.softmax(x, axis=axis)

def _gelu(x):
    return jax.nn.gelu(x, approximate=True)

def _silu(x):
    return jax.nn.silu(x)

def _sigmoid(x):
    return jax.nn.sigmoid(x)

def _layernorm(x, axis=-1, eps=1e-05):
    m = jnp.mean(x, axis=axis, keepdims=True)
    v = jnp.var(x, axis=axis, keepdims=True)
    return (x - m) / jnp.sqrt(v + eps)

def _scatter_add(tgt, idx, src, axis=0):
    return tgt.at[idx].add(src)

def _segment_sum(src, seg, n):
    return jax.ops.segment_sum(src, seg, n)
kernel_name = 'mk_decoder_preln_d4_seqx_r4_383344'

def setup_inputs(seed: int=0):
    np.random.seed(seed)
    _w = jnp.asarray

    def _rec_inputs():
        import jax
        import jax.numpy as jnp
        _rk = jax.random.key(seed)
        x = -0.000125 + 0.9999 * jax.random.normal(jax.random.fold_in(_rk, 1), (4, 512, 256), jnp.float32)
        _lenS = 512 - jax.random.randint(jax.random.fold_in(_rk, 7), (4,), 0, max(1, 512 // 4) + 1, jnp.int32)
        _lenS2 = 64 - jax.random.randint(jax.random.fold_in(_rk, 8), (4,), 0, max(1, 64 // 4) + 1, jnp.int32)
        _ctx_768P = jax.random.normal(jax.random.fold_in(_rk, 11), (4, 16, 192), jnp.float32)
        _ctx_768c = jax.random.dirichlet(jax.random.fold_in(_rk, 511), 0.3 * jnp.ones((16,), jnp.float32), (4, 64))
        _ctx_768t = jnp.einsum('bsk,bkd->bsd', _ctx_768c, _ctx_768P)
        _ctx_768t = _ctx_768t * jax.lax.rsqrt(jnp.mean(jnp.square(_ctx_768t)) + 1e-12) * 0.953939
        ctx_768 = 0.00272024 + 0.999456 * (_ctx_768t + 0.3 * jax.random.normal(jax.random.fold_in(_rk, 611), (4, 64, 192), jnp.float32))
        return (x, ctx_768)
    x, ctx_768 = _rec_inputs()

    def _L0_attn_setup():
        import jax, jax.numpy as jnp
        import numpy as np
        D_MODEL = 256
        N_HEADS = 16
        D_HEAD = D_MODEL // N_HEADS
        WINDOW = 64
        CAUSAL = True
        NEG = -1000000000.0

        def build_sliding_window_mask(seq_len, window_size, causal=True):
            i = jnp.arange(seq_len)[:, None]
            j = jnp.arange(seq_len)[None, :]
            if causal:
                attend = (j <= i) & (j >= i - window_size)
            else:
                half = window_size // 2
                attend = jnp.abs(j - i) <= half
            return jnp.where(attend, 0.0, NEG).astype(jnp.float32)
        key = jax.random.key(seed)
        k0, k1, k2, k3, k4 = jax.random.split(key, 5)
        B, T = (1, 1024)
        s = 1.0 / np.sqrt(D_MODEL)
        return {'x': jax.random.normal(k0, (B, T, D_MODEL), dtype=jnp.float32), 'Wq': jax.random.normal(k1, (D_MODEL, D_MODEL), dtype=jnp.float32) * s, 'Wk': jax.random.normal(k2, (D_MODEL, D_MODEL), dtype=jnp.float32) * s, 'Wv': jax.random.normal(k3, (D_MODEL, D_MODEL), dtype=jnp.float32) * s, 'Wo': jax.random.normal(k4, (D_MODEL, D_MODEL), dtype=jnp.float32) * s}
    _L0_attn_all = _L0_attn_setup()
    _L0_attn_in = {k: v for k, v in _L0_attn_all.items() if k in ('Wq', 'Wk', 'Wv', 'Wo')}
    del _L0_attn_all

    def _L0_xattn_setup():
        import jax, jax.numpy as jnp
        import numpy as np
        HEADS = 16
        DIM_HEAD = 64
        SCALE = DIM_HEAD ** (-0.5)
        QUERY_DIM = 256
        CONTEXT_DIM = 192
        INNER_DIM = HEADS * DIM_HEAD
        key = jax.random.key(seed)
        ks = jax.random.split(key, 7)
        B, Nq, Nk = (8, 1024, 77)
        x = jax.random.normal(ks[0], (B, Nq, QUERY_DIM), dtype=jnp.float32)
        context = jax.random.normal(ks[1], (B, Nk, CONTEXT_DIM), dtype=jnp.float32)
        Wq = jax.random.normal(ks[2], (QUERY_DIM, INNER_DIM), dtype=jnp.float32) * QUERY_DIM ** (-0.5)
        Wk = jax.random.normal(ks[3], (CONTEXT_DIM, INNER_DIM), dtype=jnp.float32) * CONTEXT_DIM ** (-0.5)
        Wv = jax.random.normal(ks[4], (CONTEXT_DIM, INNER_DIM), dtype=jnp.float32) * CONTEXT_DIM ** (-0.5)
        Wo = jax.random.normal(ks[5], (INNER_DIM, QUERY_DIM), dtype=jnp.float32) * INNER_DIM ** (-0.5)
        bo = jnp.zeros((QUERY_DIM,), dtype=jnp.float32)
        return {'x': x, 'context': context, 'Wq': Wq, 'Wk': Wk, 'Wv': Wv, 'Wo': Wo, 'bo': bo}
    _L0_xattn_all = _L0_xattn_setup()
    _L0_xattn_in = {k: v for k, v in _L0_xattn_all.items() if k in ('Wq', 'Wk', 'Wv', 'Wo', 'bo')}
    del _L0_xattn_all

    def _L0_ffn_setup():
        import math
        import jax, jax.numpy as jnp
        import numpy as np
        NUM_EXPERTS = 8
        TOP_K = 2
        CAPACITY_FACTOR = 1.0
        B, S, H, I = (4, 512, 256, 1024)
        key = jax.random.key(seed)
        k_x, k_rw, k_wi, k_wo = jax.random.split(key, 4)
        x = jax.random.normal(k_x, (B, S, H), dtype=jnp.float32)
        lim = math.sqrt(6.0 / (H + NUM_EXPERTS))
        router_w = jax.random.uniform(k_rw, (NUM_EXPERTS, H), minval=-lim, maxval=lim, dtype=jnp.float32)
        router_b = jnp.zeros((NUM_EXPERTS,), dtype=jnp.float32)
        experts_inter = jax.random.normal(k_wi, (NUM_EXPERTS - 1, H, I), dtype=jnp.float32) / math.sqrt(H)
        experts_out = jax.random.normal(k_wo, (NUM_EXPERTS - 1, I, H), dtype=jnp.float32) / math.sqrt(I)
        return {'x': x, 'router_w': router_w, 'router_b': router_b, 'experts_inter': experts_inter, 'experts_out': experts_out}
    _L0_ffn_all = _L0_ffn_setup()
    _L0_ffn_in = {k: v for k, v in _L0_ffn_all.items() if k in ('router_w', 'router_b', 'experts_inter', 'experts_out')}
    del _L0_ffn_all

    def _L1_attn_setup():
        import jax, jax.numpy as jnp
        import numpy as np
        EMBED_DIM = 256
        NUM_HEADS = 16
        HEAD_DIM = EMBED_DIM // NUM_HEADS
        key = jax.random.key(seed)
        ks = jax.random.split(key, 9)
        B, S, D = (4, 512, EMBED_DIM)
        s = 1.0 / np.sqrt(D)
        inp = {'x': jax.random.normal(ks[0], (B, S, D), dtype=jnp.float32), 'Wq': jax.random.uniform(ks[1], (D, D), jnp.float32, -s, s), 'bq': jax.random.uniform(ks[2], (D,), jnp.float32, -s, s), 'Wk': jax.random.uniform(ks[3], (D, D), jnp.float32, -s, s), 'bk': jax.random.uniform(ks[4], (D,), jnp.float32, -s, s), 'Wv': jax.random.uniform(ks[5], (D, D), jnp.float32, -s, s), 'bv': jax.random.uniform(ks[6], (D,), jnp.float32, -s, s), 'Wo': jax.random.uniform(ks[7], (D, D), jnp.float32, -s, s), 'bo': jax.random.uniform(ks[8], (D,), jnp.float32, -s, s)}
        return inp
    _L1_attn_all = _L1_attn_setup()
    _L1_attn_in = {k: v for k, v in _L1_attn_all.items() if k in ('Wq', 'bq', 'Wk', 'bk', 'Wv', 'bv', 'Wo', 'bo')}
    del _L1_attn_all

    def _L1_xattn_setup():
        import jax, jax.numpy as jnp
        import numpy as np
        N_HEADS = 16
        key = jax.random.key(seed)
        ks = jax.random.split(key, 8)
        b, l, m = (8, 256, 256)
        d_embed, d_cross = (256, 192)
        s_q = 1.0 / np.sqrt(d_embed)
        s_kv = 1.0 / np.sqrt(d_cross)
        return {'x': jax.random.normal(ks[0], (b, l, d_embed), jnp.float32), 'y': jax.random.normal(ks[1], (b, m, d_cross), jnp.float32), 'Wq': jax.random.normal(ks[2], (d_embed, d_embed), jnp.float32) * s_q, 'bq': jax.random.normal(ks[3], (d_embed,), jnp.float32) * 0.01, 'Wkv': jax.random.normal(ks[4], (2 * d_embed, d_cross), jnp.float32) * s_kv, 'bkv': jax.random.normal(ks[5], (2 * d_embed,), jnp.float32) * 0.01, 'Wo': jax.random.normal(ks[6], (d_embed, d_embed), jnp.float32) * s_q, 'bo': jax.random.normal(ks[7], (d_embed,), jnp.float32) * 0.01}
    _L1_xattn_all = _L1_xattn_setup()
    _L1_xattn_in = {k: v for k, v in _L1_xattn_all.items() if k in ('Wq', 'bq', 'Wkv', 'bkv', 'Wo', 'bo')}
    del _L1_xattn_all

    def _L1_ffn_setup():
        import jax, jax.numpy as jnp
        import numpy as np
        key = jax.random.key(seed)
        ks = jax.random.split(key, 5)
        B, Sq, M, E, H = (4, 512, 256, 8, 1024)
        x = jax.random.normal(ks[0], (B, Sq, M), dtype=jnp.float32)
        wg = jax.random.normal(ks[1], (M, E), dtype=jnp.float32) * (1.0 / np.sqrt(M))
        w1 = jax.random.normal(ks[2], (E, M, H), dtype=jnp.float32) * (1.0 / np.sqrt(M))
        b1 = jnp.zeros((E, H), dtype=jnp.float32)
        w2 = jax.random.normal(ks[3], (E, H, M), dtype=jnp.float32) * (1.0 / np.sqrt(H))
        b2 = jnp.zeros((E, M), dtype=jnp.float32)
        return {'x': x, 'wg': wg, 'w1': w1, 'b1': b1, 'w2': w2, 'b2': b2}
    _L1_ffn_all = _L1_ffn_setup()
    _L1_ffn_in = {k: v for k, v in _L1_ffn_all.items() if k in ('wg', 'w1', 'b1', 'w2', 'b2')}
    del _L1_ffn_all

    def _L2_attn_setup():
        import jax, jax.numpy as jnp
        import numpy as np
        D_MODEL, D_STATE, D_CONV, EXPAND = (256, 16, 4, 2)
        D_INNER = EXPAND * D_MODEL
        B_SZ, L_SEQ = (2, 512)
        LN_EPS = 1e-05

        def _selective_scan(u, dt, A, Bp, Cp):

            def step(h, inp):
                dt_t, B_t, C_t, u_t = inp
                dA = jnp.exp(jnp.clip(dt_t[:, :, None] * A, -20.0, 0.0))
                dB_u = jnp.clip(dt_t[:, :, None] * B_t[:, None, :] * u_t[:, :, None], -10.0, 10.0)
                h = jnp.clip(h * dA + dB_u, -100.0, 100.0)
                y = jnp.einsum('bdn,bn->bd', h, C_t)
                return (h, y)
            h0 = jnp.zeros((u.shape[0], u.shape[2], A.shape[0]), dtype=u.dtype)
            xs = (jnp.swapaxes(dt, 0, 1), jnp.swapaxes(Bp, 0, 1), jnp.swapaxes(Cp, 0, 1), jnp.swapaxes(u, 0, 1))
            _, ys = jax.lax.scan(step, h0, xs)
            return jnp.swapaxes(ys, 0, 1)
        key = jax.random.key(seed)
        ks = jax.random.split(key, 8)
        x = jax.random.normal(ks[0], (B_SZ, L_SEQ, D_MODEL), dtype=jnp.float32)
        W_in = jax.random.normal(ks[1], (2 * D_INNER, D_MODEL), dtype=jnp.float32) * (1.0 / np.sqrt(D_MODEL))
        conv_w = jax.random.normal(ks[2], (D_INNER, 1, D_CONV), dtype=jnp.float32) * (1.0 / np.sqrt(D_CONV))
        conv_b = jax.random.normal(ks[3], (D_INNER,), dtype=jnp.float32) * 0.01
        W_x = jax.random.normal(ks[4], (2 * D_STATE + 1, D_INNER), dtype=jnp.float32) * (1.0 / np.sqrt(D_INNER))
        W_dt = jax.random.uniform(ks[5], (D_INNER, 1), dtype=jnp.float32, minval=-0.01, maxval=0.01)
        b_dt = jnp.full((D_INNER,), 0.1, dtype=jnp.float32)
        A_log = jnp.log(jnp.arange(1, D_STATE + 1, dtype=jnp.float32) * 0.1)
        D_param = jnp.ones((D_INNER,), dtype=jnp.float32)
        W_out = jax.random.normal(ks[6], (D_MODEL, D_INNER), dtype=jnp.float32) * (1.0 / np.sqrt(D_INNER))
        ln_g = jnp.ones((D_INNER,), dtype=jnp.float32)
        ln_b = jnp.zeros((D_INNER,), dtype=jnp.float32)
        return {'x': x, 'W_in': W_in, 'conv_w': conv_w, 'conv_b': conv_b, 'W_x': W_x, 'W_dt': W_dt, 'b_dt': b_dt, 'A_log': A_log, 'D_param': D_param, 'W_out': W_out, 'ln_g': ln_g, 'ln_b': ln_b}
    _L2_attn_all = _L2_attn_setup()
    _L2_attn_in = {k: v for k, v in _L2_attn_all.items() if k in ('W_in', 'conv_w', 'conv_b', 'W_x', 'W_dt', 'b_dt', 'A_log', 'D_param', 'W_out', 'ln_g', 'ln_b')}
    del _L2_attn_all

    def _L2_xattn_setup():
        import jax, jax.numpy as jnp
        import numpy as np
        DIM = 256
        CTX_DIM = 192
        H = 16
        DH = 64
        INNER = H * DH
        EPS = 1e-05

        def layer_norm(x, gamma, beta):
            mu = jnp.mean(x, axis=-1, keepdims=True)
            var = jnp.mean(jnp.square(x - mu), axis=-1, keepdims=True)
            return (x - mu) * jax.lax.rsqrt(var + EPS) * gamma + beta
        key = jax.random.key(seed)
        ks = jax.random.split(key, 8)
        B, N, M = (4, 512, 512)
        x = jax.random.normal(ks[0], (B, N, DIM), dtype=jnp.float32)
        context = jax.random.normal(ks[1], (B, M, CTX_DIM), dtype=jnp.float32)
        g_x = jnp.ones((DIM,), jnp.float32)
        b_x = jnp.zeros((DIM,), jnp.float32)
        g_c = jnp.ones((CTX_DIM,), jnp.float32)
        b_c = jnp.zeros((CTX_DIM,), jnp.float32)
        Wq = jax.random.normal(ks[2], (DIM, INNER), dtype=jnp.float32) / np.sqrt(DIM)
        Wk = jax.random.normal(ks[3], (CTX_DIM, INNER), dtype=jnp.float32) / np.sqrt(CTX_DIM)
        Wv = jax.random.normal(ks[4], (CTX_DIM, INNER), dtype=jnp.float32) / np.sqrt(CTX_DIM)
        Wo = jax.random.normal(ks[5], (INNER, DIM), dtype=jnp.float32) / np.sqrt(INNER)
        return {'x': x, 'context': context, 'g_x': g_x, 'b_x': b_x, 'g_c': g_c, 'b_c': b_c, 'Wq': Wq, 'Wk': Wk, 'Wv': Wv, 'Wo': Wo}
    _L2_xattn_all = _L2_xattn_setup()
    _L2_xattn_in = {k: v for k, v in _L2_xattn_all.items() if k in ('g_x', 'b_x', 'g_c', 'b_c', 'Wq', 'Wk', 'Wv', 'Wo')}
    del _L2_xattn_all

    def _L2_ffn_setup():
        import jax, jax.numpy as jnp
        import numpy as np
        BLOCK = 32
        W_BITS = 4
        ACT_BITS = 16

        def act_qdq(x):
            qmax = 2.0 ** (ACT_BITS - 1) - 1.0
            scale = jnp.maximum(jnp.max(jnp.abs(x)) / qmax, 1e-12)
            return jnp.clip(jnp.round(x / scale), -qmax - 1.0, qmax) * scale

        def fixed_qdq_u16(x):
            scale = 1.0 / 65536.0
            return jnp.clip(jnp.round(x / scale), 0.0, 65535.0) * scale

        def lpbq_dequant(w):
            O, I = w.shape
            qmax = 2.0 ** (W_BITS - 1) - 1.0
            wb = w.reshape(O, I // BLOCK, BLOCK)
            s = jnp.maximum(jnp.max(jnp.abs(wb), axis=-1, keepdims=True) / qmax, 1e-12)
            wq = jnp.clip(jnp.round(wb / s), -qmax - 1.0, qmax) * s
            return wq.reshape(O, I)
        key = jax.random.key(seed)
        k1, k2, k3, k4 = jax.random.split(key, 4)
        B, S, H, I = (2, 1024, 256, 768)
        x = jax.random.normal(k1, (B, S, H), jnp.float32)
        w_gate = jax.random.normal(k2, (I, H), jnp.float32) * 0.02
        w_up = jax.random.normal(k3, (I, H), jnp.float32) * 0.02
        w_down = jax.random.normal(k4, (H, I), jnp.float32) * 0.02
        return {'x': x, 'w_gate': w_gate, 'w_up': w_up, 'w_down': w_down}
    _L2_ffn_all = _L2_ffn_setup()
    _L2_ffn_in = {k: v for k, v in _L2_ffn_all.items() if k in ('w_gate', 'w_up', 'w_down')}
    del _L2_ffn_all

    def _L3_attn_setup():
        import jax, jax.numpy as jnp
        import numpy as np
        LN_EPS = 1e-05
        CLAMP = 1000000.0
        key = jax.random.key(seed)
        k0, k1, k2, k3 = jax.random.split(key, 4)
        Bsz, L, D, N = (8, 512, 256, 64)
        x = jax.random.normal(k0, (Bsz, L, D), dtype=jnp.float32)
        A = jax.random.normal(k1, (N, N), dtype=jnp.float32) * 0.01
        B = jax.random.normal(k2, (N, D), dtype=jnp.float32) * 0.01
        C = jax.random.normal(k3, (D, N), dtype=jnp.float32) * 0.01
        gamma = jnp.ones((D,), dtype=jnp.float32)
        beta = jnp.zeros((D,), dtype=jnp.float32)
        return {'x': x, 'A': A, 'B': B, 'C': C, 'gamma': gamma, 'beta': beta}
    _L3_attn_all = _L3_attn_setup()
    _L3_attn_in = {k: v for k, v in _L3_attn_all.items() if k in ('A', 'B', 'C', 'gamma', 'beta')}
    del _L3_attn_all

    def _L3_xattn_setup():
        import jax, jax.numpy as jnp
        import numpy as np
        NUM_HEADS = 16
        CLAMP = 10000.0
        key = jax.random.key(seed)
        ks = jax.random.split(key, 8)
        B, Nq, Nkv, Cq, Ckv = (4, 512, 512, 256, 192)
        s_q = 1.0 / np.sqrt(Cq)
        s_kv = 1.0 / np.sqrt(Ckv)
        return {'query': jax.random.normal(ks[0], (B, Nq, Cq), jnp.float32), 'key_value': jax.random.normal(ks[1], (B, Nkv, Ckv), jnp.float32), 'Wq': jax.random.normal(ks[2], (Cq, Cq), jnp.float32) * s_q, 'bq': jnp.zeros((Cq,), jnp.float32), 'Wk': jax.random.normal(ks[3], (Ckv, Cq), jnp.float32) * s_kv, 'bk': jnp.zeros((Cq,), jnp.float32), 'Wv': jax.random.normal(ks[4], (Ckv, Cq), jnp.float32) * s_kv, 'bv': jnp.zeros((Cq,), jnp.float32), 'Wo': jax.random.normal(ks[5], (Cq, Cq), jnp.float32) * s_q, 'bo': jnp.zeros((Cq,), jnp.float32)}
    _L3_xattn_all = _L3_xattn_setup()
    _L3_xattn_in = {k: v for k, v in _L3_xattn_all.items() if k in ('Wq', 'bq', 'Wk', 'bk', 'Wv', 'bv', 'Wo', 'bo')}
    del _L3_xattn_all

    def _L3_ffn_setup():
        import jax, jax.numpy as jnp
        import numpy as np
        EXPERT_NUM = 8
        CAPACITY = 100
        key = jax.random.key(seed)
        k1, k2, k3 = jax.random.split(key, 3)
        B, S, H, E = (8, 512, 256, EXPERT_NUM)
        x = jax.random.normal(k1, (B, S, H), dtype=jnp.float32)
        w_gate = jax.random.normal(k2, (H, E), dtype=jnp.float32) * 0.02
        w_expert = jax.random.normal(k3, (H, H), dtype=jnp.float32) * 0.02
        b_expert = jnp.zeros((H,), dtype=jnp.float32)
        return {'x': x, 'w_gate': w_gate, 'w_expert': w_expert, 'b_expert': b_expert}
    _L3_ffn_all = _L3_ffn_setup()
    _L3_ffn_in = {k: v for k, v in _L3_ffn_all.items() if k in ('w_gate', 'w_expert', 'b_expert')}
    del _L3_ffn_all
    return {'x': x, 'ctx_768': ctx_768, 'L0_attn_Wq': _L0_attn_in['Wq'], 'L0_attn_Wk': _L0_attn_in['Wk'], 'L0_attn_Wv': _L0_attn_in['Wv'], 'L0_attn_Wo': _L0_attn_in['Wo'], 'L0_xattn_Wq': _L0_xattn_in['Wq'], 'L0_xattn_Wk': _L0_xattn_in['Wk'], 'L0_xattn_Wv': _L0_xattn_in['Wv'], 'L0_xattn_Wo': _L0_xattn_in['Wo'], 'L0_xattn_bo': _L0_xattn_in['bo'], 'L0_ffn_router_w': _L0_ffn_in['router_w'], 'L0_ffn_router_b': _L0_ffn_in['router_b'], 'L0_ffn_experts_inter': _L0_ffn_in['experts_inter'], 'L0_ffn_experts_out': _L0_ffn_in['experts_out'], 'L1_attn_Wq': _L1_attn_in['Wq'], 'L1_attn_bq': _L1_attn_in['bq'], 'L1_attn_Wk': _L1_attn_in['Wk'], 'L1_attn_bk': _L1_attn_in['bk'], 'L1_attn_Wv': _L1_attn_in['Wv'], 'L1_attn_bv': _L1_attn_in['bv'], 'L1_attn_Wo': _L1_attn_in['Wo'], 'L1_attn_bo': _L1_attn_in['bo'], 'L1_xattn_Wq': _L1_xattn_in['Wq'], 'L1_xattn_bq': _L1_xattn_in['bq'], 'L1_xattn_Wkv': _L1_xattn_in['Wkv'], 'L1_xattn_bkv': _L1_xattn_in['bkv'], 'L1_xattn_Wo': _L1_xattn_in['Wo'], 'L1_xattn_bo': _L1_xattn_in['bo'], 'L1_ffn_wg': _L1_ffn_in['wg'], 'L1_ffn_w1': _L1_ffn_in['w1'], 'L1_ffn_b1': _L1_ffn_in['b1'], 'L1_ffn_w2': _L1_ffn_in['w2'], 'L1_ffn_b2': _L1_ffn_in['b2'], 'L2_attn_W_in': _L2_attn_in['W_in'], 'L2_attn_conv_w': _L2_attn_in['conv_w'], 'L2_attn_conv_b': _L2_attn_in['conv_b'], 'L2_attn_W_x': _L2_attn_in['W_x'], 'L2_attn_W_dt': _L2_attn_in['W_dt'], 'L2_attn_b_dt': _L2_attn_in['b_dt'], 'L2_attn_A_log': _L2_attn_in['A_log'], 'L2_attn_D_param': _L2_attn_in['D_param'], 'L2_attn_W_out': _L2_attn_in['W_out'], 'L2_attn_ln_g': _L2_attn_in['ln_g'], 'L2_attn_ln_b': _L2_attn_in['ln_b'], 'L2_xattn_g_x': _L2_xattn_in['g_x'], 'L2_xattn_b_x': _L2_xattn_in['b_x'], 'L2_xattn_g_c': _L2_xattn_in['g_c'], 'L2_xattn_b_c': _L2_xattn_in['b_c'], 'L2_xattn_Wq': _L2_xattn_in['Wq'], 'L2_xattn_Wk': _L2_xattn_in['Wk'], 'L2_xattn_Wv': _L2_xattn_in['Wv'], 'L2_xattn_Wo': _L2_xattn_in['Wo'], 'L2_ffn_w_gate': _L2_ffn_in['w_gate'], 'L2_ffn_w_up': _L2_ffn_in['w_up'], 'L2_ffn_w_down': _L2_ffn_in['w_down'], 'L3_attn_A': _L3_attn_in['A'], 'L3_attn_B': _L3_attn_in['B'], 'L3_attn_C': _L3_attn_in['C'], 'L3_attn_gamma': _L3_attn_in['gamma'], 'L3_attn_beta': _L3_attn_in['beta'], 'L3_xattn_Wq': _L3_xattn_in['Wq'], 'L3_xattn_bq': _L3_xattn_in['bq'], 'L3_xattn_Wk': _L3_xattn_in['Wk'], 'L3_xattn_bk': _L3_xattn_in['bk'], 'L3_xattn_Wv': _L3_xattn_in['Wv'], 'L3_xattn_bv': _L3_xattn_in['bv'], 'L3_xattn_Wo': _L3_xattn_in['Wo'], 'L3_xattn_bo': _L3_xattn_in['bo'], 'L3_ffn_w_gate': _L3_ffn_in['w_gate'], 'L3_ffn_w_expert': _L3_ffn_in['w_expert'], 'L3_ffn_b_expert': _L3_ffn_in['b_expert']}

def reference(x, ctx_768, L0_attn_Wq, L0_attn_Wk, L0_attn_Wv, L0_attn_Wo, L0_xattn_Wq, L0_xattn_Wk, L0_xattn_Wv, L0_xattn_Wo, L0_xattn_bo, L0_ffn_router_w, L0_ffn_router_b, L0_ffn_experts_inter, L0_ffn_experts_out, L1_attn_Wq, L1_attn_bq, L1_attn_Wk, L1_attn_bk, L1_attn_Wv, L1_attn_bv, L1_attn_Wo, L1_attn_bo, L1_xattn_Wq, L1_xattn_bq, L1_xattn_Wkv, L1_xattn_bkv, L1_xattn_Wo, L1_xattn_bo, L1_ffn_wg, L1_ffn_w1, L1_ffn_b1, L1_ffn_w2, L1_ffn_b2, L2_attn_W_in, L2_attn_conv_w, L2_attn_conv_b, L2_attn_W_x, L2_attn_W_dt, L2_attn_b_dt, L2_attn_A_log, L2_attn_D_param, L2_attn_W_out, L2_attn_ln_g, L2_attn_ln_b, L2_xattn_g_x, L2_xattn_b_x, L2_xattn_g_c, L2_xattn_b_c, L2_xattn_Wq, L2_xattn_Wk, L2_xattn_Wv, L2_xattn_Wo, L2_ffn_w_gate, L2_ffn_w_up, L2_ffn_w_down, L3_attn_A, L3_attn_B, L3_attn_C, L3_attn_gamma, L3_attn_beta, L3_xattn_Wq, L3_xattn_bq, L3_xattn_Wk, L3_xattn_bk, L3_xattn_Wv, L3_xattn_bv, L3_xattn_Wo, L3_xattn_bo, L3_ffn_w_gate, L3_ffn_w_expert, L3_ffn_b_expert):
    import jax
    import jax.numpy as jnp

    def _L0_attn_ref(x, Wq, Wk, Wv, Wo):
        import jax, jax.numpy as jnp
        import numpy as np
        D_MODEL = 256
        N_HEADS = 16
        D_HEAD = D_MODEL // N_HEADS
        WINDOW = 64
        CAUSAL = True
        NEG = -1000000000.0

        def build_sliding_window_mask(seq_len, window_size, causal=True):
            i = jnp.arange(seq_len)[:, None]
            j = jnp.arange(seq_len)[None, :]
            if causal:
                attend = (j <= i) & (j >= i - window_size)
            else:
                half = window_size // 2
                attend = jnp.abs(j - i) <= half
            return jnp.where(attend, 0.0, NEG).astype(jnp.float32)
        B, T, _ = x.shape

        def split_heads(y):
            return y.reshape(B, T, N_HEADS, D_HEAD).transpose(0, 2, 1, 3)
        Q = split_heads(x @ Wq.T)
        K = split_heads(x @ Wk.T)
        V = split_heads(x @ Wv.T)
        scale = 1.0 / np.sqrt(D_HEAD)
        mask = build_sliding_window_mask(T, WINDOW, causal=CAUSAL)
        scores = jnp.einsum('bhqd,bhkd->bhqk', Q, K) * scale + mask
        weights = jax.nn.softmax(scores, axis=-1)
        out = jnp.einsum('bhqk,bhkd->bhqd', weights, V)
        out = out.transpose(0, 2, 1, 3).reshape(B, T, D_MODEL)
        return out @ Wo.T

    def _L0_xattn_ref(x, context, Wq, Wk, Wv, Wo, bo):
        import jax, jax.numpy as jnp
        import numpy as np
        HEADS = 16
        DIM_HEAD = 64
        SCALE = DIM_HEAD ** (-0.5)
        QUERY_DIM = 256
        CONTEXT_DIM = 192
        INNER_DIM = HEADS * DIM_HEAD
        B, Nq, _ = x.shape
        Nk = context.shape[1]
        q = x @ Wq
        k = context @ Wk
        v = context @ Wv
        q = q.reshape(B, Nq, HEADS, DIM_HEAD).transpose(0, 2, 1, 3)
        k = k.reshape(B, Nk, HEADS, DIM_HEAD).transpose(0, 2, 1, 3)
        v = v.reshape(B, Nk, HEADS, DIM_HEAD).transpose(0, 2, 1, 3)
        sim = jnp.einsum('bhid,bhjd->bhij', q, k) * SCALE
        attn = jax.nn.softmax(sim, axis=-1)
        out = jnp.einsum('bhij,bhjd->bhid', attn, v)
        out = out.transpose(0, 2, 1, 3).reshape(B, Nq, INNER_DIM)
        return out @ Wo + bo

    def _L0_ffn_ref(x, router_w, router_b, experts_inter, experts_out):
        import math
        import jax, jax.numpy as jnp
        import numpy as np
        NUM_EXPERTS = 8
        TOP_K = 2
        CAPACITY_FACTOR = 1.0
        B, S, H, I = (4, 512, 256, 1024)
        batch, seq, hidden = x.shape
        n_exp = router_w.shape[0]
        n_tok = batch * seq
        cap = math.ceil(n_tok / n_exp * CAPACITY_FACTOR)
        logits = jnp.einsum('bsh,eh->bse', x, router_w) + router_b
        weights_flat = jax.nn.softmax(logits, axis=-1).reshape(n_tok, n_exp)
        x_flat = x.reshape(n_tok, hidden)
        topk_vals, topk_idx = jax.lax.top_k(weights_flat, TOP_K)
        rows = jnp.arange(n_tok)[:, None]
        topk_flat = jnp.zeros_like(weights_flat).at[rows, topk_idx].set(topk_vals)
        routing_mask = (topk_flat > 0).astype(jnp.int32)
        noop_w = topk_flat[:, -1]
        noop_mask = routing_mask[:, -1].astype(x.dtype)
        expert_w = topk_flat[:, :-1]
        expert_mask = routing_mask[:, :-1]
        sorted_indices = jnp.argsort(-expert_mask, axis=0)[:cap]
        sorted_mask = jnp.take_along_axis(expert_mask, sorted_indices, axis=0)
        used_idx = (sorted_indices * sorted_mask).reshape(-1)
        inputs = x_flat[used_idx] * sorted_mask.reshape(-1).astype(x.dtype)[:, None]
        inputs = inputs.reshape(cap, n_exp - 1, hidden)
        in_w = jnp.take_along_axis(expert_w, sorted_indices, axis=0)
        h = jax.nn.relu(jnp.einsum('ceh,ehi->cei', inputs, experts_inter))
        out = jnp.einsum('cei,eih->ceh', h, experts_out) * in_w[..., None]
        combined = jnp.zeros_like(x_flat).at[used_idx].add(out.reshape(-1, hidden))
        combined = combined + x_flat * (noop_w * noop_mask)[:, None]
        return combined.reshape(batch, seq, hidden)

    def _L1_attn_ref(x, Wq, bq, Wk, bk, Wv, bv, Wo, bo):
        import jax, jax.numpy as jnp
        import numpy as np
        EMBED_DIM = 256
        NUM_HEADS = 16
        HEAD_DIM = EMBED_DIM // NUM_HEADS
        B, S, D = x.shape
        H, Hd = (NUM_HEADS, HEAD_DIM)
        scale = 1.0 / jnp.sqrt(jnp.asarray(Hd, x.dtype))

        def split_heads(t):
            return t.reshape(B, S, H, Hd).transpose(0, 2, 1, 3)
        q = split_heads(x @ Wq + bq)
        k = split_heads(x @ Wk + bk)
        v = split_heads(x @ Wv + bv)
        scores = jnp.einsum('bhqd,bhkd->bhqk', q, k) * scale
        attn = jax.nn.softmax(scores, axis=-1)
        out = jnp.einsum('bhqk,bhkd->bhqd', attn, v)
        out = out.transpose(0, 2, 1, 3).reshape(B, S, D)
        return out @ Wo + bo

    def _L1_xattn_ref(x, y, Wq, bq, Wkv, bkv, Wo, bo):
        import jax, jax.numpy as jnp
        import numpy as np
        N_HEADS = 16
        b, l, d = x.shape
        m = y.shape[1]
        h = N_HEADS
        dh = d // h
        q = (jnp.einsum('bld,ed->ble', x, Wq) + bq).reshape(b, l, h, dh)
        kv = (jnp.einsum('bmc,ec->bme', y, Wkv) + bkv).reshape(b, m, h, 2 * dh)
        k, v = (kv[..., :dh], kv[..., dh:])
        scale = 1.0 / jnp.sqrt(jnp.asarray(dh, x.dtype))
        att = jax.nn.softmax(jnp.einsum('blhd,bmhd->blmh', q, k) * scale, axis=2)
        out = jnp.einsum('blmh,bmhd->blhd', att, v).reshape(b, l, d)
        return jnp.einsum('bld,ed->ble', out, Wo) + bo

    def _L1_ffn_ref(x, wg, w1, b1, w2, b2):
        import jax, jax.numpy as jnp
        import numpy as np
        B, Sq, M = x.shape
        E = wg.shape[1]
        S = B * Sq
        C = S // E
        xt = x.reshape(S, M)
        gates = jax.nn.softmax(xt @ wg, axis=-1)
        expert_idx = jnp.argmax(gates, axis=-1)
        mask1 = jax.nn.one_hot(expert_idx, E, dtype=xt.dtype)
        locations = jnp.cumsum(mask1, axis=0) - 1.0
        pos = jnp.sum(locations * mask1, axis=1).astype(jnp.int32)
        keep = (pos < C).astype(xt.dtype)
        gate_val = jnp.sum(gates * mask1, axis=1) * keep
        slot = expert_idx.astype(jnp.int32) * C + jnp.clip(pos, 0, C - 1)
        disp = jnp.zeros((E * C, M), dtype=xt.dtype).at[slot].add(xt * keep[:, None])
        disp = disp.reshape(E, C, M)
        h = jax.nn.relu(jnp.einsum('ecm,emh->ech', disp, w1) + b1[:, None, :])
        eo = jnp.einsum('ech,ehm->ecm', h, w2) + b2[:, None, :]
        out = eo.reshape(E * C, M)[slot] * gate_val[:, None]
        return out.reshape(B, Sq, M)

    def _L2_attn_ref(x, W_in, conv_w, conv_b, W_x, W_dt, b_dt, A_log, D_param, W_out, ln_g, ln_b):
        import jax, jax.numpy as jnp
        import numpy as np
        D_MODEL, D_STATE, D_CONV, EXPAND = (256, 16, 4, 2)
        D_INNER = EXPAND * D_MODEL
        B_SZ, L_SEQ = (2, 512)
        LN_EPS = 1e-05

        def _selective_scan(u, dt, A, Bp, Cp):

            def step(h, inp):
                dt_t, B_t, C_t, u_t = inp
                dA = jnp.exp(jnp.clip(dt_t[:, :, None] * A, -20.0, 0.0))
                dB_u = jnp.clip(dt_t[:, :, None] * B_t[:, None, :] * u_t[:, :, None], -10.0, 10.0)
                h = jnp.clip(h * dA + dB_u, -100.0, 100.0)
                y = jnp.einsum('bdn,bn->bd', h, C_t)
                return (h, y)
            h0 = jnp.zeros((u.shape[0], u.shape[2], A.shape[0]), dtype=u.dtype)
            xs = (jnp.swapaxes(dt, 0, 1), jnp.swapaxes(Bp, 0, 1), jnp.swapaxes(Cp, 0, 1), jnp.swapaxes(u, 0, 1))
            _, ys = jax.lax.scan(step, h0, xs)
            return jnp.swapaxes(ys, 0, 1)
        B, L, _ = x.shape
        d_state = A_log.shape[0]
        d_inner = D_param.shape[0]
        xz = jnp.einsum('bld,ed->ble', x, W_in)
        xc, z = (xz[..., :d_inner], xz[..., d_inner:])
        xt = jnp.swapaxes(xc, 1, 2)
        conv = jax.lax.conv_general_dilated(xt, conv_w, window_strides=(1,), padding=[(conv_w.shape[-1] - 1, 0)], feature_group_count=d_inner, dimension_numbers=('NCH', 'OIH', 'NCH'))
        conv = conv + conv_b[None, :, None]
        u = jax.nn.silu(jnp.swapaxes(conv, 1, 2))
        x_dbl = jnp.einsum('bld,ed->ble', u, W_x)
        dt_raw = x_dbl[..., :1]
        Bp = x_dbl[..., 1:1 + d_state]
        Cp = x_dbl[..., 1 + d_state:]
        dt = jnp.clip(jax.nn.softplus(jnp.einsum('blo,eo->ble', dt_raw, W_dt) + b_dt), 0.0001, 10.0)
        A = -jnp.exp(jnp.minimum(A_log, 5.0))
        y = _selective_scan(u, dt, A, Bp, Cp)
        mu = jnp.mean(y, axis=-1, keepdims=True)
        var = jnp.mean(jnp.square(y - mu), axis=-1, keepdims=True)
        yn = (y - mu) * jax.lax.rsqrt(var + LN_EPS) * ln_g + ln_b
        y = yn + D_param * u
        y = y * jax.nn.silu(z)
        return jnp.einsum('ble,de->bld', y, W_out)

    def _L2_xattn_ref(x, context, g_x, b_x, g_c, b_c, Wq, Wk, Wv, Wo):
        import jax, jax.numpy as jnp
        import numpy as np
        DIM = 256
        CTX_DIM = 192
        H = 16
        DH = 64
        INNER = H * DH
        EPS = 1e-05

        def layer_norm(x, gamma, beta):
            mu = jnp.mean(x, axis=-1, keepdims=True)
            var = jnp.mean(jnp.square(x - mu), axis=-1, keepdims=True)
            return (x - mu) * jax.lax.rsqrt(var + EPS) * gamma + beta
        B, N, _ = x.shape
        M = context.shape[1]
        xn = layer_norm(x, g_x, b_x)
        cn = layer_norm(context, g_c, b_c)
        q = (xn @ Wq).reshape(B, N, H, DH).transpose(0, 2, 1, 3)
        k = (cn @ Wk).reshape(B, M, H, DH).transpose(0, 2, 1, 3)
        v = (cn @ Wv).reshape(B, M, H, DH).transpose(0, 2, 1, 3)
        scale = jnp.float32(1.0 / np.sqrt(DH))
        sim = jnp.einsum('bhid,bhjd->bhij', q, k) * scale
        attn = jax.nn.softmax(sim, axis=-1)
        out = jnp.einsum('bhij,bhjd->bhid', attn, v)
        out = out.transpose(0, 2, 1, 3).reshape(B, N, INNER)
        return out @ Wo

    def _L2_ffn_ref(x, w_gate, w_up, w_down):
        import jax, jax.numpy as jnp
        import numpy as np
        BLOCK = 32
        W_BITS = 4
        ACT_BITS = 16

        def act_qdq(x):
            qmax = 2.0 ** (ACT_BITS - 1) - 1.0
            scale = jnp.maximum(jnp.max(jnp.abs(x)) / qmax, 1e-12)
            return jnp.clip(jnp.round(x / scale), -qmax - 1.0, qmax) * scale

        def fixed_qdq_u16(x):
            scale = 1.0 / 65536.0
            return jnp.clip(jnp.round(x / scale), 0.0, 65535.0) * scale

        def lpbq_dequant(w):
            O, I = w.shape
            qmax = 2.0 ** (W_BITS - 1) - 1.0
            wb = w.reshape(O, I // BLOCK, BLOCK)
            s = jnp.maximum(jnp.max(jnp.abs(wb), axis=-1, keepdims=True) / qmax, 1e-12)
            wq = jnp.clip(jnp.round(wb / s), -qmax - 1.0, qmax) * s
            return wq.reshape(O, I)
        x = act_qdq(x)
        up = act_qdq(x @ lpbq_dequant(w_up).T)
        gate = act_qdq(x @ lpbq_dequant(w_gate).T)
        sig = fixed_qdq_u16(jax.nn.sigmoid(gate))
        gate = act_qdq(gate * sig)
        o = act_qdq(gate * up)
        return o @ lpbq_dequant(w_down).T

    def _L3_attn_ref(x, A, B, C, gamma, beta):
        import jax, jax.numpy as jnp
        import numpy as np
        LN_EPS = 1e-05
        CLAMP = 1000000.0
        Bsz = x.shape[0]
        N = A.shape[0]
        uB = jnp.einsum('bld,nd->lbn', x, B)

        def step(state, u_t):
            s = state @ A.T + u_t
            return (s, s)
        init = jnp.zeros((Bsz, N), dtype=x.dtype)
        _, states = jax.lax.scan(step, init, uB)
        y = jnp.einsum('lbn,dn->bld', states, C)
        act = jax.nn.gelu(y, approximate=False)
        mean = jnp.mean(act, axis=-1, keepdims=True)
        var = jnp.var(act, axis=-1, keepdims=True)
        norm = (act - mean) / jnp.sqrt(var + LN_EPS) * gamma + beta
        return jnp.nan_to_num(norm, nan=0.0, posinf=CLAMP, neginf=-CLAMP)

    def _L3_xattn_ref(query, key_value, Wq, bq, Wk, bk, Wv, bv, Wo, bo):
        import jax, jax.numpy as jnp
        import numpy as np
        NUM_HEADS = 16
        CLAMP = 10000.0
        B, Nq, Cq = query.shape
        Nkv = key_value.shape[1]
        H = NUM_HEADS
        D = Cq // H
        scale = D ** (-0.5)
        q = (query @ Wq + bq).reshape(B, Nq, H, D).transpose(0, 2, 1, 3)
        k = (key_value @ Wk + bk).reshape(B, Nkv, H, D).transpose(0, 2, 1, 3)
        v = (key_value @ Wv + bv).reshape(B, Nkv, H, D).transpose(0, 2, 1, 3)
        attn = jnp.einsum('bhqd,bhkd->bhqk', q, k) * scale
        attn = jnp.clip(attn, -CLAMP, CLAMP)
        attn = jax.nn.softmax(attn, axis=-1)
        attn = jnp.where(jnp.any(jnp.isnan(attn)), jnp.asarray(1.0 / Nkv, attn.dtype), attn)
        x = jnp.einsum('bhqk,bhkd->bqhd', attn, v).reshape(B, Nq, Cq)
        return x @ Wo + bo

    def _L3_ffn_ref(x, w_gate, w_expert, b_expert):
        import jax, jax.numpy as jnp
        import numpy as np
        EXPERT_NUM = 8
        CAPACITY = 100
        B, S, H = x.shape
        E, C = (EXPERT_NUM, CAPACITY)
        hs = x.reshape(-1, H)
        logits = hs @ w_gate
        probs = jax.nn.softmax(logits, axis=1)
        best = jnp.argmax(probs, axis=1)
        mask = jax.nn.one_hot(best, E, dtype=jnp.int32)
        gate = jnp.sum(probs * mask.astype(probs.dtype), axis=1)
        locations = jnp.cumsum(mask, axis=0) - 1
        mask = mask * (locations < C).astype(jnp.int32)
        loc_sum = jnp.sum(locations * mask, axis=1)
        new_gates = gate[:, None] * mask.astype(probs.dtype)
        loc_oh = jax.nn.one_hot(loc_sum, C, dtype=probs.dtype)
        combine = new_gates[:, :, None] * loc_oh[:, None, :]
        dispatch = (combine != 0).astype(hs.dtype)
        dispatched = jnp.einsum('tec,th->ech', dispatch, hs).reshape(E * C, H)
        expert_out = dispatched @ w_expert + b_expert
        combined = combine.reshape(-1, E * C) @ expert_out
        return combined.reshape(B, S, H)
    x = x + _L0_attn_ref(_layernorm(x, axis=-1), L0_attn_Wq, L0_attn_Wk, L0_attn_Wv, L0_attn_Wo)
    x = x + _L0_xattn_ref(_layernorm(x, axis=-1), ctx_768, L0_xattn_Wq, L0_xattn_Wk, L0_xattn_Wv, L0_xattn_Wo, L0_xattn_bo)
    x = x + _L0_ffn_ref(_layernorm(x, axis=-1), L0_ffn_router_w, L0_ffn_router_b, L0_ffn_experts_inter, L0_ffn_experts_out)
    x = x + _L1_attn_ref(_layernorm(x, axis=-1), L1_attn_Wq, L1_attn_bq, L1_attn_Wk, L1_attn_bk, L1_attn_Wv, L1_attn_bv, L1_attn_Wo, L1_attn_bo)
    x = x + _L1_xattn_ref(_layernorm(x, axis=-1), ctx_768, L1_xattn_Wq, L1_xattn_bq, L1_xattn_Wkv, L1_xattn_bkv, L1_xattn_Wo, L1_xattn_bo)
    x = x + _L1_ffn_ref(_layernorm(x, axis=-1), L1_ffn_wg, L1_ffn_w1, L1_ffn_b1, L1_ffn_w2, L1_ffn_b2)
    x = x + _L2_attn_ref(_layernorm(x, axis=-1), L2_attn_W_in, L2_attn_conv_w, L2_attn_conv_b, L2_attn_W_x, L2_attn_W_dt, L2_attn_b_dt, L2_attn_A_log, L2_attn_D_param, L2_attn_W_out, L2_attn_ln_g, L2_attn_ln_b)
    x = x + _L2_xattn_ref(_layernorm(x, axis=-1), ctx_768, L2_xattn_g_x, L2_xattn_b_x, L2_xattn_g_c, L2_xattn_b_c, L2_xattn_Wq, L2_xattn_Wk, L2_xattn_Wv, L2_xattn_Wo)
    x = x + _L2_ffn_ref(_layernorm(x, axis=-1), L2_ffn_w_gate, L2_ffn_w_up, L2_ffn_w_down)
    x = x + _L3_attn_ref(_layernorm(x, axis=-1), L3_attn_A, L3_attn_B, L3_attn_C, L3_attn_gamma, L3_attn_beta)
    x = x + _L3_xattn_ref(_layernorm(x, axis=-1), ctx_768, L3_xattn_Wq, L3_xattn_bq, L3_xattn_Wk, L3_xattn_bk, L3_xattn_Wv, L3_xattn_bv, L3_xattn_Wo, L3_xattn_bo)
    x = x + _L3_ffn_ref(_layernorm(x, axis=-1), L3_ffn_w_gate, L3_ffn_w_expert, L3_ffn_b_expert)
    return x

_drawn_inputs = setup_inputs


def setup_inputs(seed=0):
    import zlib

    import numpy as np

    out = dict(_drawn_inputs(seed))
    spreads = {'L0_xattn_bo': (0.0, 0.1),
     'L0_ffn_router_b': (0.0, 0.1),
     'L1_ffn_b1': (0.0, 0.372),
     'L1_ffn_b2': (0.0, 0.1),
     'L2_attn_b_dt': (0.10000000149011612, 0.6),
     'L2_attn_D_param': (1.0, 0.2),
     'L2_attn_ln_g': (1.0, 0.2),
     'L2_attn_ln_b': (0.0, 0.1),
     'L2_xattn_g_x': (1.0, 0.6),
     'L2_xattn_b_x': (0.0, 0.696),
     'L2_xattn_g_c': (1.0, 0.2),
     'L2_xattn_b_c': (0.0, 0.1),
     'L3_attn_gamma': (1.0, 0.2),
     'L3_attn_beta': (0.0, 0.1),
     'L3_xattn_bq': (0.0, 0.66),
     'L3_xattn_bk': (0.0, 2.0),
     'L3_xattn_bv': (0.0, 0.1),
     'L3_xattn_bo': (0.0, 0.1),
     'L3_ffn_b_expert': (0.0, 0.8)}
    factors = {'L1_attn_Wq': 4.804,
     'L1_attn_bq': 8.0,
     'L1_attn_Wk': 3.91,
     'L1_attn_bk': 64.0,
     'L1_xattn_bq': 7.241,
     'L1_xattn_bkv': 2.917,
     'L1_xattn_bo': 2.996,
     'L2_attn_conv_b': 5.343,
     'L2_attn_W_dt': 25.138,
     'L2_ffn_w_gate': 3.53,
     'L2_ffn_w_up': 3.429,
     'L2_ffn_w_down': 3.44,
     'L3_ffn_w_gate': 4.841,
     'L3_ffn_w_expert': 3.351}
    for name, (base, spread) in spreads.items():
        noise = np.random.default_rng([zlib.crc32(name.encode()), seed]).standard_normal(out[name].shape)
        drawn = base * np.exp(spread * noise) if base else spread * noise
        out[name] = jnp.asarray(drawn.astype(out[name].dtype))
    for name, factor in factors.items():
        out[name] = (out[name] * factor).astype(out[name].dtype)
    return out
```

```python
from contextlib import ExitStack

import concourse.bass as bass
from concourse import mybir

F32 = mybir.dt.float32
BF16 = mybir.dt.bfloat16
I32 = mybir.dt.int32
U32 = mybir.dt.uint32
ACT = mybir.ActivationFunctionType
ALU = mybir.AluOpType
AX = mybir.AxisListType.X

P = 128
BATCH, SEQ, DM = 4, 512, 256
TOK = BATCH * SEQ
TILES = TOK // P
QT = SEQ // P
KC = DM // P
HEADS = 16
BANK = 512
NBLK = TOK // BANK
LN_EPS = 1e-5


class Scope:

    def __init__(self, nc, prefix):
        self.nc, self.prefix, self.stack, self.sems = nc, prefix, ExitStack(), []

    def __enter__(self):
        self.stack.__enter__()
        return self

    def __exit__(self, *a):
        if self.sems:
            self.nc.clear_and_free_semaphores(self.sems)
            self.nc.all_engine_barrier()
        return self.stack.__exit__(*a)

    def sb(self, name, shape, dt=F32):
        return self.stack.enter_context(self.nc.sbuf_tensor(f"{self.prefix}_{name}", list(shape), dt))

    def ps(self, name, shape, dt=F32):
        return self.stack.enter_context(self.nc.psum_tensor(f"{self.prefix}_{name}", list(shape), dt))

    def sem(self, name):
        self.sems.append(self.nc.alloc_semaphore(f"{self.prefix}_{name}"))
        return self.sems[-1]

    def block(self):
        return self.nc.Block()


class Chain:

    def __init__(self, eng, sem, base=0):
        self.eng, self.sem, self.base, self.n = eng, sem, base, 0

    def step(self, ins):
        self.n += 1
        ins.then_inc(self.sem, 1)
        self.eng.wait_ge(self.sem, self.base + self.n)


def setup_constants(nc, S, c):
    c["ident"] = S.sb("ident", [P, P])
    c["ones"] = S.sb("ones", [P, P])
    made = S.sem("const_made")
    with S.block() as block:
        @block.gpsimd
        def _(pool):
            nc.gpsimd.memset(c["ident"][:], 0.0).then_inc(made, 1)
            nc.gpsimd.memset(c["ones"][:], 1.0).then_inc(made, 1)
            pool.wait_ge(made, 2)
            nc.gpsimd.affine_select(out=c["ident"][:], in_=c["ident"][:], compare_op=ALU.not_equal, fill=1.0,
                                    base=0, pattern=[[-1, P]], channel_multiplier=1).then_inc(made, 1)
            pool.wait_ge(made, 3)


def row_stats_to_affine(nc, ch, act_sem, dve_sem_val, st, mean, rstd, tmp, half):
    ch.step(nc.vector.tensor_tensor(mean, st[:, :, 1], st[:, :, 4], ALU.add))
    ch.step(nc.vector.tensor_scalar(mean, mean, 0.5, None, ALU.mult))
    ch.step(nc.vector.tensor_tensor(tmp, st[:, :, 1], mean, ALU.subtract))
    ch.step(nc.vector.tensor_tensor(tmp, tmp, tmp, ALU.mult))
    ch.step(nc.vector.tensor_tensor(rstd, st[:, :, 2], st[:, :, 5], ALU.add))
    ch.step(nc.vector.tensor_scalar(rstd, rstd, 1.0 / (2 * half), LN_EPS, ALU.mult, ALU.add))
    ch.step(nc.vector.tensor_tensor(rstd, rstd, tmp, ALU.add))


def normalise(nc, name, c, affine=None):
    x, xn, xnT, ident = c["x"], c["xn"], c["xnT"], c["ident"]
    rounds = 1 if affine is None else 2
    with Scope(nc, name) as S:
        st = S.sb("stats", [P, TILES, 6])
        mean, rstd, tmp = (S.sb(n, [P, TILES]) for n in ("mean", "rstd", "tmp"))
        gb = S.sb("gb", [P, 2, DM]) if affine else None
        pt = S.ps("pt", [P, 4, KC * 2, P])
        var_ready, std_ready, step = S.sem("var_ready"), S.sem("std_ready"), S.sem("step")
        xn_ready, tr_ready, tr_free, gb_loaded = (S.sem(n) for n in ("xn_ready", "tr_ready", "tr_free", "gb_loaded"))
        with S.block() as block:
            if affine:
                @block.sync
                def _(sp):
                    for j in range(2):
                        sp.dma_start(gb[:, j, :], affine[j][None, :].to_broadcast([P, DM])).then_inc(gb_loaded, 16)

            @block.vector
            def _(dve):
                ch = Chain(dve, step)
                for r in range(rounds):
                    src = x if r == 0 else xn
                    with dve.Fori(0, TILES) as i:
                        nc.vector.bn_stats(st[:, i, :], src[:, i, :]).then_inc(step, 1)
                    ch.n += TILES
                    dve.wait_ge(step, ch.n)
                    row_stats_to_affine(nc, ch, None, None, st, mean[:], rstd[:], tmp[:], DM // 2)
                    nc.vector.tensor_copy(tmp[:], rstd[:]).then_inc(var_ready, 1)
                    dve.wait_ge(std_ready, r + 1)
                    ch.step(nc.vector.reciprocal(rstd[:], tmp[:]))
                    last_round = r == rounds - 1
                    done = xn_ready if (last_round and not affine) else step
                    with dve.Fori(0, TILES) as i:
                        nc.vector.tensor_scalar(xn[:, i, :], src[:, i, :], mean[:, bass.ds(i, 1)], rstd[:, bass.ds(i, 1)],
                                                ALU.subtract, ALU.mult).then_inc(done, 1)
                    if done is step:
                        ch.n += TILES
                        dve.wait_ge(step, ch.n)
                if affine:
                    dve.wait_ge(gb_loaded, 32)
                    ch.step(nc.vector.tensor_tensor(xn[:], xn[:], gb[:, None, 0, :].to_broadcast([P, TILES, DM]), ALU.mult))
                    nc.vector.tensor_tensor(xn[:], xn[:], gb[:, None, 1, :].to_broadcast([P, TILES, DM]), ALU.add).then_inc(xn_ready, TILES)

            @block.scalar
            def _(act):
                for r in range(rounds):
                    act.wait_ge(var_ready, r + 1)
                    nc.scalar.activation(tmp[:], tmp[:], ACT.Sqrt).then_inc(std_ready, 1)
                for k in range(4):
                    act.sem_inc(tr_free, 1)
                with act.Fori(0, TILES // 8) as g:
                    for u in range(4):
                        act.wait_ge(tr_ready, g * 4 + (u + 1))
                        for kc in range(KC):
                            ins = nc.scalar.copy(xnT[:, kc, bass.ds((g * 4 + u) * 2 * P, 2 * P)],
                                                 pt[:, u, 2 * kc:2 * kc + 2, :])
                        ins.then_inc(tr_free, 1)

            @block.tensor
            def _(pe):
                for g in range(TILES // 2):
                    pe.wait_ge(xn_ready, 2 * g + 2)
                    pe.wait_ge(tr_free, g + 1)
                    for kc in range(KC):
                        for v in range(2):
                            ins = nc.tensor.transpose(pt[:, g % 4, 2 * kc + v, :], xn[:, 2 * g + v, kc * P:(kc + 1) * P], ident[:])
                    ins.then_inc(tr_ready, 1)


def transpose_weights(nc, S, name, c, loads, jobs):
    ident = c["ident"]
    groups = [jobs[j:j + 4] for j in range(0, len(jobs), 4)]
    BANKS = 4
    with Scope(nc, name) as T:
        pt = T.ps("wt", [P, BANKS, 4, P])
        loaded, tr_ready = T.sem("loaded"), T.sem("tr_ready")
        copied = [T.sem("act_copied"), T.sem("dve_copied")]
        with T.block() as block:
            @block.sync
            def _(sp):
                for dst, src in loads:
                    sp.dma_start(dst, src).then_inc(loaded, 16)
                sp.wait_ge(loaded, 16 * len(loads))

            if groups:
                @block.tensor
                def _(pe):
                    pe.wait_ge(loaded, 16 * len(loads))
                    for g, group in enumerate(groups):
                        if g >= BANKS:
                            pe.wait_ge(copied[g % 2], (g - BANKS) // 2 + 1)
                        for j, (dst, src) in enumerate(group):
                            r, n = src.shape[0], src.shape[1]
                            ins = nc.tensor.transpose(pt[0:n, g % BANKS, j, 0:r], src, ident[0:r, 0:r])
                        ins.then_inc(tr_ready, 1)

                def copy_out(eng, copy, half):
                    for g in range(half, len(groups), 2):
                        eng.wait_ge(tr_ready, g + 1)
                        for j, (dst, src) in enumerate(groups[g]):
                            ps = pt[0:src.shape[1], g % BANKS, j, 0:src.shape[0]]
                            if len(dst.shape) == 3:
                                ps = ps.rearrange("p (a b) -> p a b", b=dst.shape[2])
                            ins = copy(dst, ps)
                        ins.then_inc(copied[half], 1)

                @block.scalar
                def _(act):
                    copy_out(act, nc.scalar.copy, 0)

                @block.vector
                def _(dve):
                    copy_out(dve, nc.vector.tensor_copy, 1)


HP = 32
HD = DM // HEADS
QC = HEADS * HP // P


def self_attention(nc, name, c, wts, given, window):
    x, xnT, ident = c["x"], c["xnT"], c["ident"]
    Wq, Wk, Wv, Wo = (wts[n] for n in ("Wq", "Wk", "Wv", "Wo"))
    bq, bk, bv, bo = (wts.get(n) for n in ("bq", "bk", "bv", "bo"))
    NK = 2 * P if window else SEQ
    with Scope(nc, name) as S:
        xb = S.sb("xb", [P, KC, SEQ])
        qT = S.sb("qT", [P, QC, SEQ])
        kT = S.sb("kT", [P, QC, SEQ])
        v = S.sb("v", [P, QT, DM])
        wo = S.sb("wo", [P, KC, DM])
        mask = S.sb("mask", [P, NK]) if window else None
        wq = S.sb("wq", [P, KC, QC * P])
        wk = S.sb("wk", [P, KC, QC * P])
        wv = S.sb("wv", [P, KC, DM])
        biased = bq is not None
        if biased:
            bqk = S.sb("bqk", [P, 2, QC])
            bqk_scaled = S.sb("bqk_scaled", [P, 2, QC])
            bvb = S.sb("bvb", [P, DM])
        zeroed = S.sem("zeroed")
        if biased:
            bob = S.sb("bob", [P, DM])
        with S.block() as block:
            @block.gpsimd
            def _(pool):
                nc.gpsimd.memset(wq[:], 0.0)
                nc.gpsimd.memset(wk[:], 0.0)
                if biased:
                    nc.gpsimd.memset(bqk[:], 0.0)
                if window:
                    nc.gpsimd.memset(mask[:], 0.0).then_inc(zeroed, 1)
                    pool.wait_ge(zeroed, 1)
                    nc.gpsimd.affine_select(out=mask[:], in_=mask[:], compare_op=ALU.is_ge, fill=-1e9, base=P,
                                            pattern=[[-1, NK]], channel_multiplier=1).then_inc(zeroed, 1)
                    pool.wait_ge(zeroed, 2)
                    nc.gpsimd.affine_select(out=mask[:], in_=mask[:], compare_op=ALU.is_ge, fill=-1e9, base=64 - P,
                                            pattern=[[1, NK]], channel_multiplier=-1)
        with Scope(nc, name + "r") as R:
            raw = R.sb("raw", [P, 4, KC, DM])
            loads, jobs = [], []

            def padded(dst, kc, o):
                return dst[:, kc, o * 8 * HP:(o + 1) * 8 * HP].rearrange("p (h w) -> p h w", w=HP)[:, :, 0:HD]

            if given:
                loads += [(raw[:, n], w.rearrange("(k p) n -> p k n", p=P)) for n, w in enumerate((Wq, Wk))]
                loads += [(wv[:], Wv.rearrange("(k p) n -> p k n", p=P)), (wo[:], Wo.rearrange("(k p) n -> p k n", p=P))]
                loads += [(bvb[:], bv[None, :].to_broadcast([P, DM])), (bob[:], bo[None, :].to_broadcast([P, DM]))]
                for n, b in enumerate((bq, bk)):
                    for h in range(4):
                        loads.append((bqk[HP * h:HP * h + HD, n, :], b.rearrange("(c h w) -> h w c", h=4, w=HD)[h]))
            else:
                loads += [(raw[:, n], w.rearrange("(k p) n -> p k n", p=P)) for n, w in enumerate((Wq, Wk, Wv, Wo))]
                for kc in range(KC):
                    for o in range(KC):
                        for n, dst in enumerate((wq, wk)):
                            jobs.append((padded(dst, kc, o), raw[:, n, o, kc * P:(kc + 1) * P]))
                        for n, dst in ((2, wv), (3, wo)):
                            jobs.append((dst[:, kc, o * P:(o + 1) * P], raw[:, n, o, kc * P:(kc + 1) * P]))
            with nc.allow_non_contiguous_dma(reason="bias vectors by feature"):
                transpose_weights(nc, R, name + "t", c, loads, jobs)
            if given:
                with R.block() as block:
                    @block.vector
                    def _(dve):
                        nc.vector.tensor_scalar(bqk_scaled[:, 0, :], bqk[:, 0, :], HD ** -0.5, None, ALU.mult)
                        nc.vector.tensor_copy(bqk_scaled[:, 1, :], bqk[:, 1, :])
                        for n, dst in enumerate((wq, wk)):
                            for kc in range(KC):
                                nc.vector.tensor_copy(dst[:, kc, :].rearrange("p (h w) -> p h w", w=HP)[:, :, 0:HD],
                                                      raw[:, n, kc, :].rearrange("p (h w) -> p h w", w=HD))

        s_ps = S.ps("s_ps", [P, 2, BANK])
        t_ps = S.ps("t_ps", [P, 2, BANK])
        o_ps = S.ps("o_ps", [P, BANK])
        y_ps = S.ps("y_ps", [P, BANK])
        pq = S.ps("pq", [P, 2, BANK])
        x_staged, proj_ready, proj_free_d, proj_free_a = (S.sem(n) for n in ("x_staged", "proj_ready", "proj_free_d", "proj_free_a"))
        probs = S.sb("probs", [P, 2, NK])
        masked = S.sb("masked", [P, 2, NK]) if window else None
        probsT = S.sb("probsT", [P, 2, BANK])
        negmax = S.sb("negmax", [P, 2])
        sums = S.sb("sums", [P, HEADS])
        rsum = S.sb("rsum", [P, HEADS])
        o_sb = S.sb("o_sb", [P, DM])
        oT = S.sb("oT", [P, KC, P])
        (scores_ready, max_ready, probs_ready, pT_ready, pT_copied_a, pT_copied_d, pv_done, o_ready, o_norm, oT_ready,
         oT_copied, y_ready, y_added, step) = (S.sem(n) for n in (
             "scores_ready", "max_ready", "probs_ready", "pT_ready", "pT_copied_a", "pT_copied_d", "pv_done", "o_ready",
             "o_norm", "oT_ready", "oT_copied", "y_ready", "y_added", "step"))
        H = HEADS

        NPROJ = 2 * QC + QT
        HALF = NPROJ // 2

        def tiles(eng, project, body):
            with eng.Fori(0, BATCH) as b:
                project(b)
                for q in range(QT):
                    k0 = max(q - 1, 0) if window else 0
                    body(b * QT + q, q, k0, (q - k0 + 1) if window else QT)

        def project_out(eng, free, b, half):
            for j in range(half, NPROJ, 2):
                eng.wait_ge(proj_ready, b * NPROJ + (j + 1))
                if j < 2 * QC:
                    n, m = j // QC, j % QC
                    dst, scale = ((qT, HD ** -0.5), (kT, 1.0))[n]
                    out = dst[:, m, :]
                    if biased:
                        if half:
                            ins = nc.vector.tensor_scalar(out, pq[:, half, :], bqk[:, n, m:m + 1], scale, ALU.add, ALU.mult)
                        else:
                            ins = nc.scalar.activation(out, pq[:, half, :], ACT.Identity, bias=bqk_scaled[:, n, m:m + 1], scale=scale)
                    elif half:
                        ins = nc.vector.tensor_scalar(out, pq[:, half, :], scale, None, ALU.mult)
                    else:
                        ins = nc.scalar.mul(out, pq[:, half, :], scale)
                else:
                    out, src = v[:, j - 2 * QC, :], pq[:, half, 0:DM]
                    ins = nc.vector.tensor_copy(out, src) if half else nc.scalar.copy(out, src)
                ins.then_inc(free, 1)

        with S.block() as block:
            @block.tensor
            def _(pe):
                def body(t, q, k0, nb):
                    def scores(h):
                        pe.wait_ge(probs_ready, t * H + (h - 2 + 1 + 2))
                        r = HP * (h % 4)
                        nc.tensor.matmul(s_ps[:, h % 2, 0:nb * P], qT[r:r + HP, h // 4, q * P:(q + 1) * P],
                                         kT[r:r + HP, h // 4, k0 * P:(k0 + nb) * P], start=True, stop=True).then_inc(scores_ready, 1)

                    def turn(h):
                        pe.wait_ge(probs_ready, t * H + (h + 1 + 2))
                        pe.wait_ge(pT_copied_a if h % 2 else pT_copied_d, t * (H // 2) + (h // 2 + 1))
                        for kb in range(nb):
                            ins = nc.tensor.transpose(t_ps[:, h % 2, kb * P:(kb + 1) * P], probs[:, h % 2, kb * P:(kb + 1) * P], ident[:])
                        ins.then_inc(pT_ready, 1)

                    def pv(h):
                        pe.wait_ge(pT_copied_a if h % 2 else pT_copied_d, t * (H // 2) + (h // 2 + 2))
                        if h == 0:
                            pe.wait_ge(o_norm, t + 1)
                        for kb in range(nb):
                            ins = nc.tensor.matmul(o_ps[:, h * HD:(h + 1) * HD], probsT[:, h % 2, kb * P:(kb + 1) * P],
                                                   v[:, k0 + kb, h * HD:(h + 1) * HD], start=kb == 0, stop=kb == nb - 1)
                        ins.then_inc(pv_done, 1)

                    scores(0)
                    for h in range(H):
                        if h + 1 < H:
                            scores(h + 1)
                        turn(h)
                        if h > 0:
                            pv(h - 1)
                    pv(H - 1)
                    pe.wait_ge(o_norm, t + 2)
                    pe.wait_ge(y_added, t + 1)
                    for kc in range(KC):
                        ins = nc.tensor.transpose(y_ps[:, kc * P:(kc + 1) * P], o_sb[:, kc * P:(kc + 1) * P], ident[:])
                    ins.then_inc(oT_ready, 1)
                    pe.wait_ge(oT_copied, t + 1)
                    for kc in range(KC):
                        ins = nc.tensor.matmul(y_ps[:, DM:2 * DM], oT[:, kc, :], wo[:, kc, :], start=kc == 0, stop=kc == KC - 1)
                    ins.then_inc(y_ready, 1)

                def project(b):
                    pe.wait_ge(x_staged, b + 1)
                    for j in range(NPROJ):
                        pe.wait_ge(proj_free_d if j % 2 else proj_free_a, b * HALF + (j // 2 + 1))
                        for kc in range(KC):
                            if j < 2 * QC:
                                ins = nc.tensor.matmul(pq[:, j % 2, :], (wq, wk)[j // QC][:, kc, j % QC * P:(j % QC + 1) * P],
                                                       xb[:, kc, :], start=kc == 0, stop=kc == KC - 1)
                            else:
                                u = j - 2 * QC
                                ins = nc.tensor.matmul(pq[:, j % 2, 0:DM], xb[:, kc, u * P:(u + 1) * P], wv[:, kc, :],
                                                       start=kc == 0, stop=kc == KC - 1)
                        ins.then_inc(proj_ready, 1)
                    pe.wait_ge(proj_free_a, b * HALF + (HALF + 1))
                    pe.wait_ge(proj_free_d, b * HALF + (HALF + 1))

                tiles(pe, project, body)

            @block.gpsimd
            def _(pool):
                nc.gpsimd.tensor_copy(xb[:], xnT[:, :, 0:SEQ]).then_inc(x_staged, 1)
                with pool.Fori(1, BATCH) as b:
                    pool.wait_ge(proj_ready, b * NPROJ)
                    nc.gpsimd.tensor_copy(xb[:], xnT[:, :, bass.ds(b * SEQ, SEQ)]).then_inc(x_staged, 1)

            @block.vector
            def _(dve):
                dve.sem_inc(pT_copied_d, 1)
                dve.sem_inc(proj_free_d, 1)
                dve.sem_inc(o_norm, 1)
                dve.sem_inc(y_added, 1)
                STEPS = 1 + 2 * biased + window * HEADS

                def body(t, q, k0, nb):
                    n = nb * P
                    ch = Chain(dve, step, t * STEPS)

                    def row_max(h):
                        dve.wait_ge(scores_ready, t * H + (h + 1))
                        dve.wait_ge(probs_ready, t * H + (h - 2 + 1 + 2))
                        src = s_ps
                        if window:
                            src = masked
                            ch.step(nc.vector.tensor_tensor(masked[:, h % 2, 0:n], s_ps[:, h % 2, 0:n], mask[:, NK - n:NK], ALU.add))
                        nc.vector.tensor_reduce(negmax[:, h % 2:h % 2 + 1], src[:, h % 2, 0:n], AX, ALU.max,
                                                negate=True).then_inc(max_ready, 1)

                    def copy_out(h):
                        dve.wait_ge(pT_ready, t * H + (h + 1))
                        nc.vector.tensor_copy(probsT[:, h % 2, 0:n], t_ps[:, h % 2, 0:n]).then_inc(pT_copied_d, 1)

                    row_max(0)
                    for h in range(H):
                        if h + 1 < H:
                            row_max(h + 1)
                        if h % 2 == 0:
                            copy_out(h)
                    dve.wait_ge(probs_ready, t * H + (H + 2))
                    ch.step(nc.vector.reciprocal(rsum[:], sums[:]))
                    dve.wait_ge(pv_done, t * H + H)
                    normed = nc.vector.tensor_tensor(o_sb[:].rearrange("p (h w) -> p h w", w=HD),
                                                     o_ps[:, 0:DM].rearrange("p (h w) -> p h w", w=HD),
                                                     rsum[:, :, None].to_broadcast([P, H, HD]), ALU.mult)
                    if biased:
                        ch.step(normed)
                        normed = nc.vector.tensor_tensor(o_sb[:], o_sb[:], bvb[:], ALU.add)
                    normed.then_inc(o_norm, 1)
                    dve.wait_ge(oT_ready, t + 1)
                    nc.vector.tensor_copy(oT[:], y_ps[:, 0:DM]).then_inc(oT_copied, 1)
                    if bo is not None:
                        ch.step(nc.vector.tensor_tensor(x[:, t, :], x[:, t, :], bob[:], ALU.add))
                    dve.wait_ge(y_ready, t + 1)
                    nc.vector.tensor_tensor(x[:, t, :], x[:, t, :], y_ps[:, DM:2 * DM], ALU.add).then_inc(y_added, 1)

                tiles(dve, lambda b: project_out(dve, proj_free_d, b, 1), body)

            @block.scalar
            def _(act):
                act.sem_inc(pT_copied_a, 1)
                act.sem_inc(proj_free_a, 1)
                act.sem_inc(probs_ready, 2)

                def body(t, q, k0, nb):
                    n = nb * P

                    def exp(h):
                        act.wait_ge(max_ready, t * H + (h + 1))
                        if h >= 2:
                            act.wait_ge(pT_ready, t * H + (h - 1))
                        src = masked if window else s_ps
                        nc.scalar.activation(probs[:, h % 2, 0:n], src[:, h % 2, 0:n], ACT.Exp, bias=negmax[:, h % 2:h % 2 + 1],
                                             accum_out=sums[:, h:h + 1]).then_inc(probs_ready, 1)

                    for h in range(H):
                        exp(h)
                        if h % 2 == 0 and h >= 2:
                            copy_out(t, h - 1, n)
                    copy_out(t, H - 1, n)

                def copy_out(t, h, n):
                    act.wait_ge(pT_ready, t * H + (h + 1))
                    nc.scalar.copy(probsT[:, h % 2, 0:n], t_ps[:, h % 2, 0:n]).then_inc(pT_copied_a, 1)

                tiles(act, lambda b: project_out(act, proj_free_a, b, 0), body)


CTX, CD = 64, 192
CTOK = BATCH * CTX
CT = CTOK // P
CK = ((0, P), (P, CD - P))
HK = HEADS * CTX


def cross_attention(nc, name, c, wts, dh, out_in=False, norm_ctx=False, clamp=None):
    x, xnT, ident, ones = c["x"], c["xnT"], c["ident"], c["ones"]
    inner = HEADS * dh
    NC = inner // P
    HC = P // dh
    bq, bo = wts.get("bq"), wts.get("bo")
    kv_biased = "bk" in wts or "bkv" in wts
    with Scope(nc, name) as S:
        qk = S.sb("qk", [P, BATCH, KC, HK])
        vo = S.sb("vo", [P, BATCH, HK // P, DM])
        brow = S.sb("brow", [1, BATCH, HK]) if bq is not None else None
        bob = S.sb("bob", [P, DM]) if bo is not None else None
        with Scope(nc, name + "p") as W:
            wqT = W.sb("wqT", [P, NC, DM])
            wo = W.sb("wo", [P, NC, DM])
            wkv = W.sb("wkv", [P, 2, 2, inner])
            ctxT = W.sb("ctxT", [P, 2, CTOK])
            kvT = W.sb("kvT", [P, 2, NC, CTOK])
            ctx = W.sb("ctx", [P, CT, CD])
            heads = W.sb("heads", [P, HC])
            bkv_col = W.sb("bkv_col", [P, 2, NC]) if kv_biased else None
            bq_col = W.sb("bq_col", [P, NC]) if bq is not None else None
            diag = W.sb("diag", [P, 2, 2, HK])
            made = W.sem("made")
            with W.block() as block:
                @block.gpsimd
                def _(pool):
                    nc.gpsimd.memset(heads[:], 1.0).then_inc(made, 1)
                    pool.wait_ge(made, 1)
                    nc.gpsimd.affine_select(out=heads[:], in_=heads[:], compare_op=ALU.is_ge, fill=0.0, base=0,
                                            pattern=[[-dh, HC]], channel_multiplier=1).then_inc(made, 1)
                    pool.wait_ge(made, 2)
                    nc.gpsimd.affine_select(out=heads[:], in_=heads[:], compare_op=ALU.is_ge, fill=0.0, base=dh - 1,
                                            pattern=[[dh, HC]], channel_multiplier=-1)
            with Scope(nc, name + "r") as R:
                loads = [(ctx[:], c["ctx_dram"])]
                jobs = []
                if out_in:
                    raw = R.sb("raw", [P, 2, 2, CD])
                    rawo = R.sb("rawo", [P, KC, DM])
                    per_head = wts["Wkv"].rearrange("(h n w) c -> h n w c", n=2, w=dh)
                    bias_head = wts["bkv"].rearrange("(h n w) -> h n w", n=2, w=dh)
                    for h in range(HEADS):
                        r = h % HC * dh
                        for n in range(2):
                            loads.append((raw[r:r + dh, n, h // HC, :], per_head[h, n]))
                            loads.append((bkv_col[r:r + dh, n, h // HC:h // HC + 1], bias_head[h, n][:, None]))
                    loads.append((wqT[:], wts["Wq"].rearrange("(c p) d -> p c d", p=P)))
                    loads.append((rawo[:], wts["Wo"].rearrange("(c p) d -> p c d", p=P)))
                    for n in range(2):
                        for o in range(NC):
                            for k, (k0, kn) in enumerate(CK):
                                jobs.append((wkv[0:kn, k, n, o * P:(o + 1) * P], raw[:, n, o, k0:k0 + kn]))
                    for k in range(KC):
                        for o in range(KC):
                            jobs.append((wo[:, k, o * P:(o + 1) * P], rawo[:, o, k * P:(k + 1) * P]))
                else:
                    raw = R.sb("raw", [P, KC, inner])
                    loads.append((raw[:], wts["Wq"].rearrange("(k p) n -> p k n", p=P)))
                    loads.append((wo[:], wts["Wo"].rearrange("(c p) n -> p c n", p=P)))
                    for n, w in enumerate(("Wk", "Wv")):
                        for k, (k0, kn) in enumerate(CK):
                            loads.append((wkv[0:kn, k, n, :], wts[w][k0:k0 + kn, :]))
                    for cc in range(NC):
                        for k in range(KC):
                            jobs.append((wqT[:, cc, k * P:(k + 1) * P], raw[:, k, cc * P:(cc + 1) * P]))
                    if kv_biased:
                        for n, b in enumerate(("bk", "bv")):
                            loads.append((bkv_col[:, n, :], wts[b].rearrange("(c p) -> p c", p=P)))
                if bq is not None:
                    loads.append((bq_col[:], bq.rearrange("(c p) -> p c", p=P)))
                if bo is not None:
                    loads.append((bob[:], bo[None, :].to_broadcast([P, DM])))
                if norm_ctx:
                    gc = R.sb("gc", [P, 2, CD])
                    loads.append((gc[:, 0, :], wts["g_c"][None, :].to_broadcast([P, CD])))
                    loads.append((gc[:, 1, :], wts["b_c"][None, :].to_broadcast([P, CD])))
                with nc.allow_non_contiguous_dma(reason="bias vectors by feature"):
                    transpose_weights(nc, R, name + "t", c, loads, jobs)
                if norm_ctx:
                    st, mean, rstd, tmp = R.sb("st", [P, CT, 6]), R.sb("mean", [P, CT]), R.sb("rstd", [P, CT]), R.sb("tmp", [P, CT])
                    step, var_ready, std_ready = R.sem("step"), R.sem("var_ready"), R.sem("std_ready")
                    with R.block() as block:
                        @block.vector
                        def _(dve):
                            ch = Chain(dve, step)
                            for i in range(CT):
                                ch.step(nc.vector.bn_stats(st[:, i, :], ctx[:, i, :]))
                            row_stats_to_affine(nc, ch, None, None, st, mean[:], rstd[:], tmp[:], CD // 2)
                            nc.vector.tensor_copy(tmp[:], rstd[:]).then_inc(var_ready, 1)
                            dve.wait_ge(std_ready, 1)
                            ch.step(nc.vector.reciprocal(rstd[:], tmp[:]))
                            for i in range(CT):
                                ch.step(nc.vector.tensor_scalar(ctx[:, i, :], ctx[:, i, :], mean[:, i:i + 1], rstd[:, i:i + 1],
                                                                ALU.subtract, ALU.mult))
                            ch.step(nc.vector.tensor_tensor(ctx[:], ctx[:], gc[:, None, 0, :].to_broadcast([P, CT, CD]), ALU.mult))
                            nc.vector.tensor_tensor(ctx[:], ctx[:], gc[:, None, 1, :].to_broadcast([P, CT, CD]), ALU.add)

                        @block.scalar
                        def _(act):
                            act.wait_ge(var_ready, 1)
                            nc.scalar.activation(tmp[:], tmp[:], ACT.Sqrt).then_inc(std_ready, 1)

            jobs = [(ctxT[0:kn, k, i * P:(i + 1) * P], ctx[:, i, k0:k0 + kn]) for i in range(CT) for k, (k0, kn) in enumerate(CK)]
            transpose_weights(nc, W, name + "c", c, [], jobs)

            with Scope(nc, name + "k") as R:
                kv_ps = R.ps("kv_ps", [P, 4, BANK])
                kv_ready, kv_free = R.sem("kv_ready"), R.sem("kv_free")
                with R.block() as block:
                    @block.tensor
                    def _(pe):
                        for j in range(2 * NC):
                            if j >= 4:
                                pe.wait_ge(kv_free, j - 3)
                            for k, (k0, kn) in enumerate(CK):
                                ins = nc.tensor.matmul(kv_ps[:, j % 4, 0:CTOK], wkv[0:kn, k, j // NC, j % NC * P:(j % NC + 1) * P],
                                                       ctxT[0:kn, k, :], start=k == 0, stop=k == 1)
                            ins.then_inc(kv_ready, 1)

                    @block.vector
                    def _(dve):
                        for j in range(2 * NC):
                            n, cc = j // NC, j % NC
                            dve.wait_ge(kv_ready, j + 1)
                            scale = dh ** -0.5 if n == 0 else 1.0
                            if kv_biased:
                                ins = nc.vector.tensor_scalar(kvT[:, n, cc, :], kv_ps[:, j % 4, 0:CTOK], bkv_col[:, n, cc:cc + 1], scale, ALU.add, ALU.mult)
                            else:
                                ins = nc.vector.tensor_scalar(kvT[:, n, cc, :], kv_ps[:, j % 4, 0:CTOK], scale, None, ALU.mult)
                            ins.then_inc(kv_free, 1)

            with Scope(nc, name + "g") as R:
                qk_ps = R.ps("qk_ps", [P, KC, HK])
                vo_ps = R.ps("vo_ps", [P, 4, 2, DM])
                diag_ready, qk_ready, vo_ready, qk_copied, vo_copied, b_ready, b_copied = (R.sem(n) for n in (
                    "diag_ready", "qk_ready", "vo_ready", "qk_copied", "vo_copied", "b_ready", "b_copied"))
                CW = HC * CTX
                with R.block() as block:
                    @block.gpsimd
                    def _(pool):
                        for b in range(BATCH):
                            if b >= 2:
                                pool.wait_ge(vo_ready, b - 1)
                            for n in range(2):
                                for cc in range(NC):
                                    ins = nc.gpsimd.tensor_tensor(
                                        diag[:, b % 2, n, cc * CW:(cc + 1) * CW].rearrange("p (h k) -> p h k", k=CTX),
                                        kvT[:, n, cc, None, b * CTX:(b + 1) * CTX].to_broadcast([P, HC, CTX]),
                                        heads[:, :, None].to_broadcast([P, HC, CTX]), ALU.mult)
                            ins.then_inc(diag_ready, 1)

                    @block.tensor
                    def _(pe):
                        for b in range(BATCH):
                            pe.wait_ge(diag_ready, b + 1)
                            if b:
                                pe.wait_ge(qk_copied, b)
                            for k in range(KC):
                                for cc in range(NC):
                                    ins = nc.tensor.matmul(qk_ps[:, k, cc * CW:(cc + 1) * CW], wqT[:, cc, k * P:(k + 1) * P],
                                                           diag[:, b % 2, 0, cc * CW:(cc + 1) * CW], start=True, stop=True)
                            ins.then_inc(qk_ready, 1)
                            if bq is not None:
                                pe.wait_ge(qk_copied, b + 1)
                                for cc in range(NC):
                                    ins = nc.tensor.matmul(qk_ps[0:1, 0, cc * CW:(cc + 1) * CW], bq_col[:, cc:cc + 1],
                                                           diag[:, b % 2, 0, cc * CW:(cc + 1) * CW], start=True, stop=True)
                                ins.then_inc(b_ready, 1)
                                pe.wait_ge(b_copied, b + 1)
                            if b:
                                pe.wait_ge(vo_copied, b)
                            for j in range(HK // P):
                                ins = nc.tensor.matmul(vo_ps[:, j // 2, j % 2, :], diag[:, b % 2, 1, j * P:(j + 1) * P],
                                                       wo[:, j * P // CW, :], start=True, stop=True)
                            ins.then_inc(vo_ready, 1)

                    @block.vector
                    def _(dve):
                        for b in range(BATCH):
                            dve.wait_ge(qk_ready, b + 1)
                            nc.vector.tensor_copy(qk[:, b], qk_ps[:]).then_inc(qk_copied, 1)
                            if bq is not None:
                                dve.wait_ge(b_ready, b + 1)
                                nc.vector.tensor_copy(brow[0:1, b, :], qk_ps[0:1, 0, :]).then_inc(b_copied, 1)

                    @block.scalar
                    def _(act):
                        for b in range(BATCH):
                            act.wait_ge(vo_ready, b + 1)
                            nc.scalar.copy(vo[:, b].rearrange("p j n -> p (j n)"), vo_ps[:].rearrange("p a b n -> p (a b n)")).then_inc(vo_copied, 1)

        s_ps = S.ps("s_ps", [P, 2, HK])
        t_ps = S.ps("t_ps", [P, HK])
        y_ps = S.ps("y_ps", [P, BANK])
        x_now = S.sb("x_now", [P, QT, KC, P])
        shifted = S.sb("shifted", [P, 2, HEADS, CTX])
        probs = S.sb("probs", [P, 2, HEADS, CTX])
        probsT = S.sb("probsT", [P, 2, HK])
        negmax = S.sb("negmax", [P, 2, HEADS])
        rsum = S.sb("rsum", [P, 2, HEADS])
        (x_staged, scores_ready, shifted_ready, exp_ready, sum_ready, probs_ready, pT_ready, pT_copied, y_ready, y_added, step) = (
            S.sem(n) for n in ("x_staged", "scores_ready", "shifted_ready", "exp_ready", "sum_ready", "probs_ready", "pT_ready",
                               "pT_copied", "y_ready", "y_added", "step"))
        clamped = S.sb("clamped", [P, 2, HEADS, CTX]) if clamp else None

        def tiles(eng, body):
            with eng.Fori(0, BATCH) as b:
                for q in range(QT):
                    body(b, q, b * QT + q)

        with S.block() as block:
            @block.gpsimd
            def _(pool):
                with pool.Fori(0, BATCH) as b:
                    for q in range(QT):
                        nc.gpsimd.tensor_copy(x_now[:, q], xnT[:, :, bass.ds((b * QT + q) * P, P)]).then_inc(x_staged, 1)
                    for q in range(QT):
                        t = b * QT + q
                        pool.wait_ge(sum_ready, t + 1)
                        nc.gpsimd.tensor_tensor(probs[:, q % 2], shifted[:, q % 2], rsum[:, q % 2, :, None].to_broadcast([P, HEADS, CTX]),
                                                ALU.mult).then_inc(probs_ready, 1)

            @block.tensor
            def _(pe):
                def scores(b, q, t):
                    pe.wait_ge(x_staged, t + 1)
                    pe.wait_ge(shifted_ready, t + 1)
                    for half in range(2):
                        cols = bass.ts(half, BANK)
                        for k in range(KC):
                            ins = nc.tensor.matmul(s_ps[:, q % 2, cols], x_now[:, q, k, :], qk[:, b, k, cols],
                                                   start=k == 0, stop=k == KC - 1 and bq is None)
                        if bq is not None:
                            ins = nc.tensor.matmul(s_ps[:, q % 2, cols], ones[0:1, :], brow[0:1, b, cols], start=False, stop=True)
                    ins.then_inc(scores_ready, 1)

                def output(b, q, t):
                    pe.wait_ge(probs_ready, t + 1)
                    pe.wait_ge(pT_copied, t + 1)
                    for j in range(HK // P):
                        ins = nc.tensor.transpose(t_ps[:, j * P:(j + 1) * P], probs[:, q % 2, 2 * j:2 * j + 2, :].rearrange("p h k -> p (h k)"), ident[:])
                    ins.then_inc(pT_ready, 1)
                    pe.wait_ge(pT_copied, t + 2)
                    pe.wait_ge(y_added, t + 1)
                    for j in range(HK // P):
                        ins = nc.tensor.matmul(y_ps[:, 0:DM], probsT[:, q % 2, j * P:(j + 1) * P], vo[:, b, j, :],
                                               start=j == 0, stop=j == HK // P - 1)
                    ins.then_inc(y_ready, 1)

                with pe.Fori(0, BATCH) as b:
                    scores(b, 0, b * QT)
                    for q in range(QT):
                        if q + 1 < QT:
                            scores(b, q + 1, b * QT + (q + 1))
                        output(b, q, b * QT + q)

            @block.vector
            def _(dve):
                dve.sem_inc(y_added, 1)
                dve.sem_inc(shifted_ready, 2)
                STEPS = 2 + (clamp is not None) + (bo is not None)

                def shift(b, q, t):
                    ch = Chain(dve, step, t * STEPS)
                    dve.wait_ge(scores_ready, t + 1)
                    src = s_ps[:, q % 2].rearrange("p (h k) -> p h k", k=CTX)
                    if clamp:
                        ch.step(nc.vector.tensor_scalar(clamped[:, q % 2], src, clamp, -clamp, ALU.min, ALU.max))
                        src = clamped[:, q % 2]
                    ch.step(nc.vector.tensor_reduce(negmax[:, q % 2], src, AX, ALU.max, negate=True))
                    nc.vector.tensor_tensor(shifted[:, q % 2], src, negmax[:, q % 2, :, None].to_broadcast([P, HEADS, CTX]),
                                            ALU.add).then_inc(shifted_ready, 1)

                def finish(b, q, t):
                    ch = Chain(dve, step, t * STEPS + (STEPS - 1 - (bo is not None)))
                    dve.wait_ge(exp_ready, t + 1)
                    ch.step(nc.vector.tensor_reduce(rsum[:, q % 2], shifted[:, q % 2], AX, ALU.add))
                    nc.vector.reciprocal(rsum[:, q % 2], rsum[:, q % 2]).then_inc(sum_ready, 1)
                    if bo is not None:
                        ch.step(nc.vector.tensor_tensor(x[:, t, :], x[:, t, :], bob[:], ALU.add))

                def add(b, q, t):
                    dve.wait_ge(y_ready, t + 1)
                    nc.vector.tensor_tensor(x[:, t, :], x[:, t, :], y_ps[:, 0:DM], ALU.add).then_inc(y_added, 1)

                with dve.Fori(0, BATCH) as b:
                    for q in range(QT):
                        t = b * QT + q
                        shift(b, q, t)
                        finish(b, q, t)
                        if q > 0:
                            add(b, q - 1, b * QT + (q - 1))
                    add(b, QT - 1, b * QT + (QT - 1))

            @block.scalar
            def _(act):
                act.sem_inc(pT_copied, 1)

                def body(b, q, t):
                    act.wait_ge(shifted_ready, t + 3)
                    nc.scalar.activation(shifted[:, q % 2], shifted[:, q % 2], ACT.Exp).then_inc(exp_ready, 1)
                    act.wait_ge(pT_ready, t + 1)
                    nc.scalar.copy(probsT[:, q % 2], t_ps[:]).then_inc(pT_copied, 1)

                tiles(act, body)


NE = 8
BIG = 1 << 20


def route(nc, S, name, c, gate_w, gate_b, transposed, choices, capacity, dropped_expert=None):
    xnT, ident, ones = c["xnT"], c["ident"], c["ones"]
    T3 = [P, TILES, NE]
    res = {n: [S.sb(f"{n}{j}", [P, TILES]) for j in range(choices)] for n in ("weight", "keep", "slot")}
    with Scope(nc, name) as R:
        wg = R.sb("wg", [P, KC, NE])
        loads, jobs = [], []
        if transposed:
            raw = R.sb("raw", [NE, DM])
            loads.append((raw[:], gate_w))
            jobs = [(wg[:, k, :], raw[:, k * P:(k + 1) * P]) for k in range(KC)]
        else:
            loads.append((wg[:], gate_w.rearrange("(k p) e -> p k e", p=P)))
        bias = None
        if gate_b is not None:
            bias = R.sb("bias", [P, NE])
            loads.append((bias[:], gate_b[None, :].to_broadcast([P, NE])))
        transpose_weights(nc, R, name + "t", c, loads, jobs)

        lg_ps = R.ps("lg_ps", [P, BANK])
        pos_ps = R.ps("pos_ps", [P, BANK])
        tot_ps = R.ps("tot_ps", [P, BANK])
        logits, probs, scratch, mask = (R.sb(n, T3) for n in ("logits", "probs", "scratch", "mask"))
        onehot = [R.sb(f"onehot{j}", T3) for j in range(choices)]
        place, totals, sums_a, sums_b = (R.sb(n, T3) for n in ("place", "totals", "sums_a", "sums_b"))
        small, small2 = R.sb("small", [P, TILES]), R.sb("small2", [P, TILES])
        number = R.sb("number", [P, NE])
        before = R.sb("before", [P, P])
        lg_ready, shifted_ready, exp_ready, mask_ready, counts_ready, step, made = (R.sem(n) for n in (
            "lg_ready", "shifted_ready", "exp_ready", "mask_ready", "counts_ready", "step", "made"))

        def per_tile(a):
            return a[:, :, None].to_broadcast(T3)

        def per_expert(a):
            return a[:, None, :].to_broadcast(T3)

        with R.block() as block:
            @block.gpsimd
            def _(pool):
                nc.gpsimd.iota(number[:], pattern=[[1, NE]], base=0, channel_multiplier=0,
                               allow_small_or_imprecise_dtypes=True).then_inc(made, 1)
                nc.gpsimd.memset(before[:], 1.0).then_inc(made, 1)
                pool.wait_ge(made, 2)
                nc.gpsimd.affine_select(out=before[:], in_=before[:], compare_op=ALU.is_ge, fill=0.0, base=-1,
                                        pattern=[[1, P]], channel_multiplier=-1).then_inc(made, 1)

            @block.tensor
            def _(pe):
                for t in range(TILES):
                    for k in range(KC):
                        ins = nc.tensor.matmul(lg_ps[:, t * NE:(t + 1) * NE], xnT[:, k, t * P:(t + 1) * P], wg[:, k, :],
                                               start=k == 0, stop=k == KC - 1)
                ins.then_inc(lg_ready, 1)
                pe.wait_ge(made, 3)
                pe.wait_ge(mask_ready, 1)
                flat = mask[:].rearrange("p t e -> p (t e)")
                nc.tensor.matmul(pos_ps[:, 0:TILES * NE], before[:], flat, start=True, stop=True)
                nc.tensor.matmul(tot_ps[:, 0:TILES * NE], ones[:], flat, start=True, stop=True).then_inc(counts_ready, 1)

            @block.scalar
            def _(act):
                act.wait_ge(shifted_ready, 1)
                nc.scalar.activation(probs[:], logits[:], ACT.Exp).then_inc(exp_ready, 1)

            @block.vector
            def _(dve):
                ch = Chain(dve, step)
                v = nc.vector
                dve.wait_ge(lg_ready, 1)
                lg = lg_ps[:, 0:TILES * NE].rearrange("p (t e) -> p t e", e=NE)
                if bias is not None:
                    ch.step(v.tensor_tensor(logits[:], lg, per_expert(bias), ALU.add))
                else:
                    ch.step(v.tensor_copy(logits[:], lg))
                ch.step(v.tensor_reduce(small[:], logits[:], AX, ALU.max))
                v.tensor_tensor(logits[:], logits[:], per_tile(small), ALU.subtract).then_inc(shifted_ready, 1)
                dve.wait_ge(exp_ready, 1)
                ch.step(v.tensor_reduce(small[:], probs[:], AX, ALU.add))
                ch.step(v.reciprocal(small[:], small[:]))
                ch.step(v.tensor_tensor(probs[:], probs[:], per_tile(small), ALU.mult))
                dve.wait_ge(made, 3)
                for j in range(choices):
                    w = res["weight"][j]
                    ch.step(v.tensor_reduce(w[:], probs[:], AX, ALU.max))
                    ch.step(v.tensor_tensor(scratch[:], probs[:], per_tile(w), ALU.not_equal))
                    ch.step(v.tensor_scalar(scratch[:], scratch[:], 100.0, None, ALU.mult))
                    ch.step(v.tensor_tensor(scratch[:], scratch[:], per_expert(number), ALU.add))
                    ch.step(v.tensor_reduce(small[:], scratch[:], AX, ALU.min))
                    ch.step(v.tensor_tensor(onehot[j][:], per_tile(small), per_expert(number), ALU.is_equal))
                    if j + 1 < choices:
                        ch.step(v.tensor_scalar(scratch[:], onehot[j][:], 4.0, None, ALU.mult))
                        ch.step(v.tensor_tensor(probs[:], probs[:], scratch[:], ALU.subtract))
                for j in range(choices):
                    ch.step(v.tensor_scalar(small[:], res["weight"][j][:], 0.0, None, ALU.is_gt))
                    ch.step(v.tensor_tensor(onehot[j][:], onehot[j][:], per_tile(small), ALU.mult))
                if choices == 1:
                    ins = v.tensor_copy(mask[:], onehot[0][:])
                else:
                    ins = v.tensor_tensor(mask[:], onehot[0][:], onehot[1][:], ALU.add)
                ins.then_inc(mask_ready, 1)
                dve.wait_ge(counts_ready, 1)
                tot = tot_ps[:, 0:TILES * NE].rearrange("p (t e) -> p t e", e=NE)
                ch.step(v.tensor_copy(totals[:], tot))
                ch.step(v.tensor_copy(sums_a[:], tot))
                src, dst = sums_a, sums_b
                for d in (1, 2, 4, 8):
                    ch.step(v.tensor_copy(dst[:, 0:d, :], src[:, 0:d, :]))
                    ch.step(v.tensor_tensor(dst[:, d:, :], src[:, d:, :], src[:, 0:TILES - d, :], ALU.add))
                    src, dst = dst, src
                ch.step(v.tensor_tensor(place[:], src[:], totals[:], ALU.subtract))
                ch.step(v.tensor_tensor(place[:], place[:], pos_ps[:, 0:TILES * NE].rearrange("p (t e) -> p t e", e=NE), ALU.add))
                ch.step(v.tensor_scalar(scratch[:], place[:], float(capacity), None, ALU.is_ge))
                if dropped_expert is not None:
                    ch.step(v.memset(scratch[:, :, dropped_expert:dropped_expert + 1], 1.0))
                ch.step(v.tensor_scalar(sums_a[:], scratch[:], float(BIG), None, ALU.mult))
                ch.step(v.tensor_tensor(place[:], place[:], sums_a[:], ALU.add))
                ch.step(v.tensor_scalar(small2[:, 0:NE], number[:], float(capacity), None, ALU.mult))
                ch.step(v.tensor_tensor(place[:], place[:], per_expert(small2[:, 0:NE]), ALU.add))
                ch.step(v.tensor_scalar(scratch[:], scratch[:], -1.0, 1.0, ALU.mult, ALU.add))
                for j in range(choices):
                    ch.step(v.tensor_tensor(sums_a[:], onehot[j][:], place[:], ALU.mult))
                    ch.step(v.tensor_reduce(res["slot"][j][:], sums_a[:], AX, ALU.add))
                    ch.step(v.tensor_scalar(small[:], res["weight"][j][:], 0.0, float(BIG), ALU.is_le, ALU.mult))
                    ch.step(v.tensor_tensor(res["slot"][j][:], res["slot"][j][:], small[:], ALU.add))
                    ch.step(v.tensor_tensor(sums_a[:], onehot[j][:], scratch[:], ALU.mult))
                    ch.step(v.tensor_reduce(res["keep"][j][:], sums_a[:], AX, ALU.add))
                if dropped_expert is not None:
                    noop = S.noop
                    for j in range(choices):
                        ch.step(v.tensor_tensor(small[:], onehot[j][:, :, dropped_expert], res["weight"][j][:], ALU.mult))
                        if j == 0:
                            ch.step(v.tensor_copy(noop[:], small[:]))
                        else:
                            ch.step(v.tensor_tensor(noop[:], noop[:], small[:], ALU.add))
    return res


def gated_linear(nc, name, c, wts, capacity):
    x, xnT = c["x"], c["xnT"]
    with Scope(nc, name) as S:
        r = route(nc, S, name + "r", c, wts["w_gate"], None, False, 1, capacity)
        w, bb = S.sb("w", [P, KC, DM]), S.sb("bb", [P, DM])
        transpose_weights(nc, S, name + "t", c, [(w[:], wts["w_expert"].rearrange("(k p) n -> p k n", p=P)),
                                                 (bb[:], wts["b_expert"][None, :].to_broadcast([P, DM]))], [])
        y_ps = S.ps("y_ps", [P, 4, BANK])
        scale, biased = S.sb("scale", [P, TILES]), S.sb("biased", [P, 2, DM])
        y_ready, y_read, step = S.sem("y_ready"), S.sem("y_read"), S.sem("step")
        with S.block() as block:
            @block.tensor
            def _(pe):
                for t in range(TILES):
                    if t >= 4:
                        pe.wait_ge(y_read, t - 3)
                    for k in range(KC):
                        ins = nc.tensor.matmul(y_ps[:, t % 4, 0:DM], xnT[:, k, t * P:(t + 1) * P], w[:, k, :], start=k == 0, stop=k == KC - 1)
                    ins.then_inc(y_ready, 1)

            @block.vector
            def _(dve):
                ch = Chain(dve, step)
                ch.step(nc.vector.tensor_tensor(scale[:], r["weight"][0][:], r["keep"][0][:], ALU.mult))
                with dve.Fori(0, TILES // 4) as g:
                    for u in range(4):
                        t = g * 4 + u
                        dve.wait_ge(y_ready, t + 1)
                        nc.vector.tensor_tensor(biased[:, u % 2, :], y_ps[:, u, 0:DM], bb[:], ALU.add).then_inc(y_read, 1)
                        dve.wait_ge(y_read, t + 1)
                        nc.vector.scalar_tensor_tensor(out=x[:, t, :], in0=biased[:, u % 2, :], scalar=scale[:, bass.ds(t, 1)],
                                                       in1=x[:, t, :], op0=ALU.mult, op1=ALU.add).then_inc(step, 1)


def mixture(nc, name, c, wts, n_exp, choices, disp, eout, filled):
    x, xn, ident, ones = c["x"], c["xn"], c["ident"], c["ones"]
    cap = TOK // NE
    CTL = cap // P
    HID = 1024
    HC = HID // P
    l0 = choices == 2
    w1 = wts["experts_inter" if l0 else "w1"]
    w2 = wts["experts_out" if l0 else "w2"]
    rows = n_exp * cap
    with Scope(nc, name) as S:
        S.noop = S.sb("noop", [P, TILES]) if l0 else None
        if l0:
            r = route(nc, S, name + "r", c, wts["router_w"], wts["router_b"], True, 2, cap, dropped_expert=NE - 1)
        else:
            r = route(nc, S, name + "r", c, wts["wg"], None, False, 1, cap)
        slot_i = [S.sb(f"slot_i{j}", [P, TILES], U32) for j in range(choices)]
        back_i = [S.sb(f"back_i{j}", [P, TILES], U32) for j in range(choices)]
        back_f = S.sb("back_f", [P, TILES])
        w1_sb, w2_sb = S.sb("w1", [P, 2, KC, HID]), S.sb("w2", [P, 2, HC, DM])
        b1_sb = None if l0 else S.sb("b1", [P, NE, HC])
        b2_sb = None if l0 else S.sb("b2", [1, NE, DM])
        if not l0:
            with Scope(nc, name + "b") as B:
                rawb = B.sb("rawb", [NE * HC, P])
                transpose_weights(nc, B, name + "bt", c, [(rawb[:], wts["b1"].rearrange("e (c p) -> (e c) p", p=P))],
                                  [(b1_sb[:].rearrange("p e c -> p (e c)"), rawb[:])])
        xe = S.sb("xe", [P, 2, CTL, DM])
        xeT = S.sb("xeT", [P, 2, KC, cap])
        hT = S.sb("hT", [P, 2, HC, cap])
        ye = S.sb("ye", [P, 2, CTL, DM])
        back = S.sb("back", [P, 2, 4, DM])
        (index_ready, scattered, loaded0, loaded1, bias_loaded, stored0, stored1, xeT_ready, xeT_copied, h_ready, h_copied,
         y_ready, y_copied, added, step) = (S.sem(n) for n in (
             "index_ready", "scattered", "loaded0", "loaded1", "bias_loaded", "stored0", "stored1", "xeT_ready", "xeT_copied",
             "h_ready", "h_copied", "y_ready", "y_copied", "added", "step"))
        loaded, stored = (loaded0, loaded1), (stored0, stored1)
        h_copied_d = S.sem("h_copied_d")
        gathered = [S.sem(f"gathered{n}") for n in range(8)]
        x_loaded = (S.sem("x_loaded0"), S.sem("x_loaded1"))
        t_ps = S.ps("t_ps", [P, KC, cap])
        h_ps = S.ps("h_ps", [P, 4, BANK])
        y_ps = S.ps("y_ps", [P, 2, BANK])

        def experts(eng, body):
            with eng.Fori(0, n_exp // 2) as g:
                for u in range(2):
                    body(g * 2 + u, u, g)
            if n_exp % 2:
                body(n_exp - 1, 0, n_exp // 2)

        with S.block() as block:
            @block.vector
            def _(dve):
                ch = Chain(dve, step)
                for j in range(choices):
                    ch.step(nc.vector.tensor_scalar(back_f[:], r["slot"][j][:], float(rows - 1), None, ALU.min))
                    ch.step(nc.vector.tensor_copy(back_i[j][:], back_f[:]))
                    ch.step(nc.vector.tensor_copy(slot_i[j][:], r["slot"][j][:]))
                    ch.step(nc.vector.tensor_tensor(r["weight"][j][:], r["weight"][j][:], r["keep"][j][:], ALU.mult))
                nc.vector.tensor_copy(back_f[:], back_f[:]).then_inc(index_ready, 1)

                base = ch.n

                def body(e, u, turn):
                    dve.wait_ge(xeT_ready, e + 1)
                    nc.vector.tensor_copy(xeT[:, u], t_ps[:]).then_inc(xeT_copied, 1)
                    for m in range(1, HC, 2):
                        dve.wait_ge(h_ready, e * HC + (m + 1))
                        if l0:
                            ins = nc.vector.tensor_scalar(hT[:, u, m, :], h_ps[:, m % 4, 0:cap], 0.0, None, ALU.max)
                        else:
                            ins = nc.vector.tensor_scalar(hT[:, u, m, :], h_ps[:, m % 4, 0:cap], b1_sb[:, bass.ds(e, 1), m], 0.0, ALU.add, ALU.max)
                        ins.then_inc(h_copied_d, 1)
                    dve.wait_ge(y_ready, e * CTL + 2)
                    dve.wait_ge(stored[u], 16 * turn + 16)
                    nc.vector.tensor_copy(ye[:, u], y_ps[:, :, 0:DM]).then_inc(y_copied, 1)

                experts(dve, body)
                for k in range(TILES * choices // 4):
                    for i in range(4):
                        t, j = (k * 4 + i) // choices, (k * 4 + i) % choices
                        dve.wait_ge(gathered[k % 2 * 4 + i], 16 * (k // 2 + 1))
                        ins = nc.vector.scalar_tensor_tensor(out=x[:, t, :], in0=back[:, k % 2, i, :], scalar=r["weight"][j][:, t:t + 1],
                                                             in1=x[:, t, :], op0=ALU.mult, op1=ALU.add)
                        ins.then_inc(added, 1)
                        dve.wait_ge(added, k * 4 + i + 1)
                if l0:
                    for t in range(TILES):
                        nc.vector.scalar_tensor_tensor(out=x[:, t, :], in0=xn[:, t, :], scalar=S.noop[:, t:t + 1],
                                                       in1=x[:, t, :], op0=ALU.mult, op1=ALU.add)

            @block.gpsimd
            def _(pool):
                pool.wait_ge(filled, 16)
                pool.wait_ge(index_ready, 1)
                for t in range(TILES):
                    for j in range(choices):
                        nc.gpsimd.indirect_dma_start(out=disp, out_offset=bass.IndirectOffsetOnAxis(ap=slot_i[j][:, t:t + 1], axis=0),
                                                     in_=xn[:, t, :], in_offset=None, bounds_check=rows - 1,
                                                     oob_is_err=False).then_inc(scattered, 16)
                pool.wait_ge(stored0, 16 * (1 + (n_exp + 1) // 2))
                pool.wait_ge(stored1, 16 * (1 + n_exp // 2))
                for k in range(TILES * choices // 4):
                    if k >= 2:
                        pool.wait_ge(added, 4 * (k - 1))
                    for i in range(4):
                        t, j = (k * 4 + i) // choices, (k * 4 + i) % choices
                        nc.gpsimd.indirect_dma_start(out=back[:, k % 2, i, :], out_offset=None, in_=eout,
                                                     in_offset=bass.IndirectOffsetOnAxis(ap=back_i[j][:, t:t + 1], axis=0),
                                                     bounds_check=rows - 1, oob_is_err=False).then_inc(gathered[k % 2 * 4 + i], 16)

            @block.sync
            def _(sp):
                sp.sem_inc(stored0, 16)
                sp.sem_inc(stored1, 16)
                if not l0:
                    sp.dma_start(b2_sb[0:1], wts["b2"][None, :, :]).then_inc(bias_loaded, 16)

                def weights(e, u, turn):
                    sp.dma_start(w1_sb[:, u], w1[bass.ds(e, 1)].rearrange("e (k p) n -> p (e k) n", p=P)).then_inc(loaded[u], 16)
                    sp.dma_start(w2_sb[:, u], w2[bass.ds(e, 1)].rearrange("e (k p) n -> p (e k) n", p=P)).then_inc(loaded[u], 16)

                def inputs(e, u, turn):
                    sp.dma_start(xe[:, u], disp[bass.ds(e * cap, cap), :].rearrange("(t p) d -> p t d", p=P)).then_inc(x_loaded[u], 16)

                weights(0, 0, 0)
                weights(1, 1, 0)
                sp.wait_ge(scattered, 16 * TILES * choices)
                inputs(0, 0, 0)
                inputs(1, 1, 0)
                with sp.Fori(0, n_exp // 2 - 1) as g:
                    for u in range(2):
                        sp.wait_ge(y_ready, (g * 2 + u + 1) * CTL)
                        weights(g * 2 + (u + 2), u, g)
                        inputs(g * 2 + (u + 2), u, g)
                if n_exp % 2:
                    sp.wait_ge(y_ready, (n_exp - 2) * CTL)
                    weights(n_exp - 1, 0, 0)
                    inputs(n_exp - 1, 0, 0)
                sp.wait_ge(stored0, 16 * (1 + (n_exp + 1) // 2))
                sp.wait_ge(stored1, 16 * (1 + n_exp // 2))

            @block.tensor
            def _(pe):
                def body(e, u, turn):
                    pe.wait_ge(x_loaded[u], 16 * turn + 16)
                    pe.wait_ge(xeT_copied, e + 1)
                    for k in range(KC):
                        for s in range(CTL):
                            ins = nc.tensor.transpose(t_ps[:, k, s * P:(s + 1) * P], xe[:, u, s, k * P:(k + 1) * P], ident[:])
                    ins.then_inc(xeT_ready, 1)
                    pe.wait_ge(loaded[u], 32 * turn + 32)
                    pe.wait_ge(xeT_copied, e + 2)
                    for m in range(HC):
                        pe.wait_ge(h_copied_d if m % 2 else h_copied, e * (HC // 2) + (m // 2 + 1))
                        for k in range(KC):
                            ins = nc.tensor.matmul(h_ps[:, m % 4, 0:cap], w1_sb[:, u, k, m * P:(m + 1) * P], xeT[:, u, k, :],
                                                   start=k == 0, stop=k == KC - 1)
                        ins.then_inc(h_ready, 1)
                    pe.wait_ge(h_copied, e * (HC // 2) + (HC // 2 + 2))
                    pe.wait_ge(h_copied_d, e * (HC // 2) + (HC // 2 + 2))
                    pe.wait_ge(y_copied, e + 1)
                    for s in range(CTL):
                        for m in range(HC):
                            ins = nc.tensor.matmul(y_ps[:, s, 0:DM], hT[:, u, m, s * P:(s + 1) * P], w2_sb[:, u, m, :],
                                                   start=m == 0, stop=m == HC - 1 and l0)
                        if not l0:
                            ins = nc.tensor.matmul(y_ps[:, s, 0:DM], ones[0:1, :], b2_sb[0:1, bass.ds(e, 1), :].rearrange("o e n -> o (e n)"), start=False, stop=True)
                        ins.then_inc(y_ready, 1)

                pe.sem_inc(xeT_copied, 1)
                pe.sem_inc(h_copied, 2)
                pe.sem_inc(h_copied_d, 2)
                pe.sem_inc(y_copied, 1)
                if not l0:
                    pe.wait_ge(bias_loaded, 16)
                experts(pe, body)

            @block.scalar
            def _(act):
                def body(e, u, turn):
                    for m in range(0, HC, 2):
                        act.wait_ge(h_ready, e * HC + (m + 1))
                        bias = 0.0 if l0 else b1_sb[:, bass.ds(e, 1), m]
                        nc.scalar.activation(hT[:, u, m, :], h_ps[:, m % 4, 0:cap], ACT.Relu, bias=bias).then_inc(h_copied, 1)
                    act.wait_ge(y_copied, e + 2)
                    act.dma_start(eout[bass.ds(e * cap, cap), :].rearrange("(t p) d -> p t d", p=P), ye[:, u]).then_inc(stored[u], 16)

                experts(act, body)


ROUND = 1.5 * 2.0 ** 23
QMAX = 32767.0


def quantised_ffn(nc, name, c, wts):
    x, xn, xnT, ident, ones = c["x"], c["xn"], c["xnT"], c["ident"], c["ones"]
    FF = 768
    FC = FF // P
    QB = 32
    with Scope(nc, name) as S:
        wT = S.sb("wT", [P, 2, KC, FF])
        wdT = S.sb("wdT", [P, FC, DM])
        with Scope(nc, name + "w") as R:
            raw = R.sb("raw", [P, 3, FC * DM])
            q = R.sb("q", [P, 3, FC * DM])
            NB = 3 * FC * DM // QB
            peak, inv = R.sb("peak", [P, NB]), R.sb("inv", [P, NB])
            transpose_weights(nc, R, name + "l", c, [
                (raw[:, 0].rearrange("p (t n) -> p t n", n=DM), wts["w_up"].rearrange("(t p) n -> p t n", p=P)),
                (raw[:, 1].rearrange("p (t n) -> p t n", n=DM), wts["w_gate"].rearrange("(t p) n -> p t n", p=P)),
                (raw[:, 2].rearrange("p (t n) -> p t n", n=FF), wts["w_down"].rearrange("(t p) n -> p t n", p=P))], [])
            step = R.sem("step")
            with R.block() as block:
                @block.vector
                def _(dve):
                    ch, v = Chain(dve, step), nc.vector
                    blocks = raw[:].rearrange("p a (b k) -> p (a b) k", k=QB)
                    qb = q[:].rearrange("p a (b k) -> p (a b) k", k=QB)
                    ch.step(v.tensor_reduce(peak[:], blocks, AX, ALU.max, apply_absolute_value=True))
                    ch.step(v.tensor_scalar(peak[:], peak[:], 1.0 / 7.0, 1e-12, ALU.mult, ALU.max))
                    ch.step(v.reciprocal(inv[:], peak[:]))
                    ch.step(v.tensor_tensor(qb, blocks, inv[:, :, None].to_broadcast([P, NB, QB]), ALU.mult))
                    ch.step(v.tensor_scalar(q[:], q[:], ROUND, ROUND, ALU.add, ALU.subtract))
                    ch.step(v.tensor_scalar(q[:], q[:], -8.0, 7.0, ALU.max, ALU.min))
                    ch.step(v.tensor_tensor(qb, qb, peak[:, :, None].to_broadcast([P, NB, QB]), ALU.mult))
            jobs = []
            for n in range(2):
                for t in range(FC):
                    for k in range(KC):
                        jobs.append((wT[:, n, k, t * P:(t + 1) * P], q[:, n, t * DM + k * P:t * DM + (k + 1) * P]))
            for t in range(KC):
                for k in range(FC):
                    jobs.append((wdT[:, k, t * P:(t + 1) * P], q[:, 2, t * FF + k * P:t * FF + (k + 1) * P]))
            transpose_weights(nc, R, name + "t", c, [], jobs)

        up, gate = S.sb("up", [P, FC, TOK]), S.sb("gate", [P, FC, TOK])
        scratch = xn[:].rearrange("p t n -> p (t n)").rearrange("p (u n) -> p u n", u=2)
        QN = 5
        peaks = S.sb("peaks", [P, QN, FC])
        peak = S.sb("peak", [P, QN])
        row = S.sb("row", [1, QN, 2])
        scale = S.sb("scale", [P, QN, 2])
        ff_ps = S.ps("ff_ps", [P, 4, BANK])
        r_ps = S.ps("r_ps", [P, BANK])
        y_ps = S.ps("y_ps", [P, 2, BANK])
        (step, peak_ready, row_ps_ready, row_ready, all_ready, x_quantised, ff_ready, ff_copied, rounded, sig_ready, o_ready,
         y_ready, y_added) = (S.sem(n) for n in ("step", "peak_ready", "row_ps_ready", "row_ready", "all_ready", "x_quantised", "ff_ready",
                                                 "ff_copied", "rounded", "sig_ready", "o_ready", "y_ready", "y_added"))
        with S.block() as block:
            @block.vector
            def _(dve):
                ch, v = Chain(dve, step), nc.vector

                def find_scale(n, cols):
                    v.tensor_reduce(peak[:, n:n + 1], peaks[:, n, 0:cols], AX, ALU.max).then_inc(peak_ready, 1)
                    dve.wait_ge(row_ps_ready, n + 1)
                    ch.step(v.tensor_reduce(row[0:1, n, 0:1], r_ps[0:1, 0:P], AX, ALU.max))
                    ch.step(v.tensor_scalar(row[0:1, n, 0:1], row[0:1, n, 0:1], 1.0 / QMAX, 1e-12, ALU.mult, ALU.max))
                    v.reciprocal(row[0:1, n, 1:2], row[0:1, n, 0:1]).then_inc(row_ready, 1)
                    dve.wait_ge(all_ready, n + 1)
                    ch.step(v.tensor_copy(scale[:, n, :], r_ps[:, 256:258]))

                def quantise(n, a):
                    ch.step(v.tensor_scalar(a, a, scale[:, n, 1:2], ROUND, ALU.mult, ALU.add))
                    return v.tensor_scalar(a, a, ROUND, scale[:, n, 0:1], ALU.subtract, ALU.mult)

                ch.step(v.tensor_reduce(peaks[:, 0, 0:1], xnT[:].rearrange("p k n -> p (k n)"), AX, ALU.max, apply_absolute_value=True))
                find_scale(0, 1)
                quantise(0, xnT[:].rearrange("p k n -> p (k n)")).then_inc(x_quantised, 1)
                for n, a in enumerate((up, gate)):
                    for m in range(FC):
                        dve.wait_ge(ff_copied, (n * FC + m + 1) * NBLK)
                        ch.step(v.tensor_reduce(peaks[:, 1 + n, m:m + 1], a[:, m, :], AX, ALU.max, apply_absolute_value=True))
                    find_scale(1 + n, FC)
                    for m in range(FC):
                        quantise(1 + n, a[:, m, :]).then_inc(rounded, 1)
                for m in range(FC):
                    s = scratch[:, m % 2, :]
                    dve.wait_ge(sig_ready, m + 1)
                    dve.wait_ge(rounded, 2 * FC)
                    ch.step(v.tensor_scalar(s, s, 65536.0, ROUND, ALU.mult, ALU.add))
                    ch.step(v.tensor_scalar(s, s, ROUND, 0.0, ALU.subtract, ALU.max))
                    ch.step(v.tensor_scalar(s, s, 65535.0, 1.0 / 65536.0, ALU.min, ALU.mult))
                    v.tensor_tensor(gate[:, m, :], gate[:, m, :], s, ALU.mult).then_inc(rounded, 1)
                    dve.wait_ge(rounded, 2 * FC + m + 1)
                    ch.step(v.tensor_reduce(peaks[:, 3, m:m + 1], gate[:, m, :], AX, ALU.max, apply_absolute_value=True))
                find_scale(3, FC)
                for m in range(FC):
                    ch.step(quantise(3, gate[:, m, :]))
                    ch.step(v.tensor_tensor(up[:, m, :], up[:, m, :], gate[:, m, :], ALU.mult))
                    ch.step(v.tensor_reduce(peaks[:, 4, m:m + 1], up[:, m, :], AX, ALU.max, apply_absolute_value=True))
                find_scale(4, FC)
                for m in range(FC):
                    quantise(4, up[:, m, :]).then_inc(o_ready, 1)
                with dve.Fori(0, TILES // 2) as g:
                    for u in range(2):
                        dve.wait_ge(y_ready, g * 2 + (u + 1))
                        v.tensor_tensor(x[:, g * 2 + u, :], x[:, g * 2 + u, :], y_ps[:, u, 0:DM], ALU.add).then_inc(y_added, 1)

            @block.tensor
            def _(pe):
                def share_peak(n):
                    pe.wait_ge(peak_ready, n + 1)
                    nc.tensor.transpose(r_ps[0:1, 0:P], peak[:, n:n + 1], ident[:]).then_inc(row_ps_ready, 1)
                    pe.wait_ge(row_ready, n + 1)
                    nc.tensor.matmul(r_ps[:, 256:258], ones[0:1, :], row[0:1, n, :], start=True, stop=True).then_inc(all_ready, 1)

                share_peak(0)
                pe.wait_ge(x_quantised, 1)
                for n in range(2):
                    for m in range(FC):
                        for b in range(NBLK):
                            j = (n * FC + m) * NBLK + b
                            if j >= 4:
                                pe.wait_ge(ff_copied, j - 3)
                            for k in range(KC):
                                ins = nc.tensor.matmul(ff_ps[:, j % 4, :], wT[:, n, k, m * P:(m + 1) * P], xnT[:, k, b * BANK:(b + 1) * BANK],
                                                       start=k == 0, stop=k == KC - 1)
                            ins.then_inc(ff_ready, 1)
                    share_peak(1 + n)
                share_peak(3)
                share_peak(4)
                pe.wait_ge(o_ready, FC)
                for t in range(TILES):
                    if t >= 2:
                        pe.wait_ge(y_added, t - 1)
                    for m in range(FC):
                        ins = nc.tensor.matmul(y_ps[:, t % 2, 0:DM], up[:, m, t * P:(t + 1) * P], wdT[:, m, :], start=m == 0, stop=m == FC - 1)
                    ins.then_inc(y_ready, 1)

            @block.scalar
            def _(act):
                NT = FC * NBLK
                for j in range(2 * NT):
                    act.wait_ge(ff_ready, j + 1)
                    a, i = (up, gate)[j // NT], j % NT
                    nc.scalar.copy(a[:, i // NBLK, i % NBLK * BANK:(i % NBLK + 1) * BANK], ff_ps[:, j % 4, :]).then_inc(ff_copied, 1)
                for m in range(FC):
                    act.wait_ge(rounded, FC + m + 1)
                    if m >= 2:
                        act.wait_ge(rounded, 2 * FC + m - 1)
                    nc.scalar.activation(scratch[:, m % 2, :], gate[:, m, :], ACT.Sigmoid).then_inc(sig_ready, 1)


def state_space(nc, name, c, wts):
    x, xn, xnT, ident = c["x"], c["xn"], c["xnT"], c["ident"]
    NS = 64
    ROUNDS = 9
    with Scope(nc, name) as S:
        bT = S.sb("bT", [P, 2, KC, P])
        cT = S.sb("cT", [P, DM])
        pw = S.sb("pw", [P, 2, 2, P])
        gb = S.sb("gb", [P, 2, DM])
        with Scope(nc, name + "w") as R:
            rawb, rawc = R.sb("rawb", [NS, DM]), R.sb("rawc", [P, KC, 2, NS])
            zeroed = R.sem("zeroed")
            with R.block() as block:
                @block.vector
                def _(dve):
                    nc.vector.memset(bT[:], 0.0)
                    nc.vector.memset(pw[:], 0.0)
            loads = [(rawb[:], wts["B"]), (pw[0:NS, 0, 0, 0:NS], wts["A"]), (pw[NS:P, 0, 0, NS:P], wts["A"])]
            loads += [(rawc[:, :, n, :], wts["C"].rearrange("(k p) n -> p k n", p=P)) for n in range(2)]
            loads += [(gb[:, j, :], wts[g][None, :].to_broadcast([P, DM])) for j, g in enumerate(("gamma", "beta"))]
            jobs = [(bT[:, h, k, h * NS:(h + 1) * NS], rawb[:, k * P:(k + 1) * P]) for h in range(2) for k in range(KC)]
            jobs += [(cT[:, k * P:(k + 1) * P], rawc[:, k].rearrange("p a n -> p (a n)")) for k in range(KC)]
            jobs += [(pw[:, 0, 1, :], pw[:, 0, 0, :])]
            transpose_weights(nc, R, name + "t", c, loads, jobs)

        X = S.sb("X", [P, 2, SEQ])
        u_ps = S.ps("u_ps", [P, 2, BANK])
        p_ps = S.ps("p_ps", [P, 2, BANK])
        y_ps = S.ps("y_ps", [P, 4, BANK])
        u_ready, added, p_ready, p_copied, y_ready, y_free = (S.sem(n) for n in ("u_ready", "added", "p_ready", "p_copied", "y_ready", "y_free"))
        with S.block() as block:
            @block.tensor
            def _(pe):
                for bb in range(2):
                    for h in range(2):
                        for k in range(KC):
                            ins = nc.tensor.matmul(u_ps[:, bb, :], bT[:, h, k, :], xnT[:, k, (2 * h + bb) * SEQ:(2 * h + bb + 1) * SEQ],
                                                   start=h == 0 and k == 0, stop=h == 1 and k == KC - 1)
                ins.then_inc(u_ready, 1)
                for r in range(ROUNDS):
                    s, i = 1 << r, r % 2
                    pe.wait_ge(added, r + 1)
                    if r:
                        pe.wait_ge(p_copied, r)
                    for bb in range(2):
                        ins = nc.tensor.matmul(u_ps[:, bb, 0:SEQ - s], pw[:, i, 1, :], X[:, bb, 0:SEQ - s], start=True, stop=True)
                    ins.then_inc(u_ready, 1)
                    if r + 1 < ROUNDS:
                        nc.tensor.matmul(p_ps[:, 0, 0:P], pw[:, i, 1, :], pw[:, i, 0, :], start=True, stop=True)
                        nc.tensor.matmul(p_ps[:, 1, 0:P], pw[:, i, 0, :], pw[:, i, 1, :], start=True, stop=True).then_inc(p_ready, 1)
                pe.wait_ge(added, ROUNDS + 1)
                for t in range(TILES):
                    b, q = t // QT, t % QT
                    h, bb = b // 2, b % 2
                    if t >= 4:
                        pe.wait_ge(y_free, t - 3)
                    nc.tensor.matmul(y_ps[:, t % 4, 0:DM], X[h * NS:(h + 1) * NS, bb, q * P:(q + 1) * P], cT[h * NS:(h + 1) * NS, :],
                                     start=True, stop=True).then_inc(y_ready, 1)

            @block.vector
            def _(dve):
                dve.wait_ge(u_ready, 1)
                nc.vector.tensor_copy(X[:], u_ps[:]).then_inc(added, 1)
                for r in range(ROUNDS):
                    s = 1 << r
                    dve.wait_ge(u_ready, r + 2)
                    nc.vector.tensor_tensor(X[:, :, s:], X[:, :, s:], u_ps[:, :, 0:SEQ - s], ALU.add).then_inc(added, 1)

            @block.scalar
            def _(act):
                for r in range(ROUNDS - 1):
                    act.wait_ge(p_ready, r + 1)
                    nc.scalar.copy(pw[:, (r + 1) % 2], p_ps[:, :, 0:P]).then_inc(p_copied, 1)
                for t in range(TILES):
                    act.wait_ge(y_ready, t + 1)
                    nc.scalar.activation(xn[:, t, :], y_ps[:, t % 4, 0:DM], ACT.Gelu).then_inc(y_free, 1)

        st, mean, rstd, tmp = S.sb("st", [P, TILES, 6]), S.sb("mean", [P, TILES]), S.sb("rstd", [P, TILES]), S.sb("tmp", [P, TILES])
        base = S.sb("base", [P, TILES, DM])
        low = S.sb("low", [P, TILES, DM])
        finite = S.sb("finite", [P, TILES, DM], I32)
        step, var_ready, std_ready = S.sem("step"), S.sem("var_ready"), S.sem("std_ready")
        with S.block() as block:
            @block.vector
            def _(dve):
                ch, v = Chain(dve, step), nc.vector
                with dve.Fori(0, TILES) as i:
                    v.bn_stats(st[:, i, :], xn[:, i, :]).then_inc(step, 1)
                ch.n += TILES
                dve.wait_ge(step, ch.n)
                row_stats_to_affine(nc, ch, None, None, st, mean[:], rstd[:], tmp[:], DM // 2)
                v.tensor_copy(tmp[:], rstd[:]).then_inc(var_ready, 1)
                dve.wait_ge(std_ready, 1)
                ch.step(v.reciprocal(rstd[:], tmp[:]))
                with dve.Fori(0, TILES) as i:
                    v.tensor_scalar(xn[:, i, :], xn[:, i, :], mean[:, bass.ds(i, 1)], rstd[:, bass.ds(i, 1)], ALU.subtract, ALU.mult).then_inc(step, 1)
                ch.n += TILES
                dve.wait_ge(step, ch.n)
                ch.step(v.tensor_tensor(xn[:], xn[:], gb[:, None, 0, :].to_broadcast([P, TILES, DM]), ALU.mult))
                ch.step(v.tensor_tensor(xn[:], xn[:], gb[:, None, 1, :].to_broadcast([P, TILES, DM]), ALU.add))
                ch.step(v.tensor_scalar(base[:], xn[:], 0.0, 1e6, ALU.max, ALU.min))
                ch.step(v.tensor_scalar(low[:], xn[:], 0.0, -1e6, ALU.min, ALU.max))
                ch.step(v.tensor_tensor(base[:], base[:], low[:], ALU.add))
                ch.step(v.tensor_scalar(finite[:], xn[:], 0.0, 0.0, ALU.mult, ALU.is_equal))
                ch.step(v.copy_predicated(base[:], finite[:], xn[:]))
                v.tensor_tensor(x[:], x[:], base[:], ALU.add)

            @block.scalar
            def _(act):
                act.wait_ge(var_ready, 1)
                nc.scalar.activation(tmp[:], tmp[:], ACT.Sqrt).then_inc(std_ready, 1)


def selective_scan(nc, name, c, wts):
    x, xn, xnT, ident, ones = c["x"], c["xn"], c["xnT"], c["ident"], c["ones"]
    DI, NST, TAPS = 512, 16, 4
    C4 = DI // P
    NX = 2 * NST + 1
    with Scope(nc, name) as S:
        winT = S.sb("winT", [P, KC, 2 * DI])
        wxT = S.sb("wxT", [P, C4, NX])
        woutT = S.sb("woutT", [P, C4, DM])
        wdt = S.sb("wdt", [1, DI])
        cols = S.sb("cols", [P, 5, C4])
        conv_w = S.sb("conv_w", [P, C4, TAPS])
        A = S.sb("A", [P, NST])
        sel = S.sb("sel", [NX, 2 * NST, P])
        hmax = S.sb("hmax", [P, BATCH * NST + 1])
        flag_f, flag = S.sb("flag_f", [P, 2]), S.sb("flag", [P, 1], I32)
        with Scope(nc, name + "w") as R:
            raw_in, raw_out, raw_x = R.sb("raw_in", [P, 8, DM]), R.sb("raw_out", [P, KC, DI]), R.sb("raw_x", [NX, DI])
            made, a_ready = R.sem("made"), R.sem("a_ready")
            loads = [(raw_in[:], wts["W_in"].rearrange("(t p) d -> p t d", p=P)), (raw_out[:], wts["W_out"].rearrange("(t p) d -> p t d", p=P)),
                     (raw_x[:], wts["W_x"]), (wdt[:], wts["W_dt"].rearrange("d o -> o d")),
                     (conv_w[:], wts["conv_w"].rearrange("(c p) o k -> p c (o k)", p=P)),
                     (A[:], wts["A_log"][None, :].to_broadcast([P, NST]))]
            for j, n in enumerate(("conv_b", "b_dt", "D_param", "ln_g", "ln_b")):
                loads.append((cols[:, j, :], wts[n].rearrange("(c p) -> p c", p=P)))
            jobs = [(winT[:, k, t * P:(t + 1) * P], raw_in[:, t, k * P:(k + 1) * P]) for t in range(8) for k in range(KC)]
            jobs += [(wxT[:, k, :], raw_x[:, k * P:(k + 1) * P]) for k in range(C4)]
            jobs += [(woutT[:, k, t * P:(t + 1) * P], raw_out[:, t, k * P:(k + 1) * P]) for t in range(KC) for k in range(C4)]
            with nc.allow_non_contiguous_dma(reason="per-channel vectors"):
                transpose_weights(nc, R, name + "t", c, loads, jobs)
            with R.block() as block:
                @block.gpsimd
                def _(pool):
                    nc.gpsimd.memset(sel[:], 1.0).then_inc(made, 1)
                    pool.wait_ge(made, 1)
                    nc.gpsimd.affine_select(out=sel[:], in_=sel[:], compare_op=ALU.is_equal, fill=0.0, base=-1,
                                            pattern=[[-1, 2 * NST], [0, P]], channel_multiplier=1)

                @block.vector
                def _(dve):
                    nc.vector.memset(hmax[:], 0.0)
                    nc.vector.tensor_scalar(A[:], A[:], 5.0, None, ALU.min).then_inc(a_ready, 1)
                    dve.wait_ge(a_ready, 2)
                    nc.vector.tensor_scalar(A[:], A[:], -1.0, None, ALU.mult)

                @block.scalar
                def _(act):
                    act.wait_ge(a_ready, 1)
                    nc.scalar.activation(A[:], A[:], ACT.Exp).then_inc(a_ready, 1)

        T = {n: S.sb(n, shape) for n, shape in dict(
            xb=[P, KC, SEQ], xc=[P, C4, SEQ + TAPS - 1], zs=[P, C4, SEQ], u=[P, C4, SEQ], v=[P, C4, SEQ], dt=[P, C4, SEQ],
            xd=[NX, SEQ], dA=[P, 2, C4, SEQ], w=[P, 2, C4, SEQ], h=[P, 2, C4, SEQ], c_sb=[P, 2, SEQ],
            rs=[P, SEQ]).items()}
        big, b_ps, c_ps = S.ps("big", [P, 4, BANK]), S.ps("b_ps", [P, 2, BANK]), S.ps("c_ps", [P, 2, BANK])
        one_pass = dict(nc=nc, c=c, T=T, ps=(big, b_ps, c_ps), w=(winT, wxT, woutT, wdt, cols, conv_w, A, sel), hmax=hmax,
                        dims=(DI, NST, TAPS, C4, NX))
        with S.block() as block:
            @block.vector
            def _(dve):
                nc.vector.memset(T["xc"][:], 0.0)
        with Scope(nc, name + "f") as F:
            scan_pass(F, flag=None, **one_pass)
        with Scope(nc, name + "g") as F:
            step, summed, bad = F.sem("step"), F.sem("summed"), F.sem("bad")
            with F.block() as block:
                @block.vector
                def _(dve):
                    ch, v = Chain(dve, step), nc.vector
                    ch.step(v.tensor_reduce(flag_f[:, 0:1], A[:], AX, ALU.max, apply_absolute_value=True))
                    ch.step(v.tensor_scalar(flag_f[:, 0:1], flag_f[:, 0:1], 1.99, 1000.0, ALU.is_gt, ALU.mult))
                    ch.step(v.tensor_copy(hmax[:, BATCH * NST:], flag_f[:, 0:1]))
                    ch.step(v.tensor_reduce(flag_f[:, 0:1], hmax[:], AX, ALU.max))
                    v.tensor_scalar(flag_f[:, 1:2], flag_f[:, 0:1], 69.9, None, ALU.is_gt).then_inc(bad, 1)
                    dve.wait_ge(summed, 1)
                    ch.step(v.tensor_scalar(flag[:], b_ps[:, 0, 0:1], 0.5, None, ALU.is_gt))

                @block.tensor
                def _(pe):
                    pe.wait_ge(bad, 1)
                    nc.tensor.matmul(b_ps[:, 0, 0:1], ones[:], flag_f[:, 1:2], start=True, stop=True).then_inc(summed, 1)
        with Scope(nc, name + "s") as F:
            scan_pass(F, flag=flag, **one_pass)
        with S.block() as block:
            @block.vector
            def _(dve):
                nc.vector.tensor_tensor(x[:], x[:], xn[:], ALU.add)


def scan_pass(F, nc, c, T, ps, w, hmax, dims, flag):
    xn, xnT, ident, ones = c["xn"], c["xnT"], c["ident"], c["ones"]
    winT, wxT, woutT, wdt, cols, conv_w, A, sel = w
    big, b_ps, c_ps = ps
    DI, NST, TAPS, C4, NX = dims
    xb, xc, zs, u, v, dt, xd, dA, wd, h, c_sb, rs = (T[n] for n in ("xb", "xc", "zs", "u", "v", "dt", "xd", "dA", "w", "h", "c_sb", "rs"))
    y_sb, dtu = dA[:, 0], v
    CONV_B, B_DT, D_PAR, LN_G, LN_B = range(5)
    exact = flag is not None
    WIDE = [P, C4, SEQ]
    (xb_ready, xz_ready, xc_copied, z_done, conv_ready, u_ready, xd_ready, xd_copied, dt_ps_ready, dt_copied, sp_ready, dt_ready,
     brow_ready, crow_ready, w_ready, clipped, dA_ready, scan_done, checked, c_copied, hC_ready, acc_done, y_copied, mean_ready,
     yc_ready, sq_ready, var_ready, v_ready, std_ready, yf_ready, delta_ready, delta_copied, dstep, astep) = (F.sem(n) for n in (
         "xb_ready", "xz_ready", "xc_copied", "z_done", "conv_ready", "u_ready", "xd_ready", "xd_copied", "dt_ps_ready",
         "dt_copied", "sp_ready", "dt_ready", "brow_ready", "crow_ready", "w_ready", "clipped", "dA_ready", "scan_done", "checked",
         "c_copied", "hC_ready", "acc_done", "y_copied", "mean_ready", "yc_ready", "sq_ready", "var_ready", "v_ready",
         "std_ready", "yf_ready", "delta_ready", "delta_copied", "dstep", "astep"))

    def run(eng, program):
        if not exact:
            program()
            return
        with eng.If(eng.value_load(flag[0:1, 0:1], min_val=0, max_val=1) != 0):
            program()

    with F.block() as block:
        @block.gpsimd
        def _(pool):
            def program():
                def element(b, src):
                    nc.gpsimd.tensor_copy(xb[:], src).then_inc(xb_ready, 1)

                    for n in range(NST):
                        pool.wait_ge(c_copied, b * NST + (n + 3))
                        pool.wait_ge(checked, b * NST + (n + 1))
                        nc.gpsimd.tensor_tensor(h[:, n % 2], h[:, n % 2], c_sb[:, n % 2, None, :].to_broadcast(WIDE),
                                                ALU.mult).then_inc(hC_ready, 1)

                pool.sem_inc(hC_ready, 2)
                with pool.Fori(0, BATCH) as b:
                    element(b, xnT[:, :, bass.ds(b * SEQ, SEQ)])
            run(pool, program)

        @block.tensor
        def _(pe):
            def program():
                pe.sem_inc(acc_done, 2)
                with pe.Fori(0, BATCH) as b:
                    pe.wait_ge(xb_ready, b + 1)
                    pe.wait_ge(delta_copied, b * QT + 1)
                    for m in range(2 * C4):
                        if m >= C4:
                            pe.wait_ge(xc_copied, b * C4 + (m - C4 + 1))
                        for k in range(KC):
                            ins = nc.tensor.matmul(big[:, m % 4, :], winT[:, k, m * P:(m + 1) * P], xb[:, k, :], start=k == 0, stop=k == KC - 1)
                        ins.then_inc(xz_ready, 1)
                    pe.wait_ge(u_ready, b * C4 + C4)
                    pe.wait_ge(c_copied, b * NST + 2)
                    for k in range(C4):
                        ins = nc.tensor.matmul(c_ps[0:NX, 0, :], wxT[:, k, :], u[:, k, :], start=k == 0, stop=k == C4 - 1)
                    ins.then_inc(xd_ready, 1)
                    pe.wait_ge(xd_copied, b + 1)
                    pe.wait_ge(z_done, b * C4 + C4)
                    for k in range(C4):
                        ins = nc.tensor.matmul(big[:, k, :], wdt[0:1, k * P:(k + 1) * P], xd[0:1, :], start=True, stop=True)
                    ins.then_inc(dt_ps_ready, 1)
                    pe.wait_ge(dt_copied, b + 1)

                    def rows(n):
                        pe.wait_ge(w_ready, b * NST + (n + 1))
                        nc.tensor.matmul(b_ps[:, n % 2, :], sel[:, n, :], xd[:, :], start=True, stop=True).then_inc(brow_ready, 1)
                        pe.wait_ge(c_copied, b * NST + (n + 1))
                        nc.tensor.matmul(c_ps[:, n % 2, :], sel[:, NST + n, :], xd[:, :], start=True, stop=True).then_inc(crow_ready, 1)

                    rows(0)
                    rows(1)
                    for n in range(NST):
                        pe.wait_ge(hC_ready, b * NST + (n + 3))
                        for k in range(C4):
                            ins = nc.tensor.matmul(big[:, k, :], ident[:], h[:, n % 2, k, :], start=n == 0, stop=n == NST - 1)
                        ins.then_inc(acc_done, 1)
                        if n + 2 < NST:
                            rows(n + 2)
                    pe.wait_ge(y_copied, b + 1)
                    for k in range(C4):
                        ins = nc.tensor.matmul(b_ps[:, 0, :], ones[:], y_sb[:, k, :], start=k == 0, stop=k == C4 - 1)
                    ins.then_inc(mean_ready, 1)
                    pe.wait_ge(sq_ready, b + 1)
                    for k in range(C4):
                        ins = nc.tensor.matmul(b_ps[:, 1, :], ones[:], wd[:, 0, k, :], start=k == 0, stop=k == C4 - 1)
                    ins.then_inc(var_ready, 1)
                    pe.wait_ge(yf_ready, b + 1)
                    for q in range(QT):
                        for k in range(C4):
                            ins = nc.tensor.matmul(big[:, q, 0:DM], y_sb[:, k, q * P:(q + 1) * P], woutT[:, k, :], start=k == 0, stop=k == C4 - 1)
                        ins.then_inc(delta_ready, 1)
            run(pe, program)

        @block.vector
        def _(dve):
            V = nc.vector
            def program():
                dve.sem_inc(w_ready, 2)
                dve.sem_inc(scan_done, 2)
                count = {}

                def element(b, per):
                    ch = Chain(dve, dstep, b * per)
                    for m in range(C4):
                        dve.wait_ge(xz_ready, b * (2 * C4) + (m + 1))
                        V.tensor_copy(xc[:, m, TAPS - 1:], big[:, m, :]).then_inc(xc_copied, 1)
                        dve.wait_ge(xc_copied, b * C4 + (m + 1))
                        ch.step(V.tensor_scalar(v[:, m], xc[:, m, 0:SEQ], conv_w[:, m, 0:1], cols[:, CONV_B, m:m + 1], ALU.mult, ALU.add))
                        for k in range(1, TAPS):
                            ins = V.scalar_tensor_tensor(out=v[:, m], in0=xc[:, m, k:k + SEQ], scalar=conv_w[:, m, k:k + 1], in1=v[:, m],
                                                         op0=ALU.mult, op1=ALU.add)
                            if k < TAPS - 1:
                                ch.step(ins)
                        ins.then_inc(conv_ready, 1)
                    dve.wait_ge(xd_ready, b + 1)
                    V.tensor_copy(xd[:], c_ps[0:NX, 0, :]).then_inc(xd_copied, 1)
                    dve.wait_ge(dt_ps_ready, b + 1)
                    for m in range(C4):
                        ins = V.tensor_scalar(v[:, m], big[:, m, :], cols[:, B_DT, m:m + 1], None, ALU.add)
                    ins.then_inc(dt_copied, 1)
                    dve.wait_ge(sp_ready, b + 1)
                    ch.step(V.scalar_tensor_tensor(out=dt[:].rearrange("p c t -> p (c t)"), in0=v[:].rearrange("p c t -> p (c t)"), scalar=0.0,
                                                   in1=wd[:, 0].rearrange("p c t -> p (c t)"), op0=ALU.max, op1=ALU.add))
                    V.tensor_scalar(dt[:], dt[:], 1e-4, 10.0, ALU.max, ALU.min).then_inc(dt_ready, 1)
                    dve.wait_ge(dt_ready, b + 1)
                    ch.step(V.tensor_tensor(dtu[:], dt[:], u[:], ALU.mult))

                    def drive(n):
                        dve.wait_ge(brow_ready, b * NST + (n + 1))
                        V.tensor_tensor(wd[:, n % 2], dtu[:], b_ps[:, n % 2, None, :].to_broadcast(WIDE), ALU.mult).then_inc(w_ready, 1)
                        dve.wait_ge(w_ready, b * NST + (n + 3))
                        V.tensor_scalar(wd[:, n % 2], wd[:, n % 2], 10.0, -10.0, ALU.min, ALU.max).then_inc(clipped, 1)

                    def scan(n):
                        hn, dAn, wn = h[:, n % 2], dA[:, n % 2], wd[:, n % 2]
                        dve.wait_ge(clipped, b * NST + (n + 1))
                        dve.wait_ge(dA_ready, b * NST + (n + 1))
                        dve.wait_ge(acc_done, b * NST + (n + 1))
                        if not exact:
                            V.tensor_tensor_scan(out=hn.rearrange("p c t -> p (c t)"), data0=dAn.rearrange("p c t -> p (c t)"),
                                                 data1=wn.rearrange("p c t -> p (c t)"), initial=0.0, op0=ALU.mult, op1=ALU.add).then_inc(scan_done, 1)
                            dve.wait_ge(scan_done, b * NST + (n + 3))
                            V.tensor_reduce(hmax[:, bass.ds(b * NST + n, 1)], hn[:, :, 0:SEQ:4], mybir.AxisListType.XY, ALU.max,
                                            apply_absolute_value=True).then_inc(checked, 1)
                            return
                        ch.step(V.tensor_scalar(dAn, dAn, EXP_M20, None, ALU.max))
                        ch.step(V.tensor_copy(hn[:, :, 0], wn[:, :, 0]))
                        V.tensor_copy(rs[:, 0:1], rs[:, 0:1])
                        with dve.Fori(1, SEQ) as t:
                            done = (b * NST + n) * (3 * (SEQ - 1)) + (t - 1) * 3
                            V.tensor_tensor(hn[:, :, bass.ds(t, 1)], hn[:, :, bass.ds(t - 1, 1)], dAn[:, :, bass.ds(t, 1)], ALU.mult).then_inc(yc_step, 1)
                            dve.wait_ge(yc_step, done + 1)
                            V.tensor_tensor(hn[:, :, bass.ds(t, 1)], hn[:, :, bass.ds(t, 1)], wn[:, :, bass.ds(t, 1)], ALU.add).then_inc(yc_step, 1)
                            dve.wait_ge(yc_step, done + 2)
                            V.tensor_scalar(hn[:, :, bass.ds(t, 1)], hn[:, :, bass.ds(t, 1)], 100.0, -100.0, ALU.min, ALU.max).then_inc(yc_step, 1)
                            dve.wait_ge(yc_step, done + 3)
                        V.tensor_copy(rs[:, 0:1], rs[:, 0:1]).then_inc(scan_done, 1)
                        dve.wait_ge(scan_done, b * NST + (n + 3))
                        V.tensor_copy(rs[:, 0:1], rs[:, 0:1]).then_inc(checked, 1)

                    drive(0)
                    for n in range(NST):
                        if n + 1 < NST:
                            drive(n + 1)
                        scan(n)
                    dve.wait_ge(mean_ready, b + 1)
                    for m in range(C4):
                        ins = V.scalar_tensor_tensor(out=y_sb[:, m, :], in0=b_ps[:, 0, :], scalar=-1.0 / DI, in1=y_sb[:, m, :], op0=ALU.mult, op1=ALU.add)
                    ins.then_inc(yc_ready, 1)
                    dve.wait_ge(var_ready, b + 1)
                    V.tensor_scalar(rs[:], b_ps[:, 1, :], 1.0 / DI, LN_EPS, ALU.mult, ALU.add).then_inc(v_ready, 1)
                    dve.wait_ge(std_ready, b + 1)
                    ch.step(V.reciprocal(rs[:], rs[:]))
                    ch.step(V.tensor_tensor(y_sb, y_sb, rs[:, None, :].to_broadcast(WIDE), ALU.mult))
                    for m in range(C4):
                        ch.step(V.tensor_scalar(y_sb[:, m, :], y_sb[:, m, :], cols[:, LN_G, m:m + 1], cols[:, LN_B, m:m + 1], ALU.mult, ALU.add))
                        ch.step(V.scalar_tensor_tensor(out=y_sb[:, m, :], in0=u[:, m, :], scalar=cols[:, D_PAR, m:m + 1], in1=y_sb[:, m, :],
                                                       op0=ALU.mult, op1=ALU.add))
                    V.tensor_tensor(y_sb, y_sb, zs[:], ALU.mult).then_inc(yf_ready, 1)
                    count["steps"] = ch.n

                per = C4 * (TAPS - 1) + 2 + 2 + 2 * C4 + (2 * NST if exact else 0)
                with dve.Fori(0, BATCH) as b:
                    element(b, per)
                assert count["steps"] == per, (count, per)
            yc_step = F.sem("exact_step") if exact else None
            run(dve, program)

        @block.scalar
        def _(act):
            E = nc.scalar

            def program():
                act.sem_inc(delta_copied, 1)
                act.sem_inc(c_copied, 2)
                with act.Fori(0, BATCH) as b:
                    for m in range(C4):
                        act.wait_ge(xz_ready, b * (2 * C4) + (C4 + m + 1))
                        E.activation(zs[:, m, :], big[:, m, :], ACT.Silu).then_inc(z_done, 1)
                    for m in range(C4):
                        act.wait_ge(conv_ready, b * C4 + (m + 1))
                        E.activation(u[:, m, :], v[:, m, :], ACT.Silu).then_inc(u_ready, 1)
                    act.wait_ge(dt_copied, b + 1)
                    E.activation(wd[:, 0], v[:], ACT.Abs).then_inc(astep, 1)
                    act.wait_ge(astep, b * 2 + 1)
                    E.activation(wd[:, 0], wd[:, 0], ACT.Exp, scale=-1.0).then_inc(astep, 1)
                    act.wait_ge(astep, b * 2 + 2)
                    E.activation(wd[:, 0], wd[:, 0], ACT.Ln, bias=1.0).then_inc(sp_ready, 1)
                    act.wait_ge(dt_ready, b + 1)
                    for n in range(NST):
                        act.wait_ge(scan_done, b * NST + (n + 1))
                        E.activation(dA[:, n % 2], dt[:], ACT.Exp, scale=A[:, n:n + 1]).then_inc(aexp, 1)
                        act.wait_ge(aexp, b * NST + (n + 1))
                        E.mul(dA[:, n % 2, :, 0], dA[:, n % 2, :, 0], 0.0).then_inc(dA_ready, 1)
                        act.wait_ge(crow_ready, b * NST + (n + 1))
                        act.wait_ge(hC_ready, b * NST + (n + 1))
                        E.copy(c_sb[:, n % 2, :], c_ps[:, n % 2, :]).then_inc(c_copied, 1)
                    act.wait_ge(acc_done, b * NST + (NST + 2))
                    act.wait_ge(scan_done, b * NST + (NST + 2))
                    E.copy(y_sb, big[:]).then_inc(y_copied, 1)
                    act.wait_ge(yc_ready, b + 1)
                    E.activation(wd[:, 0], y_sb, ACT.Square).then_inc(sq_ready, 1)
                    act.wait_ge(v_ready, b + 1)
                    E.activation(rs[:], rs[:], ACT.Sqrt).then_inc(std_ready, 1)
                    for q in range(QT):
                        act.wait_ge(delta_ready, b * QT + (q + 1))
                        E.copy(xn[:, b * QT + q, :], big[:, q, 0:DM]).then_inc(delta_copied, 1)
            aexp = F.sem("aexp")
            run(act, program)


EXP_M20 = 2.0611536224385579e-09


ATTN, XATTN, FFN = "attn", "xattn", "ffn"


def zero_fill_slots(nc, S, c):
    zeros = S.sb("zeros", [P, DM])
    zeroed = S.sem("zeroed")
    for n, n_exp in enumerate((7, 8)):
        rows = n_exp * (TOK // NE)
        disp = nc.dram_tensor(f"slots{n}", [rows, DM], F32, kind="Internal").ap()
        eout = nc.dram_tensor(f"expert_rows{n}", [rows, DM], F32, kind="Internal").ap()
        c[f"moe{n}"] = (disp, eout, S.sem(f"slots_zeroed{n}"))
    with S.block() as block:
        @block.vector
        def _(dve):
            nc.vector.memset(zeros[:], 0.0).then_inc(zeroed, 1)

        @block.scalar
        def _(act):
            act.wait_ge(zeroed, 1)
            for n in range(2):
                disp, _, filled = c[f"moe{n}"]
                act.dma_start(disp.rearrange("(t p) d -> p t d", p=P),
                              zeros[:, None, :].to_broadcast([P, disp.shape[0] // P, DM])).then_inc(filled, 16)


def decoder_kernel(nc, w, out, first=0, last=12):
    c = {}

    def of(prefix):
        return {n[len(prefix):]: ap for n, ap in w.items() if n.startswith(prefix)}

    def stage(n):
        return first <= n < last

    with Scope(nc, "g") as S:
        c["x"] = S.sb("x", [P, TILES, DM])
        c["xn"] = S.sb("xn", [P, TILES, DM])
        c["xnT"] = S.sb("xnT", [P, KC, TOK])
        setup_constants(nc, S, c)
        x_loaded, x_stored = S.sem("x_loaded"), S.sem("x_stored")
        x_dram = w["x"].rearrange("b (t p) d -> p (b t) d", p=P)
        out_dram = out.rearrange("b (t p) d -> p (b t) d", p=P)
        c["ctx_dram"] = w["ctx_768"].rearrange("b k c -> (b k) c").rearrange("(t p) c -> p t c", p=P)
        zero_fill_slots(nc, S, c)
        with S.block() as block:
            @block.sync
            def _(sp):
                for q in range(4):
                    sp.dma_start(c["x"][:, 4 * q:4 * q + 4, :], x_dram[:, 4 * q:4 * q + 4, :]).then_inc(x_loaded, 16)
                sp.wait_ge(x_loaded, 64)
        if stage(0):
            normalise(nc, "l0a", c)
            self_attention(nc, "l0at", c, of("L0_attn_"), given=False, window=True)
        if stage(1):
            normalise(nc, "l0b", c)
            cross_attention(nc, "l0x", c, of("L0_xattn_"), dh=64)
        if stage(2):
            normalise(nc, "l0c", c)
            mixture(nc, "l0f", c, of("L0_ffn_"), 7, 2, *c["moe0"])
        if stage(3):
            normalise(nc, "l1a", c)
            self_attention(nc, "l1at", c, of("L1_attn_"), given=True, window=False)
        if stage(4):
            normalise(nc, "l1b", c)
            cross_attention(nc, "l1x", c, of("L1_xattn_"), dh=16, out_in=True)
        if stage(5):
            normalise(nc, "l1c", c)
            mixture(nc, "l1f", c, of("L1_ffn_"), 8, 1, *c["moe1"])
        if stage(6):
            normalise(nc, "l2a", c)
            selective_scan(nc, "l2s", c, of("L2_attn_"))
        if stage(7):
            l2x = of("L2_xattn_")
            normalise(nc, "l2b", c, affine=(l2x["g_x"], l2x["b_x"]))
            cross_attention(nc, "l2x", c, l2x, dh=64, norm_ctx=True)
        if stage(8):
            normalise(nc, "l2c", c)
            quantised_ffn(nc, "l2f", c, of("L2_ffn_"))
        if stage(9):
            normalise(nc, "l3a", c)
            state_space(nc, "l3s", c, of("L3_attn_"))
        if stage(10):
            normalise(nc, "l3b", c)
            cross_attention(nc, "l3x", c, of("L3_xattn_"), dh=16, clamp=1e4)
        if stage(11):
            normalise(nc, "l3c", c)
            gated_linear(nc, "l3f", c, of("L3_ffn_"), 100)
        with S.block() as block:
            @block.sync
            def _(sp):
                for q in range(4):
                    sp.dma_start(out_dram[:, 4 * q:4 * q + 4, :], c["x"][:, 4 * q:4 * q + 4, :]).then_inc(x_stored, 16)
                sp.wait_ge(x_stored, 64)
                for n in range(2):
                    sp.wait_ge(c[f"moe{n}"][2], 16)


_OUTS = [((4, 512, 256), "float32")]


def kernel(**inputs):
    import numpy as _np
    import concourse.bacc as _bacc
    from concourse import mybir as _mybir
    from concourse.bass_utils import run_bass_kernel_spmd as _run

    nc = _bacc.Bacc("TRN2", target_bir_lowering=False, num_devices=1)
    arrays, args = {}, {}
    for name, value in inputs.items():
        a = _np.ascontiguousarray(value)
        arrays[f"in_{name}_dram"] = a
        args[name] = nc.dram_tensor(f"in_{name}_dram", a.shape, _mybir.dt.from_np(a.dtype), kind="ExternalInput").ap()
    shape, dtype = _OUTS[0]
    out = nc.dram_tensor("out_0_dram", shape, _mybir.dt.from_np(_np.dtype(dtype)), kind="ExternalOutput").ap()
    decoder_kernel(nc, args, out)
    r = _run(nc, [arrays], core_ids=[0])
    return r.results[0]["out_0_dram"]
```

```python
from contextlib import ExitStack

import concourse.bass as bass
from concourse import mybir

F32 = mybir.dt.float32
BF16 = mybir.dt.bfloat16
I32 = mybir.dt.int32
U32 = mybir.dt.uint32
ACT = mybir.ActivationFunctionType
ALU = mybir.AluOpType
AX = mybir.AxisListType.X

P = 128
BATCH, SEQ, DM = 4, 512, 256
TOK = BATCH * SEQ
TILES = TOK // P
QT = SEQ // P
KC = DM // P
HEADS = 16
BANK = 512
NBLK = TOK // BANK
LN_EPS = 1e-5


class Scope:

    def __init__(self, nc, prefix):
        self.nc, self.prefix, self.stack, self.sems = nc, prefix, ExitStack(), []

    def __enter__(self):
        self.stack.__enter__()
        return self

    def __exit__(self, *a):
        if self.sems:
            self.nc.clear_and_free_semaphores(self.sems)
            self.nc.all_engine_barrier()
        return self.stack.__exit__(*a)

    def sb(self, name, shape, dt=F32):
        return self.stack.enter_context(self.nc.sbuf_tensor(f"{self.prefix}_{name}", list(shape), dt))

    def ps(self, name, shape, dt=F32):
        return self.stack.enter_context(self.nc.psum_tensor(f"{self.prefix}_{name}", list(shape), dt))

    def sem(self, name):
        self.sems.append(self.nc.alloc_semaphore(f"{self.prefix}_{name}"))
        return self.sems[-1]

    def block(self):
        return self.nc.Block()


class Chain:

    def __init__(self, eng, sem, base=0):
        self.eng, self.sem, self.base, self.n = eng, sem, base, 0

    def step(self, ins):
        self.n += 1
        ins.then_inc(self.sem, 1)
        self.eng.wait_ge(self.sem, self.base + self.n)


def setup_constants(nc, S, c):
    c["ident"] = S.sb("ident", [P, P])
    c["ones"] = S.sb("ones", [P, P])
    made = S.sem("const_made")
    with S.block() as block:
        @block.gpsimd
        def _(pool):
            nc.gpsimd.memset(c["ident"][:], 0.0).then_inc(made, 1)
            nc.gpsimd.memset(c["ones"][:], 1.0).then_inc(made, 1)
            pool.wait_ge(made, 2)
            nc.gpsimd.affine_select(out=c["ident"][:], in_=c["ident"][:], compare_op=ALU.not_equal, fill=1.0,
                                    base=0, pattern=[[-1, P]], channel_multiplier=1).then_inc(made, 1)
            pool.wait_ge(made, 3)


def row_stats_to_affine(nc, ch, st, mean, rstd, tmp, half):
    ch.step(nc.vector.tensor_tensor(mean, st[:, :, 1], st[:, :, 4], ALU.add))
    ch.step(nc.vector.tensor_scalar(mean, mean, 0.5, None, ALU.mult))
    ch.step(nc.vector.tensor_tensor(tmp, st[:, :, 1], mean, ALU.subtract))
    ch.step(nc.vector.tensor_tensor(tmp, tmp, tmp, ALU.mult))
    ch.step(nc.vector.tensor_tensor(rstd, st[:, :, 2], st[:, :, 5], ALU.add))
    ch.step(nc.vector.tensor_scalar(rstd, rstd, 1.0 / (2 * half), LN_EPS, ALU.mult, ALU.add))
    ch.step(nc.vector.tensor_tensor(rstd, rstd, tmp, ALU.add))


WBANKS = 4


def issue_loads(nc, block, loads, loaded):
    @block.sync
    def _(sp):
        for dst, src in loads[0::2]:
            sp.dma_start(dst, src).then_inc(loaded[0], 16)
        if loads:
            sp.wait_ge(loaded[0], 16 * len(loads[0::2]))

    def from_act(act):
        for dst, src in loads[1::2]:
            act.dma_start(dst, src).then_inc(loaded[1], 16)
    return from_act


def turn_blocks(nc, pe, groups, pt, ident, loads, loaded, tr_ready, copied):
    if not groups:
        return
    for j in range(2):
        if loads[j::2]:
            pe.wait_ge(loaded[j], 16 * len(loads[j::2]))
    for g, group in enumerate(groups):
        if g >= WBANKS:
            n = len(copied)
            pe.wait_ge(copied[g % n], (g - WBANKS) // n + 1)
        for j, (dst, src) in enumerate(group):
            r, n = src.shape[0], src.shape[1]
            ins = nc.tensor.transpose(pt[0:n, g % WBANKS, j, 0:r], src, ident[0:r, 0:r])
        ins.then_inc(tr_ready, 1)


def copy_blocks(eng, copy, groups, pt, tr_ready, copied, first, stride):
    for g in range(first, len(groups), stride):
        eng.wait_ge(tr_ready, g + 1)
        for j, (dst, src) in enumerate(groups[g]):
            ps = pt[0:src.shape[1], g % WBANKS, j, 0:src.shape[0]]
            if len(dst.shape) == 3:
                ps = ps.rearrange("p (a b) -> p a b", b=dst.shape[2])
            ins = copy(dst, ps)
        ins.then_inc(copied, 1)


def prepare(nc, name, c, loads, jobs):
    groups = [jobs[j:j + 4] for j in range(0, len(jobs), 4)]
    if "norm" in c:
        normalise(nc, c, *c.pop("norm"), loads, groups)
        return
    with Scope(nc, name) as T:
        pt = T.ps("wt", [P, WBANKS, 4, P])
        loaded, tr_ready = [T.sem("loaded_sp"), T.sem("loaded_act")], T.sem("tr_ready")
        copied = [T.sem("act_copied"), T.sem("dve_copied")]
        with T.block() as block:
            from_act = issue_loads(nc, block, loads, loaded)

            @block.tensor
            def _(pe):
                turn_blocks(nc, pe, groups, pt, c["ident"], loads, loaded, tr_ready, copied)

            @block.scalar
            def _(act):
                from_act(act)
                copy_blocks(act, nc.scalar.copy, groups, pt, tr_ready, copied[0], 0, 2)
                if loads[1::2]:
                    act.wait_ge(loaded[1], 16 * len(loads[1::2]))

            @block.vector
            def _(dve):
                copy_blocks(dve, nc.vector.tensor_copy, groups, pt, tr_ready, copied[1], 1, 2)


def normalise(nc, c, name, affine, loads, groups):
    x, xn, xnT, ident = c["x"], c["xn"], c["xnT"], c["ident"]
    rounds = 1 if affine is None else 2
    with Scope(nc, name) as S:
        st = S.sb("stats", [P, TILES, 6])
        mean, rstd, tmp = (S.sb(n, [P, TILES]) for n in ("mean", "rstd", "tmp"))
        gb = S.sb("gb", [P, 2, DM]) if affine else None
        wt = S.ps("wt", [P, WBANKS, 4, P])
        pt = S.ps("pt", [P, 4, KC * 2, P])
        loaded, wt_ready, wt_copied = [S.sem("loaded_sp"), S.sem("loaded_act")], S.sem("wt_ready"), S.sem("wt_copied")
        var_ready, std_ready, step = S.sem("var_ready"), S.sem("std_ready"), S.sem("step")
        xn_ready, tr_ready, gb_loaded = (S.sem(n) for n in ("xn_ready", "tr_ready", "gb_loaded"))
        tr_copied = (S.sem("tr_copied_a"), S.sem("tr_copied_d"))
        if affine:
            loads = loads + [(gb[:, j, :], affine[j][None, :].to_broadcast([P, DM])) for j in range(2)]
        with S.block() as block:
            from_act = issue_loads(nc, block, loads, loaded)

            def copy_turned(eng, copy, half):
                for g in range(half, TILES // 2, 2):
                    eng.wait_ge(tr_ready, g + 1)
                    for kc in range(KC):
                        ins = copy(xnT[:, kc, g * 2 * P:(g + 1) * 2 * P], pt[:, g % 4, 2 * kc:2 * kc + 2, :])
                    ins.then_inc(tr_copied[half], 1)

            @block.vector
            def _(dve):
                ch = Chain(dve, step)
                for r in range(rounds):
                    src = x if r == 0 else xn
                    for i in range(TILES):
                        ins = nc.vector.bn_stats(st[:, i, :], src[:, i, :])
                    ch.step(ins)
                    row_stats_to_affine(nc, ch, st, mean[:], rstd[:], tmp[:], DM // 2)
                    nc.vector.tensor_copy(tmp[:], rstd[:]).then_inc(var_ready, 1)
                    dve.wait_ge(std_ready, r + 1)
                    ch.step(nc.vector.reciprocal(rstd[:], tmp[:]))
                    last = r == rounds - 1 and not affine
                    for i in range(TILES):
                        ins = nc.vector.tensor_scalar(xn[:, i, :], src[:, i, :], mean[:, i:i + 1], rstd[:, i:i + 1], ALU.subtract, ALU.mult)
                        if last:
                            ins.then_inc(xn_ready, 1)
                    if not last:
                        ch.step(ins)
                if affine:
                    for j in range(2):
                        dve.wait_ge(loaded[j], 16 * len(loads[j::2]))
                    ch.step(nc.vector.tensor_tensor(xn[:], xn[:], gb[:, None, 0, :].to_broadcast([P, TILES, DM]), ALU.mult))
                    nc.vector.tensor_tensor(xn[:], xn[:], gb[:, None, 1, :].to_broadcast([P, TILES, DM]), ALU.add).then_inc(xn_ready, TILES)
                copy_turned(dve, nc.vector.tensor_copy, 1)

            @block.scalar
            def _(act):
                from_act(act)
                for r in range(rounds):
                    act.wait_ge(var_ready, r + 1)
                    nc.scalar.activation(tmp[:], tmp[:], ACT.Sqrt).then_inc(std_ready, 1)
                copy_blocks(act, nc.scalar.copy, groups, wt, wt_ready, wt_copied, 0, 1)
                copy_turned(act, nc.scalar.copy, 0)
                if loads[1::2]:
                    act.wait_ge(loaded[1], 16 * len(loads[1::2]))

            @block.tensor
            def _(pe):
                turn_blocks(nc, pe, groups, wt, ident, loads, loaded, wt_ready, [wt_copied])
                for g in range(TILES // 2):
                    pe.wait_ge(xn_ready, 2 * g + 2)
                    if g >= 4:
                        pe.wait_ge(tr_copied[g % 2], (g - 4) // 2 + 1)
                    for kc in range(KC):
                        for v in range(2):
                            ins = nc.tensor.transpose(pt[:, g % 4, 2 * kc + v, :], xn[:, 2 * g + v, kc * P:(kc + 1) * P], ident[:])
                    ins.then_inc(tr_ready, 1)


HD = DM // HEADS
GH = 4
HP = 32
GROUPS = HEADS // GH
Q_PARTS = (0, 0, 1, 1, 0, 2)
K_PARTS = (0, 1, 0, 1, 2, 0)


def self_attention(nc, name, c, wts, given, window):
    with Scope(nc, name) as S:
        parts = nc.dram_tensor(f"{name}_parts", [3, BATCH, 2 * DM, SEQ], BF16, kind="Internal").ap()
        v = S.sb("v", [P, TILES, DM])
        wo = S.sb("wo", [P, GROUPS, DM])
        bob = S.sb("bob", [P, DM]) if given else None
        project_heads(nc, name + "p", c, wts, given, parts, v, wo, bob)
        attend_heads(nc, name + "a", c, parts, v, wo, bob, window)


def project_heads(nc, name, c, wts, given, parts, v, wo, bob):
    xnT = c["xnT"]
    names = ("Wq", "Wk", "Wv", "Wo")
    with Scope(nc, name) as S:
        wqk = S.sb("wqk", [P, KC, 2, DM])
        wv = S.sb("wv", [P, KC, DM])
        raw = S.sb("raw", [P, 4, KC, DM])
        bqk = S.sb("bqk", [P, 2 * KC])
        bvb = S.sb("bvb", [P, DM])
        ready = S.sem("ready")
        with S.block() as block:
            @block.gpsimd
            def _(pool):
                nc.gpsimd.memset(wo[:], 0.0)
                nc.gpsimd.memset(bqk[:], 0.0)
                nc.gpsimd.memset(bvb[:], 0.0)
        loads, jobs = [], []
        if given:
            loads += [(wqk[:, :, n, :], wts[names[n]].rearrange("(k p) n -> p k n", p=P)) for n in range(2)]
            loads += [(wv[:], wts["Wv"].rearrange("(k p) n -> p k n", p=P)),
                      (bvb[:], wts["bv"][None, :].to_broadcast([P, DM])), (bob[:], wts["bo"][None, :].to_broadcast([P, DM]))]
            loads += [(bqk[:, n * KC:(n + 1) * KC], wts[b].rearrange("(c p) -> p c", p=P)) for n, b in enumerate(("bq", "bk"))]
            loads += [(wo[HP * r:HP * r + HD], wts["Wo"].rearrange("(g m d) n -> m d g n", m=GH, d=HD)[r]) for r in range(GH)]
        else:
            loads += [(raw[:, n], wts[w].rearrange("(k p) n -> p k n", p=P)) for n, w in enumerate(names)]
            for kc in range(KC):
                for o in range(KC):
                    for dst, n in ((wqk[:, kc, 0, :], 0), (wqk[:, kc, 1, :], 1), (wv[:, kc, :], 2)):
                        jobs.append((dst[:, o * P:(o + 1) * P], raw[:, n, o, kc * P:(kc + 1) * P]))
        with nc.allow_non_contiguous_dma(reason="bias vectors by feature"):
            prepare(nc, name + "t", c, loads, jobs)
        if not given:
            spread = S.sb("spread", [P, KC, GROUPS, GH, HP])
            with S.block() as block:
                @block.vector
                def _(dve):
                    nc.vector.memset(spread[:], 0.0).then_inc(ready, 1)
                    dve.wait_ge(ready, 1)
                    for o in range(KC):
                        nc.vector.tensor_copy(spread[:, o, :, :, 0:HD], raw[:, 3, o, :].rearrange("p (g m d) -> p g m d", m=GH, d=HD))
            prepare(nc, name + "o", c, [], [
                (wo[:, g, o * P:(o + 1) * P], spread[:, o, g].rearrange("p m d -> p (m d)")) for o in range(KC) for g in range(GROUPS)])
        else:
            with S.block() as block:
                @block.vector
                def _(dve):
                    nc.vector.tensor_scalar(bqk[:, 0:KC], bqk[:, 0:KC], HD ** -0.5, None, ALU.mult)

        xb = S.sb("xb", [P, KC, SEQ])
        full = S.sb("full", [P, 2 * KC, SEQ])
        part = [S.sb(n, [P, 2 * KC, SEQ], BF16) for n in ("hi", "mid", "lo")]
        qk_ps = S.ps("qk_ps", [P, 2 * KC, BANK])
        v_ps = S.ps("v_ps", [P, QT, DM])
        x_staged, qk_ready, qk_read, hi_ready, v_ready, v_read, mid_ready, lo_ready, rest_ready, parts_stored = (S.sem(n) for n in (
            "x_staged", "qk_ready", "qk_read", "hi_ready", "v_ready", "v_read", "mid_ready", "lo_ready", "rest_ready", "parts_stored"))
        with S.block() as block:
            @block.gpsimd
            def _(pool):
                pool.sem_inc(v_ready, 1)
                with pool.Fori(0, BATCH) as b:
                    pool.wait_ge(v_ready, b + 1)
                    nc.gpsimd.tensor_copy(xb[:], xnT[:, :, bass.ds(b * SEQ, SEQ)]).then_inc(x_staged, 1)

            @block.tensor
            def _(pe):
                pe.sem_inc(v_read, 1)
                pe.sem_inc(qk_read, 1)
                with pe.Fori(0, BATCH) as b:
                    pe.wait_ge(qk_read, b * (2 * KC) + 1)
                    for j in range(2 * KC):
                        for kc in range(KC):
                            ins = nc.tensor.matmul(qk_ps[:, j, :], wqk[:, kc, j // KC, j % KC * P:(j % KC + 1) * P],
                                                   xnT[:, kc, bass.ds(b * SEQ, SEQ)], start=kc == 0, stop=kc == KC - 1)
                        ins.then_inc(qk_ready, 1)
                    pe.wait_ge(x_staged, b + 1)
                    pe.wait_ge(v_read, b + 1)
                    for u in range(QT):
                        for kc in range(KC):
                            ins = nc.tensor.matmul(v_ps[:, u, :], xb[:, kc, u * P:(u + 1) * P], wv[:, kc, :], start=kc == 0, stop=kc == KC - 1)
                    ins.then_inc(v_ready, 1)

            @block.scalar
            def _(act):
                act.sem_inc(lo_ready, 1)
                act.sem_inc(parts_stored, 16)
                with act.Fori(0, BATCH) as b:
                    act.wait_ge(lo_ready, b + 1)
                    act.wait_ge(parts_stored, b * 16 + 16)
                    for j in range(2 * KC):
                        act.wait_ge(qk_ready, b * (2 * KC) + (j + 1))
                        scale = HD ** -0.5 if j < KC else 1.0
                        nc.scalar.activation(full[:, j, :], qk_ps[:, j, :], ACT.Identity, bias=bqk[:, j:j + 1], scale=scale)
                        nc.scalar.activation(part[0][:, j, :], qk_ps[:, j, :], ACT.Identity, bias=bqk[:, j:j + 1], scale=scale).then_inc(qk_read, 1)

            @block.vector
            def _(dve):
                dve.sem_inc(rest_ready, 16)
                with dve.Fori(0, BATCH) as b:
                    dve.wait_ge(qk_read, b * (2 * KC) + (2 * KC + 1))
                    nc.vector.tensor_tensor(full[:], full[:], part[0][:], ALU.subtract).then_inc(hi_ready, 1)
                    dve.wait_ge(v_ready, b + 2)
                    nc.vector.tensor_tensor(v[:, bass.ds(b * QT, QT), :], v_ps[:], bvb[:, None, :].to_broadcast([P, QT, DM]), ALU.add).then_inc(v_read, 1)
                    dve.wait_ge(hi_ready, b + 1)
                    dve.wait_ge(rest_ready, b * 32 + 16)
                    nc.vector.tensor_copy(part[1][:], full[:]).then_inc(mid_ready, 1)
                    dve.wait_ge(mid_ready, b + 1)
                    nc.vector.tensor_tensor(part[2][:], full[:], part[1][:], ALU.subtract).then_inc(lo_ready, 1)

            @block.sync
            def _(sp):
                def store(b, n, stored):
                    sp.dma_start(parts[n, bass.ds(b, 1)].rearrange("b (j p) t -> p (b j) t", p=P), part[n][:]).then_inc(stored, 16)

                with sp.Fori(0, BATCH) as b:
                    sp.wait_ge(qk_read, b * (2 * KC) + (2 * KC + 1))
                    store(b, 0, parts_stored)
                    sp.wait_ge(lo_ready, b + 2)
                    store(b, 1, rest_ready)
                    store(b, 2, rest_ready)
                sp.wait_ge(parts_stored, 16 * BATCH + 16)
                sp.wait_ge(rest_ready, 32 * BATCH + 16)


def attend_heads(nc, name, c, parts, v, wo, bob, window):
    x = c["x"]
    max_units = [(r, (2 * p, 2 * p + 1)) for r in range(GH) for p in range(QT // 2)] if window else \
        [(r, (q,)) for r in range(GH) for q in range(QT)]
    KEYS = 2 * P if window else SEQ
    prob_units = [(kt, tuple(range(GH)), min(2 * P, SEQ - kt * P)) for kt in range(QT)] if window else \
        [(kt, (2 * p, 2 * p + 1), SEQ) for kt in range(QT) for p in range(GH // 2)]
    N1, N2 = len(max_units), len(prob_units)
    W = 2 * P if window else SEQ
    UH = len(prob_units[0][1])
    NL = 2 * len(Q_PARTS)
    with Scope(nc, name) as S:
        qs, ks = (S.sb(n, [P, 2, HEADS, SEQ], BF16) for n in ("qs", "ks"))
        vb = S.sb("vb", [P, 2, QT, HEADS, HP])
        identb = S.sb("identb", [P, P], BF16)
        sel = S.sb("sel", [P, GH, P], BF16)
        den_sel = S.sb("den_sel", [P, P])
        mask = S.sb("mask", [P, 3 * P], BF16) if window else None
        maskT = S.sb("maskT", [P, 2 * P], BF16) if window else None
        nm = S.sb("nm", [P, 2, QT, GH])
        nmp = S.sb("nmp", [P, QT, 3, GH], BF16)
        nmT = S.sb("nmT", [P, 2, SEQ], BF16)
        pT = S.sb("pT", [P, 2, UH, W])
        o_raw = S.sb("o_raw", [P, GROUPS, SEQ])
        rden = S.sb("rden", [P, 2, SEQ])
        s1 = S.ps("s1", [P, 2, BANK])
        s2 = S.ps("s2", [P, 2, 2 * BANK])
        o_ps = S.ps("o_ps", [P, BANK])
        m_ps = S.ps("m_ps", [P, 2 * BANK], BF16)
        built = S.sem("built")
        loaded = [S.sem("loaded_even"), S.sem("loaded_odd")]
        (v_staged, element_done, s1_ready, max_done, nmp_ready, nmT_out, nmT_ready, s2_ready, exp_done, pv_done, o_copied,
         den_ready, rden_ready, on_ready, y_ready, y_added, step) = (S.sem(n) for n in (
             "v_staged", "element_done", "s1_ready", "max_done", "nmp_ready", "nmT_out", "nmT_ready", "s2_ready", "exp_done",
             "pv_done", "o_copied", "den_ready", "rden_ready", "on_ready", "y_ready", "y_added", "step"))
        with S.block() as block:
            @block.gpsimd
            def _(pool):
                ch = Chain(pool, built)
                ch.step(nc.gpsimd.memset(vb[:], 0.0))
                nc.gpsimd.memset(vb[:, :, :, :, HD:HD + 1], 1.0)
                ch.step(nc.gpsimd.memset(sel[:], 0.0))
                for n in range(3):
                    ch.step(nc.gpsimd.affine_select(out=sel[:], in_=sel[:], compare_op=ALU.not_equal, fill=1.0, base=-GH * n,
                                                    pattern=[[-1, GH], [0, P]], channel_multiplier=1))
                ch.step(nc.gpsimd.memset(den_sel[:], 0.0))
                ch.step(nc.gpsimd.affine_select(out=den_sel[:].rearrange("p (m d) -> p m d", d=HP), in_=den_sel[:].rearrange("p (m d) -> p m d", d=HP),
                                                compare_op=ALU.not_equal, fill=1.0, base=-HD, pattern=[[-HP, GH], [0, HP]],
                                                channel_multiplier=1))
                if window:
                    ch.step(nc.gpsimd.memset(mask[:], 0.0))
                    ch.step(nc.gpsimd.affine_select(out=mask[:], in_=mask[:], compare_op=ALU.is_ge, fill=-1e9, base=P,
                                                    pattern=[[-1, 3 * P]], channel_multiplier=1))
                    ch.step(nc.gpsimd.affine_select(out=mask[:], in_=mask[:], compare_op=ALU.is_ge, fill=-1e9, base=64 - P,
                                                    pattern=[[1, 3 * P]], channel_multiplier=-1))
                    ch.step(nc.gpsimd.memset(maskT[:], 0.0))
                    ch.step(nc.gpsimd.affine_select(out=maskT[:], in_=maskT[:], compare_op=ALU.is_ge, fill=-1e9, base=0,
                                                    pattern=[[1, 2 * P]], channel_multiplier=-1))
                    ch.step(nc.gpsimd.affine_select(out=maskT[:], in_=maskT[:], compare_op=ALU.is_ge, fill=-1e9, base=64,
                                                    pattern=[[-1, 2 * P]], channel_multiplier=1))

            @block.vector
            def _(dve):
                nc.vector.tensor_copy(identb[:], c["ident"][:])
                for stack in (qs, ks):
                    nc.vector.memset(stack[96:128], 0.0)
                nc.vector.memset(nmT[:], 0.0)

        def elements(eng, body):
            with eng.Fori(0, BATCH // 2) as bb:
                for par in range(2):
                    body(bb * 2 + par, par, bb)

        with S.block() as block:
            @block.sync
            def _(sp):
                def load(b, par, bb):
                    sp.wait_ge(element_done, b + 1)
                    for n, (stack, order) in enumerate(((qs, Q_PARTS), (ks, K_PARTS))):
                        for s, p in enumerate(order):
                            sp.dma_start(stack[HD * s:HD * (s + 1), par],
                                         parts[p, bass.ds(b, 1), n * DM:(n + 1) * DM, :].rearrange("b (h d) t -> d (b h) t", d=HD)).then_inc(loaded[par], 16)

                elements(sp, load)

            @block.gpsimd
            def _(pool):
                def stage(b, par, bb):
                    pool.wait_ge(element_done, b + 1)
                    nc.gpsimd.tensor_copy(vb[:, par, :, :, 0:HD], v[:, bass.ds(b * QT, QT), :].rearrange("p q (h w) -> p q h w", w=HD)).then_inc(v_staged, 1)

                elements(pool, stage)

            @block.tensor
            def _(pe):
                pe.sem_inc(element_done, 2)

                def element(b, par, bb):
                    def max_scores(g, j):
                        i = g * N1 + j
                        r, qts = max_units[j]
                        pe.wait_ge(max_done, b * (GROUPS * N1) + (i + 1))
                        for v_, q in enumerate(qts):
                            k0 = max(q - 1, 0) * P if window else 0
                            out = s1[:, i % 2, v_ * KEYS:(v_ + 1) * KEYS]
                            ins = nc.tensor.matmul(out, qs[:, par, g * GH + r, q * P:(q + 1) * P], ks[:, par, g * GH + r, k0:k0 + KEYS],
                                                   start=True, stop=not window)
                            if window:
                                m0 = 0 if q else P
                                ins = nc.tensor.matmul(out, identb[:], mask[:, m0:m0 + KEYS], start=False, stop=True)
                        ins.then_inc(s1_ready, 1)

                    def turn_max(g):
                        pe.wait_ge(nmp_ready, b * GROUPS + (g + 1))
                        for q in range(QT):
                            ins = nc.tensor.transpose(m_ps[0:3 * GH, q * P:(q + 1) * P], nmp[:, q].rearrange("p n r -> p (n r)"), identb[:])
                        ins.then_inc(nmT_out, 1)

                    def prob_scores(g, j):
                        u = g * N2 + j
                        kt, heads, n = prob_units[j]
                        pe.wait_ge(exp_done, b * (GROUPS * N2) + (u + 1))
                        if j == 0:
                            pe.wait_ge(nmT_ready, b * GROUPS + (g + 1))
                        q0 = kt * P if window else 0
                        for i, r in enumerate(heads):
                            out = s2[:, u % 2, i * W:i * W + n]
                            nc.tensor.matmul(out, ks[:, par, g * GH + r, kt * P:(kt + 1) * P], qs[:, par, g * GH + r, q0:q0 + n], start=True, stop=False)
                            if window:
                                nc.tensor.matmul(out, identb[:], maskT[:, 0:n], start=False, stop=False)
                            ins = nc.tensor.matmul(out, sel[:, r, :], nmT[:, g % 2, q0:q0 + n], start=False, stop=True)
                        ins.then_inc(s2_ready, 1)

                    def weigh(g, j):
                        u = g * N2 + j
                        kt, heads, n = prob_units[j]
                        pe.wait_ge(exp_done, b * (GROUPS * N2) + (u + 3))
                        if j == 0:
                            pe.wait_ge(o_copied, b * GROUPS + (g + 1))
                        q0 = kt * P if window else 0
                        for i, r in enumerate(heads):
                            ins = nc.tensor.matmul(o_ps[HP * r:HP * r + HP, q0:q0 + n], vb[:, par, kt, g * GH + r, :],
                                                   pT[:, u % 2, i, 0:n], start=kt == 0, stop=kt == QT - 1, skip_group_check=window)
                        ins.then_inc(pv_done, 1)

                    pe.wait_ge(loaded[par], bb * (16 * NL) + 16 * NL)
                    pe.wait_ge(y_added, b * QT + 1)
                    for j in range(N1):
                        max_scores(0, j)
                    turn_max(0)
                    pe.wait_ge(v_staged, b + 1)
                    pending = None
                    for g in range(GROUPS):
                        ahead = 0
                        for j in range(N2):
                            prob_scores(g, j)
                            while g + 1 < GROUPS and ahead < min(N1, 3 * (j + 1)):
                                max_scores(g + 1, ahead)
                                ahead += 1
                            if pending:
                                weigh(*pending)
                            pending = (g, j)
                        if g + 1 < GROUPS:
                            turn_max(g + 1)
                    weigh(*pending)
                    for g in range(GROUPS):
                        pe.wait_ge(o_copied, b * GROUPS + (g + 2))
                        if g >= 2:
                            pe.wait_ge(rden_ready, b * GROUPS + (g - 1))
                        nc.tensor.matmul(s1[:, g % 2, :], den_sel[:], o_raw[:, g, :], start=True, stop=True).then_inc(den_ready, 1)
                    pe.wait_ge(on_ready, b * GROUPS + GROUPS)
                    for q in range(QT):
                        if q >= 2:
                            pe.wait_ge(y_added, b * QT + q)
                        for g in range(GROUPS):
                            ins = nc.tensor.matmul(s1[:, q % 2, 0:DM], o_raw[:, g, q * P:(q + 1) * P], wo[:, g, :], start=g == 0, stop=g == GROUPS - 1)
                            if q == 0 and g == 0:
                                ins.then_inc(element_done, 1)
                        ins.then_inc(y_ready, 1)

                elements(pe, element)

            @block.vector
            def _(dve):
                V = nc.vector
                dve.sem_inc(max_done, 2)
                dve.sem_inc(y_added, 1)
                STEPS = 3 * GROUPS + QT * (bob is not None)

                def element(b, par, bb):
                    ch = Chain(dve, step, b * STEPS)

                    def maxima(g):
                        for j, (r, qts) in enumerate(max_units):
                            dve.wait_ge(s1_ready, b * (GROUPS * N1) + (g * N1 + j + 1))
                            V.tensor_reduce(nm[:, g % 2, qts[0]:qts[-1] + 1, r], s1[:, j % 2, :].rearrange("p (q k) -> p q k", k=KEYS), AX, ALU.max,
                                            negate=True).then_inc(max_done, 1)
                        dve.wait_ge(max_done, b * (GROUPS * N1) + ((g + 1) * N1 + 2))
                        val = nm[:, g % 2]
                        ch.step(V.tensor_copy(nmp[:, :, 0, :], val))
                        ch.step(V.tensor_tensor(val, val, nmp[:, :, 0, :], ALU.subtract))
                        ch.step(V.tensor_copy(nmp[:, :, 1, :], val))
                        V.tensor_tensor(nmp[:, :, 2, :], val, nmp[:, :, 1, :], ALU.subtract).then_inc(nmp_ready, 1)
                        dve.wait_ge(nmT_out, b * GROUPS + (g + 1))
                        V.tensor_copy(nmT[0:3 * GH, g % 2, :], m_ps[0:3 * GH, 0:SEQ]).then_inc(nmT_ready, 1)

                    for g in range(GROUPS):
                        maxima(g)
                    for g in range(GROUPS):
                        dve.wait_ge(den_ready, b * GROUPS + (g + 1))
                        V.reciprocal(rden[:, g % 2, :], s1[:, g % 2, :]).then_inc(rden_ready, 1)
                        dve.wait_ge(rden_ready, b * GROUPS + (g + 1))
                        V.tensor_tensor(o_raw[:, g, :], o_raw[:, g, :], rden[:, g % 2, :], ALU.mult).then_inc(on_ready, 1)
                    for q in range(QT):
                        if bob is not None:
                            ch.step(V.tensor_tensor(x[:, b * QT + q, :], x[:, b * QT + q, :], bob[:], ALU.add))
                        dve.wait_ge(y_ready, b * QT + (q + 1))
                        V.tensor_tensor(x[:, b * QT + q, :], x[:, b * QT + q, :], s1[:, q % 2, 0:DM], ALU.add).then_inc(y_added, 1)

                elements(dve, element)

            @block.scalar
            def _(act):
                act.sem_inc(exp_done, 2)
                act.sem_inc(pv_done, 2)
                act.sem_inc(o_copied, 1)

                def element(b, par, bb):
                    def copy_out(g):
                        act.wait_ge(pv_done, b * (GROUPS * N2) + ((g + 1) * N2 + 2))
                        if g == 0:
                            act.wait_ge(y_added, b * QT + 1)
                        nc.scalar.copy(o_raw[:, g, :], o_ps[:]).then_inc(o_copied, 1)

                    for g in range(GROUPS):
                        for j in range(N2):
                            u = g * N2 + j
                            n = prob_units[j][2]
                            act.wait_ge(s2_ready, b * (GROUPS * N2) + (u + 1))
                            act.wait_ge(pv_done, b * (GROUPS * N2) + (u + 1))
                            nc.scalar.activation(pT[:, u % 2, :, 0:n], s2[:, u % 2, :].rearrange("p (h t) -> p h t", t=W)[:, :, 0:n],
                                                 ACT.Exp).then_inc(exp_done, 1)
                            if j == 0 and g:
                                copy_out(g - 1)
                    copy_out(GROUPS - 1)

                elements(act, element)


CTX, CD = 64, 192
CTOK = BATCH * CTX
CT = CTOK // P
CK = ((0, P), (P, CD - P))
HK = HEADS * CTX


def cross_attention(nc, name, c, wts, dh, out_in=False, norm_ctx=False, clamp=None):
    x, xnT, ident, ones = c["x"], c["xnT"], c["ident"], c["ones"]
    inner = HEADS * dh
    NC = inner // P
    HC = P // dh
    bq, bo = wts.get("bq"), wts.get("bo")
    kv_biased = "bk" in wts or "bkv" in wts
    with Scope(nc, name) as S:
        qk = S.sb("qk", [P, BATCH, KC, HK])
        vo = S.sb("vo", [P, BATCH, HK // P, DM])
        brow = S.sb("brow", [1, BATCH, HK]) if bq is not None else None
        bob = S.sb("bob", [P, DM]) if bo is not None else None
        with Scope(nc, name + "p") as W:
            wqT = W.sb("wqT", [P, NC, DM])
            wo = W.sb("wo", [P, NC, DM])
            wkv = W.sb("wkv", [P, 2, 2, inner])
            ctxT = W.sb("ctxT", [P, 2, CTOK])
            kvT = W.sb("kvT", [P, 2, NC, CTOK])
            ctx = W.sb("ctx", [P, CT, CD])
            heads = W.sb("heads", [P, HC])
            bkv_col = W.sb("bkv_col", [P, 2, NC]) if kv_biased else None
            bq_col = W.sb("bq_col", [P, NC]) if bq is not None else None
            diag = W.sb("diag", [P, 2, 2, HK])
            made = W.sem("made")
            with W.block() as block:
                @block.gpsimd
                def _(pool):
                    nc.gpsimd.memset(heads[:], 1.0).then_inc(made, 1)
                    pool.wait_ge(made, 1)
                    nc.gpsimd.affine_select(out=heads[:], in_=heads[:], compare_op=ALU.is_ge, fill=0.0, base=0,
                                            pattern=[[-dh, HC]], channel_multiplier=1).then_inc(made, 1)
                    pool.wait_ge(made, 2)
                    nc.gpsimd.affine_select(out=heads[:], in_=heads[:], compare_op=ALU.is_ge, fill=0.0, base=dh - 1,
                                            pattern=[[dh, HC]], channel_multiplier=-1)
            with Scope(nc, name + "r") as R:
                loads = [(ctx[:], c["ctx_dram"])]
                jobs = []
                if out_in:
                    raw = R.sb("raw", [P, 2, 2, CD])
                    rawo = R.sb("rawo", [P, KC, DM])
                    per_head = wts["Wkv"].rearrange("(h n w) c -> h n w c", n=2, w=dh)
                    bias_head = wts["bkv"].rearrange("(h n w) -> h n w", n=2, w=dh)
                    for r in range(HC):
                        for n in range(2):
                            loads.append((raw[r * dh:(r + 1) * dh, n], per_head[r::HC, n].rearrange("c w d -> w c d")))
                            loads.append((bkv_col[r * dh:(r + 1) * dh, n], bias_head[r::HC, n].rearrange("c w -> w c")))
                    loads.append((wqT[:], wts["Wq"].rearrange("(c p) d -> p c d", p=P)))
                    loads.append((rawo[:], wts["Wo"].rearrange("(c p) d -> p c d", p=P)))
                    for n in range(2):
                        for o in range(NC):
                            for k, (k0, kn) in enumerate(CK):
                                jobs.append((wkv[0:kn, k, n, o * P:(o + 1) * P], raw[:, n, o, k0:k0 + kn]))
                    for k in range(KC):
                        for o in range(KC):
                            jobs.append((wo[:, k, o * P:(o + 1) * P], rawo[:, o, k * P:(k + 1) * P]))
                else:
                    raw = R.sb("raw", [P, KC, inner])
                    loads.append((raw[:], wts["Wq"].rearrange("(k p) n -> p k n", p=P)))
                    loads.append((wo[:], wts["Wo"].rearrange("(c p) n -> p c n", p=P)))
                    for n, w in enumerate(("Wk", "Wv")):
                        for k, (k0, kn) in enumerate(CK):
                            loads.append((wkv[0:kn, k, n, :], wts[w][k0:k0 + kn, :]))
                    for cc in range(NC):
                        for k in range(KC):
                            jobs.append((wqT[:, cc, k * P:(k + 1) * P], raw[:, k, cc * P:(cc + 1) * P]))
                    if kv_biased:
                        for n, b in enumerate(("bk", "bv")):
                            loads.append((bkv_col[:, n, :], wts[b].rearrange("(c p) -> p c", p=P)))
                if bq is not None:
                    loads.append((bq_col[:], bq.rearrange("(c p) -> p c", p=P)))
                if bo is not None:
                    loads.append((bob[:], bo[None, :].to_broadcast([P, DM])))
                if norm_ctx:
                    gc = R.sb("gc", [P, 2, CD])
                    loads.append((gc[:, 0, :], wts["g_c"][None, :].to_broadcast([P, CD])))
                    loads.append((gc[:, 1, :], wts["b_c"][None, :].to_broadcast([P, CD])))
                with nc.allow_non_contiguous_dma(reason="bias vectors by feature"):
                    prepare(nc, name + "t", c, loads, jobs)
                if norm_ctx:
                    st, mean, rstd, tmp = R.sb("st", [P, CT, 6]), R.sb("mean", [P, CT]), R.sb("rstd", [P, CT]), R.sb("tmp", [P, CT])
                    step, var_ready, std_ready = R.sem("step"), R.sem("var_ready"), R.sem("std_ready")
                    with R.block() as block:
                        @block.vector
                        def _(dve):
                            ch = Chain(dve, step)
                            for i in range(CT):
                                ch.step(nc.vector.bn_stats(st[:, i, :], ctx[:, i, :]))
                            row_stats_to_affine(nc, ch, st, mean[:], rstd[:], tmp[:], CD // 2)
                            nc.vector.tensor_copy(tmp[:], rstd[:]).then_inc(var_ready, 1)
                            dve.wait_ge(std_ready, 1)
                            ch.step(nc.vector.reciprocal(rstd[:], tmp[:]))
                            for i in range(CT):
                                ch.step(nc.vector.tensor_scalar(ctx[:, i, :], ctx[:, i, :], mean[:, i:i + 1], rstd[:, i:i + 1],
                                                                ALU.subtract, ALU.mult))
                            ch.step(nc.vector.tensor_tensor(ctx[:], ctx[:], gc[:, None, 0, :].to_broadcast([P, CT, CD]), ALU.mult))
                            nc.vector.tensor_tensor(ctx[:], ctx[:], gc[:, None, 1, :].to_broadcast([P, CT, CD]), ALU.add)

                        @block.scalar
                        def _(act):
                            act.wait_ge(var_ready, 1)
                            nc.scalar.activation(tmp[:], tmp[:], ACT.Sqrt).then_inc(std_ready, 1)

            jobs = [(ctxT[0:kn, k, i * P:(i + 1) * P], ctx[:, i, k0:k0 + kn]) for i in range(CT) for k, (k0, kn) in enumerate(CK)]
            prepare(nc, name + "c", c, [], jobs)

            with Scope(nc, name + "k") as R:
                kv_ps = R.ps("kv_ps", [P, 4, BANK])
                kv_ready, kv_free = R.sem("kv_ready"), R.sem("kv_free")
                with R.block() as block:
                    @block.tensor
                    def _(pe):
                        for j in range(2 * NC):
                            if j >= 4:
                                pe.wait_ge(kv_free, j - 3)
                            for k, (k0, kn) in enumerate(CK):
                                ins = nc.tensor.matmul(kv_ps[:, j % 4, 0:CTOK], wkv[0:kn, k, j // NC, j % NC * P:(j % NC + 1) * P],
                                                       ctxT[0:kn, k, :], start=k == 0, stop=k == 1)
                            ins.then_inc(kv_ready, 1)

                    @block.vector
                    def _(dve):
                        for j in range(2 * NC):
                            n, cc = j // NC, j % NC
                            dve.wait_ge(kv_ready, j + 1)
                            scale = dh ** -0.5 if n == 0 else 1.0
                            if kv_biased:
                                ins = nc.vector.tensor_scalar(kvT[:, n, cc, :], kv_ps[:, j % 4, 0:CTOK], bkv_col[:, n, cc:cc + 1], scale, ALU.add, ALU.mult)
                            else:
                                ins = nc.vector.tensor_scalar(kvT[:, n, cc, :], kv_ps[:, j % 4, 0:CTOK], scale, None, ALU.mult)
                            ins.then_inc(kv_free, 1)

            with Scope(nc, name + "g") as R:
                qk_ps = R.ps("qk_ps", [P, KC, HK])
                vo_ps = R.ps("vo_ps", [P, 4, 2, DM])
                diag_ready, qk_ready, vo_ready, qk_copied, vo_copied, b_ready, b_copied = (R.sem(n) for n in (
                    "diag_ready", "qk_ready", "vo_ready", "qk_copied", "vo_copied", "b_ready", "b_copied"))
                CW = HC * CTX
                with R.block() as block:
                    @block.gpsimd
                    def _(pool):
                        for b in range(BATCH):
                            if b >= 2:
                                pool.wait_ge(vo_ready, b - 1)
                            for n in range(2):
                                for cc in range(NC):
                                    ins = nc.gpsimd.tensor_tensor(
                                        diag[:, b % 2, n, cc * CW:(cc + 1) * CW].rearrange("p (h k) -> p h k", k=CTX),
                                        kvT[:, n, cc, None, b * CTX:(b + 1) * CTX].to_broadcast([P, HC, CTX]),
                                        heads[:, :, None].to_broadcast([P, HC, CTX]), ALU.mult)
                            ins.then_inc(diag_ready, 1)

                    @block.tensor
                    def _(pe):
                        for b in range(BATCH):
                            pe.wait_ge(diag_ready, b + 1)
                            if b:
                                pe.wait_ge(qk_copied, b)
                            for k in range(KC):
                                for cc in range(NC):
                                    ins = nc.tensor.matmul(qk_ps[:, k, cc * CW:(cc + 1) * CW], wqT[:, cc, k * P:(k + 1) * P],
                                                           diag[:, b % 2, 0, cc * CW:(cc + 1) * CW], start=True, stop=True)
                            ins.then_inc(qk_ready, 1)
                            if bq is not None:
                                pe.wait_ge(qk_copied, b + 1)
                                for cc in range(NC):
                                    ins = nc.tensor.matmul(qk_ps[0:1, 0, cc * CW:(cc + 1) * CW], bq_col[:, cc:cc + 1],
                                                           diag[:, b % 2, 0, cc * CW:(cc + 1) * CW], start=True, stop=True)
                                ins.then_inc(b_ready, 1)
                                pe.wait_ge(b_copied, b + 1)
                            if b:
                                pe.wait_ge(vo_copied, b)
                            for j in range(HK // P):
                                ins = nc.tensor.matmul(vo_ps[:, j // 2, j % 2, :], diag[:, b % 2, 1, j * P:(j + 1) * P],
                                                       wo[:, j * P // CW, :], start=True, stop=True)
                            ins.then_inc(vo_ready, 1)

                    @block.vector
                    def _(dve):
                        for b in range(BATCH):
                            dve.wait_ge(qk_ready, b + 1)
                            nc.vector.tensor_copy(qk[:, b], qk_ps[:]).then_inc(qk_copied, 1)
                            if bq is not None:
                                dve.wait_ge(b_ready, b + 1)
                                nc.vector.tensor_copy(brow[0:1, b, :], qk_ps[0:1, 0, :]).then_inc(b_copied, 1)

                    @block.scalar
                    def _(act):
                        for b in range(BATCH):
                            act.wait_ge(vo_ready, b + 1)
                            nc.scalar.copy(vo[:, b].rearrange("p j n -> p (j n)"), vo_ps[:].rearrange("p a b n -> p (a b n)")).then_inc(vo_copied, 1)

        s_ps = S.ps("s_ps", [P, 2, HK])
        t_ps = S.ps("t_ps", [P, HK])
        y_ps = S.ps("y_ps", [P, BANK])
        x_now = S.sb("x_now", [P, QT, KC, P])
        shifted = S.sb("shifted", [P, 2, HEADS, CTX])
        probs = S.sb("probs", [P, 2, HEADS, CTX])
        probsT = S.sb("probsT", [P, 2, HK])
        negmax = S.sb("negmax", [P, 2, HEADS])
        rsum = S.sb("rsum", [P, 2, HEADS])
        (x_staged, scores_ready, shifted_ready, exp_ready, sum_ready, probs_ready, pT_ready, pT_copied, y_ready, y_added, shift_step,
         finish_step, bias_step) = (S.sem(n) for n in (
             "x_staged", "scores_ready", "shifted_ready", "exp_ready", "sum_ready", "probs_ready", "pT_ready", "pT_copied",
             "y_ready", "y_added", "shift_step", "finish_step", "bias_step"))
        clamped = S.sb("clamped", [P, 2, HEADS, CTX]) if clamp else None

        def tiles(eng, body):
            def element(b, more):
                for q in range(QT):
                    body(b, q, b * QT + q, more + QT - 1 - q)

            element(0, QT)
            with eng.Fori(1, BATCH - 1) as b:
                element(b, QT)
            element(BATCH - 1, 0)

        def following(b, q, d):
            b2, q2 = b + (q + d) // QT, (q + d) % QT
            return b2, q2, b2 * QT + q2

        with S.block() as block:
            @block.gpsimd
            def _(pool):
                pool.sem_inc(probs_ready, 1)
                for q in range(QT):
                    nc.gpsimd.tensor_copy(x_now[:, q], xnT[:, :, q * P:(q + 1) * P]).then_inc(x_staged, 1)

                def body(b, q, t, left):
                    pool.wait_ge(sum_ready, t + 1)
                    pool.wait_ge(pT_ready, t + 1)
                    nc.gpsimd.tensor_tensor(probs[:, q % 2], shifted[:, q % 2], rsum[:, q % 2, :, None].to_broadcast([P, HEADS, CTX]),
                                            ALU.mult).then_inc(probs_ready, 1)
                    if left >= QT:
                        nc.gpsimd.tensor_copy(x_now[:, q], xnT[:, :, bass.ds((b * QT + (q + QT)) * P, P)]).then_inc(x_staged, 1)

                tiles(pool, body)

            @block.tensor
            def _(pe):
                pe.sem_inc(pT_ready, 2)

                def scores(b, q, t):
                    pe.wait_ge(x_staged, t + 1)
                    pe.wait_ge(shifted_ready, t + 1)
                    for half in range(2):
                        cols = bass.ts(half, BANK)
                        for k in range(KC):
                            ins = nc.tensor.matmul(s_ps[:, q % 2, cols], x_now[:, q, k, :], qk[:, b, k, cols],
                                                   start=k == 0, stop=k == KC - 1 and bq is None)
                        if bq is not None:
                            ins = nc.tensor.matmul(s_ps[:, q % 2, cols], ones[0:1, :], brow[0:1, b, cols], start=False, stop=True)
                    ins.then_inc(scores_ready, 1)

                def body(b, q, t, left):
                    pe.wait_ge(probs_ready, t + 2)
                    pe.wait_ge(pT_copied, t + 1)
                    for j in range(HK // P):
                        ins = nc.tensor.transpose(t_ps[:, j * P:(j + 1) * P], probs[:, q % 2, 2 * j:2 * j + 2, :].rearrange("p h k -> p (h k)"), ident[:])
                    ins.then_inc(pT_ready, 1)
                    if left >= 2:
                        scores(*following(b, q, 2))
                    pe.wait_ge(pT_copied, t + 2)
                    pe.wait_ge(y_added, t + 1)
                    for j in range(HK // P):
                        ins = nc.tensor.matmul(y_ps[:, 0:DM], probsT[:, q % 2, j * P:(j + 1) * P], vo[:, b, j, :],
                                               start=j == 0, stop=j == HK // P - 1)
                    ins.then_inc(y_ready, 1)

                scores(0, 0, 0)
                scores(0, 1, 1)
                tiles(pe, body)

            @block.vector
            def _(dve):
                dve.sem_inc(y_added, 1)
                dve.sem_inc(shifted_ready, 2)
                SHIFT_STEPS = 1 + (clamp is not None)

                def shift(b, q, t):
                    ch = Chain(dve, shift_step, t * SHIFT_STEPS)
                    dve.wait_ge(scores_ready, t + 1)
                    src = s_ps[:, q % 2].rearrange("p (h k) -> p h k", k=CTX)
                    if clamp:
                        ch.step(nc.vector.tensor_scalar(clamped[:, q % 2], src, clamp, -clamp, ALU.min, ALU.max))
                        src = clamped[:, q % 2]
                    ch.step(nc.vector.tensor_reduce(negmax[:, q % 2], src, AX, ALU.max, negate=True))
                    if not (isinstance(t, int) and t < 2):
                        dve.wait_ge(probs_ready, t)
                    nc.vector.tensor_tensor(shifted[:, q % 2], src, negmax[:, q % 2, :, None].to_broadcast([P, HEADS, CTX]),
                                            ALU.add).then_inc(shifted_ready, 1)

                def finish(b, q, t):
                    dve.wait_ge(exp_ready, t + 1)
                    Chain(dve, finish_step, t).step(nc.vector.tensor_reduce(rsum[:, q % 2], shifted[:, q % 2], AX, ALU.add))
                    nc.vector.reciprocal(rsum[:, q % 2], rsum[:, q % 2]).then_inc(sum_ready, 1)

                def body(b, q, t, left):
                    if left >= 1:
                        finish(*following(b, q, 1))
                    if left >= 2:
                        shift(*following(b, q, 2))
                    if bo is not None:
                        Chain(dve, bias_step, t).step(nc.vector.tensor_tensor(x[:, t, :], x[:, t, :], bob[:], ALU.add))
                    dve.wait_ge(y_ready, t + 1)
                    nc.vector.tensor_tensor(x[:, t, :], x[:, t, :], y_ps[:, 0:DM], ALU.add).then_inc(y_added, 1)

                shift(0, 0, 0)
                shift(0, 1, 1)
                finish(0, 0, 0)
                tiles(dve, body)

            @block.scalar
            def _(act):
                act.sem_inc(pT_copied, 1)

                def exp(b, q, t):
                    act.wait_ge(shifted_ready, t + 3)
                    nc.scalar.activation(shifted[:, q % 2], shifted[:, q % 2], ACT.Exp).then_inc(exp_ready, 1)

                def body(b, q, t, left):
                    act.wait_ge(pT_ready, t + 3)
                    nc.scalar.copy(probsT[:, q % 2], t_ps[:]).then_inc(pT_copied, 1)
                    if left >= 2:
                        exp(*following(b, q, 2))

                exp(0, 0, 0)
                exp(0, 1, 1)
                tiles(act, body)


NE = 8
BIG = 1 << 20


def route(nc, S, name, c, gate_w, gate_b, transposed, choices, capacity, dropped_expert=None):
    xnT, ident, ones = c["xnT"], c["ident"], c["ones"]
    T3 = [P, TILES, NE]
    res = {n: [S.sb(f"{n}{j}", [P, TILES]) for j in range(choices)] for n in ("weight", "keep", "slot")}
    with Scope(nc, name) as R:
        wg = R.sb("wg", [P, KC, NE])
        loads, jobs = [], []
        if transposed:
            raw = R.sb("raw", [NE, DM])
            loads.append((raw[:], gate_w))
            jobs = [(wg[:, k, :], raw[:, k * P:(k + 1) * P]) for k in range(KC)]
        else:
            loads.append((wg[:], gate_w.rearrange("(k p) e -> p k e", p=P)))
        bias = None
        if gate_b is not None:
            bias = R.sb("bias", [P, NE])
            loads.append((bias[:], gate_b[None, :].to_broadcast([P, NE])))
        prepare(nc, name + "t", c, loads, jobs)

        lg_ps = R.ps("lg_ps", [P, BANK])
        pos_ps = R.ps("pos_ps", [P, BANK])
        tot_ps = R.ps("tot_ps", [P, BANK])
        logits, probs, scratch, mask = (R.sb(n, T3) for n in ("logits", "probs", "scratch", "mask"))
        onehot = [R.sb(f"onehot{j}", T3) for j in range(choices)]
        place, totals, sums_a, sums_b = (R.sb(n, T3) for n in ("place", "totals", "sums_a", "sums_b"))
        small, small2 = R.sb("small", [P, TILES]), R.sb("small2", [P, TILES])
        number = R.sb("number", [P, NE])
        before = R.sb("before", [P, P])
        lg_ready, shifted_ready, exp_ready, mask_ready, counts_ready, step, made = (R.sem(n) for n in (
            "lg_ready", "shifted_ready", "exp_ready", "mask_ready", "counts_ready", "step", "made"))

        def per_tile(a):
            return a[:, :, None].to_broadcast(T3)

        def per_expert(a):
            return a[:, None, :].to_broadcast(T3)

        with R.block() as block:
            @block.gpsimd
            def _(pool):
                nc.gpsimd.iota(number[:], pattern=[[1, NE]], base=0, channel_multiplier=0,
                               allow_small_or_imprecise_dtypes=True).then_inc(made, 1)
                nc.gpsimd.memset(before[:], 1.0).then_inc(made, 1)
                pool.wait_ge(made, 2)
                nc.gpsimd.affine_select(out=before[:], in_=before[:], compare_op=ALU.is_ge, fill=0.0, base=-1,
                                        pattern=[[1, P]], channel_multiplier=-1).then_inc(made, 1)

            @block.tensor
            def _(pe):
                for t in range(TILES):
                    for k in range(KC):
                        ins = nc.tensor.matmul(lg_ps[:, t * NE:(t + 1) * NE], xnT[:, k, t * P:(t + 1) * P], wg[:, k, :],
                                               start=k == 0, stop=k == KC - 1)
                ins.then_inc(lg_ready, 1)
                pe.wait_ge(made, 3)
                pe.wait_ge(mask_ready, 1)
                flat = mask[:].rearrange("p t e -> p (t e)")
                nc.tensor.matmul(pos_ps[:, 0:TILES * NE], before[:], flat, start=True, stop=True)
                nc.tensor.matmul(tot_ps[:, 0:TILES * NE], ones[:], flat, start=True, stop=True).then_inc(counts_ready, 1)

            @block.scalar
            def _(act):
                act.wait_ge(shifted_ready, 1)
                nc.scalar.activation(probs[:], logits[:], ACT.Exp).then_inc(exp_ready, 1)

            @block.vector
            def _(dve):
                ch = Chain(dve, step)
                v = nc.vector
                dve.wait_ge(lg_ready, 1)
                lg = lg_ps[:, 0:TILES * NE].rearrange("p (t e) -> p t e", e=NE)
                if bias is not None:
                    ch.step(v.tensor_tensor(logits[:], lg, per_expert(bias), ALU.add))
                else:
                    ch.step(v.tensor_copy(logits[:], lg))
                ch.step(v.tensor_reduce(small[:], logits[:], AX, ALU.max))
                v.tensor_tensor(logits[:], logits[:], per_tile(small), ALU.subtract).then_inc(shifted_ready, 1)
                dve.wait_ge(exp_ready, 1)
                ch.step(v.tensor_reduce(small[:], probs[:], AX, ALU.add))
                ch.step(v.reciprocal(small[:], small[:]))
                ch.step(v.tensor_tensor(probs[:], probs[:], per_tile(small), ALU.mult))
                dve.wait_ge(made, 3)
                for j in range(choices):
                    w = res["weight"][j]
                    ch.step(v.tensor_reduce(w[:], probs[:], AX, ALU.max))
                    ch.step(v.tensor_tensor(scratch[:], probs[:], per_tile(w), ALU.not_equal))
                    ch.step(v.tensor_scalar(scratch[:], scratch[:], 100.0, None, ALU.mult))
                    ch.step(v.tensor_tensor(scratch[:], scratch[:], per_expert(number), ALU.add))
                    ch.step(v.tensor_reduce(small[:], scratch[:], AX, ALU.min))
                    ch.step(v.tensor_tensor(onehot[j][:], per_tile(small), per_expert(number), ALU.is_equal))
                    if j + 1 < choices:
                        ch.step(v.tensor_scalar(scratch[:], onehot[j][:], 4.0, None, ALU.mult))
                        ch.step(v.tensor_tensor(probs[:], probs[:], scratch[:], ALU.subtract))
                for j in range(choices):
                    ch.step(v.tensor_scalar(small[:], res["weight"][j][:], 0.0, None, ALU.is_gt))
                    ch.step(v.tensor_tensor(onehot[j][:], onehot[j][:], per_tile(small), ALU.mult))
                if choices == 1:
                    ins = v.tensor_copy(mask[:], onehot[0][:])
                else:
                    ins = v.tensor_tensor(mask[:], onehot[0][:], onehot[1][:], ALU.add)
                ins.then_inc(mask_ready, 1)
                dve.wait_ge(counts_ready, 1)
                tot = tot_ps[:, 0:TILES * NE].rearrange("p (t e) -> p t e", e=NE)
                ch.step(v.tensor_copy(totals[:], tot))
                ch.step(v.tensor_copy(sums_a[:], tot))
                src, dst = sums_a, sums_b
                for d in (1, 2, 4, 8):
                    ch.step(v.tensor_copy(dst[:, 0:d, :], src[:, 0:d, :]))
                    ch.step(v.tensor_tensor(dst[:, d:, :], src[:, d:, :], src[:, 0:TILES - d, :], ALU.add))
                    src, dst = dst, src
                ch.step(v.tensor_tensor(place[:], src[:], totals[:], ALU.subtract))
                ch.step(v.tensor_tensor(place[:], place[:], pos_ps[:, 0:TILES * NE].rearrange("p (t e) -> p t e", e=NE), ALU.add))
                ch.step(v.tensor_scalar(scratch[:], place[:], float(capacity), None, ALU.is_ge))
                if dropped_expert is not None:
                    ch.step(v.memset(scratch[:, :, dropped_expert:dropped_expert + 1], 1.0))
                ch.step(v.tensor_scalar(sums_a[:], scratch[:], float(BIG), None, ALU.mult))
                ch.step(v.tensor_tensor(place[:], place[:], sums_a[:], ALU.add))
                ch.step(v.tensor_scalar(small2[:, 0:NE], number[:], float(capacity), None, ALU.mult))
                ch.step(v.tensor_tensor(place[:], place[:], per_expert(small2[:, 0:NE]), ALU.add))
                ch.step(v.tensor_scalar(scratch[:], scratch[:], -1.0, 1.0, ALU.mult, ALU.add))
                for j in range(choices):
                    ch.step(v.tensor_tensor(sums_a[:], onehot[j][:], place[:], ALU.mult))
                    ch.step(v.tensor_reduce(res["slot"][j][:], sums_a[:], AX, ALU.add))
                    ch.step(v.tensor_scalar(small[:], res["weight"][j][:], 0.0, float(BIG), ALU.is_le, ALU.mult))
                    ch.step(v.tensor_tensor(res["slot"][j][:], res["slot"][j][:], small[:], ALU.add))
                    ch.step(v.tensor_tensor(sums_a[:], onehot[j][:], scratch[:], ALU.mult))
                    ch.step(v.tensor_reduce(res["keep"][j][:], sums_a[:], AX, ALU.add))
                if dropped_expert is not None:
                    noop = S.noop
                    for j in range(choices):
                        ch.step(v.tensor_tensor(small[:], onehot[j][:, :, dropped_expert], res["weight"][j][:], ALU.mult))
                        if j == 0:
                            ch.step(v.tensor_copy(noop[:], small[:]))
                        else:
                            ch.step(v.tensor_tensor(noop[:], noop[:], small[:], ALU.add))
    return res


def gated_linear(nc, name, c, wts, capacity):
    x, xnT = c["x"], c["xnT"]
    with Scope(nc, name) as S:
        r = route(nc, S, name + "r", c, wts["w_gate"], None, False, 1, capacity)
        w, bb = S.sb("w", [P, KC, DM]), S.sb("bb", [P, DM])
        prepare(nc, name + "t", c, [(w[:], wts["w_expert"].rearrange("(k p) n -> p k n", p=P)),
                                                 (bb[:], wts["b_expert"][None, :].to_broadcast([P, DM]))], [])
        y_ps = S.ps("y_ps", [P, 4, BANK])
        scale, biased = S.sb("scale", [P, TILES]), S.sb("biased", [P, 2, DM])
        y_ready, y_read, step = S.sem("y_ready"), S.sem("y_read"), S.sem("step")
        with S.block() as block:
            @block.tensor
            def _(pe):
                for t in range(TILES):
                    if t >= 4:
                        pe.wait_ge(y_read, t - 3)
                    for k in range(KC):
                        ins = nc.tensor.matmul(y_ps[:, t % 4, 0:DM], xnT[:, k, t * P:(t + 1) * P], w[:, k, :], start=k == 0, stop=k == KC - 1)
                    ins.then_inc(y_ready, 1)

            @block.vector
            def _(dve):
                ch = Chain(dve, step)
                ch.step(nc.vector.tensor_tensor(scale[:], r["weight"][0][:], r["keep"][0][:], ALU.mult))
                with dve.Fori(0, TILES // 4) as g:
                    for u in range(4):
                        t = g * 4 + u
                        dve.wait_ge(y_ready, t + 1)
                        nc.vector.tensor_tensor(biased[:, u % 2, :], y_ps[:, u, 0:DM], bb[:], ALU.add).then_inc(y_read, 1)
                        dve.wait_ge(y_read, t + 1)
                        nc.vector.scalar_tensor_tensor(out=x[:, t, :], in0=biased[:, u % 2, :], scalar=scale[:, bass.ds(t, 1)],
                                                       in1=x[:, t, :], op0=ALU.mult, op1=ALU.add).then_inc(step, 1)


def mixture(nc, name, c, wts, n_exp, choices, disp, eout, filled):
    x, xn, ident, ones = c["x"], c["xn"], c["ident"], c["ones"]
    cap = TOK // NE
    CTL = cap // P
    HID = 1024
    HC = HID // P
    l0 = choices == 2
    w1 = wts["experts_inter" if l0 else "w1"]
    w2 = wts["experts_out" if l0 else "w2"]
    rows = n_exp * cap
    with Scope(nc, name) as S:
        S.noop = S.sb("noop", [P, TILES]) if l0 else None
        if l0:
            r = route(nc, S, name + "r", c, wts["router_w"], wts["router_b"], True, 2, cap, dropped_expert=NE - 1)
        else:
            r = route(nc, S, name + "r", c, wts["wg"], None, False, 1, cap)
        slot_i = [S.sb(f"slot_i{j}", [P, TILES], U32) for j in range(choices)]
        back_i = [S.sb(f"back_i{j}", [P, TILES], U32) for j in range(choices)]
        back_f = S.sb("back_f", [P, TILES])
        w1_sb, w2_sb = S.sb("w1", [P, 2, KC, HID]), S.sb("w2", [P, 2, HC, DM])
        b1_sb = None if l0 else S.sb("b1", [P, NE, HC])
        b2_sb = None if l0 else S.sb("b2", [1, NE, DM])
        if not l0:
            with Scope(nc, name + "b") as B:
                rawb = B.sb("rawb", [NE * HC, P])
                prepare(nc, name + "bt", c, [(rawb[:], wts["b1"].rearrange("e (c p) -> (e c) p", p=P))],
                                  [(b1_sb[:].rearrange("p e c -> p (e c)"), rawb[:])])
        xe = S.sb("xe", [P, 2, CTL, DM])
        xeT = S.sb("xeT", [P, 2, KC, cap])
        hT = S.sb("hT", [P, 2, HC, cap])
        ye = S.sb("ye", [P, 2, CTL, DM])
        back = S.sb("back", [P, 2, 4, DM])
        (index_ready, scattered, loaded0, loaded1, bias_loaded, stored0, stored1, xeT_ready, xeT_copied, h_ready, h_copied,
         y_ready, y_copied, added, step) = (S.sem(n) for n in (
             "index_ready", "scattered", "loaded0", "loaded1", "bias_loaded", "stored0", "stored1", "xeT_ready", "xeT_copied",
             "h_ready", "h_copied", "y_ready", "y_copied", "added", "step"))
        loaded, stored = (loaded0, loaded1), (stored0, stored1)
        h_copied_d = S.sem("h_copied_d")
        gathered = [S.sem(f"gathered{n}") for n in range(8)]
        x_loaded = (S.sem("x_loaded0"), S.sem("x_loaded1"))
        t_ps = S.ps("t_ps", [P, KC, cap])
        h_ps = S.ps("h_ps", [P, 4, BANK])
        y_ps = S.ps("y_ps", [P, 2, BANK])

        def experts(eng, body):
            with eng.Fori(0, n_exp // 2) as g:
                for u in range(2):
                    body(g * 2 + u, u, g)
            if n_exp % 2:
                body(n_exp - 1, 0, n_exp // 2)

        with S.block() as block:
            @block.vector
            def _(dve):
                ch = Chain(dve, step)
                for j in range(choices):
                    ch.step(nc.vector.tensor_scalar(back_f[:], r["slot"][j][:], float(rows - 1), None, ALU.min))
                    ch.step(nc.vector.tensor_copy(back_i[j][:], back_f[:]))
                    ch.step(nc.vector.tensor_copy(slot_i[j][:], r["slot"][j][:]))
                    ch.step(nc.vector.tensor_tensor(r["weight"][j][:], r["weight"][j][:], r["keep"][j][:], ALU.mult))
                nc.vector.tensor_copy(back_f[:], back_f[:]).then_inc(index_ready, 1)

                base = ch.n

                def body(e, u, turn):
                    dve.wait_ge(xeT_ready, e + 1)
                    nc.vector.tensor_copy(xeT[:, u], t_ps[:]).then_inc(xeT_copied, 1)
                    for m in range(1, HC, 2):
                        dve.wait_ge(h_ready, e * HC + (m + 1))
                        if l0:
                            ins = nc.vector.tensor_scalar(hT[:, u, m, :], h_ps[:, m % 4, 0:cap], 0.0, None, ALU.max)
                        else:
                            ins = nc.vector.tensor_scalar(hT[:, u, m, :], h_ps[:, m % 4, 0:cap], b1_sb[:, bass.ds(e, 1), m], 0.0, ALU.add, ALU.max)
                        ins.then_inc(h_copied_d, 1)
                    dve.wait_ge(y_ready, e * CTL + 2)
                    dve.wait_ge(stored[u], 16 * turn + 16)
                    nc.vector.tensor_copy(ye[:, u], y_ps[:, :, 0:DM]).then_inc(y_copied, 1)

                experts(dve, body)
                for k in range(TILES * choices // 4):
                    for i in range(4):
                        t, j = (k * 4 + i) // choices, (k * 4 + i) % choices
                        dve.wait_ge(gathered[k % 2 * 4 + i], 16 * (k // 2 + 1))
                        ins = nc.vector.scalar_tensor_tensor(out=x[:, t, :], in0=back[:, k % 2, i, :], scalar=r["weight"][j][:, t:t + 1],
                                                             in1=x[:, t, :], op0=ALU.mult, op1=ALU.add)
                        ins.then_inc(added, 1)
                        dve.wait_ge(added, k * 4 + i + 1)
                if l0:
                    for t in range(TILES):
                        nc.vector.scalar_tensor_tensor(out=x[:, t, :], in0=xn[:, t, :], scalar=S.noop[:, t:t + 1],
                                                       in1=x[:, t, :], op0=ALU.mult, op1=ALU.add)

            @block.gpsimd
            def _(pool):
                pool.wait_ge(filled, 16)
                pool.wait_ge(index_ready, 1)
                for t in range(TILES):
                    for j in range(choices):
                        nc.gpsimd.indirect_dma_start(out=disp, out_offset=bass.IndirectOffsetOnAxis(ap=slot_i[j][:, t:t + 1], axis=0),
                                                     in_=xn[:, t, :], in_offset=None, bounds_check=rows - 1,
                                                     oob_is_err=False).then_inc(scattered, 16)
                pool.wait_ge(stored0, 16 * (1 + (n_exp + 1) // 2))
                pool.wait_ge(stored1, 16 * (1 + n_exp // 2))
                for k in range(TILES * choices // 4):
                    if k >= 2:
                        pool.wait_ge(added, 4 * (k - 1))
                    for i in range(4):
                        t, j = (k * 4 + i) // choices, (k * 4 + i) % choices
                        nc.gpsimd.indirect_dma_start(out=back[:, k % 2, i, :], out_offset=None, in_=eout,
                                                     in_offset=bass.IndirectOffsetOnAxis(ap=back_i[j][:, t:t + 1], axis=0),
                                                     bounds_check=rows - 1, oob_is_err=False).then_inc(gathered[k % 2 * 4 + i], 16)

            @block.sync
            def _(sp):
                sp.sem_inc(stored0, 16)
                sp.sem_inc(stored1, 16)
                if not l0:
                    sp.dma_start(b2_sb[0:1], wts["b2"][None, :, :]).then_inc(bias_loaded, 16)

                def weights(e, u, turn):
                    sp.dma_start(w1_sb[:, u], w1[bass.ds(e, 1)].rearrange("e (k p) n -> p (e k) n", p=P)).then_inc(loaded[u], 16)
                    sp.dma_start(w2_sb[:, u], w2[bass.ds(e, 1)].rearrange("e (k p) n -> p (e k) n", p=P)).then_inc(loaded[u], 16)

                def inputs(e, u, turn):
                    sp.dma_start(xe[:, u], disp[bass.ds(e * cap, cap), :].rearrange("(t p) d -> p t d", p=P)).then_inc(x_loaded[u], 16)

                weights(0, 0, 0)
                weights(1, 1, 0)
                sp.wait_ge(scattered, 16 * TILES * choices)
                inputs(0, 0, 0)
                inputs(1, 1, 0)
                with sp.Fori(0, n_exp // 2 - 1) as g:
                    for u in range(2):
                        sp.wait_ge(y_ready, (g * 2 + u + 1) * CTL)
                        weights(g * 2 + (u + 2), u, g)
                        inputs(g * 2 + (u + 2), u, g)
                if n_exp % 2:
                    sp.wait_ge(y_ready, (n_exp - 2) * CTL)
                    weights(n_exp - 1, 0, 0)
                    inputs(n_exp - 1, 0, 0)
                sp.wait_ge(stored0, 16 * (1 + (n_exp + 1) // 2))
                sp.wait_ge(stored1, 16 * (1 + n_exp // 2))

            @block.tensor
            def _(pe):
                def body(e, u, turn):
                    pe.wait_ge(x_loaded[u], 16 * turn + 16)
                    pe.wait_ge(xeT_copied, e + 1)
                    for k in range(KC):
                        for s in range(CTL):
                            ins = nc.tensor.transpose(t_ps[:, k, s * P:(s + 1) * P], xe[:, u, s, k * P:(k + 1) * P], ident[:])
                    ins.then_inc(xeT_ready, 1)
                    pe.wait_ge(loaded[u], 32 * turn + 32)
                    pe.wait_ge(xeT_copied, e + 2)
                    for m in range(HC):
                        pe.wait_ge(h_copied_d if m % 2 else h_copied, e * (HC // 2) + (m // 2 + 1))
                        for k in range(KC):
                            ins = nc.tensor.matmul(h_ps[:, m % 4, 0:cap], w1_sb[:, u, k, m * P:(m + 1) * P], xeT[:, u, k, :],
                                                   start=k == 0, stop=k == KC - 1)
                        ins.then_inc(h_ready, 1)
                    pe.wait_ge(h_copied, e * (HC // 2) + (HC // 2 + 2))
                    pe.wait_ge(h_copied_d, e * (HC // 2) + (HC // 2 + 2))
                    pe.wait_ge(y_copied, e + 1)
                    for s in range(CTL):
                        for m in range(HC):
                            ins = nc.tensor.matmul(y_ps[:, s, 0:DM], hT[:, u, m, s * P:(s + 1) * P], w2_sb[:, u, m, :],
                                                   start=m == 0, stop=m == HC - 1 and l0)
                        if not l0:
                            ins = nc.tensor.matmul(y_ps[:, s, 0:DM], ones[0:1, :], b2_sb[0:1, bass.ds(e, 1), :].rearrange("o e n -> o (e n)"), start=False, stop=True)
                        ins.then_inc(y_ready, 1)

                pe.sem_inc(xeT_copied, 1)
                pe.sem_inc(h_copied, 2)
                pe.sem_inc(h_copied_d, 2)
                pe.sem_inc(y_copied, 1)
                if not l0:
                    pe.wait_ge(bias_loaded, 16)
                experts(pe, body)

            @block.scalar
            def _(act):
                def body(e, u, turn):
                    for m in range(0, HC, 2):
                        act.wait_ge(h_ready, e * HC + (m + 1))
                        bias = 0.0 if l0 else b1_sb[:, bass.ds(e, 1), m]
                        nc.scalar.activation(hT[:, u, m, :], h_ps[:, m % 4, 0:cap], ACT.Relu, bias=bias).then_inc(h_copied, 1)
                    act.wait_ge(y_copied, e + 2)
                    act.dma_start(eout[bass.ds(e * cap, cap), :].rearrange("(t p) d -> p t d", p=P), ye[:, u]).then_inc(stored[u], 16)

                experts(act, body)


ROUND = 1.5 * 2.0 ** 23
QMAX = 32767.0


def quantised_ffn(nc, name, c, wts):
    x, xn, xnT, ident, ones = c["x"], c["xn"], c["xnT"], c["ident"], c["ones"]
    FF = 768
    FC = FF // P
    QB = 32
    with Scope(nc, name) as S:
        wT = S.sb("wT", [P, 2, KC, FF])
        wdT = S.sb("wdT", [P, FC, DM])
        with Scope(nc, name + "w") as R:
            raw = R.sb("raw", [P, 3, FC * DM])
            q = R.sb("q", [P, 3, FC * DM])
            NB = 3 * FC * DM // QB
            peak, inv = R.sb("peak", [P, NB]), R.sb("inv", [P, NB])
            prepare(nc, name + "l", c, [
                (raw[:, 0].rearrange("p (t n) -> p t n", n=DM), wts["w_up"].rearrange("(t p) n -> p t n", p=P)),
                (raw[:, 1].rearrange("p (t n) -> p t n", n=DM), wts["w_gate"].rearrange("(t p) n -> p t n", p=P)),
                (raw[:, 2].rearrange("p (t n) -> p t n", n=FF), wts["w_down"].rearrange("(t p) n -> p t n", p=P))], [])
            step = R.sem("step")
            with R.block() as block:
                @block.vector
                def _(dve):
                    ch, v = Chain(dve, step), nc.vector
                    blocks = raw[:].rearrange("p a (b k) -> p (a b) k", k=QB)
                    qb = q[:].rearrange("p a (b k) -> p (a b) k", k=QB)
                    ch.step(v.tensor_reduce(peak[:], blocks, AX, ALU.max, apply_absolute_value=True))
                    ch.step(v.tensor_scalar(peak[:], peak[:], 1.0 / 7.0, 1e-12, ALU.mult, ALU.max))
                    ch.step(v.reciprocal(inv[:], peak[:]))
                    ch.step(v.tensor_tensor(qb, blocks, inv[:, :, None].to_broadcast([P, NB, QB]), ALU.mult))
                    ch.step(v.tensor_scalar(q[:], q[:], ROUND, ROUND, ALU.add, ALU.subtract))
                    ch.step(v.tensor_scalar(q[:], q[:], -8.0, 7.0, ALU.max, ALU.min))
                    ch.step(v.tensor_tensor(qb, qb, peak[:, :, None].to_broadcast([P, NB, QB]), ALU.mult))
            jobs = []
            for n in range(2):
                for t in range(FC):
                    for k in range(KC):
                        jobs.append((wT[:, n, k, t * P:(t + 1) * P], q[:, n, t * DM + k * P:t * DM + (k + 1) * P]))
            for t in range(KC):
                for k in range(FC):
                    jobs.append((wdT[:, k, t * P:(t + 1) * P], q[:, 2, t * FF + k * P:t * FF + (k + 1) * P]))
            prepare(nc, name + "t", c, [], jobs)

        up, gate = S.sb("up", [P, FC, TOK]), S.sb("gate", [P, FC, TOK])
        scratch = xn[:].rearrange("p t n -> p (t n)").rearrange("p (u n) -> p u n", u=2)
        QN = 5
        peaks = S.sb("peaks", [P, QN, FC])
        peak = S.sb("peak", [P, QN])
        row = S.sb("row", [1, QN, 2])
        scale = S.sb("scale", [P, QN, 2])
        ff_ps = S.ps("ff_ps", [P, 4, BANK])
        r_ps = S.ps("r_ps", [P, BANK])
        y_ps = S.ps("y_ps", [P, 2, BANK])
        (step, peak_ready, row_ps_ready, row_ready, all_ready, x_quantised, ff_ready, ff_copied, rounded, sig_ready, o_ready,
         y_ready, y_added) = (S.sem(n) for n in ("step", "peak_ready", "row_ps_ready", "row_ready", "all_ready", "x_quantised", "ff_ready",
                                                 "ff_copied", "rounded", "sig_ready", "o_ready", "y_ready", "y_added"))
        with S.block() as block:
            @block.vector
            def _(dve):
                ch, v = Chain(dve, step), nc.vector

                def find_scale(n, cols):
                    v.tensor_reduce(peak[:, n:n + 1], peaks[:, n, 0:cols], AX, ALU.max).then_inc(peak_ready, 1)
                    dve.wait_ge(row_ps_ready, n + 1)
                    ch.step(v.tensor_reduce(row[0:1, n, 0:1], r_ps[0:1, 0:P], AX, ALU.max))
                    ch.step(v.tensor_scalar(row[0:1, n, 0:1], row[0:1, n, 0:1], 1.0 / QMAX, 1e-12, ALU.mult, ALU.max))
                    v.reciprocal(row[0:1, n, 1:2], row[0:1, n, 0:1]).then_inc(row_ready, 1)
                    dve.wait_ge(all_ready, n + 1)
                    ch.step(v.tensor_copy(scale[:, n, :], r_ps[:, 256:258]))

                def quantise(n, a):
                    ch.step(v.tensor_scalar(a, a, scale[:, n, 1:2], ROUND, ALU.mult, ALU.add))
                    return v.tensor_scalar(a, a, ROUND, scale[:, n, 0:1], ALU.subtract, ALU.mult)

                ch.step(v.tensor_reduce(peaks[:, 0, 0:1], xnT[:].rearrange("p k n -> p (k n)"), AX, ALU.max, apply_absolute_value=True))
                find_scale(0, 1)
                quantise(0, xnT[:].rearrange("p k n -> p (k n)")).then_inc(x_quantised, 1)
                for n, a in enumerate((up, gate)):
                    for m in range(FC):
                        dve.wait_ge(ff_copied, (n * FC + m + 1) * NBLK)
                        ch.step(v.tensor_reduce(peaks[:, 1 + n, m:m + 1], a[:, m, :], AX, ALU.max, apply_absolute_value=True))
                    find_scale(1 + n, FC)
                    for m in range(FC):
                        quantise(1 + n, a[:, m, :]).then_inc(rounded, 1)
                for m in range(FC):
                    s = scratch[:, m % 2, :]
                    dve.wait_ge(sig_ready, m + 1)
                    dve.wait_ge(rounded, 2 * FC)
                    ch.step(v.tensor_scalar(s, s, 65536.0, ROUND, ALU.mult, ALU.add))
                    ch.step(v.tensor_scalar(s, s, ROUND, 0.0, ALU.subtract, ALU.max))
                    ch.step(v.tensor_scalar(s, s, 65535.0, 1.0 / 65536.0, ALU.min, ALU.mult))
                    v.tensor_tensor(gate[:, m, :], gate[:, m, :], s, ALU.mult).then_inc(rounded, 1)
                    dve.wait_ge(rounded, 2 * FC + m + 1)
                    ch.step(v.tensor_reduce(peaks[:, 3, m:m + 1], gate[:, m, :], AX, ALU.max, apply_absolute_value=True))
                find_scale(3, FC)
                for m in range(FC):
                    ch.step(quantise(3, gate[:, m, :]))
                    ch.step(v.tensor_tensor(up[:, m, :], up[:, m, :], gate[:, m, :], ALU.mult))
                    ch.step(v.tensor_reduce(peaks[:, 4, m:m + 1], up[:, m, :], AX, ALU.max, apply_absolute_value=True))
                find_scale(4, FC)
                for m in range(FC):
                    quantise(4, up[:, m, :]).then_inc(o_ready, 1)
                with dve.Fori(0, TILES // 2) as g:
                    for u in range(2):
                        dve.wait_ge(y_ready, g * 2 + (u + 1))
                        v.tensor_tensor(x[:, g * 2 + u, :], x[:, g * 2 + u, :], y_ps[:, u, 0:DM], ALU.add).then_inc(y_added, 1)

            @block.tensor
            def _(pe):
                def share_peak(n):
                    pe.wait_ge(peak_ready, n + 1)
                    nc.tensor.transpose(r_ps[0:1, 0:P], peak[:, n:n + 1], ident[:]).then_inc(row_ps_ready, 1)
                    pe.wait_ge(row_ready, n + 1)
                    nc.tensor.matmul(r_ps[:, 256:258], ones[0:1, :], row[0:1, n, :], start=True, stop=True).then_inc(all_ready, 1)

                share_peak(0)
                pe.wait_ge(x_quantised, 1)
                for n in range(2):
                    for m in range(FC):
                        for b in range(NBLK):
                            j = (n * FC + m) * NBLK + b
                            if j >= 4:
                                pe.wait_ge(ff_copied, j - 3)
                            for k in range(KC):
                                ins = nc.tensor.matmul(ff_ps[:, j % 4, :], wT[:, n, k, m * P:(m + 1) * P], xnT[:, k, b * BANK:(b + 1) * BANK],
                                                       start=k == 0, stop=k == KC - 1)
                            ins.then_inc(ff_ready, 1)
                    share_peak(1 + n)
                share_peak(3)
                share_peak(4)
                pe.wait_ge(o_ready, FC)
                for t in range(TILES):
                    if t >= 2:
                        pe.wait_ge(y_added, t - 1)
                    for m in range(FC):
                        ins = nc.tensor.matmul(y_ps[:, t % 2, 0:DM], up[:, m, t * P:(t + 1) * P], wdT[:, m, :], start=m == 0, stop=m == FC - 1)
                    ins.then_inc(y_ready, 1)

            @block.scalar
            def _(act):
                NT = FC * NBLK
                for j in range(2 * NT):
                    act.wait_ge(ff_ready, j + 1)
                    a, i = (up, gate)[j // NT], j % NT
                    nc.scalar.copy(a[:, i // NBLK, i % NBLK * BANK:(i % NBLK + 1) * BANK], ff_ps[:, j % 4, :]).then_inc(ff_copied, 1)
                for m in range(FC):
                    act.wait_ge(rounded, FC + m + 1)
                    if m >= 2:
                        act.wait_ge(rounded, 2 * FC + m - 1)
                    nc.scalar.activation(scratch[:, m % 2, :], gate[:, m, :], ACT.Sigmoid).then_inc(sig_ready, 1)


def state_space(nc, name, c, wts):
    x, xn, xnT, ident = c["x"], c["xn"], c["xnT"], c["ident"]
    NS = 64
    ROUNDS = 9
    with Scope(nc, name) as S:
        bT = S.sb("bT", [P, 2, KC, P])
        cT = S.sb("cT", [P, DM])
        pw = S.sb("pw", [P, 2, 2, P])
        gb = S.sb("gb", [P, 2, DM])
        with Scope(nc, name + "w") as R:
            rawb, rawc = R.sb("rawb", [NS, DM]), R.sb("rawc", [P, KC, 2, NS])
            zeroed = R.sem("zeroed")
            with R.block() as block:
                @block.vector
                def _(dve):
                    nc.vector.memset(bT[:], 0.0)
                    nc.vector.memset(pw[:], 0.0)
            loads = [(rawb[:], wts["B"]), (pw[0:NS, 0, 0, 0:NS], wts["A"]), (pw[NS:P, 0, 0, NS:P], wts["A"])]
            loads += [(rawc[:, :, n, :], wts["C"].rearrange("(k p) n -> p k n", p=P)) for n in range(2)]
            loads += [(gb[:, j, :], wts[g][None, :].to_broadcast([P, DM])) for j, g in enumerate(("gamma", "beta"))]
            jobs = [(bT[:, h, k, h * NS:(h + 1) * NS], rawb[:, k * P:(k + 1) * P]) for h in range(2) for k in range(KC)]
            jobs += [(cT[:, k * P:(k + 1) * P], rawc[:, k].rearrange("p a n -> p (a n)")) for k in range(KC)]
            jobs += [(pw[:, 0, 1, :], pw[:, 0, 0, :])]
            prepare(nc, name + "t", c, loads, jobs)

        X = S.sb("X", [P, 2, SEQ])
        u_ps = S.ps("u_ps", [P, 2, BANK])
        p_ps = S.ps("p_ps", [P, 2, BANK])
        y_ps = S.ps("y_ps", [P, 4, BANK])
        u_ready, added, p_ready, p_copied, y_ready, y_free = (S.sem(n) for n in ("u_ready", "added", "p_ready", "p_copied", "y_ready", "y_free"))
        with S.block() as block:
            @block.tensor
            def _(pe):
                for bb in range(2):
                    for h in range(2):
                        for k in range(KC):
                            ins = nc.tensor.matmul(u_ps[:, bb, :], bT[:, h, k, :], xnT[:, k, (2 * h + bb) * SEQ:(2 * h + bb + 1) * SEQ],
                                                   start=h == 0 and k == 0, stop=h == 1 and k == KC - 1)
                ins.then_inc(u_ready, 1)
                for r in range(ROUNDS):
                    s, i = 1 << r, r % 2
                    pe.wait_ge(added, r + 1)
                    if r:
                        pe.wait_ge(p_copied, r)
                    for bb in range(2):
                        ins = nc.tensor.matmul(u_ps[:, bb, 0:SEQ - s], pw[:, i, 1, :], X[:, bb, 0:SEQ - s], start=True, stop=True)
                    ins.then_inc(u_ready, 1)
                    if r + 1 < ROUNDS:
                        nc.tensor.matmul(p_ps[:, 0, 0:P], pw[:, i, 1, :], pw[:, i, 0, :], start=True, stop=True)
                        nc.tensor.matmul(p_ps[:, 1, 0:P], pw[:, i, 0, :], pw[:, i, 1, :], start=True, stop=True).then_inc(p_ready, 1)
                pe.wait_ge(added, ROUNDS + 1)
                for t in range(TILES):
                    b, q = t // QT, t % QT
                    h, bb = b // 2, b % 2
                    if t >= 4:
                        pe.wait_ge(y_free, t - 3)
                    nc.tensor.matmul(y_ps[:, t % 4, 0:DM], X[h * NS:(h + 1) * NS, bb, q * P:(q + 1) * P], cT[h * NS:(h + 1) * NS, :],
                                     start=True, stop=True).then_inc(y_ready, 1)

            @block.vector
            def _(dve):
                dve.wait_ge(u_ready, 1)
                nc.vector.tensor_copy(X[:], u_ps[:]).then_inc(added, 1)
                for r in range(ROUNDS):
                    s = 1 << r
                    dve.wait_ge(u_ready, r + 2)
                    nc.vector.tensor_tensor(X[:, :, s:], X[:, :, s:], u_ps[:, :, 0:SEQ - s], ALU.add).then_inc(added, 1)

            @block.scalar
            def _(act):
                for r in range(ROUNDS - 1):
                    act.wait_ge(p_ready, r + 1)
                    nc.scalar.copy(pw[:, (r + 1) % 2], p_ps[:, :, 0:P]).then_inc(p_copied, 1)
                for t in range(TILES):
                    act.wait_ge(y_ready, t + 1)
                    nc.scalar.activation(xn[:, t, :], y_ps[:, t % 4, 0:DM], ACT.Gelu).then_inc(y_free, 1)

        st, mean, rstd, tmp = S.sb("st", [P, TILES, 6]), S.sb("mean", [P, TILES]), S.sb("rstd", [P, TILES]), S.sb("tmp", [P, TILES])
        base = S.sb("base", [P, TILES, DM])
        low = S.sb("low", [P, TILES, DM])
        finite = S.sb("finite", [P, TILES, DM], I32)
        step, var_ready, std_ready = S.sem("step"), S.sem("var_ready"), S.sem("std_ready")
        with S.block() as block:
            @block.vector
            def _(dve):
                ch, v = Chain(dve, step), nc.vector
                with dve.Fori(0, TILES) as i:
                    v.bn_stats(st[:, i, :], xn[:, i, :]).then_inc(step, 1)
                ch.n += TILES
                dve.wait_ge(step, ch.n)
                row_stats_to_affine(nc, ch, st, mean[:], rstd[:], tmp[:], DM // 2)
                v.tensor_copy(tmp[:], rstd[:]).then_inc(var_ready, 1)
                dve.wait_ge(std_ready, 1)
                ch.step(v.reciprocal(rstd[:], tmp[:]))
                with dve.Fori(0, TILES) as i:
                    v.tensor_scalar(xn[:, i, :], xn[:, i, :], mean[:, bass.ds(i, 1)], rstd[:, bass.ds(i, 1)], ALU.subtract, ALU.mult).then_inc(step, 1)
                ch.n += TILES
                dve.wait_ge(step, ch.n)
                ch.step(v.tensor_tensor(xn[:], xn[:], gb[:, None, 0, :].to_broadcast([P, TILES, DM]), ALU.mult))
                ch.step(v.tensor_tensor(xn[:], xn[:], gb[:, None, 1, :].to_broadcast([P, TILES, DM]), ALU.add))
                ch.step(v.tensor_scalar(base[:], xn[:], 0.0, 1e6, ALU.max, ALU.min))
                ch.step(v.tensor_scalar(low[:], xn[:], 0.0, -1e6, ALU.min, ALU.max))
                ch.step(v.tensor_tensor(base[:], base[:], low[:], ALU.add))
                ch.step(v.tensor_scalar(finite[:], xn[:], 0.0, 0.0, ALU.mult, ALU.is_equal))
                ch.step(v.copy_predicated(base[:], finite[:], xn[:]))
                v.tensor_tensor(x[:], x[:], base[:], ALU.add)

            @block.scalar
            def _(act):
                act.wait_ge(var_ready, 1)
                nc.scalar.activation(tmp[:], tmp[:], ACT.Sqrt).then_inc(std_ready, 1)


def selective_scan(nc, name, c, wts):
    x, xn, xnT, ident, ones = c["x"], c["xn"], c["xnT"], c["ident"], c["ones"]
    DI, NST, TAPS = 512, 16, 4
    C4 = DI // P
    NX = 2 * NST + 1
    with Scope(nc, name) as S:
        winT = S.sb("winT", [P, KC, 2 * DI])
        wxT = S.sb("wxT", [P, C4, NX])
        woutT = S.sb("woutT", [P, C4, DM])
        wdt = S.sb("wdt", [NX, DI])
        cols = S.sb("cols", [P, 5, C4])
        conv_w = S.sb("conv_w", [P, C4, TAPS])
        A = S.sb("A", [P, NST])
        sel = S.sb("sel", [P, 2 * NST, P], BF16)
        hmax = S.sb("hmax", [P, BATCH * NST + 1])
        flag_f, flag = S.sb("flag_f", [P, 2]), S.sb("flag", [P, 1], I32)
        with Scope(nc, name + "w") as R:
            raw_in, raw_out, raw_x = R.sb("raw_in", [P, 8, DM]), R.sb("raw_out", [P, KC, DI]), R.sb("raw_x", [NX, DI])
            made, a_ready = R.sem("made"), R.sem("a_ready")
            loads = [(raw_in[:], wts["W_in"].rearrange("(t p) d -> p t d", p=P)), (raw_out[:], wts["W_out"].rearrange("(t p) d -> p t d", p=P)),
                     (raw_x[0:NX - 1], wts["W_x"][1:NX]), (raw_x[NX - 1:NX], wts["W_x"][0:1]),
                     (wdt[NX - 1:NX], wts["W_dt"].rearrange("d o -> o d")),
                     (conv_w[:], wts["conv_w"].rearrange("(c p) o k -> p c (o k)", p=P)),
                     (A[:], wts["A_log"][None, :].to_broadcast([P, NST]))]
            for j, n in enumerate(("conv_b", "b_dt", "D_param", "ln_g", "ln_b")):
                loads.append((cols[:, j, :], wts[n].rearrange("(c p) -> p c", p=P)))
            jobs = [(winT[:, k, t * P:(t + 1) * P], raw_in[:, t, k * P:(k + 1) * P]) for t in range(8) for k in range(KC)]
            jobs += [(wxT[:, k, :], raw_x[:, k * P:(k + 1) * P]) for k in range(C4)]
            jobs += [(woutT[:, k, t * P:(t + 1) * P], raw_out[:, t, k * P:(k + 1) * P]) for t in range(KC) for k in range(C4)]
            with nc.allow_non_contiguous_dma(reason="per-channel vectors"):
                prepare(nc, name + "t", c, loads, jobs)
            with R.block() as block:
                @block.gpsimd
                def _(pool):
                    ch = Chain(pool, made)
                    ch.step(nc.gpsimd.memset(sel[:], 0.0))
                    for n in range(3):
                        ch.step(nc.gpsimd.affine_select(out=sel[:], in_=sel[:], compare_op=ALU.not_equal, fill=1.0, base=-2 * NST * n,
                                                        pattern=[[-1, 2 * NST], [0, P]], channel_multiplier=1))

                @block.vector
                def _(dve):
                    nc.vector.memset(hmax[:], 0.0)
                    nc.vector.tensor_scalar(A[:], A[:], 5.0, None, ALU.min).then_inc(a_ready, 1)
                    dve.wait_ge(a_ready, 2)
                    nc.vector.tensor_scalar(A[:], A[:], -1.0, None, ALU.mult)

                @block.scalar
                def _(act):
                    act.wait_ge(a_ready, 1)
                    nc.scalar.activation(A[:], A[:], ACT.Exp).then_inc(a_ready, 1)

        T = {n: S.sb(n, shape) for n, shape in dict(
            xb=[P, KC, SEQ], xc=[P, C4, SEQ + TAPS - 1], zs=[P, C4, SEQ], u=[P, C4, SEQ], v=[P, C4, SEQ], dt=[P, C4, SEQ],
            xd=[NX, SEQ], dA=[P, 2, C4, SEQ], w=[P, 2, C4, SEQ], h=[P, 2, C4, SEQ], rs=[P, SEQ]).items()}
        T["xd3"] = S.sb("xd3", [P, SEQ], BF16)
        big, b_ps, c_ps = S.ps("big", [P, 4, BANK]), S.ps("b_ps", [P, 2, BANK]), S.ps("c_ps", [P, 2, BANK])
        one_pass = dict(nc=nc, c=c, T=T, ps=(big, b_ps, c_ps), w=(winT, wxT, woutT, wdt, cols, conv_w, A, sel), hmax=hmax,
                        dims=(DI, NST, TAPS, C4, NX))
        with S.block() as block:
            @block.vector
            def _(dve):
                nc.vector.memset(T["xc"][:], 0.0)
                nc.vector.memset(T["xd3"][:], 0.0)
        with Scope(nc, name + "f") as F:
            scan_pass(F, flag=None, **one_pass)
        with Scope(nc, name + "g") as F:
            step, summed, bad = F.sem("step"), F.sem("summed"), F.sem("bad")
            with F.block() as block:
                @block.vector
                def _(dve):
                    ch, v = Chain(dve, step), nc.vector
                    ch.step(v.tensor_reduce(flag_f[:, 0:1], A[:], AX, ALU.max, apply_absolute_value=True))
                    ch.step(v.tensor_scalar(flag_f[:, 0:1], flag_f[:, 0:1], 1.99, 1000.0, ALU.is_gt, ALU.mult))
                    ch.step(v.tensor_copy(hmax[:, BATCH * NST:], flag_f[:, 0:1]))
                    ch.step(v.tensor_reduce(flag_f[:, 0:1], hmax[:], AX, ALU.max))
                    v.tensor_scalar(flag_f[:, 1:2], flag_f[:, 0:1], 69.9, None, ALU.is_gt).then_inc(bad, 1)
                    dve.wait_ge(summed, 1)
                    ch.step(v.tensor_scalar(flag[:], b_ps[:, 0, 0:1], 0.5, None, ALU.is_gt))

                @block.tensor
                def _(pe):
                    pe.wait_ge(bad, 1)
                    nc.tensor.matmul(b_ps[:, 0, 0:1], ones[:], flag_f[:, 1:2], start=True, stop=True).then_inc(summed, 1)
        with Scope(nc, name + "s") as F:
            scan_pass(F, flag=flag, **one_pass)
        with S.block() as block:
            @block.vector
            def _(dve):
                nc.vector.tensor_tensor(x[:], x[:], xn[:], ALU.add)


def scan_pass(F, nc, c, T, ps, w, hmax, dims, flag):
    xn, xnT, ident, ones = c["xn"], c["xnT"], c["ident"], c["ones"]
    winT, wxT, woutT, wdt, cols, conv_w, A, sel = w
    big, b_ps, c_ps = ps
    DI, NST, TAPS, C4, NX = dims
    xb, xc, zs, u, v, dt, xd, dA, wd, h, xd3, rs = (T[n] for n in ("xb", "xc", "zs", "u", "v", "dt", "xd", "dA", "w", "h", "xd3", "rs"))
    y_sb, dtu = dA[:, 0], v
    CONV_B, B_DT, D_PAR, LN_G, LN_B = range(5)
    exact = flag is not None
    WIDE = [P, C4, SEQ]
    (xb_ready, xz_ready, xc_copied, z_done, conv_ready, u_ready, xd_ready, xd_copied, dt_ps_ready, dt_copied, sp_ready, dt_ready,
     brow_ready, crow_ready, w_ready, clipped, dA_ready, scan_done, hC_ready, acc_done, y_copied, mean_ready,
     yc_ready, sq_ready, var_ready, v_ready, std_ready, yf_ready, delta_ready, delta_copied, dstep, astep, parts_ready) = (F.sem(n) for n in (
         "xb_ready", "xz_ready", "xc_copied", "z_done", "conv_ready", "u_ready", "xd_ready", "xd_copied", "dt_ps_ready",
         "dt_copied", "sp_ready", "dt_ready", "brow_ready", "crow_ready", "w_ready", "clipped", "dA_ready", "scan_done",
         "hC_ready", "acc_done", "y_copied", "mean_ready", "yc_ready", "sq_ready", "var_ready", "v_ready",
         "std_ready", "yf_ready", "delta_ready", "delta_copied", "dstep", "astep", "parts_ready"))

    def run(eng, program):
        if not exact:
            program()
            return
        with eng.If(eng.value_load(flag[0:1, 0:1], min_val=0, max_val=1) != 0):
            program()

    with F.block() as block:
        @block.gpsimd
        def _(pool):
            def program():
                nc.gpsimd.tensor_copy(xb[:], xnT[:, :, 0:SEQ]).then_inc(xb_ready, 1)
                with pool.Fori(1, BATCH) as b:
                    pool.wait_ge(xz_ready, b * (2 * C4))
                    nc.gpsimd.tensor_copy(xb[:], xnT[:, :, bass.ds(b * SEQ, SEQ)]).then_inc(xb_ready, 1)
            run(pool, program)

        @block.tensor
        def _(pe):
            def program():
                pe.sem_inc(acc_done, 2)
                with pe.Fori(0, BATCH) as b:
                    pe.wait_ge(xb_ready, b + 1)
                    pe.wait_ge(delta_copied, b * QT + 1)
                    for m in range(2 * C4):
                        if m >= C4:
                            pe.wait_ge(xc_copied, b * C4 + (m - C4 + 1))
                        for k in range(KC):
                            ins = nc.tensor.matmul(big[:, m % 4, :], winT[:, k, m * P:(m + 1) * P], xb[:, k, :], start=k == 0, stop=k == KC - 1)
                        ins.then_inc(xz_ready, 1)
                    pe.wait_ge(u_ready, b * C4 + C4)
                    pe.wait_ge(hC_ready, b * NST + 2)
                    for k in range(C4):
                        ins = nc.tensor.matmul(c_ps[0:NX, 0, :], wxT[:, k, :], u[:, k, :], start=k == 0, stop=k == C4 - 1)
                    ins.then_inc(xd_ready, 1)
                    pe.wait_ge(xd_copied, b + 1)
                    pe.wait_ge(z_done, b * C4 + C4)
                    for k in range(C4):
                        ins = nc.tensor.matmul(big[:, k, :], wdt[NX - 1:NX, k * P:(k + 1) * P], xd[NX - 1:NX, :], start=True, stop=True)
                    ins.then_inc(dt_ps_ready, 1)
                    pe.wait_ge(dt_copied, b + 1)

                    pe.wait_ge(parts_ready, b + 1)

                    def b_row(n):
                        pe.wait_ge(w_ready, b * NST + (n + 1))
                        nc.tensor.matmul(b_ps[:, n % 2, :], sel[:, n, :], xd3[:, :], start=True, stop=True).then_inc(brow_ready, 1)

                    def c_row(n):
                        pe.wait_ge(hC_ready, b * NST + (n + 1))
                        nc.tensor.matmul(c_ps[:, n % 2, :], sel[:, NST + n, :], xd3[:, :], start=True, stop=True).then_inc(crow_ready, 1)

                    for n in range(2):
                        b_row(n)
                        c_row(n)
                    for n in range(NST):
                        if n + 2 < NST:
                            b_row(n + 2)
                            c_row(n + 2)
                        pe.wait_ge(hC_ready, b * NST + (n + 3))
                        for k in range(C4):
                            ins = nc.tensor.matmul(big[:, k, :], ident[:], dA[:, n % 2, k, :], start=n == 0, stop=n == NST - 1)
                        ins.then_inc(acc_done, 1)
                    pe.wait_ge(y_copied, b + 1)
                    for k in range(C4):
                        ins = nc.tensor.matmul(b_ps[:, 0, :], ones[:], y_sb[:, k, :], start=k == 0, stop=k == C4 - 1)
                    ins.then_inc(mean_ready, 1)
                    pe.wait_ge(sq_ready, b + 1)
                    for k in range(C4):
                        ins = nc.tensor.matmul(b_ps[:, 1, :], ones[:], wd[:, 0, k, :], start=k == 0, stop=k == C4 - 1)
                    ins.then_inc(var_ready, 1)
                    pe.wait_ge(yf_ready, b + 1)
                    for q in range(QT):
                        for k in range(C4):
                            ins = nc.tensor.matmul(big[:, q, 0:DM], y_sb[:, k, q * P:(q + 1) * P], woutT[:, k, :], start=k == 0, stop=k == C4 - 1)
                        ins.then_inc(delta_ready, 1)
            run(pe, program)

        @block.vector
        def _(dve):
            V = nc.vector
            def program():
                dve.sem_inc(w_ready, 2)
                dve.sem_inc(scan_done, 2)
                dve.sem_inc(hC_ready, 2)
                count = {}

                def element(b, per):
                    ch = Chain(dve, dstep, b * per)
                    for m in range(C4):
                        dve.wait_ge(xz_ready, b * (2 * C4) + (m + 1))
                        V.tensor_copy(xc[:, m, TAPS - 1:], big[:, m, :]).then_inc(xc_copied, 1)
                        dve.wait_ge(xc_copied, b * C4 + (m + 1))
                        ch.step(V.tensor_scalar(v[:, m], xc[:, m, 0:SEQ], conv_w[:, m, 0:1], cols[:, CONV_B, m:m + 1], ALU.mult, ALU.add))
                        for k in range(1, TAPS):
                            ins = V.scalar_tensor_tensor(out=v[:, m], in0=xc[:, m, k:k + SEQ], scalar=conv_w[:, m, k:k + 1], in1=v[:, m],
                                                         op0=ALU.mult, op1=ALU.add)
                            if k < TAPS - 1:
                                ch.step(ins)
                        ins.then_inc(conv_ready, 1)
                    dve.wait_ge(xd_ready, b + 1)
                    V.tensor_copy(xd[:], c_ps[0:NX, 0, :]).then_inc(xd_copied, 1)
                    dve.wait_ge(xd_copied, b + 1)
                    NR = 2 * NST
                    ch.step(V.tensor_copy(xd3[0:NR], xd[0:NR]))
                    ch.step(V.tensor_tensor(xd[0:NR], xd[0:NR], xd3[0:NR], ALU.subtract))
                    ch.step(V.tensor_copy(xd3[NR:2 * NR], xd[0:NR]))
                    ch.step(V.tensor_copy(xd3[2 * NR:3 * NR], xd[0:NR]))
                    ch.step(V.tensor_tensor(xd[0:NR], xd[0:NR], xd3[2 * NR:3 * NR], ALU.subtract))
                    V.tensor_copy(xd3[2 * NR:3 * NR], xd[0:NR]).then_inc(parts_ready, 1)
                    dve.wait_ge(dt_ps_ready, b + 1)
                    for m in range(C4):
                        ins = V.tensor_scalar(v[:, m], big[:, m, :], cols[:, B_DT, m:m + 1], None, ALU.add)
                    ins.then_inc(dt_copied, 1)
                    dve.wait_ge(sp_ready, b + 1)
                    ch.step(V.scalar_tensor_tensor(out=dt[:].rearrange("p c t -> p (c t)"), in0=v[:].rearrange("p c t -> p (c t)"), scalar=0.0,
                                                   in1=wd[:, 0].rearrange("p c t -> p (c t)"), op0=ALU.max, op1=ALU.add))
                    V.tensor_scalar(dt[:], dt[:], 1e-4, 10.0, ALU.max, ALU.min).then_inc(dt_ready, 1)
                    dve.wait_ge(dt_ready, b + 1)
                    ch.step(V.tensor_tensor(dtu[:], dt[:], u[:], ALU.mult))

                    def drive(n):
                        dve.wait_ge(brow_ready, b * NST + (n + 1))
                        V.tensor_tensor(wd[:, n % 2], dtu[:], b_ps[:, n % 2, None, :].to_broadcast(WIDE), ALU.mult).then_inc(w_ready, 1)
                        dve.wait_ge(w_ready, b * NST + (n + 3))
                        V.tensor_scalar(wd[:, n % 2], wd[:, n % 2], 10.0, -10.0, ALU.min, ALU.max).then_inc(clipped, 1)

                    def scan(n):
                        hn, dAn, wn = h[:, n % 2], dA[:, n % 2], wd[:, n % 2]
                        dve.wait_ge(clipped, b * NST + (n + 1))
                        dve.wait_ge(dA_ready, b * NST + (n + 1))
                        if not exact:
                            V.tensor_tensor_scan(out=hn.rearrange("p c t -> p (c t)"), data0=dAn.rearrange("p c t -> p (c t)"),
                                                 data1=wn.rearrange("p c t -> p (c t)"), initial=0.0, op0=ALU.mult, op1=ALU.add).then_inc(scan_done, 1)
                            dve.wait_ge(scan_done, b * NST + (n + 3))
                            V.tensor_reduce(hmax[:, bass.ds(b * NST + n, 1)], hn[:, :, 0:SEQ:4], mybir.AxisListType.XY, ALU.max,
                                            apply_absolute_value=True)
                            return
                        ch.step(V.tensor_scalar(dAn, dAn, EXP_M20, None, ALU.max))
                        ch.step(V.tensor_copy(hn[:, :, 0], wn[:, :, 0]))
                        V.tensor_copy(rs[:, 0:1], rs[:, 0:1])
                        with dve.Fori(1, SEQ) as t:
                            done = (b * NST + n) * (3 * (SEQ - 1)) + (t - 1) * 3
                            V.tensor_tensor(hn[:, :, bass.ds(t, 1)], hn[:, :, bass.ds(t - 1, 1)], dAn[:, :, bass.ds(t, 1)], ALU.mult).then_inc(yc_step, 1)
                            dve.wait_ge(yc_step, done + 1)
                            V.tensor_tensor(hn[:, :, bass.ds(t, 1)], hn[:, :, bass.ds(t, 1)], wn[:, :, bass.ds(t, 1)], ALU.add).then_inc(yc_step, 1)
                            dve.wait_ge(yc_step, done + 2)
                            V.tensor_scalar(hn[:, :, bass.ds(t, 1)], hn[:, :, bass.ds(t, 1)], 100.0, -100.0, ALU.min, ALU.max).then_inc(yc_step, 1)
                            dve.wait_ge(yc_step, done + 3)
                        V.tensor_copy(rs[:, 0:1], rs[:, 0:1]).then_inc(scan_done, 1)
                        dve.wait_ge(scan_done, b * NST + (n + 3))

                    def weigh(n):
                        dve.wait_ge(crow_ready, b * NST + (n + 1))
                        V.tensor_tensor(dA[:, n % 2], h[:, n % 2], c_ps[:, n % 2, None, :].to_broadcast(WIDE), ALU.mult).then_inc(hC_ready, 1)

                    drive(0)
                    for n in range(NST):
                        if n + 1 < NST:
                            drive(n + 1)
                        scan(n)
                        weigh(n)
                    dve.wait_ge(mean_ready, b + 1)
                    for m in range(C4):
                        ins = V.scalar_tensor_tensor(out=y_sb[:, m, :], in0=b_ps[:, 0, :], scalar=-1.0 / DI, in1=y_sb[:, m, :], op0=ALU.mult, op1=ALU.add)
                    ins.then_inc(yc_ready, 1)
                    dve.wait_ge(var_ready, b + 1)
                    V.tensor_scalar(rs[:], b_ps[:, 1, :], 1.0 / DI, LN_EPS, ALU.mult, ALU.add).then_inc(v_ready, 1)
                    dve.wait_ge(std_ready, b + 1)
                    ch.step(V.reciprocal(rs[:], rs[:]))
                    ch.step(V.tensor_tensor(y_sb, y_sb, rs[:, None, :].to_broadcast(WIDE), ALU.mult))
                    for m in range(C4):
                        ch.step(V.tensor_scalar(y_sb[:, m, :], y_sb[:, m, :], cols[:, LN_G, m:m + 1], cols[:, LN_B, m:m + 1], ALU.mult, ALU.add))
                        ch.step(V.scalar_tensor_tensor(out=y_sb[:, m, :], in0=u[:, m, :], scalar=cols[:, D_PAR, m:m + 1], in1=y_sb[:, m, :],
                                                       op0=ALU.mult, op1=ALU.add))
                    V.tensor_tensor(y_sb, y_sb, zs[:], ALU.mult).then_inc(yf_ready, 1)
                    count["steps"] = ch.n

                per = C4 * (TAPS - 1) + 5 + 2 + 2 + 2 * C4 + (2 * NST if exact else 0)
                with dve.Fori(0, BATCH) as b:
                    element(b, per)
                assert count["steps"] == per, (count, per)
            yc_step = F.sem("exact_step") if exact else None
            run(dve, program)

        @block.scalar
        def _(act):
            E = nc.scalar

            def program():
                act.sem_inc(delta_copied, 1)
                with act.Fori(0, BATCH) as b:
                    for m in range(C4):
                        act.wait_ge(xz_ready, b * (2 * C4) + (C4 + m + 1))
                        E.activation(zs[:, m, :], big[:, m, :], ACT.Silu).then_inc(z_done, 1)
                    for m in range(C4):
                        act.wait_ge(conv_ready, b * C4 + (m + 1))
                        E.activation(u[:, m, :], v[:, m, :], ACT.Silu).then_inc(u_ready, 1)
                    act.wait_ge(dt_copied, b + 1)
                    E.activation(wd[:, 0], v[:], ACT.Abs).then_inc(astep, 1)
                    act.wait_ge(astep, b * 2 + 1)
                    E.activation(wd[:, 0], wd[:, 0], ACT.Exp, scale=-1.0).then_inc(astep, 1)
                    act.wait_ge(astep, b * 2 + 2)
                    E.activation(wd[:, 0], wd[:, 0], ACT.Ln, bias=1.0).then_inc(sp_ready, 1)
                    act.wait_ge(dt_ready, b + 1)
                    for n in range(NST):
                        act.wait_ge(acc_done, b * NST + (n + 1))
                        E.activation(dA[:, n % 2], dt[:], ACT.Exp, scale=A[:, n:n + 1]).then_inc(aexp, 1)
                        act.wait_ge(aexp, b * NST + (n + 1))
                        E.mul(dA[:, n % 2, :, 0], dA[:, n % 2, :, 0], 0.0).then_inc(dA_ready, 1)
                    act.wait_ge(acc_done, b * NST + (NST + 2))
                    act.wait_ge(scan_done, b * NST + (NST + 2))
                    E.copy(y_sb, big[:]).then_inc(y_copied, 1)
                    act.wait_ge(yc_ready, b + 1)
                    E.activation(wd[:, 0], y_sb, ACT.Square).then_inc(sq_ready, 1)
                    act.wait_ge(v_ready, b + 1)
                    E.activation(rs[:], rs[:], ACT.Sqrt).then_inc(std_ready, 1)
                    for q in range(QT):
                        act.wait_ge(delta_ready, b * QT + (q + 1))
                        E.copy(xn[:, b * QT + q, :], big[:, q, 0:DM]).then_inc(delta_copied, 1)
            aexp = F.sem("aexp")
            run(act, program)


EXP_M20 = 2.0611536224385579e-09


ATTN, XATTN, FFN = "attn", "xattn", "ffn"


def zero_fill_slots(nc, S, c):
    zeros = S.sb("zeros", [P, DM])
    zeroed = S.sem("zeroed")
    for n, n_exp in enumerate((7, 8)):
        rows = n_exp * (TOK // NE)
        disp = nc.dram_tensor(f"slots{n}", [rows, DM], F32, kind="Internal").ap()
        eout = nc.dram_tensor(f"expert_rows{n}", [rows, DM], F32, kind="Internal").ap()
        c[f"moe{n}"] = (disp, eout, S.sem(f"slots_zeroed{n}"))
    with S.block() as block:
        @block.vector
        def _(dve):
            nc.vector.memset(zeros[:], 0.0).then_inc(zeroed, 1)

        @block.scalar
        def _(act):
            act.wait_ge(zeroed, 1)
            for n in range(2):
                disp, _, filled = c[f"moe{n}"]
                act.dma_start(disp.rearrange("(t p) d -> p t d", p=P),
                              zeros[:, None, :].to_broadcast([P, disp.shape[0] // P, DM])).then_inc(filled, 16)


def decoder_kernel(nc, w, out, first=0, last=12):
    c = {}

    def of(prefix):
        return {n[len(prefix):]: ap for n, ap in w.items() if n.startswith(prefix)}

    def stage(n):
        return first <= n < last

    with Scope(nc, "g") as S:
        c["x"] = S.sb("x", [P, TILES, DM])
        c["xn"] = S.sb("xn", [P, TILES, DM])
        c["xnT"] = S.sb("xnT", [P, KC, TOK])
        setup_constants(nc, S, c)
        x_loaded, x_stored = S.sem("x_loaded"), S.sem("x_stored")
        x_dram = w["x"].rearrange("b (t p) d -> p (b t) d", p=P)
        out_dram = out.rearrange("b (t p) d -> p (b t) d", p=P)
        c["ctx_dram"] = w["ctx_768"].rearrange("b k c -> (b k) c").rearrange("(t p) c -> p t c", p=P)
        zero_fill_slots(nc, S, c)
        with S.block() as block:
            @block.sync
            def _(sp):
                for q in range(4):
                    sp.dma_start(c["x"][:, 4 * q:4 * q + 4, :], x_dram[:, 4 * q:4 * q + 4, :]).then_inc(x_loaded, 16)
                sp.wait_ge(x_loaded, 64)
        if stage(0):
            c["norm"] = ("l0a", None)
            self_attention(nc, "l0at", c, of("L0_attn_"), given=False, window=True)
        if stage(1):
            c["norm"] = ("l0b", None)
            cross_attention(nc, "l0x", c, of("L0_xattn_"), dh=64)
        if stage(2):
            c["norm"] = ("l0c", None)
            mixture(nc, "l0f", c, of("L0_ffn_"), 7, 2, *c["moe0"])
        if stage(3):
            c["norm"] = ("l1a", None)
            self_attention(nc, "l1at", c, of("L1_attn_"), given=True, window=False)
        if stage(4):
            c["norm"] = ("l1b", None)
            cross_attention(nc, "l1x", c, of("L1_xattn_"), dh=16, out_in=True)
        if stage(5):
            c["norm"] = ("l1c", None)
            mixture(nc, "l1f", c, of("L1_ffn_"), 8, 1, *c["moe1"])
        if stage(6):
            c["norm"] = ("l2a", None)
            selective_scan(nc, "l2s", c, of("L2_attn_"))
        if stage(7):
            l2x = of("L2_xattn_")
            c["norm"] = ("l2b", (l2x["g_x"], l2x["b_x"]))
            cross_attention(nc, "l2x", c, l2x, dh=64, norm_ctx=True)
        if stage(8):
            c["norm"] = ("l2c", None)
            quantised_ffn(nc, "l2f", c, of("L2_ffn_"))
        if stage(9):
            c["norm"] = ("l3a", None)
            state_space(nc, "l3s", c, of("L3_attn_"))
        if stage(10):
            c["norm"] = ("l3b", None)
            cross_attention(nc, "l3x", c, of("L3_xattn_"), dh=16, clamp=1e4)
        if stage(11):
            c["norm"] = ("l3c", None)
            gated_linear(nc, "l3f", c, of("L3_ffn_"), 100)
        with S.block() as block:
            @block.sync
            def _(sp):
                for q in range(4):
                    sp.dma_start(out_dram[:, 4 * q:4 * q + 4, :], c["x"][:, 4 * q:4 * q + 4, :]).then_inc(x_stored, 16)
                sp.wait_ge(x_stored, 64)
                for n in range(2):
                    sp.wait_ge(c[f"moe{n}"][2], 16)


_OUTS = [((4, 512, 256), "float32")]


def kernel(**inputs):
    import numpy as _np
    import concourse.bacc as _bacc
    from concourse import mybir as _mybir
    from concourse.bass_utils import run_bass_kernel_spmd as _run

    nc = _bacc.Bacc("TRN2", target_bir_lowering=False, num_devices=1)
    arrays, args = {}, {}
    for name, value in inputs.items():
        a = _np.ascontiguousarray(value)
        arrays[f"in_{name}_dram"] = a
        args[name] = nc.dram_tensor(f"in_{name}_dram", a.shape, _mybir.dt.from_np(a.dtype), kind="ExternalInput").ap()
    shape, dtype = _OUTS[0]
    out = nc.dram_tensor("out_0_dram", shape, _mybir.dt.from_np(_np.dtype(dtype)), kind="ExternalOutput").ap()
    decoder_kernel(nc, args, out)
    r = _run(nc, [arrays], core_ids=[0])
    return r.results[0]["out_0_dram"]
```

```python
from contextlib import ExitStack

import concourse.bass as bass
from concourse import mybir

F32 = mybir.dt.float32
BF16 = mybir.dt.bfloat16
I32 = mybir.dt.int32
U32 = mybir.dt.uint32
ACT = mybir.ActivationFunctionType
ALU = mybir.AluOpType
AX = mybir.AxisListType.X

P = 128
BATCH, SEQ, DM = 4, 512, 256
TOK = BATCH * SEQ
TILES = TOK // P
QT = SEQ // P
KC = DM // P
HEADS = 16
BANK = 512
NBLK = TOK // BANK
LN_EPS = 1e-5


class Scope:

    opened = []

    def __init__(self, nc, prefix):
        self.nc, self.prefix, self.stack, self.sems = nc, prefix, ExitStack(), []

    def __enter__(self):
        self.stack.__enter__()
        self.opened.append(self)
        return self

    def __exit__(self, *a):
        self.opened.pop()
        if len(self.opened) > 1:
            self.opened[-1].sems += self.sems
        elif self.sems:
            self.nc.clear_and_free_semaphores(self.sems)
            self.nc.all_engine_barrier()
        return self.stack.__exit__(*a)

    def sb(self, name, shape, dt=F32):
        return self.stack.enter_context(self.nc.sbuf_tensor(f"{self.prefix}_{name}", list(shape), dt))

    def ps(self, name, shape, dt=F32):
        return self.stack.enter_context(self.nc.psum_tensor(f"{self.prefix}_{name}", list(shape), dt))

    def sem(self, name):
        self.sems.append(self.nc.alloc_semaphore(f"{self.prefix}_{name}"))
        return self.sems[-1]

    def block(self):
        return self.nc.Block()


class Chain:

    def __init__(self, eng, sem, base=0):
        self.eng, self.sem, self.base, self.n = eng, sem, base, 0

    def step(self, ins):
        self.n += 1
        ins.then_inc(self.sem, 1)
        self.eng.wait_ge(self.sem, self.base + self.n)


def setup_constants(nc, S, c):
    c["ident"] = S.sb("ident", [P, P])
    c["ones"] = S.sb("ones", [P, P])
    made = S.sem("const_made")
    with S.block() as block:
        @block.gpsimd
        def _(pool):
            nc.gpsimd.memset(c["ident"][:], 0.0).then_inc(made, 1)
            nc.gpsimd.memset(c["ones"][:], 1.0).then_inc(made, 1)
            pool.wait_ge(made, 2)
            nc.gpsimd.affine_select(out=c["ident"][:], in_=c["ident"][:], compare_op=ALU.not_equal, fill=1.0,
                                    base=0, pattern=[[-1, P]], channel_multiplier=1).then_inc(made, 1)
            pool.wait_ge(made, 3)


def row_stats_to_affine(nc, ch, st, mean, rstd, tmp, half):
    ch.step(nc.vector.tensor_tensor(mean, st[:, :, 1], st[:, :, 4], ALU.add))
    ch.step(nc.vector.tensor_scalar(mean, mean, 0.5, None, ALU.mult))
    ch.step(nc.vector.tensor_tensor(tmp, st[:, :, 1], mean, ALU.subtract))
    ch.step(nc.vector.tensor_tensor(tmp, tmp, tmp, ALU.mult))
    ch.step(nc.vector.tensor_tensor(rstd, st[:, :, 2], st[:, :, 5], ALU.add))
    ch.step(nc.vector.tensor_scalar(rstd, rstd, 1.0 / (2 * half), LN_EPS, ALU.mult, ALU.add))
    ch.step(nc.vector.tensor_tensor(rstd, rstd, tmp, ALU.add))


WBANKS = 4


def issue_loads(nc, block, loads, loaded):
    @block.sync
    def _(sp):
        for dst, src in loads[0::2]:
            sp.dma_start(dst, src).then_inc(loaded[0], 16)
        if loads:
            sp.wait_ge(loaded[0], 16 * len(loads[0::2]))

    def from_act(act):
        for dst, src in loads[1::2]:
            act.dma_start(dst, src).then_inc(loaded[1], 16)
    return from_act


def turn_blocks(nc, pe, groups, pt, ident, loads, loaded, tr_ready, copied):
    if not groups:
        return
    for j in range(2):
        if loads[j::2]:
            pe.wait_ge(loaded[j], 16 * len(loads[j::2]))
    for g, group in enumerate(groups):
        if g >= WBANKS:
            n = len(copied)
            pe.wait_ge(copied[g % n], (g - WBANKS) // n + 1)
        for j, (dst, src) in enumerate(group):
            r, n = src.shape[0], src.shape[1]
            ins = nc.tensor.transpose(pt[0:n, g % WBANKS, j, 0:r], src, ident[0:r, 0:r])
        ins.then_inc(tr_ready, 1)


def copy_blocks(eng, copy, groups, pt, tr_ready, copied, first, stride):
    for g in range(first, len(groups), stride):
        eng.wait_ge(tr_ready, g + 1)
        for j, (dst, src) in enumerate(groups[g]):
            ps = pt[0:src.shape[1], g % WBANKS, j, 0:src.shape[0]]
            if len(dst.shape) == 3:
                ps = ps.rearrange("p (a b) -> p a b", b=dst.shape[2])
            ins = copy(dst, ps)
        ins.then_inc(copied, 1)


def prepare(nc, name, c, loads, jobs):
    groups = [jobs[j:j + 4] for j in range(0, len(jobs), 4)]
    if "norm" in c:
        normalise(nc, c, *c.pop("norm"), loads, groups)
        return
    with Scope(nc, name) as T:
        pt = T.ps("wt", [P, WBANKS, 4, P])
        loaded, tr_ready = [T.sem("loaded_sp"), T.sem("loaded_act")], T.sem("tr_ready")
        copied = [T.sem("act_copied"), T.sem("dve_copied")]
        with T.block() as block:
            from_act = issue_loads(nc, block, loads, loaded)

            @block.tensor
            def _(pe):
                turn_blocks(nc, pe, groups, pt, c["ident"], loads, loaded, tr_ready, copied)

            @block.scalar
            def _(act):
                from_act(act)
                copy_blocks(act, nc.scalar.copy, groups, pt, tr_ready, copied[0], 0, 2)
                if loads[1::2]:
                    act.wait_ge(loaded[1], 16 * len(loads[1::2]))

            @block.vector
            def _(dve):
                copy_blocks(dve, nc.vector.tensor_copy, groups, pt, tr_ready, copied[1], 1, 2)


def normalise(nc, c, name, affine, loads, groups):
    x, xn, xnT, ident = c["x"], c["xn"], c["xnT"], c["ident"]
    rounds = 1 if affine is None else 2
    with Scope(nc, name) as S:
        st = S.sb("stats", [P, TILES, 6])
        mean, rstd, tmp = (S.sb(n, [P, TILES]) for n in ("mean", "rstd", "tmp"))
        gb = S.sb("gb", [P, 2, DM]) if affine else None
        wt = S.ps("wt", [P, WBANKS, 4, P])
        pt = S.ps("pt", [P, 4, KC * 2, P])
        loaded, wt_ready, wt_copied = [S.sem("loaded_sp"), S.sem("loaded_act")], S.sem("wt_ready"), S.sem("wt_copied")
        var_ready, std_ready, step = S.sem("var_ready"), S.sem("std_ready"), S.sem("step")
        xn_ready, tr_ready, gb_loaded = (S.sem(n) for n in ("xn_ready", "tr_ready", "gb_loaded"))
        tr_copied = (S.sem("tr_copied_a"), S.sem("tr_copied_d"))
        if affine:
            loads = loads + [(gb[:, j, :], affine[j][None, :].to_broadcast([P, DM])) for j in range(2)]
        with S.block() as block:
            from_act = issue_loads(nc, block, loads, loaded)

            def copy_turned(eng, copy, half):
                for g in range(half, TILES // 2, 2):
                    eng.wait_ge(tr_ready, g + 1)
                    for kc in range(KC):
                        ins = copy(xnT[:, kc, g * 2 * P:(g + 1) * 2 * P], pt[:, g % 4, 2 * kc:2 * kc + 2, :])
                    ins.then_inc(tr_copied[half], 1)

            @block.vector
            def _(dve):
                ch = Chain(dve, step)
                for r in range(rounds):
                    src = x if r == 0 else xn
                    for i in range(TILES):
                        ins = nc.vector.bn_stats(st[:, i, :], src[:, i, :])
                    ch.step(ins)
                    row_stats_to_affine(nc, ch, st, mean[:], rstd[:], tmp[:], DM // 2)
                    nc.vector.tensor_copy(tmp[:], rstd[:]).then_inc(var_ready, 1)
                    dve.wait_ge(std_ready, r + 1)
                    ch.step(nc.vector.reciprocal(rstd[:], tmp[:]))
                    last = r == rounds - 1 and not affine
                    for i in range(TILES):
                        ins = nc.vector.tensor_scalar(xn[:, i, :], src[:, i, :], mean[:, i:i + 1], rstd[:, i:i + 1], ALU.subtract, ALU.mult)
                        if last:
                            ins.then_inc(xn_ready, 1)
                    if not last:
                        ch.step(ins)
                if affine:
                    for j in range(2):
                        dve.wait_ge(loaded[j], 16 * len(loads[j::2]))
                    ch.step(nc.vector.tensor_tensor(xn[:], xn[:], gb[:, None, 0, :].to_broadcast([P, TILES, DM]), ALU.mult))
                    nc.vector.tensor_tensor(xn[:], xn[:], gb[:, None, 1, :].to_broadcast([P, TILES, DM]), ALU.add).then_inc(xn_ready, TILES)
                copy_turned(dve, nc.vector.tensor_copy, 1)

            @block.scalar
            def _(act):
                from_act(act)
                for r in range(rounds):
                    act.wait_ge(var_ready, r + 1)
                    nc.scalar.activation(tmp[:], tmp[:], ACT.Sqrt).then_inc(std_ready, 1)
                copy_blocks(act, nc.scalar.copy, groups, wt, wt_ready, wt_copied, 0, 1)
                copy_turned(act, nc.scalar.copy, 0)
                if loads[1::2]:
                    act.wait_ge(loaded[1], 16 * len(loads[1::2]))

            @block.tensor
            def _(pe):
                turn_blocks(nc, pe, groups, wt, ident, loads, loaded, wt_ready, [wt_copied])
                for g in range(TILES // 2):
                    pe.wait_ge(xn_ready, 2 * g + 2)
                    if g >= 4:
                        pe.wait_ge(tr_copied[g % 2], (g - 4) // 2 + 1)
                    for kc in range(KC):
                        for v in range(2):
                            ins = nc.tensor.transpose(pt[:, g % 4, 2 * kc + v, :], xn[:, 2 * g + v, kc * P:(kc + 1) * P], ident[:])
                    ins.then_inc(tr_ready, 1)


HD = DM // HEADS
GH = 4
HP = 32
GROUPS = HEADS // GH
Q_PARTS = (0, 0, 1, 1, 0, 2)
K_PARTS = (0, 1, 0, 1, 2, 0)
KROWS = HD * len(Q_PARTS)


def self_attention(nc, name, c, wts, given, window):
    with Scope(nc, name) as S:
        parts = nc.dram_tensor(f"{name}_parts", [3, BATCH, 2 * DM, SEQ], BF16, kind="Internal").ap()
        v = S.sb("v", [P, TILES, DM])
        wo = S.sb("wo", [P, GROUPS, DM])
        bob = S.sb("bob", [P, DM]) if given else None
        project_heads(nc, name + "p", c, wts, given, parts, v, wo, bob)
        attend_heads(nc, name + "a", c, parts, v, wo, bob, window)


def project_heads(nc, name, c, wts, given, parts, v, wo, bob):
    xnT = c["xnT"]
    names = ("Wq", "Wk", "Wv", "Wo")
    with Scope(nc, name) as S:
        wqk = S.sb("wqk", [P, KC, 2, DM])
        wv = S.sb("wv", [P, KC, DM])
        raw = S.sb("raw", [P, 4, KC, DM])
        bqk = S.sb("bqk", [P, 2 * KC])
        bvb = S.sb("bvb", [P, DM])
        ready = S.sem("ready")
        with S.block() as block:
            @block.gpsimd
            def _(pool):
                nc.gpsimd.memset(wo[:], 0.0)
                nc.gpsimd.memset(bqk[:], 0.0)
                nc.gpsimd.memset(bvb[:], 0.0)
        loads, jobs = [], []
        if given:
            loads += [(wqk[:, :, n, :], wts[names[n]].rearrange("(k p) n -> p k n", p=P)) for n in range(2)]
            loads += [(wv[:], wts["Wv"].rearrange("(k p) n -> p k n", p=P)),
                      (bvb[:], wts["bv"][None, :].to_broadcast([P, DM])), (bob[:], wts["bo"][None, :].to_broadcast([P, DM]))]
            loads += [(bqk[:, n * KC:(n + 1) * KC], wts[b].rearrange("(c p) -> p c", p=P)) for n, b in enumerate(("bq", "bk"))]
            loads += [(wo[HP * r:HP * r + HD], wts["Wo"].rearrange("(g m d) n -> m d g n", m=GH, d=HD)[r]) for r in range(GH)]
        else:
            loads += [(raw[:, n], wts[w].rearrange("(k p) n -> p k n", p=P)) for n, w in enumerate(names)]
            for kc in range(KC):
                for o in range(KC):
                    for dst, n in ((wqk[:, kc, 0, :], 0), (wqk[:, kc, 1, :], 1), (wv[:, kc, :], 2)):
                        jobs.append((dst[:, o * P:(o + 1) * P], raw[:, n, o, kc * P:(kc + 1) * P]))
        with nc.allow_non_contiguous_dma(reason="bias vectors by feature"):
            prepare(nc, name + "t", c, loads, jobs)
        if not given:
            spread = S.sb("spread", [P, KC, GROUPS, GH, HP])
            with S.block() as block:
                @block.vector
                def _(dve):
                    nc.vector.memset(spread[:], 0.0).then_inc(ready, 1)
                    dve.wait_ge(ready, 1)
                    for o in range(KC):
                        nc.vector.tensor_copy(spread[:, o, :, :, 0:HD], raw[:, 3, o, :].rearrange("p (g m d) -> p g m d", m=GH, d=HD))
            prepare(nc, name + "o", c, [], [
                (wo[:, g, o * P:(o + 1) * P], spread[:, o, g].rearrange("p m d -> p (m d)")) for o in range(KC) for g in range(GROUPS)])
        else:
            with S.block() as block:
                @block.vector
                def _(dve):
                    nc.vector.tensor_scalar(bqk[:, 0:KC], bqk[:, 0:KC], HD ** -0.5, None, ALU.mult)

        xb = S.sb("xb", [P, KC, SEQ])
        full = S.sb("full", [P, 2 * KC, SEQ])
        part = [S.sb(n, [P, 2 * KC, SEQ], BF16) for n in ("hi", "mid", "lo")]
        qk_ps = S.ps("qk_ps", [P, 2 * KC, BANK])
        v_ps = S.ps("v_ps", [P, QT, DM])
        x_staged, qk_ready, qk_read, hi_ready, v_ready, v_read, mid_ready, lo_ready, rest_ready, parts_stored = (S.sem(n) for n in (
            "x_staged", "qk_ready", "qk_read", "hi_ready", "v_ready", "v_read", "mid_ready", "lo_ready", "rest_ready", "parts_stored"))
        with S.block() as block:
            @block.gpsimd
            def _(pool):
                pool.sem_inc(v_ready, 1)
                with pool.Fori(0, BATCH) as b:
                    pool.wait_ge(v_ready, b + 1)
                    nc.gpsimd.tensor_copy(xb[:], xnT[:, :, bass.ds(b * SEQ, SEQ)]).then_inc(x_staged, 1)

            @block.tensor
            def _(pe):
                pe.sem_inc(v_read, 1)
                pe.sem_inc(qk_read, 1)
                with pe.Fori(0, BATCH) as b:
                    pe.wait_ge(qk_read, b * (2 * KC) + 1)
                    for j in range(2 * KC):
                        for kc in range(KC):
                            ins = nc.tensor.matmul(qk_ps[:, j, :], wqk[:, kc, j // KC, j % KC * P:(j % KC + 1) * P],
                                                   xnT[:, kc, bass.ds(b * SEQ, SEQ)], start=kc == 0, stop=kc == KC - 1)
                        ins.then_inc(qk_ready, 1)
                    pe.wait_ge(x_staged, b + 1)
                    pe.wait_ge(v_read, b + 1)
                    for u in range(QT):
                        for kc in range(KC):
                            ins = nc.tensor.matmul(v_ps[:, u, :], xb[:, kc, u * P:(u + 1) * P], wv[:, kc, :], start=kc == 0, stop=kc == KC - 1)
                    ins.then_inc(v_ready, 1)

            @block.scalar
            def _(act):
                act.sem_inc(lo_ready, 1)
                act.sem_inc(parts_stored, 16)
                with act.Fori(0, BATCH) as b:
                    act.wait_ge(lo_ready, b + 1)
                    act.wait_ge(parts_stored, b * 16 + 16)
                    for j in range(2 * KC):
                        act.wait_ge(qk_ready, b * (2 * KC) + (j + 1))
                        scale = HD ** -0.5 if j < KC else 1.0
                        nc.scalar.activation(full[:, j, :], qk_ps[:, j, :], ACT.Identity, bias=bqk[:, j:j + 1], scale=scale)
                        nc.scalar.activation(part[0][:, j, :], qk_ps[:, j, :], ACT.Identity, bias=bqk[:, j:j + 1], scale=scale).then_inc(qk_read, 1)

            @block.vector
            def _(dve):
                dve.sem_inc(rest_ready, 16)
                with dve.Fori(0, BATCH) as b:
                    dve.wait_ge(qk_read, b * (2 * KC) + (2 * KC + 1))
                    nc.vector.tensor_tensor(full[:], full[:], part[0][:], ALU.subtract).then_inc(hi_ready, 1)
                    dve.wait_ge(v_ready, b + 2)
                    nc.vector.tensor_tensor(v[:, bass.ds(b * QT, QT), :], v_ps[:], bvb[:, None, :].to_broadcast([P, QT, DM]), ALU.add).then_inc(v_read, 1)
                    dve.wait_ge(hi_ready, b + 1)
                    dve.wait_ge(rest_ready, b * 32 + 16)
                    nc.vector.tensor_copy(part[1][:], full[:]).then_inc(mid_ready, 1)
                    dve.wait_ge(mid_ready, b + 1)
                    nc.vector.tensor_tensor(part[2][:], full[:], part[1][:], ALU.subtract).then_inc(lo_ready, 1)

            @block.sync
            def _(sp):
                def store(b, n, stored):
                    sp.dma_start(parts[n, bass.ds(b, 1)].rearrange("b (j p) t -> p (b j) t", p=P), part[n][:]).then_inc(stored, 16)

                with sp.Fori(0, BATCH) as b:
                    sp.wait_ge(qk_read, b * (2 * KC) + (2 * KC + 1))
                    store(b, 0, parts_stored)
                    sp.wait_ge(lo_ready, b + 2)
                    store(b, 1, rest_ready)
                    store(b, 2, rest_ready)
                sp.wait_ge(parts_stored, 16 * BATCH + 16)
                sp.wait_ge(rest_ready, 32 * BATCH + 16)


def attend_heads(nc, name, c, parts, v, wo, bob, window):
    x = c["x"]
    max_units = [(r, (2 * p, 2 * p + 1)) for r in range(GH) for p in range(QT // 2)] if window else \
        [(r, (q,)) for r in range(GH) for q in range(QT)]
    KEYS = 2 * P if window else SEQ
    prob_units = [(kt, tuple(range(GH)), min(2 * P, SEQ - kt * P)) for kt in range(QT)] if window else \
        [(kt, (2 * p, 2 * p + 1), SEQ) for kt in range(QT) for p in range(GH // 2)]
    N1, N2 = len(max_units), len(prob_units)
    W = 2 * P if window else SEQ
    UH = len(prob_units[0][1])
    PB = 4
    WU = GH // UH
    NL = 2 * len(Q_PARTS)
    with Scope(nc, name) as S:
        qs, ks = (S.sb(n, [P, 2, HEADS, SEQ], BF16) for n in ("qs", "ks"))
        vb = S.sb("vb", [P, 2, QT, HEADS, HP])
        identb = S.sb("identb", [P, P], BF16)
        sel = S.sb("sel", [P, GH, P], BF16)
        den_sel = S.sb("den_sel", [P, P])
        mask = S.sb("mask", [P, 3 * P], BF16) if window else None
        maskT = S.sb("maskT", [P, 2 * P], BF16) if window else None
        nm = S.sb("nm", [P, 2, QT, GH])
        nmp = S.sb("nmp", [P, QT, 3, GH], BF16)
        nmT = S.sb("nmT", [P, 2, SEQ], BF16)
        pT = S.sb("pT", [P, PB, UH, W])
        o_raw = S.sb("o_raw", [P, GROUPS, SEQ])
        rden = S.sb("rden", [P, 2, SEQ])
        s1 = S.ps("s1", [P, 2, BANK])
        s2 = S.ps("s2", [P, 2, 2 * BANK])
        o_ps = S.ps("o_ps", [P, BANK])
        m_ps = S.ps("m_ps", [P, 2 * BANK], BF16)
        built, cleared = S.sem("built"), S.sem("cleared")
        CONSTANT_STEPS = 14 if window else 8
        loaded = [S.sem("loaded_even"), S.sem("loaded_odd")]
        BEFORE = 1 + QT
        USES = GROUPS * N1 + GROUPS + QT

        def use(b, local):
            return b * USES + (N1 - BEFORE + local), (N1 - BEFORE + local) % 2

        def max_use(b, g, j, ahead=False):
            if ahead:
                return use(b, 3 * N1 + BEFORE + 2 + j)
            if g == 0:
                return j, j % 2
            if g == 1:
                return use(b, (BEFORE if is_first(b) else 0) + j)
            return use(b, (g - 1) * N1 + BEFORE + (g - 2) + j)

        def sum_use(b, g):
            if g == GROUPS - 1:
                return use(b, 3 * N1 + BEFORE + 3 if is_last(b) else USES + N1)
            if g == GROUPS - 2:
                return use(b, (3 if is_last(b) else 4) * N1 + BEFORE + 2)
            return use(b, (g + 2) * N1 + BEFORE + g)

        def y_use(b, q):
            n, at = sum_use(b, GROUPS - 1)
            return n + (1 + q), (at + 1 + q) % 2

        def is_first(b):
            return isinstance(b, int) and b == 0

        def is_last(b):
            return isinstance(b, int) and b == BATCH - 1

        (v_staged, element_done, s1_ready, s1_read, nmp_ready, nmT_out, nmT_ready, s2_ready, exp_done, pv_done, o_copied,
         on_ready, nm_step, y_step) = (S.sem(n) for n in (
             "v_staged", "element_done", "s1_ready", "s1_read", "nmp_ready", "nmT_out", "nmT_ready", "s2_ready", "exp_done",
             "pv_done", "o_copied", "on_ready", "nm_step", "y_step"))

        def build_constants(pool):
            ch = Chain(pool, built)
            ch.step(nc.gpsimd.memset(vb[:], 0.0))
            ch.step(nc.gpsimd.memset(vb[:, :, :, :, HD:HD + 1], 1.0))
            ch.step(nc.gpsimd.memset(sel[:], 0.0))
            for n in range(3):
                ch.step(nc.gpsimd.affine_select(out=sel[:], in_=sel[:], compare_op=ALU.not_equal, fill=1.0, base=-GH * n,
                                                pattern=[[-1, GH], [0, P]], channel_multiplier=1))
            ch.step(nc.gpsimd.memset(den_sel[:], 0.0))
            ch.step(nc.gpsimd.affine_select(out=den_sel[:].rearrange("p (m d) -> p m d", d=HP), in_=den_sel[:].rearrange("p (m d) -> p m d", d=HP),
                                            compare_op=ALU.not_equal, fill=1.0, base=-HD, pattern=[[-HP, GH], [0, HP]],
                                            channel_multiplier=1))
            if window:
                ch.step(nc.gpsimd.memset(mask[:], 0.0))
                ch.step(nc.gpsimd.affine_select(out=mask[:], in_=mask[:], compare_op=ALU.is_ge, fill=-1e9, base=P,
                                                pattern=[[-1, 3 * P]], channel_multiplier=1))
                ch.step(nc.gpsimd.affine_select(out=mask[:], in_=mask[:], compare_op=ALU.is_ge, fill=-1e9, base=64 - P,
                                                pattern=[[1, 3 * P]], channel_multiplier=-1))
                ch.step(nc.gpsimd.memset(maskT[:], 0.0))
                ch.step(nc.gpsimd.affine_select(out=maskT[:], in_=maskT[:], compare_op=ALU.is_ge, fill=-1e9, base=0,
                                                pattern=[[1, 2 * P]], channel_multiplier=-1))
                ch.step(nc.gpsimd.affine_select(out=maskT[:], in_=maskT[:], compare_op=ALU.is_ge, fill=-1e9, base=64,
                                                pattern=[[-1, 2 * P]], channel_multiplier=1))
            assert ch.n == CONSTANT_STEPS, ch.n

        def elements(eng, body):
            with eng.Fori(0, BATCH // 2) as bb:
                for par in range(2):
                    body(bb * 2 + par, par, bb)

        def overlapped(eng, body):
            body(0, 0, 0)
            with eng.Fori(0, (BATCH - 2) // 2) as bb:
                body(bb * 2 + 1, 1, bb)
                body(bb * 2 + 2, 0, bb + 1)
            body(BATCH - 1, 1, (BATCH - 1) // 2)

        with S.block() as block:
            @block.sync
            def _(sp):
                def load(b, par, bb):
                    sp.wait_ge(element_done, b + 1)
                    for n, (stack, order) in enumerate(((qs, Q_PARTS), (ks, K_PARTS))):
                        for s, p in enumerate(order):
                            sp.dma_start(stack[HD * s:HD * (s + 1), par],
                                         parts[p, bass.ds(b, 1), n * DM:(n + 1) * DM, :].rearrange("b (h d) t -> d (b h) t", d=HD)).then_inc(loaded[par], 16)

                elements(sp, load)

            @block.gpsimd
            def _(pool):
                build_constants(pool)

                def stage(b, par, bb):
                    pool.wait_ge(element_done, b + 1)
                    nc.gpsimd.tensor_copy(vb[:, par, :, :, 0:HD], v[:, bass.ds(b * QT, QT), :].rearrange("p q (h w) -> p q h w", w=HD)).then_inc(v_staged, 1)

                elements(pool, stage)

            @block.tensor
            def _(pe):
                pe.sem_inc(element_done, 2)
                pe.wait_ge(built, CONSTANT_STEPS)
                pe.wait_ge(cleared, 2)

                def max_scores(b, par, g, j, number):
                    i, at = number
                    r, qts = max_units[j]
                    pe.wait_ge(s1_read, i + 1)
                    for v_, q in enumerate(qts):
                        k0 = max(q - 1, 0) * P if window else 0
                        out = s1[:, at, v_ * KEYS:(v_ + 1) * KEYS]
                        ins = nc.tensor.matmul(out, qs[0:KROWS, par, g * GH + r, q * P:(q + 1) * P], ks[0:KROWS, par, g * GH + r, k0:k0 + KEYS],
                                               start=True, stop=not window)
                        if window:
                            m0 = 0 if q else P
                            ins = nc.tensor.matmul(out, identb[:], mask[:, m0:m0 + KEYS], start=False, stop=True)
                    ins.then_inc(s1_ready, 1)

                def turn_max(group):
                    pe.wait_ge(nmp_ready, group + 1)
                    for q in range(QT):
                        ins = nc.tensor.transpose(m_ps[0:3 * GH, q * P:(q + 1) * P], nmp[:, q].rearrange("p n r -> p (n r)"), identb[:])
                    ins.then_inc(nmT_out, 1)

                def prob_scores(b, par, g, j):
                    u = g * N2 + j
                    kt, heads, n = prob_units[j]
                    pe.wait_ge(exp_done, b * (GROUPS * N2) + (u + 1))
                    if j == 0:
                        pe.wait_ge(nmT_ready, b * GROUPS + (g + 1))
                    q0 = kt * P if window else 0
                    for i, r in enumerate(heads):
                        out = s2[:, u % 2, i * W:i * W + n]
                        nc.tensor.matmul(out, ks[0:KROWS, par, g * GH + r, kt * P:(kt + 1) * P], qs[0:KROWS, par, g * GH + r, q0:q0 + n],
                                         start=True, stop=False)
                        if window:
                            nc.tensor.matmul(out, identb[:], maskT[:, 0:n], start=False, stop=False)
                        ins = nc.tensor.matmul(out, sel[:, r, :], nmT[:, g % 2, q0:q0 + n], start=False, stop=True)
                    ins.then_inc(s2_ready, 1)

                def weigh(b, par, g, kt):
                    u = g * N2 + kt * WU
                    n = prob_units[kt * WU][2]
                    pe.wait_ge(exp_done, b * (GROUPS * N2) + (u + WU - 1 + 3))
                    if kt == 0:
                        pe.wait_ge(o_copied, b * GROUPS + (g + 1))
                        if g == 0:
                            pe.wait_ge(v_staged, b + 1)
                    q0 = kt * P if window else 0
                    for r in range(GH):
                        ins = nc.tensor.matmul(o_ps[HP * r:HP * r + HP, q0:q0 + n], vb[:, par, kt, g * GH + r, :],
                                               pT[:, (u + r // UH) % PB, r % UH, 0:n], start=kt == 0, stop=kt == QT - 1,
                                               skip_group_check=window)
                    ins.then_inc(pv_done, WU)

                def sum_heads(b, g):
                    i, at = sum_use(b, g)
                    pe.wait_ge(o_copied, b * GROUPS + (g + 2))
                    pe.wait_ge(s1_read, i + 1)
                    nc.tensor.matmul(s1[:, at, :], den_sel[:], o_raw[:, g, :], start=True, stop=True).then_inc(s1_ready, 1)

                def outputs(b):
                    pe.wait_ge(on_ready, b * GROUPS + GROUPS)
                    for q in range(QT):
                        i, at = y_use(b, q)
                        pe.wait_ge(s1_read, i + 1)
                        for g in range(GROUPS):
                            ins = nc.tensor.matmul(s1[:, at, 0:DM], o_raw[:, g, q * P:(q + 1) * P], wo[:, g, :], start=g == 0, stop=g == GROUPS - 1)
                            if q == 0 and g == 0:
                                ins.then_inc(element_done, 1)
                        ins.then_inc(s1_ready, 1)

                def element(b, par, turn):
                    if is_first(b):
                        pe.wait_ge(loaded[0], 16 * NL)
                        for j in range(N1):
                            max_scores(0, 0, 0, j, max_use(0, 0, j))
                        turn_max(0)
                    pending = [] if is_first(b) else [(b - 1, 1 - par, GROUPS - 1, QT - 1)]
                    for g in range(GROUPS):
                        following = g + 1 if g + 1 < GROUPS else None
                        if following is None and not is_last(b):
                            pe.wait_ge(loaded[1 - par], (turn + par) * (16 * NL) + 16 * NL)
                        ahead = 0
                        for j in range(N2):
                            prob_scores(b, par, g, j)
                            while ahead < min(N1, N1 * j // (N2 - 2)) and not (following is None and is_last(b)):
                                if following is None:
                                    max_scores(b + 1, 1 - par, 0, ahead, max_use(b, 0, ahead, ahead=True))
                                else:
                                    max_scores(b, par, following, ahead, max_use(b, following, ahead))
                                ahead += 1
                            if pending:
                                weigh(*pending.pop())
                            if j % WU == WU - 1:
                                pending.append((b, par, g, j // WU))
                        if g:
                            sum_heads(b, g - 1)
                        elif not is_first(b):
                            sum_heads(b - 1, GROUPS - 1)
                        if not (following is None and is_last(b)):
                            turn_max(b * GROUPS + (g + 1))
                        if g == 0 and not is_first(b):
                            outputs(b - 1)
                    if is_last(b):
                        weigh(*pending.pop())
                        sum_heads(b, GROUPS - 1)
                        outputs(b)

                overlapped(pe, element)

            @block.vector
            def _(dve):
                V = nc.vector
                dve.sem_inc(s1_read, 2)
                V.tensor_copy(identb[:], c["ident"][:]).then_inc(cleared, 1)
                V.memset(nmT[:], 0.0).then_inc(cleared, 1)
                dve.wait_ge(cleared, 2)

                def maxima(group, g, number):
                    ch = Chain(dve, nm_step, group * 3)
                    for j, (r, qts) in enumerate(max_units):
                        i, at = number(j)
                        dve.wait_ge(s1_ready, i + 1)
                        V.tensor_reduce(nm[:, g % 2, qts[0]:qts[-1] + 1, r], s1[:, at, :].rearrange("p (q k) -> p q k", k=KEYS), AX, ALU.max,
                                        negate=True).then_inc(s1_read, 1)
                    dve.wait_ge(s1_read, i + 3)
                    val = nm[:, g % 2]
                    ch.step(V.tensor_copy(nmp[:, :, 0, :], val))
                    ch.step(V.tensor_tensor(val, val, nmp[:, :, 0, :], ALU.subtract))
                    ch.step(V.tensor_copy(nmp[:, :, 1, :], val))
                    V.tensor_tensor(nmp[:, :, 2, :], val, nmp[:, :, 1, :], ALU.subtract).then_inc(nmp_ready, 1)
                    dve.wait_ge(nmT_out, group + 1)
                    V.tensor_copy(nmT[0:3 * GH, g % 2, :], m_ps[0:3 * GH, 0:SEQ]).then_inc(nmT_ready, 1)

                def divide(b, g):
                    i, at = sum_use(b, g)
                    dve.wait_ge(s1_ready, i + 1)
                    V.reciprocal(rden[:, g % 2, :], s1[:, at, :]).then_inc(s1_read, 1)
                    dve.wait_ge(s1_read, i + 3)
                    V.tensor_tensor(o_raw[:, g, :], o_raw[:, g, :], rden[:, g % 2, :], ALU.mult).then_inc(on_ready, 1)

                def add(b):
                    for q in range(QT):
                        i, at = y_use(b, q)
                        t = b * QT + q
                        if bob is not None:
                            Chain(dve, y_step, t).step(V.tensor_tensor(x[:, t, :], x[:, t, :], bob[:], ALU.add))
                        dve.wait_ge(s1_ready, i + 1)
                        V.tensor_tensor(x[:, t, :], x[:, t, :], s1[:, at, 0:DM], ALU.add).then_inc(s1_read, 1)

                def element(b, par, turn):
                    if is_first(b):
                        maxima(0, 0, lambda j: max_use(0, 0, j))
                    for g in range(GROUPS):
                        if g + 1 < GROUPS:
                            maxima(b * GROUPS + (g + 1), g + 1, lambda j: max_use(b, g + 1, j))
                        elif not is_last(b):
                            maxima(b * GROUPS + (g + 1), 0, lambda j: max_use(b, 0, j, ahead=True))
                        if g:
                            divide(b, g - 1)
                        elif not is_first(b):
                            divide(b - 1, GROUPS - 1)
                            add(b - 1)
                    if is_last(b):
                        divide(b, GROUPS - 1)
                        add(b)

                overlapped(dve, element)

            @block.scalar
            def _(act):
                act.sem_inc(exp_done, 2)
                act.sem_inc(pv_done, PB)
                act.sem_inc(o_copied, 1)

                def copy_out(b, g):
                    act.wait_ge(pv_done, b * (GROUPS * N2) + ((g + 1) * N2 + PB))
                    if g == 0 and not is_first(b):
                        act.wait_ge(s1_read, y_use(b - 1, QT - 1)[0] + 3)
                    nc.scalar.copy(o_raw[:, g, :], o_ps[:]).then_inc(o_copied, 1)

                def element(b, par, turn):
                    for g in range(GROUPS):
                        for j in range(N2):
                            u = g * N2 + j
                            n = prob_units[j][2]
                            act.wait_ge(s2_ready, b * (GROUPS * N2) + (u + 1))
                            act.wait_ge(pv_done, b * (GROUPS * N2) + (u + 1))
                            nc.scalar.activation(pT[:, u % PB, :, 0:n], s2[:, u % 2, :].rearrange("p (h t) -> p h t", t=W)[:, :, 0:n],
                                                 ACT.Exp).then_inc(exp_done, 1)
                            if j == 0 and g:
                                copy_out(b, g - 1)
                            elif j == 0 and not is_first(b):
                                copy_out(b - 1, GROUPS - 1)
                    if is_last(b):
                        copy_out(b, GROUPS - 1)

                overlapped(act, element)


CTX, CD = 64, 192
CTOK = BATCH * CTX
CT = CTOK // P
CK = ((0, P), (P, CD - P))
HK = HEADS * CTX


def cross_attention(nc, name, c, wts, dh, out_in=False, norm_ctx=False, clamp=None):
    x, xnT, ident, ones = c["x"], c["xnT"], c["ident"], c["ones"]
    inner = HEADS * dh
    NC = inner // P
    HC = P // dh
    bq, bo = wts.get("bq"), wts.get("bo")
    kv_biased = "bk" in wts or "bkv" in wts
    with Scope(nc, name) as S:
        qk = S.sb("qk", [P, BATCH, KC, HK])
        vo = S.sb("vo", [P, BATCH, HK // P, DM])
        brow = S.sb("brow", [3 * 32, BATCH, HK], BF16) if bq is not None else None
        ones_b = S.sb("ones_b", [3 * 32, P], BF16) if bq is not None else None
        bob = S.sb("bob", [P, DM]) if bo is not None else None
        guarded = clamp is not None
        flag = S.sb("flag", [P, 1], I32) if guarded else None
        with Scope(nc, name + "p") as W:
            wqT = W.sb("wqT", [P, NC, DM])
            wo = W.sb("wo", [P, NC, DM])
            wkv = W.sb("wkv", [P, 2, 2, inner])
            ctxT = W.sb("ctxT", [P, 2, CTOK])
            kvT = W.sb("kvT", [P, 2, NC, CTOK])
            ctx = W.sb("ctx", [P, CT, CD])
            heads = W.sb("heads", [P, HC])
            bkv_col = W.sb("bkv_col", [P, 2, NC]) if kv_biased else None
            bq_col = W.sb("bq_col", [P, NC]) if bq is not None else None
            diag = W.sb("diag", [P, 2, 2, HK])
            made = W.sem("made")
            with W.block() as block:
                @block.gpsimd
                def _(pool):
                    nc.gpsimd.memset(heads[:], 1.0).then_inc(made, 1)
                    pool.wait_ge(made, 1)
                    nc.gpsimd.affine_select(out=heads[:], in_=heads[:], compare_op=ALU.is_ge, fill=0.0, base=0,
                                            pattern=[[-dh, HC]], channel_multiplier=1).then_inc(made, 1)
                    pool.wait_ge(made, 2)
                    nc.gpsimd.affine_select(out=heads[:], in_=heads[:], compare_op=ALU.is_ge, fill=0.0, base=dh - 1,
                                            pattern=[[dh, HC]], channel_multiplier=-1)
            with Scope(nc, name + "r") as R:
                loads = [(ctx[:], c["ctx_dram"])]
                jobs = []
                if out_in:
                    raw = R.sb("raw", [P, 2, 2, CD])
                    rawo = R.sb("rawo", [P, KC, DM])
                    per_head = wts["Wkv"].rearrange("(h n w) c -> h n w c", n=2, w=dh)
                    bias_head = wts["bkv"].rearrange("(h n w) -> h n w", n=2, w=dh)
                    for r in range(HC):
                        for n in range(2):
                            loads.append((raw[r * dh:(r + 1) * dh, n], per_head[r::HC, n].rearrange("c w d -> w c d")))
                            loads.append((bkv_col[r * dh:(r + 1) * dh, n], bias_head[r::HC, n].rearrange("c w -> w c")))
                    loads.append((wqT[:], wts["Wq"].rearrange("(c p) d -> p c d", p=P)))
                    loads.append((rawo[:], wts["Wo"].rearrange("(c p) d -> p c d", p=P)))
                    for n in range(2):
                        for o in range(NC):
                            for k, (k0, kn) in enumerate(CK):
                                jobs.append((wkv[0:kn, k, n, o * P:(o + 1) * P], raw[:, n, o, k0:k0 + kn]))
                    for k in range(KC):
                        for o in range(KC):
                            jobs.append((wo[:, k, o * P:(o + 1) * P], rawo[:, o, k * P:(k + 1) * P]))
                else:
                    raw = R.sb("raw", [P, KC, inner])
                    loads.append((raw[:], wts["Wq"].rearrange("(k p) n -> p k n", p=P)))
                    loads.append((wo[:], wts["Wo"].rearrange("(c p) n -> p c n", p=P)))
                    for n, w in enumerate(("Wk", "Wv")):
                        for k, (k0, kn) in enumerate(CK):
                            loads.append((wkv[0:kn, k, n, :], wts[w][k0:k0 + kn, :]))
                    for cc in range(NC):
                        for k in range(KC):
                            jobs.append((wqT[:, cc, k * P:(k + 1) * P], raw[:, k, cc * P:(cc + 1) * P]))
                    if kv_biased:
                        for n, b in enumerate(("bk", "bv")):
                            loads.append((bkv_col[:, n, :], wts[b].rearrange("(c p) -> p c", p=P)))
                if bq is not None:
                    loads.append((bq_col[:], bq.rearrange("(c p) -> p c", p=P)))
                if bo is not None:
                    loads.append((bob[:], bo[None, :].to_broadcast([P, DM])))
                if norm_ctx:
                    gc = R.sb("gc", [P, 2, CD])
                    loads.append((gc[:, 0, :], wts["g_c"][None, :].to_broadcast([P, CD])))
                    loads.append((gc[:, 1, :], wts["b_c"][None, :].to_broadcast([P, CD])))
                turn_ctx = [(ctxT[0:kn, k, i * P:(i + 1) * P], ctx[:, i, k0:k0 + kn]) for i in range(CT) for k, (k0, kn) in enumerate(CK)]
                if not norm_ctx:
                    jobs += turn_ctx
                with nc.allow_non_contiguous_dma(reason="bias vectors by feature"):
                    prepare(nc, name + "t", c, loads, jobs)
                if norm_ctx:
                    st, mean, rstd, tmp = R.sb("st", [P, CT, 6]), R.sb("mean", [P, CT]), R.sb("rstd", [P, CT]), R.sb("tmp", [P, CT])
                    step, var_ready, std_ready = R.sem("step"), R.sem("var_ready"), R.sem("std_ready")
                    with R.block() as block:
                        @block.vector
                        def _(dve):
                            ch = Chain(dve, step)
                            for i in range(CT):
                                ch.step(nc.vector.bn_stats(st[:, i, :], ctx[:, i, :]))
                            row_stats_to_affine(nc, ch, st, mean[:], rstd[:], tmp[:], CD // 2)
                            nc.vector.tensor_copy(tmp[:], rstd[:]).then_inc(var_ready, 1)
                            dve.wait_ge(std_ready, 1)
                            ch.step(nc.vector.reciprocal(rstd[:], tmp[:]))
                            for i in range(CT):
                                ch.step(nc.vector.tensor_scalar(ctx[:, i, :], ctx[:, i, :], mean[:, i:i + 1], rstd[:, i:i + 1],
                                                                ALU.subtract, ALU.mult))
                            ch.step(nc.vector.tensor_tensor(ctx[:], ctx[:], gc[:, None, 0, :].to_broadcast([P, CT, CD]), ALU.mult))
                            nc.vector.tensor_tensor(ctx[:], ctx[:], gc[:, None, 1, :].to_broadcast([P, CT, CD]), ALU.add)

                        @block.scalar
                        def _(act):
                            act.wait_ge(var_ready, 1)
                            nc.scalar.activation(tmp[:], tmp[:], ACT.Sqrt).then_inc(std_ready, 1)

            if norm_ctx:
                prepare(nc, name + "c", c, [], turn_ctx)

            with Scope(nc, name + "k") as R:
                kv_ps = R.ps("kv_ps", [P, 4, BANK])
                kv_ready, kv_free = R.sem("kv_ready"), R.sem("kv_free")
                with R.block() as block:
                    @block.tensor
                    def _(pe):
                        for j in range(2 * NC):
                            if j >= 4:
                                pe.wait_ge(kv_free, j - 3)
                            for k, (k0, kn) in enumerate(CK):
                                ins = nc.tensor.matmul(kv_ps[:, j % 4, 0:CTOK], wkv[0:kn, k, j // NC, j % NC * P:(j % NC + 1) * P],
                                                       ctxT[0:kn, k, :], start=k == 0, stop=k == 1)
                            ins.then_inc(kv_ready, 1)

                    @block.vector
                    def _(dve):
                        for j in range(2 * NC):
                            n, cc = j // NC, j % NC
                            dve.wait_ge(kv_ready, j + 1)
                            scale = dh ** -0.5 if n == 0 else 1.0
                            if kv_biased:
                                ins = nc.vector.tensor_scalar(kvT[:, n, cc, :], kv_ps[:, j % 4, 0:CTOK], bkv_col[:, n, cc:cc + 1], scale, ALU.add, ALU.mult)
                            else:
                                ins = nc.vector.tensor_scalar(kvT[:, n, cc, :], kv_ps[:, j % 4, 0:CTOK], scale, None, ALU.mult)
                            ins.then_inc(kv_free, 1)

            with Scope(nc, name + "g") as R:
                qk_ps = R.ps("qk_ps", [P, KC, HK])
                vo_ps = R.ps("vo_ps", [P, 4, 2, DM])
                k_diag_ready, v_diag_ready, qk_ready, vo_ready, qk_copied, vo_copied, b_ready, b_copied = (R.sem(n) for n in (
                    "k_diag_ready", "v_diag_ready", "qk_ready", "vo_ready", "qk_copied", "vo_copied", "b_ready", "b_copied"))
                CW = HC * CTX
                if bq is not None:
                    rest, brow_step = R.sb("rest", [1, HK]), R.sem("brow_step")
                if guarded:
                    sums, isnan = R.sb("sums", [P, 2 * BATCH + 1]), R.sb("isnan", [P, 2 * BATCH + 1])
                    junk, anynan = R.sb("junk", [P, KC * HK]), R.sb("anynan", [P, 1])
                    cleared, summed, nan_found, nan_ready, nan_step, flag_ready = (R.sem(n) for n in (
                        "cleared", "summed", "nan_found", "nan_ready", "nan_step", "flag_ready"))

                def diagonal(engine, b, n):
                    for cc in range(NC):
                        ins = engine.tensor_tensor(
                            diag[:, b % 2, n, cc * CW:(cc + 1) * CW].rearrange("p (h k) -> p h k", k=CTX),
                            kvT[:, n, cc, None, b * CTX:(b + 1) * CTX].to_broadcast([P, HC, CTX]),
                            heads[:, :, None].to_broadcast([P, HC, CTX]), ALU.mult)
                    return ins

                with R.block() as block:
                    @block.gpsimd
                    def _(pool):
                        for b in range(BATCH):
                            if b >= 2:
                                pool.wait_ge(vo_ready, b - 1)
                            diagonal(nc.gpsimd, b, 1).then_inc(v_diag_ready, 1)

                    @block.tensor
                    def _(pe):
                        for b in range(BATCH):
                            pe.wait_ge(k_diag_ready, b + 1)
                            if b:
                                pe.wait_ge(qk_copied, b)
                            for k in range(KC):
                                for cc in range(NC):
                                    ins = nc.tensor.matmul(qk_ps[:, k, cc * CW:(cc + 1) * CW], wqT[:, cc, k * P:(k + 1) * P],
                                                           diag[:, b % 2, 0, cc * CW:(cc + 1) * CW], start=True, stop=True)
                            ins.then_inc(qk_ready, 1)
                            if bq is not None:
                                pe.wait_ge(qk_copied, b + 1)
                                for cc in range(NC):
                                    ins = nc.tensor.matmul(qk_ps[0:1, 0, cc * CW:(cc + 1) * CW], bq_col[:, cc:cc + 1],
                                                           diag[:, b % 2, 0, cc * CW:(cc + 1) * CW], start=True, stop=True)
                                ins.then_inc(b_ready, 1)
                                pe.wait_ge(b_copied, b + 1)
                            pe.wait_ge(v_diag_ready, b + 1)
                            if b:
                                pe.wait_ge(vo_copied, b)
                            for j in range(HK // P):
                                ins = nc.tensor.matmul(vo_ps[:, j // 2, j % 2, :], diag[:, b % 2, 1, j * P:(j + 1) * P],
                                                       wo[:, j * P // CW, :], start=True, stop=True)
                            ins.then_inc(vo_ready, 1)
                        if guarded:
                            pe.wait_ge(nan_found, 1)
                            pe.wait_ge(vo_copied, BATCH)
                            nc.tensor.matmul(vo_ps[:, 0, 0, 0:1], ones[:], anynan[:], start=True, stop=True).then_inc(nan_ready, 1)

                    @block.vector
                    def _(dve):
                        if guarded:
                            nc.vector.memset(sums[:], 0.0).then_inc(cleared, 1)
                        if bq is not None:
                            nc.vector.memset(ones_b[:], 1.0)
                            nc.vector.memset(brow[:], 0.0).then_inc(brow_step, 1)
                            dve.wait_ge(brow_step, 1)
                        diagonal(nc.vector, 0, 0).then_inc(k_diag_ready, 1)
                        for b in range(BATCH):
                            if b + 1 < BATCH:
                                if b:
                                    dve.wait_ge(qk_ready, b)
                                    if bq is not None:
                                        dve.wait_ge(b_ready, b)
                                diagonal(nc.vector, b + 1, 0).then_inc(k_diag_ready, 1)
                            dve.wait_ge(qk_ready, b + 1)
                            nc.vector.tensor_copy(qk[:, b], qk_ps[:]).then_inc(qk_copied, 1)
                            if bq is not None:
                                dve.wait_ge(b_ready, b + 1)
                                bias_ch = Chain(dve, brow_step, 1 + 5 * b)
                                nc.vector.tensor_copy(rest[:], qk_ps[0:1, 0, :]).then_inc(b_copied, 1)
                                dve.wait_ge(b_copied, b + 1)
                                for n in range(3):
                                    bias_ch.step(nc.vector.tensor_copy(brow[32 * n:32 * n + 1, b, :], rest[:]))
                                    if n < 2:
                                        bias_ch.step(nc.vector.tensor_tensor(rest[:], rest[:], brow[32 * n:32 * n + 1, b, :], ALU.subtract))
                        if guarded:
                            v, ch = nc.vector, Chain(dve, nan_step)
                            dve.wait_ge(cleared, 1)
                            ch.step(v.tensor_reduce(sums[:, 2 * BATCH:], c["xn"][:].rearrange("p t n -> p (t n)"), AX, ALU.add))
                            dve.wait_ge(summed, 2 * BATCH)
                            ch.step(v.tensor_tensor(isnan[:], sums[:], sums[:], ALU.not_equal))
                            v.tensor_reduce(anynan[:], isnan[:], AX, ALU.max).then_inc(nan_found, 1)
                            dve.wait_ge(nan_ready, 1)
                            v.tensor_scalar(flag[:], vo_ps[:, 0, 0, 0:1], 0.5, None, ALU.is_gt)

                    @block.scalar
                    def _(act):
                        for b in range(BATCH):
                            act.wait_ge(vo_ready, b + 1)
                            nc.scalar.copy(vo[:, b].rearrange("p j n -> p (j n)"), vo_ps[:].rearrange("p a b n -> p (a b n)")).then_inc(vo_copied, 1)
                            if guarded:
                                act.wait_ge(cleared, 1)
                                act.wait_ge(brow_step, 1 + 5 * (b + 1))
                                if b:
                                    act.wait_ge(summed, 2 * b)
                                nc.scalar.activation(junk[:], qk[:, b].rearrange("p k n -> p (k n)"), ACT.Identity,
                                                     accum_out=sums[:, b:b + 1]).then_inc(summed, 1)
                                act.wait_ge(summed, 2 * b + 1)
                                nc.scalar.activation(junk[0:1, 0:HK], brow[0:1, b, :], ACT.Identity,
                                                     accum_out=sums[0:1, BATCH + b:BATCH + b + 1]).then_inc(summed, 1)

        s_ps = S.ps("s_ps", [P, 2, HK])
        t_ps = S.ps("t_ps", [P, HK])
        y_ps = S.ps("y_ps", [P, BANK])
        x_now = S.sb("x_now", [P, QT, KC, P])
        shifted = S.sb("shifted", [P, 2, HEADS, CTX])
        probs = S.sb("probs", [P, 2, HEADS, CTX])
        probsT = S.sb("probsT", [P, 2, HK])
        negmax = S.sb("negmax", [P, 2, HEADS])
        rsum = S.sb("rsum", [P, 2, HEADS])
        (x_staged, scores_ready, shifted_ready, exp_ready, sum_ready, probs_ready, pT_ready, pT_copied, y_ready, y_added, shift_step,
         finish_step, bias_step) = (S.sem(n) for n in (
             "x_staged", "scores_ready", "shifted_ready", "exp_ready", "sum_ready", "probs_ready", "pT_ready", "pT_copied",
             "y_ready", "y_added", "shift_step", "finish_step", "bias_step"))
        clamped = S.sb("clamped", [P, 2, HEADS, CTX]) if clamp else None

        def tiles(eng, body):
            def element(b, more):
                for q in range(QT):
                    body(b, q, b * QT + q, more + QT - 1 - q)

            element(0, QT)
            with eng.Fori(1, BATCH - 1) as b:
                element(b, QT)
            element(BATCH - 1, 0)

        def following(b, q, d):
            b2, q2 = b + (q + d) // QT, (q + d) % QT
            return b2, q2, b2 * QT + q2

        def run(eng, program, if_nan=False):
            if not guarded:
                program()
                return
            found = eng.value_load(flag[0:1, 0:1], min_val=0, max_val=1)
            with eng.If(found != 0 if if_nan else found == 0):
                program()

        with S.block() as block:
            @block.gpsimd
            def _(pool):
                def program():
                    pool.sem_inc(probs_ready, 1)
                    for q in range(QT):
                        nc.gpsimd.tensor_copy(x_now[:, q], xnT[:, :, q * P:(q + 1) * P]).then_inc(x_staged, 1)

                    def body(b, q, t, left):
                        pool.wait_ge(sum_ready, t + 1)
                        pool.wait_ge(pT_ready, t + 1)
                        nc.gpsimd.tensor_tensor(probs[:, q % 2], shifted[:, q % 2], rsum[:, q % 2, :, None].to_broadcast([P, HEADS, CTX]),
                                                ALU.mult).then_inc(probs_ready, 1)
                        if left >= QT:
                            nc.gpsimd.tensor_copy(x_now[:, q], xnT[:, :, bass.ds((b * QT + (q + QT)) * P, P)]).then_inc(x_staged, 1)

                    tiles(pool, body)
                run(pool, program)

            @block.tensor
            def _(pe):
                def program():
                    pe.sem_inc(pT_ready, 2)

                    def scores(b, q, t):
                        pe.wait_ge(x_staged, t + 1)
                        pe.wait_ge(shifted_ready, t + 1)
                        for half in range(2):
                            cols = bass.ts(half, BANK)
                            for k in range(KC):
                                ins = nc.tensor.matmul(s_ps[:, q % 2, cols], x_now[:, q, k, :], qk[:, b, k, cols],
                                                       start=k == 0, stop=k == KC - 1 and bq is None)
                            if bq is not None:
                                ins = nc.tensor.matmul(s_ps[:, q % 2, cols], ones_b[:], brow[:, b, cols], start=False, stop=True)
                        ins.then_inc(scores_ready, 1)

                    def body(b, q, t, left):
                        pe.wait_ge(probs_ready, t + 2)
                        pe.wait_ge(pT_copied, t + 1)
                        for j in range(HK // P):
                            ins = nc.tensor.transpose(t_ps[:, j * P:(j + 1) * P], probs[:, q % 2, 2 * j:2 * j + 2, :].rearrange("p h k -> p (h k)"), ident[:])
                        ins.then_inc(pT_ready, 1)
                        if left >= 2:
                            scores(*following(b, q, 2))
                        pe.wait_ge(pT_copied, t + 2)
                        pe.wait_ge(y_added, t + 1)
                        for j in range(HK // P):
                            ins = nc.tensor.matmul(y_ps[:, 0:DM], probsT[:, q % 2, j * P:(j + 1) * P], vo[:, b, j, :],
                                                   start=j == 0, stop=j == HK // P - 1)
                        ins.then_inc(y_ready, 1)

                    scores(0, 0, 0)
                    scores(0, 1, 1)
                    tiles(pe, body)
                run(pe, program)

            @block.vector
            def _(dve):
                def program():
                    dve.sem_inc(y_added, 1)
                    dve.sem_inc(shifted_ready, 2)
                    SHIFT_STEPS = 1 + (clamp is not None)

                    def shift(b, q, t):
                        ch = Chain(dve, shift_step, t * SHIFT_STEPS)
                        dve.wait_ge(scores_ready, t + 1)
                        src = s_ps[:, q % 2].rearrange("p (h k) -> p h k", k=CTX)
                        if clamp:
                            ch.step(nc.vector.tensor_scalar(clamped[:, q % 2], src, clamp, -clamp, ALU.min, ALU.max))
                            src = clamped[:, q % 2]
                        ch.step(nc.vector.tensor_reduce(negmax[:, q % 2], src, AX, ALU.max, negate=True))
                        if not (isinstance(t, int) and t < 2):
                            dve.wait_ge(probs_ready, t)
                        nc.vector.tensor_tensor(shifted[:, q % 2], src, negmax[:, q % 2, :, None].to_broadcast([P, HEADS, CTX]),
                                                ALU.add).then_inc(shifted_ready, 1)

                    def finish(b, q, t):
                        dve.wait_ge(exp_ready, t + 1)
                        Chain(dve, finish_step, t).step(nc.vector.tensor_reduce(rsum[:, q % 2], shifted[:, q % 2], AX, ALU.add))
                        nc.vector.reciprocal(rsum[:, q % 2], rsum[:, q % 2]).then_inc(sum_ready, 1)

                    def body(b, q, t, left):
                        if left >= 1:
                            finish(*following(b, q, 1))
                        if left >= 2:
                            shift(*following(b, q, 2))
                        if bo is not None:
                            Chain(dve, bias_step, t).step(nc.vector.tensor_tensor(x[:, t, :], x[:, t, :], bob[:], ALU.add))
                        dve.wait_ge(y_ready, t + 1)
                        nc.vector.tensor_tensor(x[:, t, :], x[:, t, :], y_ps[:, 0:DM], ALU.add).then_inc(y_added, 1)

                    shift(0, 0, 0)
                    shift(0, 1, 1)
                    finish(0, 0, 0)
                    tiles(dve, body)
                run(dve, program)

            @block.scalar
            def _(act):
                def program():
                    act.sem_inc(pT_copied, 1)

                    def exp(b, q, t):
                        act.wait_ge(shifted_ready, t + 3)
                        nc.scalar.activation(shifted[:, q % 2], shifted[:, q % 2], ACT.Exp).then_inc(exp_ready, 1)

                    def body(b, q, t, left):
                        act.wait_ge(pT_ready, t + 3)
                        nc.scalar.copy(probsT[:, q % 2], t_ps[:]).then_inc(pT_copied, 1)
                        if left >= 2:
                            exp(*following(b, q, 2))

                    exp(0, 0, 0)
                    exp(0, 1, 1)
                    tiles(act, body)
                run(act, program)
        if guarded:
            share = S.sb("share", [P, P])
            share_ready, mean_ready, mean_added, bias_added = (S.sem(n) for n in ("share_ready", "mean_ready", "mean_added", "bias_added"))
            with S.block() as block:
                @block.tensor
                def _(pe):
                    def program():
                        pe.wait_ge(share_ready, 1)
                        for b in range(BATCH):
                            if b:
                                pe.wait_ge(mean_added, b)
                            for j in range(HK // P):
                                ins = nc.tensor.matmul(y_ps[:, 0:DM], share[:], vo[:, b, j, :], start=j == 0, stop=j == HK // P - 1)
                            ins.then_inc(mean_ready, 1)
                    run(pe, program, True)

                @block.vector
                def _(dve):
                    def program():
                        nc.vector.memset(share[:], 1.0 / CTX).then_inc(share_ready, 1)
                        nc.vector.tensor_tensor(x[:], x[:], bob[:, None, :].to_broadcast([P, TILES, DM]), ALU.add).then_inc(bias_added, 1)
                        dve.wait_ge(bias_added, 1)
                        for b in range(BATCH):
                            dve.wait_ge(mean_ready, b + 1)
                            tiles_b = x[:, b * QT:(b + 1) * QT, :]
                            nc.vector.tensor_tensor(tiles_b, tiles_b, y_ps[:, None, 0:DM].to_broadcast([P, QT, DM]), ALU.add).then_inc(mean_added, 1)
                    run(dve, program, True)


NE = 8
BIG = 1 << 20


def route(nc, S, name, c, gate_w, gate_b, transposed, choices, capacity, dropped_expert=None):
    xnT, ident, ones = c["xnT"], c["ident"], c["ones"]
    T3 = [P, TILES, NE]
    res = {n: [S.sb(f"{n}{j}", [P, TILES]) for j in range(choices)] for n in ("weight", "keep", "slot")}
    with Scope(nc, name) as R:
        wg = R.sb("wg", [P, KC, NE])
        loads, jobs = [], []
        if transposed:
            raw = R.sb("raw", [NE, DM])
            loads.append((raw[:], gate_w))
            jobs = [(wg[:, k, :], raw[:, k * P:(k + 1) * P]) for k in range(KC)]
        else:
            loads.append((wg[:], gate_w.rearrange("(k p) e -> p k e", p=P)))
        bias = None
        if gate_b is not None:
            bias = R.sb("bias", [P, NE])
            loads.append((bias[:], gate_b[None, :].to_broadcast([P, NE])))
        prepare(nc, name + "t", c, loads, jobs)

        lg_ps = R.ps("lg_ps", [P, BANK])
        pos_ps = R.ps("pos_ps", [P, BANK])
        tot_ps = R.ps("tot_ps", [P, BANK])
        logits, probs, scratch, mask = (R.sb(n, T3) for n in ("logits", "probs", "scratch", "mask"))
        onehot = [R.sb(f"onehot{j}", T3) for j in range(choices)]
        place, totals, sums_a, sums_b = (R.sb(n, T3) for n in ("place", "totals", "sums_a", "sums_b"))
        small, small2 = R.sb("small", [P, TILES]), R.sb("small2", [P, TILES])
        number = R.sb("number", [P, NE])
        before = R.sb("before", [P, P])
        lg_ready, shifted_ready, exp_ready, mask_ready, counts_ready, step, made = (R.sem(n) for n in (
            "lg_ready", "shifted_ready", "exp_ready", "mask_ready", "counts_ready", "step", "made"))

        def per_tile(a):
            return a[:, :, None].to_broadcast(T3)

        def per_expert(a):
            return a[:, None, :].to_broadcast(T3)

        with R.block() as block:
            @block.gpsimd
            def _(pool):
                nc.gpsimd.iota(number[:], pattern=[[1, NE]], base=0, channel_multiplier=0,
                               allow_small_or_imprecise_dtypes=True).then_inc(made, 1)
                nc.gpsimd.memset(before[:], 1.0).then_inc(made, 1)
                pool.wait_ge(made, 2)
                nc.gpsimd.affine_select(out=before[:], in_=before[:], compare_op=ALU.is_ge, fill=0.0, base=-1,
                                        pattern=[[1, P]], channel_multiplier=-1).then_inc(made, 1)

            @block.tensor
            def _(pe):
                for t in range(TILES):
                    for k in range(KC):
                        ins = nc.tensor.matmul(lg_ps[:, t * NE:(t + 1) * NE], xnT[:, k, t * P:(t + 1) * P], wg[:, k, :],
                                               start=k == 0, stop=k == KC - 1)
                ins.then_inc(lg_ready, 1)
                pe.wait_ge(made, 3)
                pe.wait_ge(mask_ready, 1)
                flat = mask[:].rearrange("p t e -> p (t e)")
                nc.tensor.matmul(pos_ps[:, 0:TILES * NE], before[:], flat, start=True, stop=True)
                nc.tensor.matmul(tot_ps[:, 0:TILES * NE], ones[:], flat, start=True, stop=True).then_inc(counts_ready, 1)

            @block.scalar
            def _(act):
                act.wait_ge(shifted_ready, 1)
                nc.scalar.activation(probs[:], logits[:], ACT.Exp).then_inc(exp_ready, 1)

            @block.vector
            def _(dve):
                ch = Chain(dve, step)
                v = nc.vector
                dve.wait_ge(lg_ready, 1)
                lg = lg_ps[:, 0:TILES * NE].rearrange("p (t e) -> p t e", e=NE)
                if bias is not None:
                    ch.step(v.tensor_tensor(logits[:], lg, per_expert(bias), ALU.add))
                else:
                    ch.step(v.tensor_copy(logits[:], lg))
                ch.step(v.tensor_reduce(small[:], logits[:], AX, ALU.max))
                v.tensor_tensor(logits[:], logits[:], per_tile(small), ALU.subtract).then_inc(shifted_ready, 1)
                dve.wait_ge(exp_ready, 1)
                ch.step(v.tensor_reduce(small[:], probs[:], AX, ALU.add))
                ch.step(v.reciprocal(small[:], small[:]))
                ch.step(v.tensor_tensor(probs[:], probs[:], per_tile(small), ALU.mult))
                dve.wait_ge(made, 3)
                for j in range(choices):
                    w = res["weight"][j]
                    ch.step(v.tensor_reduce(w[:], probs[:], AX, ALU.max))
                    ch.step(v.tensor_tensor(scratch[:], probs[:], per_tile(w), ALU.not_equal))
                    ch.step(v.tensor_scalar(scratch[:], scratch[:], 100.0, None, ALU.mult))
                    ch.step(v.tensor_tensor(scratch[:], scratch[:], per_expert(number), ALU.add))
                    ch.step(v.tensor_reduce(small[:], scratch[:], AX, ALU.min))
                    ch.step(v.tensor_tensor(onehot[j][:], per_tile(small), per_expert(number), ALU.is_equal))
                    if j + 1 < choices:
                        ch.step(v.tensor_scalar(scratch[:], onehot[j][:], 4.0, None, ALU.mult))
                        ch.step(v.tensor_tensor(probs[:], probs[:], scratch[:], ALU.subtract))
                for j in range(choices):
                    ch.step(v.tensor_scalar(small[:], res["weight"][j][:], 0.0, None, ALU.is_gt))
                    ch.step(v.tensor_tensor(onehot[j][:], onehot[j][:], per_tile(small), ALU.mult))
                if choices == 1:
                    ins = v.tensor_copy(mask[:], onehot[0][:])
                else:
                    ins = v.tensor_tensor(mask[:], onehot[0][:], onehot[1][:], ALU.add)
                ins.then_inc(mask_ready, 1)
                dve.wait_ge(counts_ready, 1)
                tot = tot_ps[:, 0:TILES * NE].rearrange("p (t e) -> p t e", e=NE)
                ch.step(v.tensor_copy(totals[:], tot))
                ch.step(v.tensor_copy(sums_a[:], tot))
                src, dst = sums_a, sums_b
                for d in (1, 2, 4, 8):
                    ch.step(v.tensor_copy(dst[:, 0:d, :], src[:, 0:d, :]))
                    ch.step(v.tensor_tensor(dst[:, d:, :], src[:, d:, :], src[:, 0:TILES - d, :], ALU.add))
                    src, dst = dst, src
                ch.step(v.tensor_tensor(place[:], src[:], totals[:], ALU.subtract))
                ch.step(v.tensor_tensor(place[:], place[:], pos_ps[:, 0:TILES * NE].rearrange("p (t e) -> p t e", e=NE), ALU.add))
                ch.step(v.tensor_scalar(scratch[:], place[:], float(capacity), None, ALU.is_ge))
                if dropped_expert is not None:
                    ch.step(v.memset(scratch[:, :, dropped_expert:dropped_expert + 1], 1.0))
                ch.step(v.tensor_scalar(sums_a[:], scratch[:], float(BIG), None, ALU.mult))
                ch.step(v.tensor_tensor(place[:], place[:], sums_a[:], ALU.add))
                ch.step(v.tensor_scalar(small2[:, 0:NE], number[:], float(capacity), None, ALU.mult))
                ch.step(v.tensor_tensor(place[:], place[:], per_expert(small2[:, 0:NE]), ALU.add))
                ch.step(v.tensor_scalar(scratch[:], scratch[:], -1.0, 1.0, ALU.mult, ALU.add))
                for j in range(choices):
                    ch.step(v.tensor_tensor(sums_a[:], onehot[j][:], place[:], ALU.mult))
                    ch.step(v.tensor_reduce(res["slot"][j][:], sums_a[:], AX, ALU.add))
                    ch.step(v.tensor_scalar(small[:], res["weight"][j][:], 0.0, float(BIG), ALU.is_le, ALU.mult))
                    ch.step(v.tensor_tensor(res["slot"][j][:], res["slot"][j][:], small[:], ALU.add))
                    ch.step(v.tensor_tensor(sums_a[:], onehot[j][:], scratch[:], ALU.mult))
                    ch.step(v.tensor_reduce(res["keep"][j][:], sums_a[:], AX, ALU.add))
                if dropped_expert is not None:
                    noop = S.noop
                    for j in range(choices):
                        ch.step(v.tensor_tensor(small[:], onehot[j][:, :, dropped_expert], res["weight"][j][:], ALU.mult))
                        if j == 0:
                            ch.step(v.tensor_copy(noop[:], small[:]))
                        else:
                            ch.step(v.tensor_tensor(noop[:], noop[:], small[:], ALU.add))
    return res


def gated_linear(nc, name, c, wts, capacity):
    x, xnT = c["x"], c["xnT"]
    with Scope(nc, name) as S:
        r = route(nc, S, name + "r", c, wts["w_gate"], None, False, 1, capacity)
        w, bb = S.sb("w", [P, KC, DM]), S.sb("bb", [P, DM])
        prepare(nc, name + "t", c, [(w[:], wts["w_expert"].rearrange("(k p) n -> p k n", p=P)),
                                                 (bb[:], wts["b_expert"][None, :].to_broadcast([P, DM]))], [])
        y_ps = S.ps("y_ps", [P, 4, BANK])
        scale, biased = S.sb("scale", [P, TILES]), S.sb("biased", [P, 2, DM])
        y_ready, y_read, step = S.sem("y_ready"), S.sem("y_read"), S.sem("step")
        with S.block() as block:
            @block.tensor
            def _(pe):
                for t in range(TILES):
                    if t >= 4:
                        pe.wait_ge(y_read, t - 3)
                    for k in range(KC):
                        ins = nc.tensor.matmul(y_ps[:, t % 4, 0:DM], xnT[:, k, t * P:(t + 1) * P], w[:, k, :], start=k == 0, stop=k == KC - 1)
                    ins.then_inc(y_ready, 1)

            @block.vector
            def _(dve):
                ch = Chain(dve, step)
                ch.step(nc.vector.tensor_tensor(scale[:], r["weight"][0][:], r["keep"][0][:], ALU.mult))
                with dve.Fori(0, TILES // 4) as g:
                    for u in range(4):
                        t = g * 4 + u
                        dve.wait_ge(y_ready, t + 1)
                        nc.vector.tensor_tensor(biased[:, u % 2, :], y_ps[:, u, 0:DM], bb[:], ALU.add).then_inc(y_read, 1)
                        dve.wait_ge(y_read, t + 1)
                        nc.vector.scalar_tensor_tensor(out=x[:, t, :], in0=biased[:, u % 2, :], scalar=scale[:, bass.ds(t, 1)],
                                                       in1=x[:, t, :], op0=ALU.mult, op1=ALU.add).then_inc(step, 1)


def mixture(nc, name, c, wts, n_exp, choices, disp, eout, filled):
    x, xn, ident, ones = c["x"], c["xn"], c["ident"], c["ones"]
    cap = TOK // NE
    CTL = cap // P
    HID = 1024
    HC = HID // P
    l0 = choices == 2
    w1 = wts["experts_inter" if l0 else "w1"]
    w2 = wts["experts_out" if l0 else "w2"]
    rows = n_exp * cap
    with Scope(nc, name) as S:
        S.noop = S.sb("noop", [P, TILES]) if l0 else None
        if l0:
            r = route(nc, S, name + "r", c, wts["router_w"], wts["router_b"], True, 2, cap, dropped_expert=NE - 1)
        else:
            r = route(nc, S, name + "r", c, wts["wg"], None, False, 1, cap)
        slot_i = [S.sb(f"slot_i{j}", [P, TILES], U32) for j in range(choices)]
        back_i = [S.sb(f"back_i{j}", [P, TILES], U32) for j in range(choices)]
        back_f = S.sb("back_f", [P, TILES])
        w1_sb, w2_sb = S.sb("w1", [P, 2, KC, HID]), S.sb("w2", [P, 2, HC, DM])
        b1_sb = None if l0 else S.sb("b1", [P, NE, HC])
        b2_sb = None if l0 else S.sb("b2", [1, NE, DM])
        if not l0:
            with Scope(nc, name + "b") as B:
                rawb = B.sb("rawb", [NE * HC, P])
                prepare(nc, name + "bt", c, [(rawb[:], wts["b1"].rearrange("e (c p) -> (e c) p", p=P))],
                                  [(b1_sb[:].rearrange("p e c -> p (e c)"), rawb[:])])
        xe = S.sb("xe", [P, 2, CTL, DM])
        xeT = S.sb("xeT", [P, 2, KC, cap])
        hT = S.sb("hT", [P, 2, HC, cap])
        ye = S.sb("ye", [P, 2, CTL, DM])
        back = S.sb("back", [P, 2, 4, DM])
        (index_ready, scattered, loaded0, loaded1, bias_loaded, stored0, stored1, xeT_ready, xeT_copied, h_ready, h_copied,
         y_ready, y_copied, added, step) = (S.sem(n) for n in (
             "index_ready", "scattered", "loaded0", "loaded1", "bias_loaded", "stored0", "stored1", "xeT_ready", "xeT_copied",
             "h_ready", "h_copied", "y_ready", "y_copied", "added", "step"))
        loaded, stored = (loaded0, loaded1), (stored0, stored1)
        h_copied_d = S.sem("h_copied_d")
        gathered = [S.sem(f"gathered{n}") for n in range(8)]
        x_loaded = (S.sem("x_loaded0"), S.sem("x_loaded1"))
        t_ps = S.ps("t_ps", [P, KC, cap])
        h_ps = S.ps("h_ps", [P, 4, BANK])
        y_ps = S.ps("y_ps", [P, 2, BANK])

        def experts(eng, body):
            with eng.Fori(0, n_exp // 2) as g:
                for u in range(2):
                    body(g * 2 + u, u, g)
            if n_exp % 2:
                body(n_exp - 1, 0, n_exp // 2)

        def experts_ahead(eng, body):
            with eng.Fori(0, (n_exp - 1) // 2) as g:
                for u in range(2):
                    body(g * 2 + u, u, g, True)
            for e in range((n_exp - 1) // 2 * 2, n_exp):
                body(e, e % 2, e // 2, e + 1 < n_exp)

        with S.block() as block:
            @block.vector
            def _(dve):
                ch = Chain(dve, step)
                for j in range(choices):
                    ch.step(nc.vector.tensor_scalar(back_f[:], r["slot"][j][:], float(rows - 1), None, ALU.min))
                    ch.step(nc.vector.tensor_copy(back_i[j][:], back_f[:]))
                    ch.step(nc.vector.tensor_tensor(r["weight"][j][:], r["weight"][j][:], r["keep"][j][:], ALU.mult))
                    nc.vector.tensor_copy(slot_i[j][:], r["slot"][j][:]).then_inc(index_ready, 1)

                def turned(e, u):
                    dve.wait_ge(xeT_ready, e + 1)
                    nc.vector.tensor_copy(xeT[:, u], t_ps[:]).then_inc(xeT_copied, 1)

                def body(e, u, turn, more):
                    for m in range(1, HC, 2):
                        dve.wait_ge(h_ready, e * HC + (m + 1))
                        if l0:
                            ins = nc.vector.tensor_scalar(hT[:, u, m, :], h_ps[:, m % 4, 0:cap], 0.0, None, ALU.max)
                        else:
                            ins = nc.vector.tensor_scalar(hT[:, u, m, :], h_ps[:, m % 4, 0:cap], b1_sb[:, bass.ds(e, 1), m], 0.0, ALU.add, ALU.max)
                        ins.then_inc(h_copied_d, 1)
                    if more:
                        turned(e + 1, 1 - u)
                    dve.wait_ge(y_ready, e * CTL + 2)
                    dve.wait_ge(stored[u], 16 * turn + 16)
                    nc.vector.tensor_copy(ye[:, u], y_ps[:, :, 0:DM]).then_inc(y_copied, 1)

                turned(0, 0)
                experts_ahead(dve, body)
                for k in range(TILES * choices // 4):
                    for i in range(4):
                        t, j = (k * 4 + i) // choices, (k * 4 + i) % choices
                        dve.wait_ge(gathered[k % 2 * 4 + i], 16 * (k // 2 + 1))
                        ins = nc.vector.scalar_tensor_tensor(out=x[:, t, :], in0=back[:, k % 2, i, :], scalar=r["weight"][j][:, t:t + 1],
                                                             in1=x[:, t, :], op0=ALU.mult, op1=ALU.add)
                        ins.then_inc(added, 1)
                        dve.wait_ge(added, k * 4 + i + 1)
                if l0:
                    for t in range(TILES):
                        nc.vector.scalar_tensor_tensor(out=x[:, t, :], in0=xn[:, t, :], scalar=S.noop[:, t:t + 1],
                                                       in1=x[:, t, :], op0=ALU.mult, op1=ALU.add)

            @block.gpsimd
            def _(pool):
                pool.wait_ge(filled, 16)
                pool.wait_ge(index_ready, choices)
                for t in range(TILES):
                    for j in range(choices):
                        nc.gpsimd.indirect_dma_start(out=disp, out_offset=bass.IndirectOffsetOnAxis(ap=slot_i[j][:, t:t + 1], axis=0),
                                                     in_=xn[:, t, :], in_offset=None, bounds_check=rows - 1,
                                                     oob_is_err=False).then_inc(scattered, 16)
                pool.wait_ge(stored0, 16 * (1 + (n_exp + 1) // 2))
                pool.wait_ge(stored1, 16 * (1 + n_exp // 2))
                for k in range(TILES * choices // 4):
                    if k >= 2:
                        pool.wait_ge(added, 4 * (k - 1))
                    for i in range(4):
                        t, j = (k * 4 + i) // choices, (k * 4 + i) % choices
                        nc.gpsimd.indirect_dma_start(out=back[:, k % 2, i, :], out_offset=None, in_=eout,
                                                     in_offset=bass.IndirectOffsetOnAxis(ap=back_i[j][:, t:t + 1], axis=0),
                                                     bounds_check=rows - 1, oob_is_err=False).then_inc(gathered[k % 2 * 4 + i], 16)

            @block.sync
            def _(sp):
                sp.sem_inc(stored0, 16)
                sp.sem_inc(stored1, 16)
                if not l0:
                    sp.dma_start(b2_sb[0:1], wts["b2"][None, :, :]).then_inc(bias_loaded, 16)

                def weights(e, u, turn):
                    sp.dma_start(w1_sb[:, u], w1[bass.ds(e, 1)].rearrange("e (k p) n -> p (e k) n", p=P)).then_inc(loaded[u], 16)
                    sp.dma_start(w2_sb[:, u], w2[bass.ds(e, 1)].rearrange("e (k p) n -> p (e k) n", p=P)).then_inc(loaded[u], 16)

                def inputs(e, u, turn):
                    sp.dma_start(xe[:, u], disp[bass.ds(e * cap, cap), :].rearrange("(t p) d -> p t d", p=P)).then_inc(x_loaded[u], 16)

                weights(0, 0, 0)
                weights(1, 1, 0)
                sp.wait_ge(scattered, 16 * TILES * choices)
                inputs(0, 0, 0)
                inputs(1, 1, 0)
                with sp.Fori(0, n_exp // 2 - 1) as g:
                    for u in range(2):
                        sp.wait_ge(xeT_ready, g * 2 + (u + 1))
                        inputs(g * 2 + (u + 2), u, g)
                        sp.wait_ge(y_ready, (g * 2 + u + 1) * CTL)
                        weights(g * 2 + (u + 2), u, g)
                if n_exp % 2:
                    sp.wait_ge(xeT_ready, n_exp - 2)
                    inputs(n_exp - 1, 0, 0)
                    sp.wait_ge(y_ready, (n_exp - 2) * CTL)
                    weights(n_exp - 1, 0, 0)
                sp.wait_ge(stored0, 16 * (1 + (n_exp + 1) // 2))
                sp.wait_ge(stored1, 16 * (1 + n_exp // 2))

            @block.tensor
            def _(pe):
                def turn_rows(e, u, turn):
                    pe.wait_ge(x_loaded[u], 16 * turn + 16)
                    pe.wait_ge(xeT_copied, e + 1)
                    for k in range(KC):
                        for s in range(CTL):
                            ins = nc.tensor.transpose(t_ps[:, k, s * P:(s + 1) * P], xe[:, u, s, k * P:(k + 1) * P], ident[:])
                    ins.then_inc(xeT_ready, 1)

                def body(e, u, turn, more):
                    pe.wait_ge(loaded[u], 32 * turn + 32)
                    pe.wait_ge(xeT_copied, e + 2)
                    for m in range(HC):
                        pe.wait_ge(h_copied_d if m % 2 else h_copied, e * (HC // 2) + (m // 2 + 1))
                        for k in range(KC):
                            ins = nc.tensor.matmul(h_ps[:, m % 4, 0:cap], w1_sb[:, u, k, m * P:(m + 1) * P], xeT[:, u, k, :],
                                                   start=k == 0, stop=k == KC - 1)
                        ins.then_inc(h_ready, 1)
                    if more:
                        turn_rows(e + 1, 1 - u, turn + u)
                    pe.wait_ge(h_copied, e * (HC // 2) + (HC // 2 + 2))
                    pe.wait_ge(h_copied_d, e * (HC // 2) + (HC // 2 + 2))
                    pe.wait_ge(y_copied, e + 1)
                    for s in range(CTL):
                        for m in range(HC):
                            ins = nc.tensor.matmul(y_ps[:, s, 0:DM], hT[:, u, m, s * P:(s + 1) * P], w2_sb[:, u, m, :],
                                                   start=m == 0, stop=m == HC - 1 and l0)
                        if not l0:
                            ins = nc.tensor.matmul(y_ps[:, s, 0:DM], ones[0:1, :], b2_sb[0:1, bass.ds(e, 1), :].rearrange("o e n -> o (e n)"), start=False, stop=True)
                        ins.then_inc(y_ready, 1)

                pe.sem_inc(xeT_copied, 1)
                pe.sem_inc(h_copied, 2)
                pe.sem_inc(h_copied_d, 2)
                pe.sem_inc(y_copied, 1)
                if not l0:
                    pe.wait_ge(bias_loaded, 16)
                turn_rows(0, 0, 0)
                experts_ahead(pe, body)

            @block.scalar
            def _(act):
                def body(e, u, turn):
                    for m in range(0, HC, 2):
                        act.wait_ge(h_ready, e * HC + (m + 1))
                        bias = 0.0 if l0 else b1_sb[:, bass.ds(e, 1), m]
                        nc.scalar.activation(hT[:, u, m, :], h_ps[:, m % 4, 0:cap], ACT.Relu, bias=bias).then_inc(h_copied, 1)
                    act.wait_ge(y_copied, e + 2)
                    act.dma_start(eout[bass.ds(e * cap, cap), :].rearrange("(t p) d -> p t d", p=P), ye[:, u]).then_inc(stored[u], 16)

                experts(act, body)


ROUND = 1.5 * 2.0 ** 23
QMAX = 32767.0


def quantised_ffn(nc, name, c, wts):
    x, xn, xnT, ident, ones = c["x"], c["xn"], c["xnT"], c["ident"], c["ones"]
    FF = 768
    FC = FF // P
    QB = 32
    with Scope(nc, name) as S:
        wT = S.sb("wT", [P, 2, KC, FF])
        wdT = S.sb("wdT", [P, FC, DM])
        with Scope(nc, name + "w") as R:
            raw = R.sb("raw", [P, 3, FC * DM])
            q = R.sb("q", [P, 3, FC * DM])
            NB = 3 * FC * DM // QB
            peak, inv = R.sb("peak", [P, NB]), R.sb("inv", [P, NB])
            prepare(nc, name + "l", c, [
                (raw[:, 0].rearrange("p (t n) -> p t n", n=DM), wts["w_up"].rearrange("(t p) n -> p t n", p=P)),
                (raw[:, 1].rearrange("p (t n) -> p t n", n=DM), wts["w_gate"].rearrange("(t p) n -> p t n", p=P)),
                (raw[:, 2].rearrange("p (t n) -> p t n", n=FF), wts["w_down"].rearrange("(t p) n -> p t n", p=P))], [])
            step = R.sem("step")
            with R.block() as block:
                @block.vector
                def _(dve):
                    ch, v = Chain(dve, step), nc.vector
                    blocks = raw[:].rearrange("p a (b k) -> p (a b) k", k=QB)
                    qb = q[:].rearrange("p a (b k) -> p (a b) k", k=QB)
                    ch.step(v.tensor_reduce(peak[:], blocks, AX, ALU.max, apply_absolute_value=True))
                    ch.step(v.tensor_scalar(peak[:], peak[:], 1.0 / 7.0, 1e-12, ALU.mult, ALU.max))
                    ch.step(v.reciprocal(inv[:], peak[:]))
                    ch.step(v.tensor_tensor(qb, blocks, inv[:, :, None].to_broadcast([P, NB, QB]), ALU.mult))
                    ch.step(v.tensor_scalar(q[:], q[:], ROUND, ROUND, ALU.add, ALU.subtract))
                    ch.step(v.tensor_scalar(q[:], q[:], -8.0, 7.0, ALU.max, ALU.min))
                    ch.step(v.tensor_tensor(qb, qb, peak[:, :, None].to_broadcast([P, NB, QB]), ALU.mult))
            jobs = []
            for n in range(2):
                for t in range(FC):
                    for k in range(KC):
                        jobs.append((wT[:, n, k, t * P:(t + 1) * P], q[:, n, t * DM + k * P:t * DM + (k + 1) * P]))
            for t in range(KC):
                for k in range(FC):
                    jobs.append((wdT[:, k, t * P:(t + 1) * P], q[:, 2, t * FF + k * P:t * FF + (k + 1) * P]))
            prepare(nc, name + "t", c, [], jobs)

        up, gate = S.sb("up", [P, FC, TOK]), S.sb("gate", [P, FC, TOK])
        scratch = xn[:].rearrange("p t n -> p (t n)").rearrange("p (u n) -> p u n", u=2)
        QN = 5
        peaks = S.sb("peaks", [P, QN, FC])
        peak = S.sb("peak", [P, QN])
        row = S.sb("row", [1, QN, 2])
        scale = S.sb("scale", [P, QN, 2])
        ff_ps = S.ps("ff_ps", [P, 4, BANK])
        r_ps = S.ps("r_ps", [P, BANK])
        y_ps = S.ps("y_ps", [P, 2, BANK])
        (step, peak_ready, row_ps_ready, row_ready, all_ready, x_quantised, ff_ready, ff_copied, rounded, sig_ready, o_ready,
         y_ready, y_added) = (S.sem(n) for n in ("step", "peak_ready", "row_ps_ready", "row_ready", "all_ready", "x_quantised", "ff_ready",
                                                 "ff_copied", "rounded", "sig_ready", "o_ready", "y_ready", "y_added"))
        round_col = S.sb("round_col", [P, 1])
        scale_ready, scaled, sig_made, sig_used = (S.sem(n) for n in ("scale_ready", "scaled", "sig_made", "sig_used"))
        with S.block() as block:
            @block.vector
            def _(dve):
                ch, v = Chain(dve, step), nc.vector
                ch.step(v.memset(round_col[:], ROUND))

                def find_scale(n, cols):
                    v.tensor_reduce(peak[:, n:n + 1], peaks[:, n, 0:cols], AX, ALU.max).then_inc(peak_ready, 1)
                    dve.wait_ge(row_ps_ready, n + 1)
                    ch.step(v.tensor_reduce(row[0:1, n, 0:1], r_ps[0:1, 0:P], AX, ALU.max))
                    ch.step(v.tensor_scalar(row[0:1, n, 0:1], row[0:1, n, 0:1], 1.0 / QMAX, 1e-12, ALU.mult, ALU.max))
                    v.reciprocal(row[0:1, n, 1:2], row[0:1, n, 0:1]).then_inc(row_ready, 1)
                    dve.wait_ge(all_ready, n + 1)
                    v.tensor_copy(scale[:, n, :], r_ps[:, 256:258]).then_inc(scale_ready, 1)
                    dve.wait_ge(scale_ready, n + 1)

                def quantise(n, a):
                    ch.step(v.tensor_scalar(a, a, scale[:, n, 1:2], ROUND, ALU.mult, ALU.add))
                    return back(n, a)

                def back(n, a):
                    return v.tensor_scalar(a, a, ROUND, scale[:, n, 0:1], ALU.subtract, ALU.mult)

                ch.step(v.tensor_reduce(peaks[:, 0, 0:1], xnT[:].rearrange("p k n -> p (k n)"), AX, ALU.max, apply_absolute_value=True))
                find_scale(0, 1)
                quantise(0, xnT[:].rearrange("p k n -> p (k n)")).then_inc(x_quantised, 1)
                for n, a in enumerate((up, gate)):
                    for m in range(FC):
                        dve.wait_ge(ff_copied, (n * FC + m + 1) * NBLK)
                        ch.step(v.tensor_reduce(peaks[:, 1 + n, m:m + 1], a[:, m, :], AX, ALU.max, apply_absolute_value=True))
                    find_scale(1 + n, FC)
                    if n == 0:
                        for m in range(FC):
                            ch.step(quantise(1, up[:, m, :]))

                def gate_back(m):
                    dve.wait_ge(scaled, m + 1)
                    back(2, gate[:, m, :]).then_inc(rounded, 1)

                gate_back(0)
                for m in range(FC):
                    if m + 1 < FC:
                        gate_back(m + 1)
                    s = scratch[:, m % 2, :]
                    dve.wait_ge(sig_ready, m + 1)
                    dve.wait_ge(rounded, m + 1)
                    ch.step(v.tensor_scalar(s, s, ROUND, 0.0, ALU.subtract, ALU.max))
                    ch.step(v.tensor_scalar(s, s, 65535.0, 1.0 / 65536.0, ALU.min, ALU.mult))
                    v.tensor_tensor(gate[:, m, :], gate[:, m, :], s, ALU.mult).then_inc(sig_used, 1)
                    dve.wait_ge(sig_used, m + 1)
                    ch.step(v.tensor_reduce(peaks[:, 3, m:m + 1], gate[:, m, :], AX, ALU.max, apply_absolute_value=True))
                find_scale(3, FC)
                for m in range(FC):
                    dve.wait_ge(scaled, FC + m + 1)
                    ch.step(back(3, gate[:, m, :]))
                    ch.step(v.tensor_tensor(up[:, m, :], up[:, m, :], gate[:, m, :], ALU.mult))
                    ch.step(v.tensor_reduce(peaks[:, 4, m:m + 1], up[:, m, :], AX, ALU.max, apply_absolute_value=True))
                find_scale(4, FC)
                for b in range(NBLK):
                    dve.wait_ge(scaled, 2 * FC + b + 1)
                    back(4, up[:, :, b * BANK:(b + 1) * BANK]).then_inc(o_ready, 1)
                with dve.Fori(0, TILES // 2) as g:
                    for u in range(2):
                        dve.wait_ge(y_ready, g * 2 + (u + 1))
                        v.tensor_tensor(x[:, g * 2 + u, :], x[:, g * 2 + u, :], y_ps[:, u, 0:DM], ALU.add).then_inc(y_added, 1)

            @block.tensor
            def _(pe):
                def share_peak(n):
                    pe.wait_ge(peak_ready, n + 1)
                    nc.tensor.transpose(r_ps[0:1, 0:P], peak[:, n:n + 1], ident[:]).then_inc(row_ps_ready, 1)
                    pe.wait_ge(row_ready, n + 1)
                    nc.tensor.matmul(r_ps[:, 256:258], ones[0:1, :], row[0:1, n, :], start=True, stop=True).then_inc(all_ready, 1)

                share_peak(0)
                pe.wait_ge(x_quantised, 1)
                for n in range(2):
                    for m in range(FC):
                        for b in range(NBLK):
                            j = (n * FC + m) * NBLK + b
                            if j >= 4:
                                pe.wait_ge(ff_copied, j - 3)
                            for k in range(KC):
                                ins = nc.tensor.matmul(ff_ps[:, j % 4, :], wT[:, n, k, m * P:(m + 1) * P], xnT[:, k, b * BANK:(b + 1) * BANK],
                                                       start=k == 0, stop=k == KC - 1)
                            ins.then_inc(ff_ready, 1)
                    share_peak(1 + n)
                share_peak(3)
                share_peak(4)
                for t in range(TILES):
                    if t % QT == 0:
                        pe.wait_ge(o_ready, t // QT + 1)
                    if t >= 2:
                        pe.wait_ge(y_added, t - 1)
                    for m in range(FC):
                        ins = nc.tensor.matmul(y_ps[:, t % 2, 0:DM], up[:, m, t * P:(t + 1) * P], wdT[:, m, :], start=m == 0, stop=m == FC - 1)
                    ins.then_inc(y_ready, 1)

            @block.scalar
            def _(act):
                NT = FC * NBLK
                for j in range(2 * NT):
                    act.wait_ge(ff_ready, j + 1)
                    a, i = (up, gate)[j // NT], j % NT
                    nc.scalar.copy(a[:, i // NBLK, i % NBLK * BANK:(i % NBLK + 1) * BANK], ff_ps[:, j % 4, :]).then_inc(ff_copied, 1)

                def multiples(n, a):
                    act.wait_ge(scale_ready, n + 1)
                    nc.scalar.activation(a, a, ACT.Identity, bias=round_col[:], scale=scale[:, n, 1:2]).then_inc(scaled, 1)

                def sigmoid(m):
                    act.wait_ge(rounded, m + 1)
                    if m >= 2:
                        act.wait_ge(sig_used, m - 1)
                    s = scratch[:, m % 2, :]
                    nc.scalar.activation(s, gate[:, m, :], ACT.Sigmoid).then_inc(sig_made, 1)
                    act.wait_ge(sig_made, m + 1)
                    nc.scalar.activation(s, s, ACT.Identity, bias=round_col[:], scale=65536.0).then_inc(sig_ready, 1)

                for m in range(FC):
                    multiples(2, gate[:, m, :])
                    if m:
                        sigmoid(m - 1)
                sigmoid(FC - 1)
                for m in range(FC):
                    multiples(3, gate[:, m, :])
                for b in range(NBLK):
                    multiples(4, up[:, :, b * BANK:(b + 1) * BANK])


def state_space(nc, name, c, wts):
    x, xn, xnT, ident = c["x"], c["xn"], c["xnT"], c["ident"]
    NS = 64
    ROUNDS = 9
    with Scope(nc, name) as S:
        bT = S.sb("bT", [P, 2, KC, P])
        cT = S.sb("cT", [P, DM])
        pw = S.sb("pw", [P, 2, 2, P])
        gb = S.sb("gb", [P, 2, DM])
        with Scope(nc, name + "w") as R:
            rawb, rawc = R.sb("rawb", [NS, DM]), R.sb("rawc", [P, KC, 2, NS])
            with R.block() as block:
                @block.vector
                def _(dve):
                    nc.vector.memset(bT[:], 0.0)
                    nc.vector.memset(pw[:], 0.0)
            loads = [(rawb[:], wts["B"]), (pw[0:NS, 0, 0, 0:NS], wts["A"]), (pw[NS:P, 0, 0, NS:P], wts["A"])]
            loads += [(rawc[:, :, n, :], wts["C"].rearrange("(k p) n -> p k n", p=P)) for n in range(2)]
            loads += [(gb[:, j, :], wts[g][None, :].to_broadcast([P, DM])) for j, g in enumerate(("gamma", "beta"))]
            jobs = [(bT[:, h, k, h * NS:(h + 1) * NS], rawb[:, k * P:(k + 1) * P]) for h in range(2) for k in range(KC)]
            jobs += [(cT[:, k * P:(k + 1) * P], rawc[:, k].rearrange("p a n -> p (a n)")) for k in range(KC)]
            jobs += [(pw[:, 0, 1, :], pw[:, 0, 0, :])]
            prepare(nc, name + "t", c, loads, jobs)

        X = S.sb("X", [P, 2, SEQ])
        u_ps = S.ps("u_ps", [P, 2, BANK])
        p_ps = S.ps("p_ps", [P, 2, BANK])
        y_ps = S.ps("y_ps", [P, 4, BANK])
        u_ready, added, p_ready, p_copied, y_ready, y_free = (S.sem(n) for n in ("u_ready", "added", "p_ready", "p_copied", "y_ready", "y_free"))
        with S.block() as block:
            @block.tensor
            def _(pe):
                for bb in range(2):
                    for h in range(2):
                        for k in range(KC):
                            ins = nc.tensor.matmul(u_ps[:, bb, :], bT[:, h, k, :], xnT[:, k, (2 * h + bb) * SEQ:(2 * h + bb + 1) * SEQ],
                                                   start=h == 0 and k == 0, stop=h == 1 and k == KC - 1)
                ins.then_inc(u_ready, 1)
                for r in range(ROUNDS):
                    s, i = 1 << r, r % 2
                    pe.wait_ge(added, r + 1)
                    if r:
                        pe.wait_ge(p_copied, r)
                    for bb in range(2):
                        ins = nc.tensor.matmul(u_ps[:, bb, 0:SEQ - s], pw[:, i, 1, :], X[:, bb, 0:SEQ - s], start=True, stop=True)
                    ins.then_inc(u_ready, 1)
                    if r + 1 < ROUNDS:
                        nc.tensor.matmul(p_ps[:, 0, 0:P], pw[:, i, 1, :], pw[:, i, 0, :], start=True, stop=True)
                        nc.tensor.matmul(p_ps[:, 1, 0:P], pw[:, i, 0, :], pw[:, i, 1, :], start=True, stop=True).then_inc(p_ready, 1)
                pe.wait_ge(added, ROUNDS + 1)
                for t in range(TILES):
                    b, q = t // QT, t % QT
                    h, bb = b // 2, b % 2
                    if t >= 4:
                        pe.wait_ge(y_free, t - 3)
                    nc.tensor.matmul(y_ps[:, t % 4, 0:DM], X[h * NS:(h + 1) * NS, bb, q * P:(q + 1) * P], cT[h * NS:(h + 1) * NS, :],
                                     start=True, stop=True).then_inc(y_ready, 1)

            @block.vector
            def _(dve):
                dve.wait_ge(u_ready, 1)
                nc.vector.tensor_copy(X[:], u_ps[:]).then_inc(added, 1)
                for r in range(ROUNDS):
                    s = 1 << r
                    dve.wait_ge(u_ready, r + 2)
                    nc.vector.tensor_tensor(X[:, :, s:], X[:, :, s:], u_ps[:, :, 0:SEQ - s], ALU.add).then_inc(added, 1)

            @block.scalar
            def _(act):
                for r in range(ROUNDS - 1):
                    act.wait_ge(p_ready, r + 1)
                    nc.scalar.copy(pw[:, (r + 1) % 2], p_ps[:, :, 0:P]).then_inc(p_copied, 1)
                for t in range(TILES):
                    act.wait_ge(y_ready, t + 1)
                    nc.scalar.activation(xn[:, t, :], y_ps[:, t % 4, 0:DM], ACT.Gelu).then_inc(y_free, 1)

        st, mean, rstd, tmp = S.sb("st", [P, TILES, 6]), S.sb("mean", [P, TILES]), S.sb("rstd", [P, TILES]), S.sb("tmp", [P, TILES])
        base = S.sb("base", [P, TILES, DM])
        low = S.sb("low", [P, TILES, DM])
        finite = S.sb("finite", [P, TILES, DM], I32)
        step, var_ready, std_ready = S.sem("step"), S.sem("var_ready"), S.sem("std_ready")
        with S.block() as block:
            @block.vector
            def _(dve):
                ch, v = Chain(dve, step), nc.vector
                for i in range(TILES):
                    ins = v.bn_stats(st[:, i, :], xn[:, i, :])
                ch.step(ins)
                row_stats_to_affine(nc, ch, st, mean[:], rstd[:], tmp[:], DM // 2)
                v.tensor_copy(tmp[:], rstd[:]).then_inc(var_ready, 1)
                dve.wait_ge(std_ready, 1)
                ch.step(v.reciprocal(rstd[:], tmp[:]))
                for i in range(TILES):
                    ins = v.tensor_scalar(xn[:, i, :], xn[:, i, :], mean[:, i:i + 1], rstd[:, i:i + 1], ALU.subtract, ALU.mult)
                ch.step(ins)
                ch.step(v.tensor_tensor(xn[:], xn[:], gb[:, None, 0, :].to_broadcast([P, TILES, DM]), ALU.mult))
                ch.step(v.tensor_tensor(xn[:], xn[:], gb[:, None, 1, :].to_broadcast([P, TILES, DM]), ALU.add))
                ch.step(v.tensor_scalar(base[:], xn[:], 0.0, 1e6, ALU.max, ALU.min))
                ch.step(v.tensor_scalar(low[:], xn[:], 0.0, -1e6, ALU.min, ALU.max))
                ch.step(v.tensor_tensor(base[:], base[:], low[:], ALU.add))
                ch.step(v.tensor_scalar(finite[:], xn[:], 0.0, 0.0, ALU.mult, ALU.is_equal))
                ch.step(v.copy_predicated(base[:], finite[:], xn[:]))
                v.tensor_tensor(x[:], x[:], base[:], ALU.add)

            @block.scalar
            def _(act):
                act.wait_ge(var_ready, 1)
                nc.scalar.activation(tmp[:], tmp[:], ACT.Sqrt).then_inc(std_ready, 1)


def selective_scan(nc, name, c, wts):
    x, xn, xnT, ident, ones = c["x"], c["xn"], c["xnT"], c["ident"], c["ones"]
    DI, NST, TAPS = 512, 16, 4
    C4 = DI // P
    NX = 2 * NST + 1
    with Scope(nc, name) as S:
        winT = S.sb("winT", [P, KC, 2 * DI])
        wxT = S.sb("wxT", [P, C4, NX])
        woutT = S.sb("woutT", [P, C4, DM])
        cols = S.sb("cols", [P, 6, C4])
        conv_w = S.sb("conv_w", [P, C4, TAPS])
        A = S.sb("A", [P, NST])
        sel = S.sb("sel", [P, 2 * NST, P], BF16)
        hmax = S.sb("hmax", [P, BATCH * NST + 1])
        flag_f, flag = S.sb("flag_f", [P, 2]), S.sb("flag", [P, 1], I32)
        with Scope(nc, name + "w") as R:
            raw_in, raw_out, raw_x = R.sb("raw_in", [P, 8, DM]), R.sb("raw_out", [P, KC, DI]), R.sb("raw_x", [NX, DI])
            made, a_ready = R.sem("made"), R.sem("a_ready")
            loads = [(raw_in[:], wts["W_in"].rearrange("(t p) d -> p t d", p=P)), (raw_out[:], wts["W_out"].rearrange("(t p) d -> p t d", p=P)),
                     (raw_x[0:NX - 1], wts["W_x"][1:NX]), (raw_x[NX - 1:NX], wts["W_x"][0:1]),
                     (cols[:, 5, :], wts["W_dt"].rearrange("(c p) o -> p (c o)", p=P)),
                     (conv_w[:], wts["conv_w"].rearrange("(c p) o k -> p c (o k)", p=P)),
                     (A[:], wts["A_log"][None, :].to_broadcast([P, NST]))]
            for j, n in enumerate(("conv_b", "b_dt", "D_param", "ln_g", "ln_b")):
                loads.append((cols[:, j, :], wts[n].rearrange("(c p) -> p c", p=P)))
            jobs = [(winT[:, k, t * P:(t + 1) * P], raw_in[:, t, k * P:(k + 1) * P]) for t in range(8) for k in range(KC)]
            jobs += [(wxT[:, k, :], raw_x[:, k * P:(k + 1) * P]) for k in range(C4)]
            jobs += [(woutT[:, k, t * P:(t + 1) * P], raw_out[:, t, k * P:(k + 1) * P]) for t in range(KC) for k in range(C4)]
            with nc.allow_non_contiguous_dma(reason="per-channel vectors"):
                prepare(nc, name + "t", c, loads, jobs)
            with R.block() as block:
                @block.gpsimd
                def _(pool):
                    ch = Chain(pool, made)
                    ch.step(nc.gpsimd.memset(sel[:], 0.0))
                    for n in range(3):
                        ch.step(nc.gpsimd.affine_select(out=sel[:], in_=sel[:], compare_op=ALU.not_equal, fill=1.0, base=-2 * NST * n,
                                                        pattern=[[-1, 2 * NST], [0, P]], channel_multiplier=1))

                @block.vector
                def _(dve):
                    nc.vector.memset(hmax[:], 0.0)
                    nc.vector.tensor_scalar(A[:], A[:], 5.0, None, ALU.min).then_inc(a_ready, 1)
                    dve.wait_ge(a_ready, 2)
                    nc.vector.tensor_scalar(A[:], A[:], -1.0, None, ALU.mult)

                @block.scalar
                def _(act):
                    act.wait_ge(a_ready, 1)
                    nc.scalar.activation(A[:], A[:], ACT.Exp).then_inc(a_ready, 1)

        T = {n: S.sb(n, shape) for n, shape in dict(
            u=[P, BATCH, C4, SEQ], dt=[P, BATCH, C4, SEQ], dtu=[P, C4, SEQ], dA=[P, 3, C4, SEQ], w=[P, 2, C4, SEQ],
            h=[P, 2, C4, SEQ], rs=[P, SEQ]).items()}
        T["xd3"] = S.sb("xd3", [P, BATCH, SEQ], BF16)
        gate_dram = nc.dram_tensor(f"{name}_gate", [BATCH, P, C4, SEQ], F32, kind="Internal").ap()
        big, b_ps, c_ps = S.ps("big", [P, 4, BANK]), S.ps("b_ps", [P, 2, BANK]), S.ps("c_ps", [P, 2, BANK])
        one_pass = dict(nc=nc, c=c, T=T, ps=(big, b_ps, c_ps), w=(winT, wxT, woutT, cols, conv_w, A, sel), hmax=hmax,
                        gate_dram=gate_dram, dims=(DI, NST, TAPS, C4, NX))
        with S.block() as block:
            @block.vector
            def _(dve):
                nc.vector.memset(T["xd3"][:], 0.0)
        with Scope(nc, name + "f") as F:
            scan_pass(F, name + "f", flag=None, **one_pass)
        with Scope(nc, name + "g") as F:
            step, summed, bad = F.sem("step"), F.sem("summed"), F.sem("bad")
            with F.block() as block:
                @block.vector
                def _(dve):
                    ch, v = Chain(dve, step), nc.vector
                    ch.step(v.tensor_reduce(flag_f[:, 0:1], A[:], AX, ALU.max, apply_absolute_value=True))
                    ch.step(v.tensor_scalar(flag_f[:, 0:1], flag_f[:, 0:1], 1.99, 1000.0, ALU.is_gt, ALU.mult))
                    ch.step(v.tensor_copy(hmax[:, BATCH * NST:], flag_f[:, 0:1]))
                    ch.step(v.tensor_reduce(flag_f[:, 0:1], hmax[:], AX, ALU.max))
                    v.tensor_scalar(flag_f[:, 1:2], flag_f[:, 0:1], 69.9, None, ALU.is_gt).then_inc(bad, 1)
                    dve.wait_ge(summed, 1)
                    ch.step(v.tensor_scalar(flag[:], b_ps[:, 0, 0:1], 0.5, None, ALU.is_gt))

                @block.tensor
                def _(pe):
                    pe.wait_ge(bad, 1)
                    nc.tensor.matmul(b_ps[:, 0, 0:1], ones[:], flag_f[:, 1:2], start=True, stop=True).then_inc(summed, 1)
        with Scope(nc, name + "s") as F:
            scan_pass(F, name + "s", flag=flag, **one_pass)
        with S.block() as block:
            @block.vector
            def _(dve):
                nc.vector.tensor_tensor(x[:], x[:], xn[:], ALU.add)


def scan_pass(F, name, nc, c, T, ps, w, hmax, gate_dram, dims, flag):
    def run(eng, program):
        if flag is None:
            program()
            return
        with eng.If(eng.value_load(flag[0:1, 0:1], min_val=0, max_val=1) != 0):
            program()

    for part, block in (("i", scan_inputs), ("r", scan_states), ("o", scan_outputs)):
        with Scope(nc, name + part) as G:
            block(G, nc, c, T, ps, w, hmax, gate_dram, dims, flag is not None, run)


def scan_inputs(G, nc, c, T, ps, w, hmax, gate_dram, dims, exact, run):
    xnT = c["xnT"]
    winT, wxT, woutT, cols, conv_w, A, sel = w
    big, b_ps, c_ps = ps
    DI, NST, TAPS, C4, NX = dims
    u, dt, xd, xd3 = T["u"], T["dt"], T["rs"][0:NX], T["xd3"]
    xc = T["h"][:].rearrange("p a c t -> p (a c t)")[:, 0:C4 * (SEQ + TAPS - 1)].rearrange("p (c t) -> p c t", c=C4)
    conv, gate, pre, softplus = T["w"][:, 0], T["w"][:, 1], T["dA"][:, 0], T["dA"][:, 1]
    CONV_B, B_DT, W_DT = 0, 1, 5
    NR = 2 * NST
    (xc_ready, z_ready, xc_read, z_done, z_stored, conv_ready, u_ready, xd_ready, xd_copied, split_done, dt_ps_ready, pre_ready, sp_ready,
     conv_step, split_step, dt_step, act_step, taken) = (G.sem(n) for n in (
         "xc_ready", "z_ready", "xc_read", "z_done", "z_stored", "conv_ready", "u_ready", "xd_ready", "xd_copied", "split_done",
         "dt_ps_ready", "pre_ready", "sp_ready", "conv_step", "split_step", "dt_step", "act_step", "taken"))

    def batches(eng, first, both, last):
        first(0)
        both(0)
        with eng.Fori(1, BATCH - 1) as b:
            both(b)
        last(BATCH - 1)

    with G.block() as block:
        @block.tensor
        def _(pe):
            def project(b, half):
                for m in range(half * C4, (half + 1) * C4):
                    if half:
                        pe.wait_ge(xc_read, b * C4 + (m - C4 + 1))
                    elif not (isinstance(b, int) and b == 0):
                        pe.wait_ge(z_done, b * C4 + (m - C4 + 1))
                    for k in range(KC):
                        ins = nc.tensor.matmul(big[:, m % C4, :], winT[:, k, m * P:(m + 1) * P], xnT[:, k, bass.ds(b * SEQ, SEQ)],
                                               start=k == 0, stop=k == KC - 1)
                    ins.then_inc(z_ready if half else xc_ready, 1)

            def rows(b):
                pe.wait_ge(u_ready, b * C4 + C4)
                for k in range(C4):
                    ins = nc.tensor.matmul(c_ps[0:NX, 0, :], wxT[:, k, :], u_at(b, k), start=k == 0, stop=k == C4 - 1)
                ins.then_inc(xd_ready, 1)

            def steps(b):
                pe.wait_ge(xd_copied, b + 1)
                pe.wait_ge(pre_ready, b + 1)
                nc.tensor.matmul(b_ps[:, 0, :], c["ones"][NX - 1:NX, :], xd[NX - 1:NX, :], start=True, stop=True).then_inc(dt_ps_ready, 1)

            def u_at(b, k):
                return u[:, bass.ds(b, 1), k, :].rearrange("p b t -> p (b t)")

            def first(b):
                project(b, 0)
                project(b, 1)

            def both(b):
                rows(b)
                project(b + 1, 0)
                steps(b)
                project(b + 1, 1)

            def last(b):
                rows(b)
                steps(b)

            def program():
                pe.sem_inc(pre_ready, 1)
                batches(pe, first, both, last)
            run(pe, program)

        @block.vector
        def _(dve):
            V = nc.vector

            def convolve(b, m):
                ch = Chain(dve, conv_step, b * (C4 * (TAPS - 1)) + m * (TAPS - 1))
                dve.wait_ge(xc_ready, b * C4 + (m + 1))
                V.tensor_copy(xc[:, m, TAPS - 1:], big[:, m, :]).then_inc(xc_read, 1)
                dve.wait_ge(xc_read, b * C4 + (m + 1))
                if not (isinstance(b, int) and b == 0):
                    dve.wait_ge(u_ready, b * C4 + (m - C4 + 1))
                ch.step(V.tensor_scalar(conv[:, m], xc[:, m, 0:SEQ], conv_w[:, m, 0:1], cols[:, CONV_B, m:m + 1], ALU.mult, ALU.add))
                for k in range(1, TAPS):
                    ins = V.scalar_tensor_tensor(out=conv[:, m], in0=xc[:, m, k:k + SEQ], scalar=conv_w[:, m, k:k + 1], in1=conv[:, m],
                                                 op0=ALU.mult, op1=ALU.add)
                    if k < TAPS - 1:
                        ch.step(ins)
                ins.then_inc(conv_ready, 1)

            def split(b):
                ch = Chain(dve, split_step, b * 6)
                to = xd3[:, bass.ds(b, 1), :].rearrange("p b t -> p (b t)")
                dve.wait_ge(xd_ready, b + 1)
                ch.step(V.tensor_copy(xd, c_ps[0:NX, 0, :]))
                V.tensor_scalar(to[0:NR], xd[0:NR], 1.0, None, ALU.mult).then_inc(xd_copied, 1)
                dve.wait_ge(xd_copied, b + 1)
                ch.step(V.tensor_tensor(xd[0:NR], xd[0:NR], to[0:NR], ALU.subtract))
                ch.step(V.tensor_scalar(to[NR:2 * NR], xd[0:NR], 1.0, None, ALU.mult))
                ch.step(V.tensor_scalar(to[2 * NR:3 * NR], xd[0:NR], 1.0, None, ALU.mult))
                ch.step(V.tensor_tensor(xd[0:NR], xd[0:NR], to[2 * NR:3 * NR], ALU.subtract))
                ch.step(V.tensor_scalar(to[2 * NR:3 * NR], xd[0:NR], 1.0, None, ALU.mult))

            def bias(b):
                dve.wait_ge(dt_ps_ready, b + 1)
                for k in range(C4):
                    ins = V.tensor_scalar(pre[:, k], b_ps[:, 0, :], cols[:, W_DT, k:k + 1], cols[:, B_DT, k:k + 1], ALU.mult, ALU.add)
                ins.then_inc(pre_ready, 1)

            def clip_dt(b):
                ch = Chain(dve, dt_step, b * 2)
                dve.wait_ge(sp_ready, b + 1)
                to = dt[:, bass.ds(b, 1)].rearrange("p b c t -> p (b c t)")
                ch.step(V.scalar_tensor_tensor(out=to, in0=pre.rearrange("p c t -> p (c t)"), scalar=0.0,
                                               in1=softplus.rearrange("p c t -> p (c t)"), op0=ALU.max, op1=ALU.add))
                ch.step(V.tensor_scalar(to, to, 1e-4, 10.0, ALU.max, ALU.min))

            def first(b):
                for m in range(C4):
                    convolve(b, m)

            def both(b):
                split(b)
                convolve(b + 1, 0)
                convolve(b + 1, 1)
                if not (isinstance(b, int) and b == 0):
                    clip_dt(b - 1)
                bias(b)
                convolve(b + 1, 2)
                convolve(b + 1, 3)

            def last(b):
                split(b)
                clip_dt(b - 1)
                bias(b)
                clip_dt(b)

            def program():
                step = Chain(dve, split_done)
                step.step(V.memset(xc, 0.0))
                batches(dve, first, both, last)
            run(dve, program)

        @block.scalar
        def _(act):
            E = nc.scalar

            def activate(b):
                for m in range(C4):
                    act.wait_ge(z_ready, b * C4 + (m + 1))
                    if m == 0:
                        act.wait_ge(z_stored, b * 16 + 16)
                    E.activation(gate[:, m, :], big[:, m, :], ACT.Silu).then_inc(z_done, 1)

            def channels(b):
                for m in range(C4):
                    act.wait_ge(conv_ready, b * C4 + (m + 1))
                    act.sem_inc(taken, 1)
                    E.activation(u[:, bass.ds(b, 1), m, :], conv[:, None, m, :], ACT.Silu).then_inc(u_ready, 1)

            def softplus_tail(b):
                ch = Chain(act, act_step, b * 2)
                act.wait_ge(pre_ready, b + 2)
                ch.step(E.activation(softplus, pre, ACT.Abs))
                ch.step(E.activation(softplus, softplus, ACT.Exp, scale=-1.0))
                E.activation(softplus, softplus, ACT.Ln, bias=1.0).then_inc(sp_ready, 1)

            def first(b):
                channels(b)
                activate(b)

            def both(b):
                channels(b + 1)
                activate(b + 1)
                softplus_tail(b)

            def program():
                act.sem_inc(z_stored, 16)
                batches(act, first, both, softplus_tail)
            run(act, program)

        @block.sync
        def _(sp):
            def program():
                with sp.Fori(0, BATCH) as b:
                    sp.wait_ge(z_done, b * C4 + C4)
                    sp.dma_start(gate_dram[bass.ds(b, 1)].rearrange("b p c t -> p (b c) t"), gate).then_inc(z_stored, 16)
                sp.wait_ge(z_stored, 16 * BATCH + 16)
            run(sp, program)


def scan_states(G, nc, c, T, ps, w, hmax, gate_dram, dims, exact, run):
    ident = c["ident"]
    winT, wxT, woutT, cols, conv_w, A, sel = w
    big, b_ps, c_ps = ps
    DI, NST, TAPS, C4, NX = dims
    u_all, dt_all, dtu, xd3, dA, wd, rs = (T[n] for n in ("u", "dt", "dtu", "xd3", "dA", "w", "rs"))
    h_all, c_sb = T["h"], c["xn"][:, 0:2 * SEQ // DM, :].rearrange("p a b -> p (a b)").rearrange("p (n t) -> p n t", t=SEQ)
    WIDE = [P, C4, SEQ]
    (brow_ready, crow_ready, w_ready, clipped, dA_ready, scan_done, h_ready, c_copied, hC_ready, acc_done, y_copied, dtu_ready, exact_step,
     aexp, taken) = (G.sem(n) for n in (
         "brow_ready", "crow_ready", "w_ready", "clipped", "dA_ready", "scan_done", "h_ready", "c_copied", "hC_ready", "acc_done", "y_copied", "dtu_ready",
         "exact_step", "aexp", "taken"))

    def at(a, b):
        return a[:, bass.ds(b, 1)].rearrange("p b c t -> p (b c) t")

    with G.block() as block:
        @block.tensor
        def _(pe):
            def program():
                pe.sem_inc(acc_done, 2)
                with pe.Fori(0, BATCH) as b:
                    xd_b = xd3[:, bass.ds(b, 1), :].rearrange("p b t -> p (b t)")

                    def b_row(n):
                        pe.wait_ge(w_ready, b * NST + (n + 1))
                        nc.tensor.matmul(b_ps[:, n % 2, :], sel[:, n, :], xd_b, start=True, stop=True).then_inc(brow_ready, 1)

                    def c_row(n):
                        pe.wait_ge(c_copied, b * NST + (n + 1))
                        nc.tensor.matmul(c_ps[:, n % 2, :], sel[:, NST + n, :], xd_b, start=True, stop=True).then_inc(crow_ready, 1)

                    for n in range(2):
                        b_row(n)
                        c_row(n)
                    b_row(2)
                    pe.wait_ge(y_copied, b + 1)
                    for n in range(NST):
                        if n + 3 < NST:
                            b_row(n + 3)
                        if n + 2 < NST:
                            c_row(n + 2)
                        pe.wait_ge(hC_ready, b * NST + (n + 3))
                        for k in range(C4):
                            ins = nc.tensor.matmul(big[:, k, :], ident[:], dA[:, n % 3, k, :], start=n == 0, stop=n == NST - 1)
                        ins.then_inc(acc_done, 1)
            run(pe, program)

        @block.vector
        def _(dve):
            V = nc.vector

            def program():
                dve.sem_inc(w_ready, 2)
                with dve.Fori(0, BATCH) as b:
                    V.tensor_tensor(dtu[:], at(dt_all, b), at(u_all, b), ALU.mult).then_inc(dtu_ready, 1)
                    dve.wait_ge(dtu_ready, b + 1)

                    def drive(n):
                        dve.wait_ge(brow_ready, b * NST + (n + 1))
                        V.tensor_tensor(wd[:, n % 2], dtu[:], b_ps[:, n % 2, None, :].to_broadcast(WIDE), ALU.mult).then_inc(w_ready, 1)
                        dve.wait_ge(w_ready, b * NST + (n + 3))
                        V.tensor_scalar(wd[:, n % 2], wd[:, n % 2], 10.0, -10.0, ALU.min, ALU.max).then_inc(clipped, 1)

                    def scan(n):
                        dAn, wn, h = dA[:, n % 3], wd[:, n % 2], h_all[:, n % 2]
                        dve.wait_ge(clipped, b * NST + (n + 1))
                        dve.wait_ge(dA_ready, b * NST + (n + 1))
                        dve.wait_ge(hC_ready, b * NST + (n + 1))
                        if exact:
                            scan_steps(n, dAn, wn, h)
                            return
                        V.tensor_tensor_scan(out=h.rearrange("p c t -> p (c t)"), data0=dAn.rearrange("p c t -> p (c t)"),
                                             data1=wn.rearrange("p c t -> p (c t)"), initial=0.0, op0=ALU.mult, op1=ALU.add).then_inc(h_ready, 1)
                        dve.wait_ge(h_ready, b * NST + (n + 1))
                        V.tensor_reduce(hmax[:, bass.ds(b * NST + n, 1)], h[:, :, 0:SEQ:4], mybir.AxisListType.XY, ALU.max,
                                        apply_absolute_value=True)

                    def scan_steps(n, dAn, wn, h):
                        ch = Chain(dve, scan_done, (b * NST + n) * 2)
                        ch.step(V.tensor_scalar(dAn, dAn, EXP_M20, None, ALU.max))
                        ch.step(V.tensor_copy(h[:, :, 0], wn[:, :, 0]))
                        V.tensor_copy(rs[:, 0:1], rs[:, 0:1])
                        with dve.Fori(1, SEQ) as t:
                            st = Chain(dve, exact_step, (b * NST + n) * (3 * (SEQ - 1)) + (t - 1) * 3)
                            now, before = h[:, :, bass.ds(t, 1)], h[:, :, bass.ds(t - 1, 1)]
                            st.step(V.tensor_tensor(now, before, dAn[:, :, bass.ds(t, 1)], ALU.mult))
                            st.step(V.tensor_tensor(now, now, wn[:, :, bass.ds(t, 1)], ALU.add))
                            st.step(V.tensor_scalar(now, now, 100.0, -100.0, ALU.min, ALU.max))
                        V.tensor_copy(rs[:, 0:1], rs[:, 0:1]).then_inc(h_ready, 1)

                    drive(0)
                    for n in range(NST):
                        if n + 1 < NST:
                            drive(n + 1)
                        scan(n)
            run(dve, program)

        @block.gpsimd
        def _(pool):
            def program():
                pool.sem_inc(hC_ready, 2)
                with pool.Fori(0, BATCH) as b:
                    for n in range(NST):
                        pool.wait_ge(c_copied, b * NST + (n + 3))
                        pool.wait_ge(h_ready, b * NST + (n + 1))
                        nc.gpsimd.tensor_tensor(dA[:, n % 3], h_all[:, n % 2], c_sb[:, n % 2, None, :].to_broadcast(WIDE),
                                                ALU.mult).then_inc(hC_ready, 1)
            run(pool, program)

        @block.scalar
        def _(act):
            E = nc.scalar

            def program():
                act.sem_inc(y_copied, 1)
                act.sem_inc(c_copied, 2)
                with act.Fori(0, BATCH) as b:
                    for n in range(NST):
                        act.wait_ge(acc_done, b * NST + (max(n - 2, 0) + 2))
                        act.sem_inc(taken, 1)
                        E.activation(dA[:, n % 3], at(dt_all, b), ACT.Exp, scale=A[:, n:n + 1]).then_inc(aexp, 1)
                        act.wait_ge(aexp, b * NST + (n + 1))
                        E.mul(dA[:, n % 3, :, 0], dA[:, n % 3, :, 0], 0.0).then_inc(dA_ready, 1)
                        act.wait_ge(crow_ready, b * NST + (n + 1))
                        act.wait_ge(hC_ready, b * NST + (n + 1))
                        E.copy(c_sb[:, n % 2, :], c_ps[:, n % 2, :]).then_inc(c_copied, 1)
                    act.wait_ge(dtu_ready, b + 1)
                    act.wait_ge(acc_done, b * NST + (NST + 2))
                    act.sem_inc(taken, 1)
                    E.copy(at(dt_all, b), big[:]).then_inc(y_copied, 1)
            run(act, program)


def scan_outputs(G, nc, c, T, ps, w, hmax, gate_dram, dims, exact, run):
    xn, ones = c["xn"], c["ones"]
    winT, wxT, woutT, cols, conv_w, A, sel = w
    big, b_ps, c_ps = ps
    DI, NST, TAPS, C4, NX = dims
    u_all, y_all, rs, sq, gate = T["u"], T["dt"], T["rs"], T["dA"][:, 0], T["w"]
    y_done = T["dA"][:, 1]
    D_PAR, LN_G, LN_B = 2, 3, 4
    WIDE = [P, C4, SEQ]
    (mean_ready, centred, sq_ready, var_ready, v_ready, std_ready, yf_ready, delta_ready, delta_copied, gate_in,
     dstep, taken) = (G.sem(n) for n in (
         "mean_ready", "centred", "sq_ready", "var_ready", "v_ready", "std_ready", "yf_ready", "delta_ready", "delta_copied",
         "gate_in", "dstep", "taken"))

    def at(a, b):
        return a[:, bass.ds(b, 1)].rearrange("p b c t -> p (b c) t")

    def batches(eng, first, both, last):
        first(0)
        with eng.Fori(0, BATCH - 2) as b:
            both(b)
        both(BATCH - 2)
        last(BATCH - 1)

    with G.block() as block:
        @block.tensor
        def _(pe):
            def mean(b):
                pe.wait_ge(centred, b + 1)
                for k in range(C4):
                    ins = nc.tensor.matmul(b_ps[:, 0, :], ones[:], y_all[:, bass.ds(b, 1), k, :].rearrange("p b t -> p (b t)"),
                                           start=k == 0, stop=k == C4 - 1)
                ins.then_inc(mean_ready, 1)

            def variance(b):
                pe.wait_ge(sq_ready, b + 1)
                pe.wait_ge(v_ready, b + 1)
                for k in range(C4):
                    ins = nc.tensor.matmul(b_ps[:, 1, :], ones[:], sq[:, k, :], start=k == 0, stop=k == C4 - 1)
                ins.then_inc(var_ready, 1)

            def project(b):
                pe.wait_ge(yf_ready, b + 1)
                for q in range(QT):
                    pe.wait_ge(delta_copied, b * QT + (q + 1))
                    for k in range(C4):
                        ins = nc.tensor.matmul(big[:, q, 0:DM], y_done[:, k, q * P:(q + 1) * P], woutT[:, k, :], start=k == 0, stop=k == C4 - 1)
                    ins.then_inc(delta_ready, 1)

            def first(b):
                mean(b)
                variance(b)
                mean(b + 1)

            def both(b):
                variance(b + 1)
                if not isinstance(b, int):
                    mean(b + 2)
                project(b)

            def program():
                pe.sem_inc(centred, 1)
                batches(pe, first, both, project)
            run(pe, program)

        @block.vector
        def _(dve):
            V = nc.vector
            STEPS = 2 + 2 * C4

            def centre(b):
                dve.wait_ge(mean_ready, b + 1)
                for m in range(C4):
                    y = y_all[:, bass.ds(b, 1), m, :].rearrange("p b t -> p (b t)")
                    ins = V.scalar_tensor_tensor(out=y, in0=b_ps[:, 0, :], scalar=-1.0 / DI, in1=y, op0=ALU.mult, op1=ALU.add)
                ins.then_inc(centred, 1)

            def finish(b):
                ch = Chain(dve, dstep, b * STEPS)
                dve.wait_ge(std_ready, b + 1)
                ch.step(V.reciprocal(rs[:], rs[:]))
                dve.wait_ge(delta_ready, b * QT + 1)
                y = y_done
                ch.step(V.tensor_tensor(y, at(y_all, b), rs[:, None, :].to_broadcast(WIDE), ALU.mult))
                for m in range(C4):
                    ins = V.tensor_scalar(y[:, m, :], y[:, m, :], cols[:, LN_G, m:m + 1], cols[:, LN_B, m:m + 1], ALU.mult, ALU.add)
                    ch.step(ins)
                    u = u_all[:, bass.ds(b, 1), m, :].rearrange("p b t -> p (b t)")
                    ch.step(V.scalar_tensor_tensor(out=y[:, m, :], in0=u, scalar=cols[:, D_PAR, m:m + 1], in1=y[:, m, :],
                                                   op0=ALU.mult, op1=ALU.add))
                dve.wait_ge(gate_in, b * 16 + 16)
                V.tensor_tensor(y, y, gate[:, 0], ALU.mult).then_inc(yf_ready, 1)

            def variance(b):
                dve.wait_ge(var_ready, b + 1)
                V.tensor_scalar(rs[:], b_ps[:, 1, :], 1.0 / DI, LN_EPS, ALU.mult, ALU.add).then_inc(v_ready, 1)

            def first(b):
                centre(b)
                variance(b)

            def both(b):
                centre(b + 1)
                finish(b)
                variance(b + 1)

            def program():
                dve.sem_inc(v_ready, 1)
                dve.sem_inc(delta_ready, 1)
                batches(dve, first, both, finish)
            run(dve, program)

        @block.scalar
        def _(act):
            E = nc.scalar

            def square(b):
                act.wait_ge(centred, b + 2)
                if not (isinstance(b, int) and b == 0):
                    act.wait_ge(var_ready, b)
                act.sem_inc(taken, 1)
                E.activation(sq, at(y_all, b), ACT.Square).then_inc(sq_ready, 1)

            def root(b):
                act.wait_ge(v_ready, b + 2)
                E.activation(rs[:], rs[:], ACT.Sqrt).then_inc(std_ready, 1)

            def copy_out(b):
                for q in range(QT):
                    act.wait_ge(delta_ready, b * QT + (q + 2))
                    E.copy(xn[:, b * QT + q, :], big[:, q, 0:DM]).then_inc(delta_copied, 1)

            def first(b):
                square(b)
                root(b)

            def both(b):
                square(b + 1)
                root(b + 1)
                copy_out(b)

            def program():
                act.sem_inc(delta_copied, 4)
                batches(act, first, both, copy_out)
            run(act, program)

        @block.sync
        def _(sp):
            def program():
                sp.dma_start(gate[:, 0], gate_dram[0]).then_inc(gate_in, 16)
                with sp.Fori(1, BATCH) as b:
                    sp.wait_ge(yf_ready, b)
                    sp.dma_start(gate[:, 0], gate_dram[bass.ds(b, 1)].rearrange("b p c t -> p (b c) t")).then_inc(gate_in, 16)
            run(sp, program)


EXP_M20 = 2.0611536224385579e-09


def zero_fill_slots(nc, S, c):
    zeros = S.sb("zeros", [P, DM])
    zeroed = S.sem("zeroed")
    for n, n_exp in enumerate((7, 8)):
        rows = n_exp * (TOK // NE)
        disp = nc.dram_tensor(f"slots{n}", [rows, DM], F32, kind="Internal").ap()
        eout = nc.dram_tensor(f"expert_rows{n}", [rows, DM], F32, kind="Internal").ap()
        c[f"moe{n}"] = (disp, eout, S.sem(f"slots_zeroed{n}"))
    with S.block() as block:
        @block.vector
        def _(dve):
            nc.vector.memset(zeros[:], 0.0).then_inc(zeroed, 1)

        @block.scalar
        def _(act):
            act.wait_ge(zeroed, 1)
            for n in range(2):
                disp, _, filled = c[f"moe{n}"]
                act.dma_start(disp.rearrange("(t p) d -> p t d", p=P),
                              zeros[:, None, :].to_broadcast([P, disp.shape[0] // P, DM])).then_inc(filled, 16)


def decoder_kernel(nc, w, out, first=0, last=12):
    c = {}

    def of(prefix):
        return {n[len(prefix):]: ap for n, ap in w.items() if n.startswith(prefix)}

    def stage(n):
        return first <= n < last

    with Scope(nc, "g") as S:
        c["x"] = S.sb("x", [P, TILES, DM])
        c["xn"] = S.sb("xn", [P, TILES, DM])
        c["xnT"] = S.sb("xnT", [P, KC, TOK])
        setup_constants(nc, S, c)
        x_loaded, x_stored = S.sem("x_loaded"), S.sem("x_stored")
        x_dram = w["x"].rearrange("b (t p) d -> p (b t) d", p=P)
        out_dram = out.rearrange("b (t p) d -> p (b t) d", p=P)
        c["ctx_dram"] = w["ctx_768"].rearrange("b k c -> (b k) c").rearrange("(t p) c -> p t c", p=P)
        zero_fill_slots(nc, S, c)
        with S.block() as block:
            @block.sync
            def _(sp):
                for q in range(4):
                    sp.dma_start(c["x"][:, 4 * q:4 * q + 4, :], x_dram[:, 4 * q:4 * q + 4, :]).then_inc(x_loaded, 16)
                sp.wait_ge(x_loaded, 64)
        if stage(0):
            c["norm"] = ("l0a", None)
            self_attention(nc, "l0at", c, of("L0_attn_"), given=False, window=True)
        if stage(1):
            c["norm"] = ("l0b", None)
            cross_attention(nc, "l0x", c, of("L0_xattn_"), dh=64)
        if stage(2):
            c["norm"] = ("l0c", None)
            mixture(nc, "l0f", c, of("L0_ffn_"), 7, 2, *c["moe0"])
        if stage(3):
            c["norm"] = ("l1a", None)
            self_attention(nc, "l1at", c, of("L1_attn_"), given=True, window=False)
        if stage(4):
            c["norm"] = ("l1b", None)
            cross_attention(nc, "l1x", c, of("L1_xattn_"), dh=16, out_in=True)
        if stage(5):
            c["norm"] = ("l1c", None)
            mixture(nc, "l1f", c, of("L1_ffn_"), 8, 1, *c["moe1"])
        if stage(6):
            c["norm"] = ("l2a", None)
            selective_scan(nc, "l2s", c, of("L2_attn_"))
        if stage(7):
            l2x = of("L2_xattn_")
            c["norm"] = ("l2b", (l2x["g_x"], l2x["b_x"]))
            cross_attention(nc, "l2x", c, l2x, dh=64, norm_ctx=True)
        if stage(8):
            c["norm"] = ("l2c", None)
            quantised_ffn(nc, "l2f", c, of("L2_ffn_"))
        if stage(9):
            c["norm"] = ("l3a", None)
            state_space(nc, "l3s", c, of("L3_attn_"))
        if stage(10):
            c["norm"] = ("l3b", None)
            cross_attention(nc, "l3x", c, of("L3_xattn_"), dh=16, clamp=1e4)
        if stage(11):
            c["norm"] = ("l3c", None)
            gated_linear(nc, "l3f", c, of("L3_ffn_"), 100)
        with S.block() as block:
            @block.sync
            def _(sp):
                for q in range(4):
                    sp.dma_start(out_dram[:, 4 * q:4 * q + 4, :], c["x"][:, 4 * q:4 * q + 4, :]).then_inc(x_stored, 16)
                sp.wait_ge(x_stored, 64)
                for n in range(2):
                    sp.wait_ge(c[f"moe{n}"][2], 16)


_OUTS = [((4, 512, 256), "float32")]


def kernel(**inputs):
    import numpy as _np
    import concourse.bacc as _bacc
    from concourse import mybir as _mybir
    from concourse.bass_utils import run_bass_kernel_spmd as _run

    nc = _bacc.Bacc("TRN2", target_bir_lowering=False, num_devices=1)
    arrays, args = {}, {}
    for name, value in inputs.items():
        a = _np.ascontiguousarray(value)
        arrays[f"in_{name}_dram"] = a
        args[name] = nc.dram_tensor(f"in_{name}_dram", a.shape, _mybir.dt.from_np(a.dtype), kind="ExternalInput").ap()
    shape, dtype = _OUTS[0]
    out = nc.dram_tensor("out_0_dram", shape, _mybir.dt.from_np(_np.dtype(dtype)), kind="ExternalOutput").ap()
    decoder_kernel(nc, args, out)
    r = _run(nc, [arrays], core_ids=[0])
    return r.results[0]["out_0_dram"]
```
